# Optimizing a Trainium2 kernel written in Bass

```python
import numpy as np
import jax
import jax.numpy as jnp

def _softmax(x, axis=-1):
    return jax.nn.softmax(x, axis=axis)

def _gelu(x):
    return jax.nn.gelu(x, approximate=True)

def _silu(x):
    return jax.nn.silu(x)

def _sigmoid(x):
    return jax.nn.sigmoid(x)

def _layernorm(x, axis=-1, eps=1e-05):
    m = jnp.mean(x, axis=axis, keepdims=True)
    v = jnp.var(x, axis=axis, keepdims=True)
    return (x - m) / jnp.sqrt(v + eps)

def _scatter_add(tgt, idx, src, axis=0):
    return tgt.at[idx].add(src)

def _segment_sum(src, seg, n):
    return jax.ops.segment_sum(src, seg, n)
kernel_name = 'mk_perceiver_d4_seqx_r8_461422'

def setup_inputs(seed: int=0):
    np.random.seed(seed)
    _w = jnp.asarray

    def _rec_inputs():
        import jax
        import jax.numpy as jnp
        _rk = jax.random.key(seed)
        x = 7.22e-05 + 1 * jax.random.normal(jax.random.fold_in(_rk, 1), (1, 128, 128), jnp.float32)
        _lenS = 128 - jax.random.randint(jax.random.fold_in(_rk, 7), (1,), 0, max(1, 128 // 4) + 1, jnp.int32)
        _lenS2 = 2048 - jax.random.randint(jax.random.fold_in(_rk, 8), (1,), 0, max(1, 2048 // 4) + 1, jnp.int32)
        _ctx_1024P = jax.random.normal(jax.random.fold_in(_rk, 11), (1, 16, 128), jnp.float32)
        _ctx_1024c = jax.random.dirichlet(jax.random.fold_in(_rk, 511), 0.3 * jnp.ones((16,), jnp.float32), (1, 2048))
        _ctx_1024t = jnp.einsum('bsk,bkd->bsd', _ctx_1024c, _ctx_1024P)
        _ctx_1024t = _ctx_1024t * jax.lax.rsqrt(jnp.mean(jnp.square(_ctx_1024t)) + 1e-12) * 0.953939
        ctx_1024 = -0.000514642 + 1.00011 * (_ctx_1024t + 0.3 * jax.random.normal(jax.random.fold_in(_rk, 611), (1, 2048, 128), jnp.float32))
        _validS = jnp.arange(128)[None, :] < _lenS[:, None]
        _validS2 = jnp.arange(2048)[None, :] < _lenS2[:, None]
        _causal = jnp.tril(jnp.ones((128, 128), dtype=bool))
        mask_Bx1x1xS2_if1 = jnp.where(jnp.ones((1, 1, 1, 2048), dtype=bool), 1, 0).astype(jnp.int32)
        return (x, ctx_1024, mask_Bx1x1xS2_if1)
    x, ctx_1024, mask_Bx1x1xS2_if1 = _rec_inputs()

    def _L0_xattn_setup():
        import jax, jax.numpy as jnp
        import numpy as np
        B, L_ENC, L_DEC, D = (16, 64, 128, 128)
        key = jax.random.key(seed)
        k1, k2, k3, k4, k5, k6 = jax.random.split(key, 6)
        encoder_hc = jax.random.normal(k1, (B, L_ENC, D), dtype=jnp.float32)
        decoder_hq = jax.random.normal(k2, (B, L_DEC, D), dtype=jnp.float32)
        w_sim = jax.random.normal(k3, (3 * D,), dtype=jnp.float32) * 0.02
        b_sim = jax.random.normal(k4, (1,), dtype=jnp.float32) * 0.02
        W_qv = jax.random.normal(k5, (4 * D, D), dtype=jnp.float32) * 0.02
        b_qv = jax.random.normal(k6, (D,), dtype=jnp.float32) * 0.02
        return {'encoder_hc': encoder_hc, 'decoder_hq': decoder_hq, 'w_sim': w_sim, 'b_sim': b_sim, 'W_qv': W_qv, 'b_qv': b_qv}
    _L0_xattn_all = _L0_xattn_setup()
    _L0_xattn_in = {k: v for k, v in _L0_xattn_all.items() if k in ('w_sim', 'b_sim', 'W_qv', 'b_qv')}
    del _L0_xattn_all

    def _L0_attn_setup():
        import math
        import jax, jax.numpy as jnp
        import numpy as np
        N_HEAD = 16

        def _rope_cos_sin(l, head_dim):
            scale = jnp.arange(0, head_dim, 2, dtype=jnp.float32)[:head_dim // 2]
            freqs = 1.0 / 10000.0 ** scale
            angles = jnp.arange(l, dtype=jnp.float32)[:, None] * freqs[None, :]
            return (jnp.cos(angles), jnp.sin(angles))

        def _rope_apply(x, cos, sin):
            b, l, h, hd = x.shape
            xp = x.astype(jnp.float32).reshape(b, l, h, hd // 2, 2)
            xr, xi = (xp[..., 0], xp[..., 1])
            c = cos[None, :, None, :]
            s = sin[None, :, None, :]
            out_r = xr * c - xi * s
            out_i = xr * s + xi * c
            out = jnp.stack([out_r, out_i], axis=-1).reshape(b, l, h, hd)
            return out.astype(x.dtype)
        key = jax.random.key(seed)
        ks = jax.random.split(key, 9)
        b, l, d = (2, 256, 128)
        sc = 1.0 / math.sqrt(d)
        inp = {'x': jax.random.normal(ks[0], (b, l, d), dtype=jnp.float32), 'Wq': jax.random.normal(ks[1], (d, d), dtype=jnp.float32) * sc, 'bq': jnp.zeros((d,), dtype=jnp.float32), 'Wk': jax.random.normal(ks[2], (d, d), dtype=jnp.float32) * sc, 'bk': jnp.zeros((d,), dtype=jnp.float32), 'Wv': jax.random.normal(ks[3], (d, d), dtype=jnp.float32) * sc, 'bv': jnp.zeros((d,), dtype=jnp.float32), 'Wo': jax.random.normal(ks[4], (d, d), dtype=jnp.float32) * sc, 'bo': jnp.zeros((d,), dtype=jnp.float32)}
        return inp
    _L0_attn_all = _L0_attn_setup()
    _L0_attn_in = {k: v for k, v in _L0_attn_all.items() if k in ('Wq', 'bq', 'Wk', 'bk', 'Wv', 'bv', 'Wo', 'bo')}
    del _L0_attn_all

    def _L0_ffn_setup():
        import jax, jax.numpy as jnp
        import numpy as np
        import math
        D = 128
        H = 16
        E = 8
        TOPK = 2
        LAT = D // 2
        KPH = LAT // H
        HD = D // H

        def _forward(hs, q_w, q_b, k_w, k_b, v_w, v_b, o_w, o_b, router_w, router_b, w1, b1, w2, b2):
            B, S, _ = hs.shape
            Q = (hs @ q_w + q_b).reshape(B, S, H, HD).transpose(0, 2, 1, 3)
            K = (hs @ k_w + k_b).reshape(B, S, H, KPH).transpose(0, 2, 1, 3)
            V = (hs @ v_w + v_b).reshape(B, S, H, KPH).transpose(0, 2, 1, 3)
            scores = jnp.einsum('bhsk,bhtk->bhst', Q[..., :KPH], K) / math.sqrt(KPH)
            attn = jax.nn.softmax(scores, axis=-1)
            ao = jnp.einsum('bhst,bhtv->bhsv', attn, V)
            ao = ao.transpose(0, 2, 1, 3).reshape(B, S, H * KPH)
            ao = jnp.concatenate([ao, jnp.zeros((B, S, D - LAT), ao.dtype)], axis=-1)
            mla_out = ao @ o_w + o_b
            probs = jax.nn.softmax(mla_out @ router_w + router_b, axis=-1)
            topw, topi = jax.lax.top_k(probs, TOPK)
            topw = topw / (topw.sum(-1, keepdims=True) + 1e-08)
            combine = jnp.sum(jax.nn.one_hot(topi, E, dtype=probs.dtype) * topw[..., None], axis=-2)
            h1 = jnp.einsum('bsd,edf->ebsf', mla_out, w1) + b1[:, None, None, :]
            h1 = jax.nn.gelu(h1, approximate=False)
            h2 = jnp.einsum('ebsf,efd->ebsd', h1, w2) + b2[:, None, None, :]
            moe_out = jnp.einsum('bse,ebsd->bsd', combine, h2)
            return hs + 0.3 * moe_out
        key = jax.random.key(seed)
        ks = jax.random.split(key, 16)
        s = 0.02
        inp = {'hidden_states': jax.random.normal(ks[0], (2, 256, D), jnp.float32), 'q_w': jax.random.normal(ks[1], (D, D), jnp.float32) * s, 'q_b': jnp.zeros((D,), jnp.float32), 'k_w': jax.random.normal(ks[2], (D, LAT), jnp.float32) * s, 'k_b': jnp.zeros((LAT,), jnp.float32), 'v_w': jax.random.normal(ks[3], (D, LAT), jnp.float32) * s, 'v_b': jnp.zeros((LAT,), jnp.float32), 'o_w': jax.random.normal(ks[4], (D, D), jnp.float32) * s, 'o_b': jnp.zeros((D,), jnp.float32), 'router_w': jax.random.normal(ks[5], (D, E), jnp.float32) * s, 'router_b': jnp.zeros((E,), jnp.float32), 'w1': jax.random.normal(ks[6], (E, D, 2 * D), jnp.float32) * s, 'b1': jnp.zeros((E, 2 * D), jnp.float32), 'w2': jax.random.normal(ks[7], (E, 2 * D, D), jnp.float32) * s, 'b2': jnp.zeros((E, D), jnp.float32)}
        return inp
    _L0_ffn_all = _L0_ffn_setup()
    _L0_ffn_in = {k: v for k, v in _L0_ffn_all.items() if k in ('q_w', 'q_b', 'k_w', 'k_b', 'v_w', 'v_b', 'o_w', 'o_b', 'router_w', 'router_b', 'w1', 'b1', 'w2', 'b2')}
    del _L0_ffn_all

    def _L1_xattn_setup():
        import jax, jax.numpy as jnp
        import numpy as np
        M, T, D, H = (2, 256, 128, 16)
        HD = D // H
        SCALE = 1.0 / np.sqrt(D).astype(np.float32)
        key = jax.random.key(seed)
        ks = jax.random.split(key, 8)

        def lin(k):
            kw, kb = jax.random.split(k)
            W = jax.random.normal(kw, (D, D), dtype=jnp.float32) * (1.0 / np.sqrt(D))
            b = jax.random.normal(kb, (D,), dtype=jnp.float32) * 0.01
            return (W, b)
        Wq, bq = lin(ks[0])
        Wk, bk = lin(ks[1])
        Wv, bv = lin(ks[2])
        Wo, bo = lin(ks[3])
        Q = jax.random.normal(ks[4], (M, T, D), dtype=jnp.float32)
        K = jax.random.normal(ks[5], (M, T, D), dtype=jnp.float32)
        V = jax.random.normal(ks[6], (M, T, D), dtype=jnp.float32)
        mask = jnp.ones((M, 1, 1, T), dtype=jnp.int32)
        return {'Q': Q, 'K': K, 'V': V, 'mask': mask, 'Wq': Wq, 'bq': bq, 'Wk': Wk, 'bk': bk, 'Wv': Wv, 'bv': bv, 'Wo': Wo, 'bo': bo}
    _L1_xattn_all = _L1_xattn_setup()
    _L1_xattn_in = {k: v for k, v in _L1_xattn_all.items() if k in ('Wq', 'bq', 'Wk', 'bk', 'Wv', 'bv', 'Wo', 'bo')}
    del _L1_xattn_all

    def _L1_attn_setup():
        import jax, jax.numpy as jnp
        import numpy as np
        NUM_HEADS = 32
        EPS = 1e-15
        key = jax.random.key(seed)
        k1, k2, k3, k4 = jax.random.split(key, 4)
        B, N, C = (8, 512, 128)
        x = jax.random.normal(k1, (B, N, C), dtype=jnp.float32)
        qkv_weight = jax.random.normal(k2, (3 * C, C), dtype=jnp.float32) * C ** (-0.5)
        proj_weight = jax.random.normal(k3, (C, C), dtype=jnp.float32) * C ** (-0.5)
        proj_bias = jax.random.normal(k4, (C,), dtype=jnp.float32) * 0.01
        return {'x': x, 'qkv_weight': qkv_weight, 'proj_weight': proj_weight, 'proj_bias': proj_bias}
    _L1_attn_all = _L1_attn_setup()
    _L1_attn_in = {k: v for k, v in _L1_attn_all.items() if k in ('qkv_weight', 'proj_weight', 'proj_bias')}
    del _L1_attn_all

    def _L1_ffn_setup():
        import jax, jax.numpy as jnp
        import numpy as np
        D = 128
        LW = 16
        DEPTH = 8
        NN = 2 ** DEPTH - 1
        NL = 2 ** DEPTH
        B, S = (2, 128)

        def _fff(x, nw, nb, w1, b1, w2, b2, act):
            node = jnp.zeros(x.shape[:2], dtype=jnp.int32)
            for _ in range(DEPTH):
                logit = jnp.einsum('bsd,bsd->bs', x, nw[node]) + nb[node]
                node = 2 * node + 1 + (logit > 0).astype(jnp.int32)
            leaf = node - NN
            h = act(jnp.einsum('bsd,bsdl->bsl', x, w1[leaf]) + b1[leaf])
            return jnp.einsum('bsl,bsld->bsd', h, w2[leaf]) + b2[leaf]

        def _forward(x, q_nw, q_nb, q_w1, q_b1, q_w2, q_b2, k_nw, k_nb, k_w1, k_b1, k_w2, k_b2, v_nw, v_nb, v_w1, v_b1, v_w2, v_b2, f_nw, f_nb, f_w1, f_b1, f_w2, f_b2):
            mu = jnp.mean(x, -1, keepdims=True)
            sd = jnp.std(x, -1, ddof=1, keepdims=True)
            xn = (x - mu) / jnp.sqrt(sd + 1e-05)
            relu = jax.nn.relu
            q = _fff(xn, q_nw, q_nb, q_w1, q_b1, q_w2, q_b2, relu)
            k = _fff(xn, k_nw, k_nb, k_w1, k_b1, k_w2, k_b2, relu)
            v = _fff(xn, v_nw, v_nb, v_w1, v_b1, v_w2, v_b2, relu)
            att = jax.nn.softmax(jnp.einsum('bqd,bkd->bqk', q, k) / jnp.sqrt(jnp.float32(D)), axis=-1)
            y = xn + jnp.einsum('bqk,bkd->bqd', att, v)
            gelu = lambda t: jax.nn.gelu(t, approximate=False)
            return y + _fff(y, f_nw, f_nb, f_w1, f_b1, f_w2, f_b2, gelu)

        def _make_fff_params(key, scale_in, scale_leaf):
            ks = jax.random.split(key, 4)
            nw = jax.random.normal(ks[0], (NN, D), jnp.float32) * scale_in
            nb = jnp.zeros((NN,), jnp.float32)
            w1 = jax.random.normal(ks[1], (NL, D, LW), jnp.float32) * scale_in
            b1 = jax.random.normal(ks[2], (NL, LW), jnp.float32) * 0.01
            w2 = jax.random.normal(ks[3], (NL, LW, D), jnp.float32) * scale_leaf
            b2 = jnp.zeros((NL, D), jnp.float32)
            return (nw, nb, w1, b1, w2, b2)
        key = jax.random.key(seed)
        kx, kq, kk, kv, kf = jax.random.split(key, 5)
        s_in = 1.0 / np.sqrt(D)
        s_lf = 1.0 / np.sqrt(LW)
        inp = {'x': jax.random.normal(kx, (B, S, D), jnp.float32)}
        for name, kk_ in (('q', kq), ('k', kk), ('v', kv), ('f', kf)):
            nw, nb, w1, b1, w2, b2 = _make_fff_params(kk_, s_in, s_lf)
            inp.update({f'{name}_nw': nw, f'{name}_nb': nb, f'{name}_w1': w1, f'{name}_b1': b1, f'{name}_w2': w2, f'{name}_b2': b2})
        return inp
    _L1_ffn_all = _L1_ffn_setup()
    _L1_ffn_in = {k: v for k, v in _L1_ffn_all.items() if k in ('q_nw', 'q_nb', 'q_w1', 'q_b1', 'q_w2', 'q_b2', 'k_nw', 'k_nb', 'k_w1', 'k_b1', 'k_w2', 'k_b2', 'v_nw', 'v_nb', 'v_w1', 'v_b1', 'v_w2', 'v_b2', 'f_nw', 'f_nb', 'f_w1', 'f_b1', 'f_w2', 'f_b2')}
    del _L1_ffn_all

    def _L2_xattn_setup():
        import jax, jax.numpy as jnp
        import numpy as np
        EMBED = 128
        HEADS = 16
        HEAD_DIM = EMBED // HEADS
        key = jax.random.key(seed)
        ks = jax.random.split(key, 7)
        B, Sd, Se = (4, 256, 256)
        dec = jax.random.normal(ks[0], (B, Sd, EMBED), dtype=jnp.float32)
        enc = jax.random.normal(ks[1], (B, Se, EMBED), dtype=jnp.float32)
        scale = 1.0 / np.sqrt(EMBED)
        W_q = jax.random.normal(ks[2], (EMBED, EMBED), dtype=jnp.float32) * scale
        W_k = jax.random.normal(ks[3], (EMBED, EMBED), dtype=jnp.float32) * scale
        W_v = jax.random.normal(ks[4], (EMBED, EMBED), dtype=jnp.float32) * scale
        W_o = jax.random.normal(ks[5], (EMBED, EMBED), dtype=jnp.float32) * scale
        b_o = jax.random.normal(ks[6], (EMBED,), dtype=jnp.float32) * 0.01
        return {'decoder_input': dec, 'encoder_output': enc, 'W_q': W_q, 'W_k': W_k, 'W_v': W_v, 'W_o': W_o, 'b_o': b_o}
    _L2_xattn_all = _L2_xattn_setup()
    _L2_xattn_in = {k: v for k, v in _L2_xattn_all.items() if k in ('W_q', 'W_k', 'W_v', 'W_o', 'b_o')}
    del _L2_xattn_all

    def _L2_attn_setup():
        import jax, jax.numpy as jnp
        import numpy as np
        DIM = 128
        HEADS = 16
        HEAD_DIM = DIM // HEADS
        NUM_FILTERS = 4
        NUM_TAPS = 101
        RES = 64

        def _fir_fft(c, sig):
            R = sig.shape[0]
            L = R + c.shape[0] - 1
            out = jnp.fft.ifft(jnp.fft.fft(sig, n=L) * jnp.fft.fft(c, n=L)).real
            return out[:R]
        key = jax.random.key(seed)
        ks = jax.random.split(key, 5)
        B, S = (2, 256)
        x = jax.random.normal(ks[0], (B, S, DIM), dtype=jnp.float32)
        Wqkv = jax.random.normal(ks[1], (3 * DIM, DIM), dtype=jnp.float32) * DIM ** (-0.5)
        Wout = jax.random.normal(ks[2], (DIM, DIM), dtype=jnp.float32) * DIM ** (-0.5)
        Wpos = jax.random.normal(ks[3], (HEADS, NUM_FILTERS), dtype=jnp.float32) * 0.5
        coeffs = jax.random.normal(ks[4], (NUM_FILTERS, NUM_TAPS), dtype=jnp.float32) * 0.05
        return {'x': x, 'Wqkv': Wqkv, 'Wout': Wout, 'Wpos': Wpos, 'coeffs': coeffs}
    _L2_attn_all = _L2_attn_setup()
    _L2_attn_in = {k: v for k, v in _L2_attn_all.items() if k in ('Wqkv', 'Wout', 'Wpos', 'coeffs')}
    del _L2_attn_all

    def _L2_ffn_setup():
        import jax, jax.numpy as jnp
        import numpy as np
        B, T, N = (2, 256, 128)
        H = 16
        E = 8
        K = 2
        FF = 4 * N
        EPS = 1e-05
        SCALE = 1.0

        def _layernorm(x, scale, bias):
            mu = x.mean(-1, keepdims=True)
            var = ((x - mu) ** 2).mean(-1, keepdims=True)
            return (x - mu) * jax.lax.rsqrt(var + EPS) * scale + bias

        def _attention(x, w_qkv, b_qkv, w_proj, b_proj):
            b, t, n = x.shape
            qkv = x @ w_qkv + b_qkv
            q, k, v = jnp.split(qkv, 3, axis=2)
            hd = n // H
            q = q.reshape(b, t, H, hd).transpose(0, 2, 1, 3)
            k = k.reshape(b, t, H, hd).transpose(0, 2, 1, 3)
            v = v.reshape(b, t, H, hd).transpose(0, 2, 1, 3)
            att = jnp.einsum('bhqd,bhkd->bhqk', q, k) / hd ** 0.5
            mask = jnp.tril(jnp.ones((1, 1, t, t), bool))
            att = jnp.where(mask, att, jnp.finfo(jnp.float32).min)
            att = jax.nn.softmax(att, axis=-1)
            y = jnp.einsum('bhqk,bhkd->bhqd', att, v)
            y = y.transpose(0, 2, 1, 3).reshape(b, t, n)
            return y @ w_proj + b_proj

        def _moe(x, w_gate, b_gate, w_fc, b_fc, w_fcproj, b_fcproj):
            b, t, n = x.shape
            xf = x.reshape(-1, n)
            bt = xf.shape[0]
            logits = xf @ w_gate + b_gate
            probs = jax.nn.softmax(logits, axis=-1)
            top_p, top_i = jax.lax.top_k(probs, K)
            out = jnp.zeros((bt, n), xf.dtype)
            expert_mask = jnp.transpose(jax.nn.one_hot(top_i, E), (2, 1, 0))
            rows = jnp.arange(bt)
            for e in range(E):
                active = expert_mask[e]
                mask = active.any(axis=0)
                cumsum = jnp.cumsum(mask) - 1
                indices = jnp.where(mask, cumsum, -1)
                sel = jnp.where(mask[:, None], xf, 0.0)
                h = jax.nn.gelu(sel @ w_fc[e] + b_fc[e], approximate=True)
                eo = h @ w_fcproj[e] + b_fcproj[e]
                rp = jnp.where(mask[:, None], top_p[rows, jnp.argmax(active, axis=0)][:, None], 0.0)
                out = out.at[indices].add(eo * rp)
            return out.reshape(b, t, n)
        key = jax.random.key(seed)
        ks = jax.random.split(key, 12)
        s = lambda fan_in: 1.0 / np.sqrt(fan_in)
        return {'x': jax.random.normal(ks[0], (B, T, N), jnp.float32), 'ln1_scale': jnp.ones((N,), jnp.float32), 'ln1_bias': jnp.zeros((N,), jnp.float32), 'w_qkv': jax.random.normal(ks[1], (N, 3 * N), jnp.float32) * s(N), 'b_qkv': jnp.zeros((3 * N,), jnp.float32), 'w_attnproj': jax.random.normal(ks[2], (N, N), jnp.float32) * s(N), 'b_attnproj': jnp.zeros((N,), jnp.float32), 'ln2_scale': jnp.ones((N,), jnp.float32), 'ln2_bias': jnp.zeros((N,), jnp.float32), 'w_gate': jax.random.normal(ks[3], (N, E), jnp.float32) * s(N), 'b_gate': jnp.zeros((E,), jnp.float32), 'w_fc': jax.random.normal(ks[4], (E, N, FF), jnp.float32) * s(N), 'b_fc': jnp.zeros((E, FF), jnp.float32), 'w_fcproj': jax.random.normal(ks[5], (E, FF, N), jnp.float32) * s(FF), 'b_fcproj': jnp.zeros((E, N), jnp.float32)}
    _L2_ffn_all = _L2_ffn_setup()
    _L2_ffn_in = {k: v for k, v in _L2_ffn_all.items() if k in ('ln1_scale', 'ln1_bias', 'w_qkv', 'b_qkv', 'w_attnproj', 'b_attnproj', 'ln2_scale', 'ln2_bias', 'w_gate', 'b_gate', 'w_fc', 'b_fc', 'w_fcproj', 'b_fcproj')}
    del _L2_ffn_all

    def _L3_xattn_setup():
        import jax, jax.numpy as jnp
        import numpy as np
        DIM = 128
        HEADS = 16
        HEAD_DIM = 64
        INNER = HEADS * HEAD_DIM

        def _split_heads(t):
            b, n, _ = t.shape
            return t.reshape(b, n, HEADS, HEAD_DIM).transpose(0, 2, 1, 3)
        key = jax.random.key(seed)
        ks = jax.random.split(key, 7)
        b, n, m = (2, 256, 256)
        s = 0.02
        return {'x': jax.random.normal(ks[0], (b, n, DIM), dtype=jnp.float32), 'context': jax.random.normal(ks[1], (b, m, DIM), dtype=jnp.float32), 'w_kv': jax.random.normal(ks[2], (DIM, 2 * INNER), dtype=jnp.float32) * s, 'w_q': jax.random.normal(ks[3], (DIM, INNER), dtype=jnp.float32) * s, 'w_out1': jax.random.normal(ks[4], (INNER, DIM), dtype=jnp.float32) * s, 'w_out2': jax.random.normal(ks[5], (DIM, DIM), dtype=jnp.float32) * s, 'gamma': jnp.ones((DIM,), dtype=jnp.float32)}
    _L3_xattn_all = _L3_xattn_setup()
    _L3_xattn_in = {k: v for k, v in _L3_xattn_all.items() if k in ('w_kv', 'w_q', 'w_out1', 'w_out2', 'gamma')}
    del _L3_xattn_all

    def _L3_attn_setup():
        import jax, jax.numpy as jnp
        import numpy as np
        B, T, C = (2, 256, 128)
        H = 16
        D = C // H
        HID = C // 4
        FF = 4 * C

        def _rms_norm(x):
            eps = jnp.finfo(x.dtype).eps
            return x * jax.lax.rsqrt(jnp.mean(jnp.square(x), axis=-1, keepdims=True) + eps)
        key = jax.random.key(seed)
        ks = jax.random.split(key, 11)
        s = lambda fan_in: 1.0 / np.sqrt(fan_in)
        inp = {'x': jax.random.normal(ks[0], (B, T, C), jnp.float32), 'Wq': jax.random.uniform(ks[1], (C, C), jnp.float32, -s(C), s(C)), 'Wk': jax.random.uniform(ks[2], (C, C), jnp.float32, -s(C), s(C)), 'Wv': jax.random.uniform(ks[3], (C, C), jnp.float32, -s(C), s(C)), 'Wm1': jax.random.uniform(ks[4], (HID, C), jnp.float32, -s(C), s(C)), 'bm1': jax.random.uniform(ks[5], (HID,), jnp.float32, -s(C), s(C)), 'Wm2': jax.random.uniform(ks[6], (H, HID), jnp.float32, -s(HID), s(HID)), 'bm2': jax.random.uniform(ks[7], (H,), jnp.float32, -s(HID), s(HID)), 'Wproj': jax.random.uniform(ks[8], (C, C), jnp.float32, -s(C), s(C)), 'Wfc': jax.random.uniform(ks[9], (FF, C), jnp.float32, -s(C), s(C)), 'Wcp': jax.random.uniform(ks[10], (C, FF), jnp.float32, -s(FF), s(FF))}
        return inp
    _L3_attn_all = _L3_attn_setup()
    _L3_attn_in = {k: v for k, v in _L3_attn_all.items() if k in ('Wq', 'Wk', 'Wv', 'Wm1', 'bm1', 'Wm2', 'bm2', 'Wproj', 'Wfc', 'Wcp')}
    del _L3_attn_all

    def _L3_ffn_setup():
        import jax, jax.numpy as jnp
        import numpy as np
        E, K = (8, 2)
        key = jax.random.key(seed)
        ks = jax.random.split(key, 5)
        B, S, H, I = (2, 128, 128, 512)
        scale_h = 1.0 / np.sqrt(H)
        scale_i = 1.0 / np.sqrt(I)
        return {'hidden_states': jax.random.normal(ks[0], (B, S, H), jnp.float32), 'conf_w': jax.random.normal(ks[1], (E, H), jnp.float32) * 0.1 * scale_h, 'conf_b': jnp.zeros((E,), jnp.float32), 'gate_w': jax.random.normal(ks[2], (E, I, H), jnp.float32) * scale_h, 'up_w': jax.random.normal(ks[3], (E, I, H), jnp.float32) * scale_h, 'down_w': jax.random.normal(ks[4], (E, H, I), jnp.float32) * scale_i, 'wealth': jnp.ones((E,), jnp.float32)}
    _L3_ffn_all = _L3_ffn_setup()
    _L3_ffn_in = {k: v for k, v in _L3_ffn_all.items() if k in ('conf_w', 'conf_b', 'gate_w', 'up_w', 'down_w', 'wealth')}
    del _L3_ffn_all
    return {'x': x, 'ctx_1024': ctx_1024, 'mask_Bx1x1xS2_if1': mask_Bx1x1xS2_if1, 'L0_xattn_w_sim': _L0_xattn_in['w_sim'], 'L0_xattn_b_sim': _L0_xattn_in['b_sim'], 'L0_xattn_W_qv': _L0_xattn_in['W_qv'], 'L0_xattn_b_qv': _L0_xattn_in['b_qv'], 'L0_attn_Wq': _L0_attn_in['Wq'], 'L0_attn_bq': _L0_attn_in['bq'], 'L0_attn_Wk': _L0_attn_in['Wk'], 'L0_attn_bk': _L0_attn_in['bk'], 'L0_attn_Wv': _L0_attn_in['Wv'], 'L0_attn_bv': _L0_attn_in['bv'], 'L0_attn_Wo': _L0_attn_in['Wo'], 'L0_attn_bo': _L0_attn_in['bo'], 'L0_ffn_q_w': _L0_ffn_in['q_w'], 'L0_ffn_q_b': _L0_ffn_in['q_b'], 'L0_ffn_k_w': _L0_ffn_in['k_w'], 'L0_ffn_k_b': _L0_ffn_in['k_b'], 'L0_ffn_v_w': _L0_ffn_in['v_w'], 'L0_ffn_v_b': _L0_ffn_in['v_b'], 'L0_ffn_o_w': _L0_ffn_in['o_w'], 'L0_ffn_o_b': _L0_ffn_in['o_b'], 'L0_ffn_router_w': _L0_ffn_in['router_w'], 'L0_ffn_router_b': _L0_ffn_in['router_b'], 'L0_ffn_w1': _L0_ffn_in['w1'], 'L0_ffn_b1': _L0_ffn_in['b1'], 'L0_ffn_w2': _L0_ffn_in['w2'], 'L0_ffn_b2': _L0_ffn_in['b2'], 'L1_xattn_Wq': _L1_xattn_in['Wq'], 'L1_xattn_bq': _L1_xattn_in['bq'], 'L1_xattn_Wk': _L1_xattn_in['Wk'], 'L1_xattn_bk': _L1_xattn_in['bk'], 'L1_xattn_Wv': _L1_xattn_in['Wv'], 'L1_xattn_bv': _L1_xattn_in['bv'], 'L1_xattn_Wo': _L1_xattn_in['Wo'], 'L1_xattn_bo': _L1_xattn_in['bo'], 'L1_attn_qkv_weight': _L1_attn_in['qkv_weight'], 'L1_attn_proj_weight': _L1_attn_in['proj_weight'], 'L1_attn_proj_bias': _L1_attn_in['proj_bias'], 'L1_ffn_q_nw': _L1_ffn_in['q_nw'], 'L1_ffn_q_nb': _L1_ffn_in['q_nb'], 'L1_ffn_q_w1': _L1_ffn_in['q_w1'], 'L1_ffn_q_b1': _L1_ffn_in['q_b1'], 'L1_ffn_q_w2': _L1_ffn_in['q_w2'], 'L1_ffn_q_b2': _L1_ffn_in['q_b2'], 'L1_ffn_k_nw': _L1_ffn_in['k_nw'], 'L1_ffn_k_nb': _L1_ffn_in['k_nb'], 'L1_ffn_k_w1': _L1_ffn_in['k_w1'], 'L1_ffn_k_b1': _L1_ffn_in['k_b1'], 'L1_ffn_k_w2': _L1_ffn_in['k_w2'], 'L1_ffn_k_b2': _L1_ffn_in['k_b2'], 'L1_ffn_v_nw': _L1_ffn_in['v_nw'], 'L1_ffn_v_nb': _L1_ffn_in['v_nb'], 'L1_ffn_v_w1': _L1_ffn_in['v_w1'], 'L1_ffn_v_b1': _L1_ffn_in['v_b1'], 'L1_ffn_v_w2': _L1_ffn_in['v_w2'], 'L1_ffn_v_b2': _L1_ffn_in['v_b2'], 'L1_ffn_f_nw': _L1_ffn_in['f_nw'], 'L1_ffn_f_nb': _L1_ffn_in['f_nb'], 'L1_ffn_f_w1': _L1_ffn_in['f_w1'], 'L1_ffn_f_b1': _L1_ffn_in['f_b1'], 'L1_ffn_f_w2': _L1_ffn_in['f_w2'], 'L1_ffn_f_b2': _L1_ffn_in['f_b2'], 'L2_xattn_W_q': _L2_xattn_in['W_q'], 'L2_xattn_W_k': _L2_xattn_in['W_k'], 'L2_xattn_W_v': _L2_xattn_in['W_v'], 'L2_xattn_W_o': _L2_xattn_in['W_o'], 'L2_xattn_b_o': _L2_xattn_in['b_o'], 'L2_attn_Wqkv': _L2_attn_in['Wqkv'], 'L2_attn_Wout': _L2_attn_in['Wout'], 'L2_attn_Wpos': _L2_attn_in['Wpos'], 'L2_attn_coeffs': _L2_attn_in['coeffs'], 'L2_ffn_ln1_scale': _L2_ffn_in['ln1_scale'], 'L2_ffn_ln1_bias': _L2_ffn_in['ln1_bias'], 'L2_ffn_w_qkv': _L2_ffn_in['w_qkv'], 'L2_ffn_b_qkv': _L2_ffn_in['b_qkv'], 'L2_ffn_w_attnproj': _L2_ffn_in['w_attnproj'], 'L2_ffn_b_attnproj': _L2_ffn_in['b_attnproj'], 'L2_ffn_ln2_scale': _L2_ffn_in['ln2_scale'], 'L2_ffn_ln2_bias': _L2_ffn_in['ln2_bias'], 'L2_ffn_w_gate': _L2_ffn_in['w_gate'], 'L2_ffn_b_gate': _L2_ffn_in['b_gate'], 'L2_ffn_w_fc': _L2_ffn_in['w_fc'], 'L2_ffn_b_fc': _L2_ffn_in['b_fc'], 'L2_ffn_w_fcproj': _L2_ffn_in['w_fcproj'], 'L2_ffn_b_fcproj': _L2_ffn_in['b_fcproj'], 'L3_xattn_w_kv': _L3_xattn_in['w_kv'], 'L3_xattn_w_q': _L3_xattn_in['w_q'], 'L3_xattn_w_out1': _L3_xattn_in['w_out1'], 'L3_xattn_w_out2': _L3_xattn_in['w_out2'], 'L3_xattn_gamma': _L3_xattn_in['gamma'], 'L3_attn_Wq': _L3_attn_in['Wq'], 'L3_attn_Wk': _L3_attn_in['Wk'], 'L3_attn_Wv': _L3_attn_in['Wv'], 'L3_attn_Wm1': _L3_attn_in['Wm1'], 'L3_attn_bm1': _L3_attn_in['bm1'], 'L3_attn_Wm2': _L3_attn_in['Wm2'], 'L3_attn_bm2': _L3_attn_in['bm2'], 'L3_attn_Wproj': _L3_attn_in['Wproj'], 'L3_attn_Wfc': _L3_attn_in['Wfc'], 'L3_attn_Wcp': _L3_attn_in['Wcp'], 'L3_ffn_conf_w': _L3_ffn_in['conf_w'], 'L3_ffn_conf_b': _L3_ffn_in['conf_b'], 'L3_ffn_gate_w': _L3_ffn_in['gate_w'], 'L3_ffn_up_w': _L3_ffn_in['up_w'], 'L3_ffn_down_w': _L3_ffn_in['down_w'], 'L3_ffn_wealth': _L3_ffn_in['wealth']}

def reference(x, ctx_1024, mask_Bx1x1xS2_if1, L0_xattn_w_sim, L0_xattn_b_sim, L0_xattn_W_qv, L0_xattn_b_qv, L0_attn_Wq, L0_attn_bq, L0_attn_Wk, L0_attn_bk, L0_attn_Wv, L0_attn_bv, L0_attn_Wo, L0_attn_bo, L0_ffn_q_w, L0_ffn_q_b, L0_ffn_k_w, L0_ffn_k_b, L0_ffn_v_w, L0_ffn_v_b, L0_ffn_o_w, L0_ffn_o_b, L0_ffn_router_w, L0_ffn_router_b, L0_ffn_w1, L0_ffn_b1, L0_ffn_w2, L0_ffn_b2, L1_xattn_Wq, L1_xattn_bq, L1_xattn_Wk, L1_xattn_bk, L1_xattn_Wv, L1_xattn_bv, L1_xattn_Wo, L1_xattn_bo, L1_attn_qkv_weight, L1_attn_proj_weight, L1_attn_proj_bias, L1_ffn_q_nw, L1_ffn_q_nb, L1_ffn_q_w1, L1_ffn_q_b1, L1_ffn_q_w2, L1_ffn_q_b2, L1_ffn_k_nw, L1_ffn_k_nb, L1_ffn_k_w1, L1_ffn_k_b1, L1_ffn_k_w2, L1_ffn_k_b2, L1_ffn_v_nw, L1_ffn_v_nb, L1_ffn_v_w1, L1_ffn_v_b1, L1_ffn_v_w2, L1_ffn_v_b2, L1_ffn_f_nw, L1_ffn_f_nb, L1_ffn_f_w1, L1_ffn_f_b1, L1_ffn_f_w2, L1_ffn_f_b2, L2_xattn_W_q, L2_xattn_W_k, L2_xattn_W_v, L2_xattn_W_o, L2_xattn_b_o, L2_attn_Wqkv, L2_attn_Wout, L2_attn_Wpos, L2_attn_coeffs, L2_ffn_ln1_scale, L2_ffn_ln1_bias, L2_ffn_w_qkv, L2_ffn_b_qkv, L2_ffn_w_attnproj, L2_ffn_b_attnproj, L2_ffn_ln2_scale, L2_ffn_ln2_bias, L2_ffn_w_gate, L2_ffn_b_gate, L2_ffn_w_fc, L2_ffn_b_fc, L2_ffn_w_fcproj, L2_ffn_b_fcproj, L3_xattn_w_kv, L3_xattn_w_q, L3_xattn_w_out1, L3_xattn_w_out2, L3_xattn_gamma, L3_attn_Wq, L3_attn_Wk, L3_attn_Wv, L3_attn_Wm1, L3_attn_bm1, L3_attn_Wm2, L3_attn_bm2, L3_attn_Wproj, L3_attn_Wfc, L3_attn_Wcp, L3_ffn_conf_w, L3_ffn_conf_b, L3_ffn_gate_w, L3_ffn_up_w, L3_ffn_down_w, L3_ffn_wealth):
    import jax
    import jax.numpy as jnp

    def _L0_xattn_ref(encoder_hc, decoder_hq, w_sim, b_sim, W_qv, b_qv):
        import jax, jax.numpy as jnp
        import numpy as np
        B, L_ENC, L_DEC, D = (16, 64, 128, 128)
        d = encoder_hc.shape[-1]
        w1, w2, w3 = (w_sim[:d], w_sim[d:2 * d], w_sim[2 * d:])
        Sim = (encoder_hc @ w1)[:, :, None] + (decoder_hq @ w2)[:, None, :] + jnp.einsum('bid,bjd->bij', encoder_hc * w3, decoder_hq) + b_sim[0]
        A = jax.nn.softmax(Sim, axis=2)
        hq_hat = jnp.einsum('bij,bjd->bid', A, decoder_hq)
        Batt = jax.nn.softmax(jnp.max(Sim, axis=2), axis=1)
        hc_bar = jnp.einsum('bi,bid->bd', Batt, encoder_hc)[:, None, :]
        hc_hat = jnp.broadcast_to(hc_bar, encoder_hc.shape)
        feats = jnp.concatenate([encoder_hc, hq_hat, encoder_hc * hq_hat, encoder_hc * hc_hat], axis=-1)
        hcq = feats @ W_qv + b_qv
        return hcq

    def _L0_attn_ref(x, Wq, bq, Wk, bk, Wv, bv, Wo, bo):
        import math
        import jax, jax.numpy as jnp
        import numpy as np
        N_HEAD = 16

        def _rope_cos_sin(l, head_dim):
            scale = jnp.arange(0, head_dim, 2, dtype=jnp.float32)[:head_dim // 2]
            freqs = 1.0 / 10000.0 ** scale
            angles = jnp.arange(l, dtype=jnp.float32)[:, None] * freqs[None, :]
            return (jnp.cos(angles), jnp.sin(angles))

        def _rope_apply(x, cos, sin):
            b, l, h, hd = x.shape
            xp = x.astype(jnp.float32).reshape(b, l, h, hd // 2, 2)
            xr, xi = (xp[..., 0], xp[..., 1])
            c = cos[None, :, None, :]
            s = sin[None, :, None, :]
            out_r = xr * c - xi * s
            out_i = xr * s + xi * c
            out = jnp.stack([out_r, out_i], axis=-1).reshape(b, l, h, hd)
            return out.astype(x.dtype)
        b, l, d = x.shape
        h = N_HEAD
        hd = d // h
        q = (x @ Wq + bq).reshape(b, l, h, hd)
        k = (x @ Wk + bk).reshape(b, l, h, hd)
        v = (x @ Wv + bv).reshape(b, l, h, hd)
        cos, sin = _rope_cos_sin(l, hd)
        q = _rope_apply(q, cos, sin)
        k = _rope_apply(k, cos, sin)
        score = jnp.einsum('blhd,bmhd->bhlm', q, k) / math.sqrt(hd)
        ctx = jnp.einsum('bhlm,bmhd->blhd', score, v).reshape(b, l, d)
        return ctx @ Wo + bo

    def _L0_ffn_ref(hidden_states, q_w, q_b, k_w, k_b, v_w, v_b, o_w, o_b, router_w, router_b, w1, b1, w2, b2):
        import jax, jax.numpy as jnp
        import numpy as np
        import math
        D = 128
        H = 16
        E = 8
        TOPK = 2
        LAT = D // 2
        KPH = LAT // H
        HD = D // H

        def _forward(hs, q_w, q_b, k_w, k_b, v_w, v_b, o_w, o_b, router_w, router_b, w1, b1, w2, b2):
            B, S, _ = hs.shape
            Q = (hs @ q_w + q_b).reshape(B, S, H, HD).transpose(0, 2, 1, 3)
            K = (hs @ k_w + k_b).reshape(B, S, H, KPH).transpose(0, 2, 1, 3)
            V = (hs @ v_w + v_b).reshape(B, S, H, KPH).transpose(0, 2, 1, 3)
            scores = jnp.einsum('bhsk,bhtk->bhst', Q[..., :KPH], K) / math.sqrt(KPH)
            attn = jax.nn.softmax(scores, axis=-1)
            ao = jnp.einsum('bhst,bhtv->bhsv', attn, V)
            ao = ao.transpose(0, 2, 1, 3).reshape(B, S, H * KPH)
            ao = jnp.concatenate([ao, jnp.zeros((B, S, D - LAT), ao.dtype)], axis=-1)
            mla_out = ao @ o_w + o_b
            probs = jax.nn.softmax(mla_out @ router_w + router_b, axis=-1)
            topw, topi = jax.lax.top_k(probs, TOPK)
            topw = topw / (topw.sum(-1, keepdims=True) + 1e-08)
            combine = jnp.sum(jax.nn.one_hot(topi, E, dtype=probs.dtype) * topw[..., None], axis=-2)
            h1 = jnp.einsum('bsd,edf->ebsf', mla_out, w1) + b1[:, None, None, :]
            h1 = jax.nn.gelu(h1, approximate=False)
            h2 = jnp.einsum('ebsf,efd->ebsd', h1, w2) + b2[:, None, None, :]
            moe_out = jnp.einsum('bse,ebsd->bsd', combine, h2)
            return hs + 0.3 * moe_out
        return _forward(hidden_states, q_w, q_b, k_w, k_b, v_w, v_b, o_w, o_b, router_w, router_b, w1, b1, w2, b2)

    def _L1_xattn_ref(Q, K, V, mask, Wq, bq, Wk, bk, Wv, bv, Wo, bo):
        import jax, jax.numpy as jnp
        import numpy as np
        M, T, D, H = (2, 256, 128, 16)
        HD = D // H
        SCALE = 1.0 / np.sqrt(D).astype(np.float32)
        m = Q.shape[0]
        q = (Q @ Wq.T + bq).reshape(m, -1, H, HD)
        k = (K @ Wk.T + bk).reshape(m, -1, H, HD)
        v = (V @ Wv.T + bv).reshape(m, -1, H, HD)
        energy = jnp.einsum('mqhd,mkhd->mhqk', q, k) * SCALE
        if mask is not None:
            energy = jnp.where(mask == 0, jnp.float32(-1e+20), energy)
        attn = jax.nn.softmax(energy, axis=3)
        out = jnp.einsum('mhqk,mkhd->mqhd', attn, v)
        concat = out.reshape(m, -1, H * HD)
        return concat @ Wo.T + bo

    def _L1_attn_ref(x, qkv_weight, proj_weight, proj_bias):
        import jax, jax.numpy as jnp
        import numpy as np
        NUM_HEADS = 32
        EPS = 1e-15
        B, N, C = x.shape
        H = NUM_HEADS
        D = C // H
        qkv = jax.nn.relu(jnp.einsum('bnc,oc->bno', x, qkv_weight))
        qkv = qkv.reshape(B, N, 3, H, D)
        q, k, v = (qkv[:, :, 0], qkv[:, :, 1], qkv[:, :, 2])
        v_pad = jnp.concatenate([v, jnp.ones((B, N, H, 1), dtype=v.dtype)], axis=-1)
        vk = jnp.einsum('bnhe,bnhd->bhed', v_pad.astype(jnp.float32), k.astype(jnp.float32))
        vk_q = jnp.einsum('bhed,bnhd->bnhe', vk, q.astype(jnp.float32))
        proj_input = (vk_q[..., :D] / (vk_q[..., D:] + EPS)).astype(qkv.dtype)
        proj_input = proj_input.reshape(B, N, C)
        y = jnp.einsum('bnc,oc->bno', proj_input, proj_weight) + proj_bias
        return y

    def _L1_ffn_ref(x, q_nw, q_nb, q_w1, q_b1, q_w2, q_b2, k_nw, k_nb, k_w1, k_b1, k_w2, k_b2, v_nw, v_nb, v_w1, v_b1, v_w2, v_b2, f_nw, f_nb, f_w1, f_b1, f_w2, f_b2):
        import jax, jax.numpy as jnp
        import numpy as np
        D = 128
        LW = 16
        DEPTH = 8
        NN = 2 ** DEPTH - 1
        NL = 2 ** DEPTH
        B, S = (2, 128)

        def _fff(x, nw, nb, w1, b1, w2, b2, act):
            node = jnp.zeros(x.shape[:2], dtype=jnp.int32)
            for _ in range(DEPTH):
                logit = jnp.einsum('bsd,bsd->bs', x, nw[node]) + nb[node]
                node = 2 * node + 1 + (logit > 0).astype(jnp.int32)
            leaf = node - NN
            h = act(jnp.einsum('bsd,bsdl->bsl', x, w1[leaf]) + b1[leaf])
            return jnp.einsum('bsl,bsld->bsd', h, w2[leaf]) + b2[leaf]

        def _forward(x, q_nw, q_nb, q_w1, q_b1, q_w2, q_b2, k_nw, k_nb, k_w1, k_b1, k_w2, k_b2, v_nw, v_nb, v_w1, v_b1, v_w2, v_b2, f_nw, f_nb, f_w1, f_b1, f_w2, f_b2):
            mu = jnp.mean(x, -1, keepdims=True)
            sd = jnp.std(x, -1, ddof=1, keepdims=True)
            xn = (x - mu) / jnp.sqrt(sd + 1e-05)
            relu = jax.nn.relu
            q = _fff(xn, q_nw, q_nb, q_w1, q_b1, q_w2, q_b2, relu)
            k = _fff(xn, k_nw, k_nb, k_w1, k_b1, k_w2, k_b2, relu)
            v = _fff(xn, v_nw, v_nb, v_w1, v_b1, v_w2, v_b2, relu)
            att = jax.nn.softmax(jnp.einsum('bqd,bkd->bqk', q, k) / jnp.sqrt(jnp.float32(D)), axis=-1)
            y = xn + jnp.einsum('bqk,bkd->bqd', att, v)
            gelu = lambda t: jax.nn.gelu(t, approximate=False)
            return y + _fff(y, f_nw, f_nb, f_w1, f_b1, f_w2, f_b2, gelu)

        def _make_fff_params(key, scale_in, scale_leaf):
            ks = jax.random.split(key, 4)
            nw = jax.random.normal(ks[0], (NN, D), jnp.float32) * scale_in
            nb = jnp.zeros((NN,), jnp.float32)
            w1 = jax.random.normal(ks[1], (NL, D, LW), jnp.float32) * scale_in
            b1 = jax.random.normal(ks[2], (NL, LW), jnp.float32) * 0.01
            w2 = jax.random.normal(ks[3], (NL, LW, D), jnp.float32) * scale_leaf
            b2 = jnp.zeros((NL, D), jnp.float32)
            return (nw, nb, w1, b1, w2, b2)
        return _forward(x, q_nw, q_nb, q_w1, q_b1, q_w2, q_b2, k_nw, k_nb, k_w1, k_b1, k_w2, k_b2, v_nw, v_nb, v_w1, v_b1, v_w2, v_b2, f_nw, f_nb, f_w1, f_b1, f_w2, f_b2)

    def _L2_xattn_ref(decoder_input, encoder_output, W_q, W_k, W_v, W_o, b_o):
        import jax, jax.numpy as jnp
        import numpy as np
        EMBED = 128
        HEADS = 16
        HEAD_DIM = EMBED // HEADS
        B, Sd, E = decoder_input.shape
        Se = encoder_output.shape[1]
        Q = (decoder_input @ W_q).reshape(B, Sd, HEADS, HEAD_DIM)
        K = (encoder_output @ W_k).reshape(B, Se, HEADS, HEAD_DIM)
        V = (encoder_output @ W_v).reshape(B, Se, HEADS, HEAD_DIM)
        scores = jnp.einsum('bqhd,bkhd->bhqk', Q, K) / jnp.sqrt(jnp.float32(HEAD_DIM))
        attn = jax.nn.softmax(scores, axis=-1)
        out = jnp.einsum('bhqk,bkhd->bqhd', attn, V).reshape(B, Sd, E)
        return out @ W_o + b_o

    def _L2_attn_ref(x, Wqkv, Wout, Wpos, coeffs):
        import jax, jax.numpy as jnp
        import numpy as np
        DIM = 128
        HEADS = 16
        HEAD_DIM = DIM // HEADS
        NUM_FILTERS = 4
        NUM_TAPS = 101
        RES = 64

        def _fir_fft(c, sig):
            R = sig.shape[0]
            L = R + c.shape[0] - 1
            out = jnp.fft.ifft(jnp.fft.fft(sig, n=L) * jnp.fft.fft(c, n=L)).real
            return out[:R]
        B, S, D = x.shape
        scale = HEAD_DIM ** (-0.5)
        proto = jnp.linspace(0.0, 1.0, RES).astype(x.dtype)
        table = jax.vmap(_fir_fft, in_axes=(0, None))(coeffs, proto).T
        r = jnp.arange(S)
        rel = jnp.abs(r[None, :] - r[:, None]).astype(jnp.float32) / max(S - 1, 1)
        idx = jnp.clip(jnp.round(rel * (RES - 1)).astype(jnp.int32), 0, RES - 1)
        pos_feat = table[idx]
        pos_bias = jnp.einsum('ijf,hf->hij', pos_feat, Wpos)
        qkv = jnp.einsum('bsd,ed->bse', x, Wqkv)
        q, k, v = jnp.split(qkv, 3, axis=-1)
        q = q.reshape(B, S, HEADS, HEAD_DIM)
        k = k.reshape(B, S, HEADS, HEAD_DIM)
        v = v.reshape(B, S, HEADS, HEAD_DIM)
        logits = jnp.einsum('bihd,bjhd->bhij', q, k) * scale + pos_bias[None]
        attn = jax.nn.softmax(logits, axis=-1)
        out = jnp.einsum('bhij,bjhd->bihd', attn, v).reshape(B, S, D)
        return jnp.einsum('bsd,ed->bse', out, Wout)

    def _L2_ffn_ref(x, ln1_scale, ln1_bias, w_qkv, b_qkv, w_attnproj, b_attnproj, ln2_scale, ln2_bias, w_gate, b_gate, w_fc, b_fc, w_fcproj, b_fcproj):
        import jax, jax.numpy as jnp
        import numpy as np
        B, T, N = (2, 256, 128)
        H = 16
        E = 8
        K = 2
        FF = 4 * N
        EPS = 1e-05
        SCALE = 1.0

        def _layernorm(x, scale, bias):
            mu = x.mean(-1, keepdims=True)
            var = ((x - mu) ** 2).mean(-1, keepdims=True)
            return (x - mu) * jax.lax.rsqrt(var + EPS) * scale + bias

        def _attention(x, w_qkv, b_qkv, w_proj, b_proj):
            b, t, n = x.shape
            qkv = x @ w_qkv + b_qkv
            q, k, v = jnp.split(qkv, 3, axis=2)
            hd = n // H
            q = q.reshape(b, t, H, hd).transpose(0, 2, 1, 3)
            k = k.reshape(b, t, H, hd).transpose(0, 2, 1, 3)
            v = v.reshape(b, t, H, hd).transpose(0, 2, 1, 3)
            att = jnp.einsum('bhqd,bhkd->bhqk', q, k) / hd ** 0.5
            mask = jnp.tril(jnp.ones((1, 1, t, t), bool))
            att = jnp.where(mask, att, jnp.finfo(jnp.float32).min)
            att = jax.nn.softmax(att, axis=-1)
            y = jnp.einsum('bhqk,bhkd->bhqd', att, v)
            y = y.transpose(0, 2, 1, 3).reshape(b, t, n)
            return y @ w_proj + b_proj

        def _moe(x, w_gate, b_gate, w_fc, b_fc, w_fcproj, b_fcproj):
            b, t, n = x.shape
            xf = x.reshape(-1, n)
            bt = xf.shape[0]
            logits = xf @ w_gate + b_gate
            probs = jax.nn.softmax(logits, axis=-1)
            top_p, top_i = jax.lax.top_k(probs, K)
            out = jnp.zeros((bt, n), xf.dtype)
            expert_mask = jnp.transpose(jax.nn.one_hot(top_i, E), (2, 1, 0))
            rows = jnp.arange(bt)
            for e in range(E):
                active = expert_mask[e]
                mask = active.any(axis=0)
                cumsum = jnp.cumsum(mask) - 1
                indices = jnp.where(mask, cumsum, -1)
                sel = jnp.where(mask[:, None], xf, 0.0)
                h = jax.nn.gelu(sel @ w_fc[e] + b_fc[e], approximate=True)
                eo = h @ w_fcproj[e] + b_fcproj[e]
                rp = jnp.where(mask[:, None], top_p[rows, jnp.argmax(active, axis=0)][:, None], 0.0)
                out = out.at[indices].add(eo * rp)
            return out.reshape(b, t, n)
        x = x + SCALE * _attention(_layernorm(x, ln1_scale, ln1_bias), w_qkv, b_qkv, w_attnproj, b_attnproj)
        x = x + SCALE * _moe(_layernorm(x, ln2_scale, ln2_bias), w_gate, b_gate, w_fc, b_fc, w_fcproj, b_fcproj)
        return x

    def _L3_xattn_ref(x, context, w_kv, w_q, w_out1, w_out2, gamma):
        import jax, jax.numpy as jnp
        import numpy as np
        DIM = 128
        HEADS = 16
        HEAD_DIM = 64
        INNER = HEADS * HEAD_DIM

        def _split_heads(t):
            b, n, _ = t.shape
            return t.reshape(b, n, HEADS, HEAD_DIM).transpose(0, 2, 1, 3)
        scale = HEAD_DIM ** (-0.5)
        kv = context @ w_kv
        k, v = jnp.split(kv, 2, axis=-1)
        q = _split_heads(x @ w_q)
        k = _split_heads(k)
        v = _split_heads(v)
        dots = jnp.einsum('bhid,bhjd->bhij', q, k) * scale
        attn = jax.nn.softmax(dots, axis=-1)
        out = jnp.einsum('bhij,bhjd->bhid', attn, v)
        b, h, n, d = out.shape
        out = out.transpose(0, 2, 1, 3).reshape(b, n, h * d)
        out = jax.nn.relu(out @ w_out1) @ w_out2
        mean = jnp.mean(out, axis=-1, keepdims=True)
        var = jnp.var(out, axis=-1, keepdims=True)
        return (out - mean) * jax.lax.rsqrt(var + 1e-05) * gamma

    def _L3_attn_ref(x, Wq, Wk, Wv, Wm1, bm1, Wm2, bm2, Wproj, Wfc, Wcp):
        import jax, jax.numpy as jnp
        import numpy as np
        B, T, C = (2, 256, 128)
        H = 16
        D = C // H
        HID = C // 4
        FF = 4 * C

        def _rms_norm(x):
            eps = jnp.finfo(x.dtype).eps
            return x * jax.lax.rsqrt(jnp.mean(jnp.square(x), axis=-1, keepdims=True) + eps)
        b, t, c = x.shape
        h = Wm2.shape[0]
        d = c // h
        q = (x @ Wq.T).reshape(b, t, h, d)
        k = (x @ Wk.T).reshape(b, t, h, d)
        v = (x @ Wv.T).reshape(b, t, h, d)
        surprise = jax.nn.sigmoid(jnp.maximum(x @ Wm1.T + bm1, 0.0) @ Wm2.T + bm2)
        decay = 1.0 - surprise
        qT = jnp.transpose(q, (1, 0, 2, 3))
        kT = jnp.transpose(k, (1, 0, 2, 3))
        vT = jnp.transpose(v, (1, 0, 2, 3))
        dT = jnp.transpose(decay, (1, 0, 2))
        gT = jnp.transpose(surprise, (1, 0, 2))

        def step(state, inp):
            qt, kt, vt, dt, gt = inp
            state = state * dt[..., None, None] + gt[..., None, None] * (kt[..., :, None] * vt[..., None, :])
            yt = jnp.einsum('bhd,bhde->bhe', qt, state)
            return (state, yt)
        state0 = jnp.zeros((b, h, d, d), x.dtype)
        _, ys = jax.lax.scan(step, state0, (qT, kT, vT, dT, gT))
        y = jnp.transpose(ys, (1, 0, 2, 3)).reshape(b, t, c)
        y = y @ Wproj.T
        yn = _rms_norm(y)
        mlp = jnp.square(jnp.maximum(yn @ Wfc.T, 0.0)) @ Wcp.T
        return y + mlp

    def _L3_ffn_ref(hidden_states, conf_w, conf_b, gate_w, up_w, down_w, wealth):
        import jax, jax.numpy as jnp
        import numpy as np
        E, K = (8, 2)
        x = hidden_states
        confidences = jax.nn.sigmoid(jnp.einsum('bsh,eh->bse', x, conf_w) + conf_b)
        bids = confidences * wealth
        top_bids, selected_experts = jax.lax.top_k(bids, K)
        sorted_bids = -jnp.sort(-bids, axis=-1)
        payments = jnp.broadcast_to(sorted_bids[..., K:K + 1], top_bids.shape)
        routing_weights = jax.nn.softmax(top_bids, axis=-1)
        combine = jnp.sum(jax.nn.one_hot(selected_experts, E, dtype=x.dtype) * routing_weights[..., None], axis=2)

        def ffn(gw, uw, dw):
            g = jnp.einsum('bsh,ih->bsi', x, gw)
            u = jnp.einsum('bsh,ih->bsi', x, uw)
            return jnp.einsum('bsi,hi->bsh', jax.nn.silu(g) * u, dw)
        expert_out = jax.vmap(ffn)(gate_w, up_w, down_w)
        output = jnp.einsum('ebsh,bse->bsh', expert_out, combine)
        return output
    x = x + _L0_xattn_ref(_layernorm(x, axis=-1), ctx_1024, L0_xattn_w_sim, L0_xattn_b_sim, L0_xattn_W_qv, L0_xattn_b_qv)
    x = x + _L0_attn_ref(_layernorm(x, axis=-1), L0_attn_Wq, L0_attn_bq, L0_attn_Wk, L0_attn_bk, L0_attn_Wv, L0_attn_bv, L0_attn_Wo, L0_attn_bo)
    x = x + _L0_ffn_ref(_layernorm(x, axis=-1), L0_ffn_q_w, L0_ffn_q_b, L0_ffn_k_w, L0_ffn_k_b, L0_ffn_v_w, L0_ffn_v_b, L0_ffn_o_w, L0_ffn_o_b, L0_ffn_router_w, L0_ffn_router_b, L0_ffn_w1, L0_ffn_b1, L0_ffn_w2, L0_ffn_b2)
    x = x + _L1_xattn_ref(_layernorm(x, axis=-1), ctx_1024, ctx_1024, mask_Bx1x1xS2_if1, L1_xattn_Wq, L1_xattn_bq, L1_xattn_Wk, L1_xattn_bk, L1_xattn_Wv, L1_xattn_bv, L1_xattn_Wo, L1_xattn_bo)
    x = x + _L1_attn_ref(_layernorm(x, axis=-1), L1_attn_qkv_weight, L1_attn_proj_weight, L1_attn_proj_bias)
    x = x + _L1_ffn_ref(_layernorm(x, axis=-1), L1_ffn_q_nw, L1_ffn_q_nb, L1_ffn_q_w1, L1_ffn_q_b1, L1_ffn_q_w2, L1_ffn_q_b2, L1_ffn_k_nw, L1_ffn_k_nb, L1_ffn_k_w1, L1_ffn_k_b1, L1_ffn_k_w2, L1_ffn_k_b2, L1_ffn_v_nw, L1_ffn_v_nb, L1_ffn_v_w1, L1_ffn_v_b1, L1_ffn_v_w2, L1_ffn_v_b2, L1_ffn_f_nw, L1_ffn_f_nb, L1_ffn_f_w1, L1_ffn_f_b1, L1_ffn_f_w2, L1_ffn_f_b2)
    x = x + _L2_xattn_ref(_layernorm(x, axis=-1), ctx_1024, L2_xattn_W_q, L2_xattn_W_k, L2_xattn_W_v, L2_xattn_W_o, L2_xattn_b_o)
    x = x + _L2_attn_ref(_layernorm(x, axis=-1), L2_attn_Wqkv, L2_attn_Wout, L2_attn_Wpos, L2_attn_coeffs)
    x = x + _L2_ffn_ref(_layernorm(x, axis=-1), L2_ffn_ln1_scale, L2_ffn_ln1_bias, L2_ffn_w_qkv, L2_ffn_b_qkv, L2_ffn_w_attnproj, L2_ffn_b_attnproj, L2_ffn_ln2_scale, L2_ffn_ln2_bias, L2_ffn_w_gate, L2_ffn_b_gate, L2_ffn_w_fc, L2_ffn_b_fc, L2_ffn_w_fcproj, L2_ffn_b_fcproj)
    x = x + _L3_xattn_ref(_layernorm(x, axis=-1), ctx_1024, L3_xattn_w_kv, L3_xattn_w_q, L3_xattn_w_out1, L3_xattn_w_out2, L3_xattn_gamma)
    x = x + _L3_attn_ref(_layernorm(x, axis=-1), L3_attn_Wq, L3_attn_Wk, L3_attn_Wv, L3_attn_Wm1, L3_attn_bm1, L3_attn_Wm2, L3_attn_bm2, L3_attn_Wproj, L3_attn_Wfc, L3_attn_Wcp)
    x = x + _L3_ffn_ref(_layernorm(x, axis=-1), L3_ffn_conf_w, L3_ffn_conf_b, L3_ffn_gate_w, L3_ffn_up_w, L3_ffn_down_w, L3_ffn_wealth)
    return x

_drawn_inputs = setup_inputs


def setup_inputs(seed=0):
    import zlib

    import numpy as np

    out = dict(_drawn_inputs(seed))
    spreads = {'L0_attn_bq': (0.0, 0.1),
     'L0_attn_bk': (0.0, 0.1),
     'L0_attn_bv': (0.0, 0.1),
     'L0_attn_bo': (0.0, 0.493),
     'L0_ffn_q_b': (0.0, 0.8),
     'L0_ffn_k_b': (0.0, 2.0),
     'L0_ffn_v_b': (0.0, 0.8),
     'L0_ffn_o_b': (0.0, 0.8),
     'L0_ffn_router_b': (0.0, 0.8),
     'L0_ffn_b1': (0.0, 0.8),
     'L0_ffn_b2': (0.0, 0.8),
     'L1_ffn_q_nb': (0.0, 0.8),
     'L1_ffn_q_b2': (0.0, 0.8),
     'L1_ffn_k_nb': (0.0, 0.43),
     'L1_ffn_k_b2': (0.0, 0.8),
     'L1_ffn_v_nb': (0.0, 0.318),
     'L1_ffn_v_b2': (0.0, 0.47),
     'L1_ffn_f_nb': (0.0, 0.305),
     'L1_ffn_f_b2': (0.0, 0.682),
     'L2_ffn_ln1_scale': (1.0, 0.6),
     'L2_ffn_ln1_bias': (0.0, 0.426),
     'L2_ffn_b_qkv': (0.0, 0.446),
     'L2_ffn_b_attnproj': (0.0, 0.484),
     'L2_ffn_ln2_scale': (1.0, 0.6),
     'L2_ffn_ln2_bias': (0.0, 0.463),
     'L2_ffn_b_gate': (0.0, 0.438),
     'L2_ffn_b_fc': (0.0, 0.8),
     'L2_ffn_b_fcproj': (0.0, 0.8),
     'L3_xattn_gamma': (1.0, 0.6),
     'L3_ffn_conf_b': (0.0, 2.0),
     'L3_ffn_wealth': (1.0, 0.6)}
    factors = {'L0_ffn_q_w': 8.0,
     'L0_ffn_k_w': 8.0,
     'L0_ffn_v_w': 8.0,
     'L0_ffn_o_w': 8.0,
     'L0_ffn_router_w': 8.0,
     'L0_ffn_w1': 8.0,
     'L0_ffn_w2': 4.79,
     'L1_xattn_Wq': 4.414,
     'L1_xattn_bq': 8.0,
     'L1_xattn_Wk': 6.558,
     'L1_xattn_bk': 64.0,
     'L1_xattn_bv': 8.0,
     'L1_xattn_bo': 5.353,
     'L1_attn_qkv_weight': 4.304,
     'L1_attn_proj_bias': 8.0,
     'L1_ffn_q_nw': 4.0,
     'L1_ffn_q_w1': 5.011,
     'L1_ffn_q_b1': 8.0,
     'L1_ffn_q_w2': 4.635,
     'L1_ffn_k_nw': 3.583,
     'L1_ffn_k_w1': 4.237,
     'L1_ffn_k_b1': 8.0,
     'L1_ffn_k_w2': 3.849,
     'L1_ffn_v_nw': 2.705,
     'L1_ffn_v_w1': 3.205,
     'L1_ffn_v_b1': 8.0,
     'L1_ffn_f_b1': 8.0,
     'L2_xattn_W_q': 3.674,
     'L2_xattn_W_k': 3.626,
     'L2_xattn_b_o': 8.0,
     'L2_attn_Wqkv': 4.148,
     'L2_attn_Wout': 3.346,
     'L2_attn_Wpos': 8.0,
     'L2_attn_coeffs': 8.0,
     'L2_ffn_w_gate': 3.577,
     'L2_ffn_w_fc': 3.749,
     'L2_ffn_w_fcproj': 3.371,
     'L3_xattn_w_q': 8.0,
     'L3_attn_Wq': 3.608,
     'L3_attn_Wk': 3.692,
     'L3_attn_Wv': 3.626,
     'L3_attn_Wm1': 8.0,
     'L3_attn_bm1': 8.0,
     'L3_attn_Wm2': 8.0,
     'L3_attn_bm2': 8.0,
     'L3_attn_Wproj': 3.603,
     'L3_attn_Wfc': 4.759,
     'L3_attn_Wcp': 4.394,
     'L3_ffn_conf_w': 49.416,
     'L3_ffn_gate_w': 8.0,
     'L3_ffn_up_w': 8.0,
     'L3_ffn_down_w': 8.0}
    for name, (base, spread) in spreads.items():
        noise = np.random.default_rng([zlib.crc32(name.encode()), seed]).standard_normal(out[name].shape)
        drawn = base * np.exp(spread * noise) if base else spread * noise
        out[name] = jnp.asarray(drawn.astype(out[name].dtype))
    for name, factor in factors.items():
        out[name] = (out[name] * factor).astype(out[name].dtype)
    return out
```

```python
from contextlib import ExitStack

import numpy as np

import concourse.bass as bass
from concourse import mybir

F32 = mybir.dt.float32
BF16 = mybir.dt.bfloat16
I32 = mybir.dt.int32
ALU = mybir.AluOpType
ACT = mybir.ActivationFunctionType
AX = mybir.AxisListType

P = 128
CTX = 2048
KT_N = CTX // P
BANK = 512
NB = CTX // BANK
H = 16
E = 8
LEAVES = 256
NODES = LEAVES - 1
DEPTH = 8
LW = 16
CH = LEAVES * LW // P
EPS = 1e-5
HIDDEN = -1e30

CONST = [("ident", P), ("causal", P), ("cos", P), ("sin", P), ("tri", P), ("iota1", P), ("hm8", H),
         ("hm4", H), ("bm8", P), ("bm4", P), ("before", E * E), ("gather", 16), ("flip", P),
         ("ramp", 64), ("dist", 255)]
COLS = [("w2", 1), ("w3", 1), ("l0f_qb", 1), ("l0f_kb", 1), ("l0f_b1", 16), ("l1x_bq", 1), ("l1x_bk", 1),
        ("fff_b1", 4 * CH), ("l2f_bq", 1), ("l2f_bk", 1), ("l2f_bfc", 32), ("l3a_bm1", 1), ("l3a_bm2", 1)]
ROWS = [("b_sim", 1), ("w1", P), ("l0x_b", P), ("l0a_bq", P), ("l0a_bk", P), ("l0a_bv", P), ("l0a_bo", P),
        ("l0f_vb", 64), ("l0f_ob", P), ("l0f_rb", E), ("l1x_bv", P), ("l1x_bo", P), ("l1a_b", P),
        ("l2x_b", P), ("ln1_s", P), ("ln1_b", P), ("l2f_bv", P), ("l2f_ap", P), ("ln2_s", P), ("ln2_b", P),
        ("l2f_gb", E), ("l3x_g", P), ("conf_b", E), ("wealth", E)]
W_A = [("l0x", 4 * P), ("l0a_q", P), ("l0a_k", P), ("l0a_v", P), ("l0a_o", P),
       ("l0f_q", 64), ("l0f_k", 64), ("l0f_v", 64), ("l0f_o", P), ("l0f_r", E),
       ("l1x_q", P), ("l1x_k", P), ("l1x_v", P), ("l1x_o", P),
       ("l1a_qkv", 3 * P), ("l1a_p", P), ("coeff", 4), ("wpos", H)]
W_L0F = [("w1", E * 2 * P), ("w2", E * 2 * P)]
W_FFF = [("w1", LEAVES * LW), ("w2", LEAVES * LW)]
W_B = [("l2x_q", P), ("l2x_k", P), ("l2x_v", P), ("l2x_o", P), ("l2a_qkv", 3 * P), ("l2a_o", P),
       ("l2f_qkv", 3 * P), ("l2f_p", P), ("l2f_g", E), ("l3x_q", 8 * P), ("l3x_k", 8 * P), ("l3x_v", 8 * P),
       ("l3x_o1", 8 * P), ("l3x_o2", P)]
W_C = [("q", P), ("k", P), ("v", P), ("m1", 32), ("m2", H), ("p", P), ("fc", 4 * P), ("cp", 4 * P), ("conf", E)]
W_L2F = [("w1", E * 4 * P), ("w2", E * 4 * P)]
W_L3F = [("gate", E * 4 * P), ("up", E * 4 * P)]
W_L3D = [("down", E * 4 * P)]
PACKS = {"const": CONST, "cols": COLS, "w_a": W_A, "w_l0f": W_L0F, "w_q": W_FFF, "w_k": W_FFF, "w_v": W_FFF,
         "w_f": W_FFF, "w_b": W_B, "w_c": W_C, "w_l2f": W_L2F, "w_l3f": W_L3F, "w_l3d": W_L3D}
STAGES = ("l0x", "l0a", "l0f", "l1x", "l1a", "l1f", "l2x", "l2a", "l2f", "l3x", "l3a", "l3f")
DEBUG = False


def width(pack):
    return sum(n for _, n in pack)


class Steps:

    def __init__(self, sem):
        self.sem, self.order, self.value, self.taken = sem, [], {}, 0

    def plan(self, *names):
        for n in names:
            assert n not in self.value, n
            self.order.append(n)
            self.value[n] = len(self.order)

    def at(self, name):
        return self.value[name]

    def now(self, name):
        assert self.order[self.taken] == name, (self.order[self.taken], name)
        self.taken += 1
        return 1


def build(nc, dram, out, scratch, dbg=None):
    ctx = ExitStack()
    with ctx:
        def sb(name, shape, dt=F32):
            return ctx.enter_context(nc.sbuf_tensor(name, shape, dt))

        def sem(name):
            return ctx.enter_context(nc.semaphore(name))

        ps = ctx.enter_context(nc.psum_tensor("banks", [P, 8, BANK], F32))
        tiles = {n: sb("p_" + n, [P, width(PACKS[n])]) for n in ("const", "cols", "w_a")}
        rows_t = sb("p_rows", [P, width(ROWS)])
        REG = 2 * LEAVES * LW
        region = sb("region", [P, 3 * REG])
        ctxT = sb("ctxT", [P, CTX])
        keysT = sb("keysT", [P, CTX])
        values = sb("values", [P, KT_N, H * 9])
        probs = sb("probs", [P, 2, CTX])
        probsT = sb("probsT", [P, 4, BANK])
        xs = sb("xs", [P, 2, P])
        xb = sb("xb", [P, P])
        xn = sb("xn", [P, P])
        xnT = sb("xnT", [P, P])
        tA = sb("tA", [P, P])
        tB = sb("tB", [P, P])
        tC = sb("tC", [P, P])
        tD = sb("tD", [P, P])
        tE = sb("tE", [P, P])
        tF = sb("tF", [P, P])
        tG = sb("tG", [P, P])
        st = sb("st", [P, 6])
        mv = sb("mv", [P, 4])
        half = sb("half", [P, 2])
        one = sb("one", [P, P])
        oneb = sb("oneb", [P, P], BF16)
        identb = sb("identb", [P, P], BF16)
        picks = sb("picks", [P, 16 * P], BF16)
        causalb = sb("causalb", [P, P], BF16)
        small = sb("small", [P, 64])
        small2 = sb("small2", [P, 64])
        small3 = sb("small3", [P, 64])
        small4 = sb("small4", [P, 64])
        seen = sb("seen", [P, 4])
        nmax = sb("nmax", [P, H])
        vaug = sb("vaug", [P, H * 9])
        maskb = sb("maskb", [1, CTX], BF16)
        ffb2 = values[:, :, :].rearrange("p a b -> p (a b)")[:, 0:8 * P]
        shared = sb("shared", [P, 16 * P])
        nodew = shared[:, 0:4 * NODES]
        nbias = shared[:, 8 * P:8 * P + 4 * NODES]
        maskTb = sb("maskTb", [P, 2, P], BF16)
        maskT = sb("maskT", [P, 2, P])
        U = ps[:, 6, :]
        at = {}
        for n, pack in (*((n, PACKS[n]) for n in tiles), ("rows", ROWS)):
            base = rows_t if n == "rows" else tiles[n]
            o = 0
            for name, w in pack:
                at[name if n != "w_a" else "w_" + name] = base[:, o:o + w]
                o += w

        def inside(base, pack):
            o = base
            for name, w in PACKS[pack]:
                at[pack + "." + name] = region[:, o:o + w]
                o += w
            return o

        for i, t in enumerate(("w_q", "w_k", "w_v")):
            inside(i * REG, t)
        inside(0, "w_f")
        inside(2 * REG, "w_l0f")
        inside(2 * REG, "w_l2f")
        assert inside(inside(REG, "w_b"), "w_c") <= 2 * REG
        inside(0, "w_l3f")
        inside(2 * REG, "w_l3d")
        sbq = sb("sbq", [P, CTX])
        b2rows = sbq[:, 8 * P:]
        ident = at["ident"]

        T, V, A, G = (Steps(sem(n)) for n in ("tensor_steps", "vector_steps", "scalar_steps", "gpsimd_steps"))
        v_link, a_link, g_link = sem("vector_link"), sem("scalar_link"), sem("gpsimd_link")
        loads = {n: sem("loaded_" + n) for n in
                 ("x", "const", "cols", "rows", "w_a", "ctxT", "ctx", "mask", "w_l0f", "l0f_b2", "node", "ffb2", "w_q",
                  "w_k", "w_v", "w_f", "w_b", "w_c", "w_l2f", "l2f_b2", "w_l3f", "w_l3d", "ctx2", "bias")}
        load_n = {}
        stored = sem("stored")
        bias_out = sem("bias_stored")
        linked = {"v": 0, "a": 0, "g": 0}

        def vl(dve, ins):
            linked["v"] += 1
            ins.then_inc(v_link, 1)
            dve.wait_ge(v_link, linked["v"])

        def al(act, ins):
            linked["a"] += 1
            ins.then_inc(a_link, 1)
            act.wait_ge(a_link, linked["a"])

        def gl(pool, ins):
            linked["g"] += 1
            ins.then_inc(g_link, 1)
            pool.wait_ge(g_link, linked["g"])

        parts = {"pe": [], "dve": [], "act": [], "pool": [], "sp": []}

        def on(engine):
            def add(f):
                parts[engine].append(f)
                return f
            return add

        def mm(o, lhsT, rhs, start=True, stop=True):
            return nc.tensor.matmul(o, lhsT, rhs, start=start, stop=stop)

        def tr(o, i, n=P):
            return nc.tensor.transpose(o, i, ident[0:n, 0:n])

        def bc(ap, axis, shape):
            return ap.unsqueeze(axis).broadcast_to(shape)

        x_at = {n: i % 2 for i, n in enumerate(STAGES)}

        def load(name, dst, src):
            load_n[name] = load_n.get(name, 0) + 16
            nc.sync.dma_start(dst, src).then_inc(loads[name], 16)

        def loaded(eng, name):
            eng.wait_ge(loads[name], {"node": 32}.get(name, 16))

        @on("sp")
        def _(sp):
            load("x", xs[:, 0, :], dram["x"])
            load("mask", keysT[0:1, :].bitcast(I32), dram["mask"])
            load("const", tiles["const"][:, :], dram["const"])
            load("cols", tiles["cols"][:, :], dram["cols"])
            load("rows", rows_t[:, :], dram["rows"].partition_broadcast(P))
            load("ctxT", ctxT[:, :], dram["ctxT"])
            load("ctx", values[:, :, 0:P], dram["ctx"])
            load("w_a", tiles["w_a"][:, :], dram["w_a"])
            load("w_l0f", region[:, 2 * REG:2 * REG + width(W_L0F)], dram["w_l0f"])
            load("l0f_b2", b2rows, dram["l0f_b2"].partition_broadcast(P))
            load("w_q", region[:, 0:REG], dram["w_q"])
            load("node", nodew, dram["node"])
            load("node", nbias, dram["nbias"].partition_broadcast(P))
            load("w_k", region[:, REG:2 * REG], dram["w_k"])
            sp.wait_ge(V.sem, V.at("d.3"))
            nc.sync.dma_start(scratch, dists[:, :]).then_inc(bias_out, 16)
            sp.wait_ge(V.sem, V.at("l0f.x"))
            load("w_v", region[:, 2 * REG:3 * REG], dram["w_v"])
            sp.wait_ge(V.sem, V.at("l1x.o"))
            load("ffb2", ffb2, dram["ffb2"])
            sp.wait_ge(T.sem, T.at(("fo", "q", 7)))
            load("w_f", region[:, 0:REG], dram["w_f"])
            sp.wait_ge(T.sem, T.at(("fo", "k", 7)))
            load("w_b", region[:, REG:REG + width(W_B)], dram["w_b"])
            load("w_c", region[:, REG + width(W_B):REG + width(W_B) + width(W_C)], dram["w_c"])
            sp.wait_ge(T.sem, T.at(("fo", "v", 7)))
            load("w_l2f", region[:, 2 * REG:3 * REG], dram["w_l2f"])
            sp.wait_ge(T.sem, T.at(("fo", "f", 7)))
            sp.wait_ge(bias_out, 16)
            sp.wait_ge(V.sem, V.at("l1f.x"))
            hankel = bass.AP(scratch.tensor, 0, [[1, P], [255, H], [1, P]])
            load("bias", biases.rearrange("p (h t) -> p h t", h=H), hankel)
            load("w_l3f", region[:, 0:REG], dram["w_l3f"])
            sp.wait_ge(V.sem, V.at("l2x.o"))
            load("ctx2", values[:, :, 0:P], dram["ctx"])
            load("l2f_b2", b2rows, dram["l2f_b2"].partition_broadcast(P))
            sp.wait_ge(V.sem, V.at("l2f.x"))
            load("w_l3d", region[:, 2 * REG:2 * REG + width(W_L3D)], dram["w_l3d"])

        def norm_plan(tag):
            V.plan(tag + ".var", tag + ".xn")
            G.plan(tag + ".rstd")

        def norm_vector(dve, tag, src, eps=EPS):
            vl(dve, nc.vector.bn_stats(st[:, :], src))
            vl(dve, nc.vector.bn_aggr(mv[:, 0:2], st[:, :]))
            nc.vector.tensor_scalar(mv[:, 2:3], mv[:, 1:2], eps, None, ALU.add).then_inc(V.sem, V.now(tag + ".var"))
            dve.wait_ge(G.sem, G.at(tag + ".rstd"))
            nc.vector.tensor_scalar(xn[:, :], src, mv[:, 0:1], mv[:, 3:4], ALU.subtract,
                                    ALU.mult).then_inc(V.sem, V.now(tag + ".xn"))

        def norm_gpsimd(pool, tag):
            pool.wait_ge(V.sem, V.at(tag + ".var"))
            nc.gpsimd.tensor_tensor(mv[:, 3:4], mv[:, 2:3], half[:, 0:1], ALU.pow).then_inc(G.sem, G.now(tag + ".rstd"))

        def turn_plan(tag):
            T.plan(tag + ".turned")
            V.plan(tag + ".T")

        def turn_tensor(pe, tag, src, ready, bank=7, n=P):
            pe.wait_ge(V.sem, V.at(ready))
            tr(ps[0:n, bank, 0:P], src, P).then_inc(T.sem, T.now(tag + ".turned"))

        def turn_vector(dve, tag, dst, bank=7, n=P):
            dve.wait_ge(T.sem, T.at(tag + ".turned"))
            nc.vector.tensor_copy(dst[0:n, :], ps[0:n, bank, 0:P]).then_inc(V.sem, V.now(tag + ".T"))

        def start_vector(dve, tag, bias):
            norm_vector(dve, tag, xs[:, x_at[tag], :])
            if bias is not None:
                nc.vector.tensor_tensor(xb[:, :], xs[:, x_at[tag], :], bias, ALU.add)
            turn_vector(dve, tag + ".xn", xnT)

        def start_tensor(pe, tag):
            turn_tensor(pe, tag + ".xn", xn[:, :], tag + ".xn")

        def start_plan(tag):
            norm_plan(tag)
            turn_plan(tag + ".xn")

        def end_vector(dve, tag, src, base, ready):
            dve.wait_ge(T.sem, T.at(ready))
            nc.vector.tensor_tensor(xs[:, 1 - x_at[tag], :], src, base, ALU.add).then_inc(V.sem, V.now(tag + ".x"))

        def ctx_plan(tag, nh):
            for h in range(nh + 1):
                if h < nh:
                    T.plan((tag, "s", h))
                    V.plan((tag, "m", h))
                if h:
                    g = h - 1
                    T.plan((tag, "t", g, 0), (tag, "t", g, 1), (tag, "pv", g, 0), (tag, "t", g, 2),
                           (tag, "pv", g, 1), (tag, "t", g, 3), (tag, "pv", g, 2), (tag, "pv", g, 3))
                    A.plan((tag, "e", g, 0), (tag, "e", g, 1))
                    V.plan((tag, "e", g, 2), (tag, "e", g, 3))
                if h < nh:
                    A.plan((tag, "exp", h))

        def evacuated(eng, tag, g, c):
            steps = A if c < 2 else V
            eng.wait_ge(steps.sem, steps.at((tag, "e", g, c)))

        def ctx_tensor(pe, tag, nh, query, keys, value, result, ready, mask=None, free=None):
            def turn(g, c):
                if c == 0:
                    pe.wait_ge(A.sem, A.at((tag, "exp", g)))
                n = 4 * g + c - 2
                if n >= 0:
                    evacuated(pe, tag, n // 4, n % 4)
                for j in range(4):
                    m = tr(ps[:, 4 + c % 2, j * P:(j + 1) * P], probs[:, g % 2, (4 * c + j) * P:(4 * c + j + 1) * P])
                m.then_inc(T.sem, T.now((tag, "t", g, c)))

            def weigh(g, c):
                evacuated(pe, tag, g, c)
                if c == 0 and free is not None:
                    free(pe, g)
                for j in range(4):
                    t = 4 * c + j
                    m = mm(result(g), probsT[:, c, j * P:(j + 1) * P], value(g, t), t == 0, t == KT_N - 1)
                m.then_inc(T.sem, T.now((tag, "pv", g, c)))

            for h in range(nh + 1):
                if h < nh:
                    ready(pe, h)
                    if h:
                        pe.wait_ge(A.sem, A.at((tag, "exp", h - 1)))
                    for b in range(NB):
                        m = mm(ps[:, b, :], query(h), keys[:, b * BANK:(b + 1) * BANK], True, mask is None)
                        if mask is not None:
                            m = mm(ps[:, b, :], oneb[0:1, :], mask[:, b * BANK:(b + 1) * BANK], False, True)
                    m.then_inc(T.sem, T.now((tag, "s", h)))
                if h:
                    g = h - 1
                    turn(g, 0)
                    turn(g, 1)
                    weigh(g, 0)
                    turn(g, 2)
                    weigh(g, 1)
                    turn(g, 3)
                    weigh(g, 2)
                    weigh(g, 3)

        def evacuate(eng, tag, g, c):
            eng.wait_ge(T.sem, T.at((tag, "t", g, c)))
            if g:
                eng.wait_ge(T.sem, T.at((tag, "pv", g - 1, c)))
            if c < 2:
                nc.scalar.copy(probsT[:, c, :], ps[:, 4 + c % 2, :]).then_inc(A.sem, A.now((tag, "e", g, c)))
            else:
                nc.vector.tensor_copy(probsT[:, c, :], ps[:, 4 + c % 2, :]).then_inc(V.sem, V.now((tag, "e", g, c)))

        def ctx_vector(dve, tag, nh, scale, after=None):
            for h in range(nh + 1):
                if h < nh:
                    dve.wait_ge(T.sem, T.at((tag, "s", h)))
                    vl(dve, nc.vector.tensor_reduce(small[:, 0:1], ps[:, 0:NB, :], AX.XY, ALU.max))
                    nc.vector.tensor_scalar(nmax[:, h:h + 1], small[:, 0:1], -scale, None,
                                            ALU.mult).then_inc(V.sem, V.now((tag, "m", h)))
                if h:
                    evacuate(dve, tag, h - 1, 2)
                    evacuate(dve, tag, h - 1, 3)
                    if after is not None:
                        after(dve, h - 1)

        def ctx_scalar(act, tag, nh, scale):
            for h in range(nh + 1):
                if h:
                    evacuate(act, tag, h - 1, 0)
                    evacuate(act, tag, h - 1, 1)
                if h < nh:
                    act.wait_ge(V.sem, V.at((tag, "m", h)))
                    nc.scalar.activation(probs[:, h % 2, :], ps[:, 0:NB, :].rearrange("p a b -> p (a b)"), ACT.Exp,
                                         bias=nmax[:, h:h + 1], scale=scale).then_inc(A.sem, A.now((tag, "exp", h)))

        def self_plan(tag):
            T.plan(*((tag, "s", g) for g in range(4)))
            V.plan(*((tag, "sub", g) for g in range(4)))
            A.plan(*((tag, "exp", g) for g in range(4)))
            T.plan((tag, "t", 0), (tag, "t", 1), (tag, "t", 2), (tag, "t", 3), tag + ".U")
            V.plan(*((tag, "e", g) for g in range(4)))
            out_plan(tag)

        def out_plan(tag):
            V.plan(tag + ".o")
            turn_plan(tag + ".o")

        def self_tensor(pe, tag, n, hd, qT, kbd, first=None):
            for g in range(4):
                mm(ps[:, g, :], qT[0:n, :], kbd[0:n, g * BANK:(g + 1) * BANK], first is None,
                   True).then_inc(T.sem, T.now((tag, "s", g)))
            for g in range(4):
                pe.wait_ge(A.sem, A.at((tag, "exp", g)))
                if g >= 2:
                    pe.wait_ge(V.sem, V.at((tag, "e", g - 2)))
                for j in range(4):
                    m = tr(ps[:, 4 + g % 2, j * P:(j + 1) * P], probs[:, 1, (4 * g + j) * P:(4 * g + j + 1) * P])
                m.then_inc(T.sem, T.now((tag, "t", g)))
            w = hd + 1
            for g in range(4):
                pe.wait_ge(V.sem, V.at((tag, "e", g)))
                for j in range(4):
                    h = 4 * g + j
                    m = mm(U[:, h * w:(h + 1) * w], probsT[:, g, j * P:(j + 1) * P], vaug[:, h * w:(h + 1) * w])
            m.then_inc(T.sem, T.now(tag + ".U"))
            turn_tensor(pe, tag + ".o", tA[:, 0:n], tag + ".o", 5, n)

        def self_vector(dve, tag, n, hd):
            for g in range(4):
                dve.wait_ge(T.sem, T.at((tag, "s", g)))
                s = ps[:, g, :].rearrange("p (h t) -> p h t", h=4)
                vl(dve, nc.vector.tensor_reduce(nmax[:, 4 * g:4 * g + 4], s, AX.X, ALU.max))
                nc.vector.tensor_tensor(probs[:, 1, g * BANK:(g + 1) * BANK].rearrange("p (h t) -> p h t", h=4), s,
                                        bc(nmax[:, 4 * g:4 * g + 4], 2, [P, 4, P]),
                                        ALU.subtract).then_inc(V.sem, V.now((tag, "sub", g)))
            for g in range(4):
                dve.wait_ge(T.sem, T.at((tag, "t", g)))
                nc.vector.tensor_copy(probsT[:, g, :], ps[:, 4 + g % 2, :]).then_inc(V.sem, V.now((tag, "e", g)))
            dve.wait_ge(T.sem, T.at(tag + ".U"))
            out_vector(dve, tag, n, hd)

        def out_vector(dve, tag, n, hd):
            u = U[:, 0:H * (hd + 1)].rearrange("p (h w) -> p h w", h=H)
            vl(dve, nc.vector.reciprocal(small[:, 0:H], u[:, :, hd]))
            nc.vector.tensor_tensor(tA[:, 0:n].rearrange("p (h w) -> p h w", h=H), u[:, :, 0:hd],
                                    bc(small[:, 0:H], 2, [P, H, hd]), ALU.mult).then_inc(V.sem, V.now(tag + ".o"))
            turn_vector(dve, tag + ".o", tB, 5, n)

        def self_scalar(act, tag, scale):
            for g in range(4):
                act.wait_ge(V.sem, V.at((tag, "sub", g)))
                p = probs[:, 1, g * BANK:(g + 1) * BANK]
                nc.scalar.activation(p, p, ACT.Exp, scale=scale).then_inc(A.sem, A.now((tag, "exp", g)))

        def spread_heads(dst, src, heads, n):
            return nc.vector.tensor_tensor(dst.rearrange("p (h t) -> p h t", h=H)[0:n], bc(src[0:n, :], 1, [n, H, P]),
                                           bc(heads[0:n, :], 2, [n, H, P]), ALU.mult)

        def top2(dve, vals, mask):
            mine, other = bc(vals, 2, [P, E, E]), bc(vals, 1, [P, E, E])
            v3 = small2[:, :].rearrange("p (a b) -> p a b", a=E)
            w3 = small3[:, :].rearrange("p (a b) -> p a b", a=E)
            nc.vector.tensor_tensor(w3, other, mine, ALU.is_gt)
            vl(dve, nc.vector.tensor_tensor(v3, other, mine, ALU.is_ge))
            vl(dve, nc.vector.tensor_tensor(small2[:, :], small2[:, :], at["before"], ALU.mult))
            vl(dve, nc.vector.tensor_tensor(small2[:, :], small2[:, :], small3[:, :], ALU.max))
            vl(dve, nc.vector.tensor_reduce(small3[:, 0:E], v3, AX.X, ALU.add))
            vl(dve, nc.vector.tensor_scalar(mask, small3[:, 0:E], 1.5, None, ALU.is_lt))

        def moe_plan(tag):
            for g in range(tag_groups[tag] + 1):
                if g < tag_groups[tag]:
                    T.plan((tag, "h", g))
                    A.plan((tag, "a", g))
                    V.plan((tag, "g", g))
                if g:
                    T.plan((tag, "o", g - 1))

        tag_groups = {"l0f": 4, "l2f": 8, "l3f": 8}

        def moe_tensor(pe, tag, w_in, w_gate, w_out, xT, per):
            ng = tag_groups[tag]
            for g in range(ng + 1):
                if g < ng:
                    if g >= 2:
                        pe.wait_ge(V.sem, V.at((tag, "g", g - 2)))
                    for j in range(4):
                        c = 4 * g + j
                        m = mm(ps[:, g % 2, j * P:(j + 1) * P], w_in[:, c * P:(c + 1) * P], xT)
                        if w_gate is not None:
                            m = mm(ps[:, 2 + g % 2, j * P:(j + 1) * P], w_gate[:, c * P:(c + 1) * P], xT)
                    m.then_inc(T.sem, T.now((tag, "h", g)))
                if g:
                    pe.wait_ge(V.sem, V.at((tag, "g", g - 1)))
                    for j in range(4):
                        c = 4 * (g - 1) + j
                        e = c // per
                        m = mm(ps[:, 4 + e // 4, (e % 4) * P:(e % 4 + 1) * P],
                               probs[:, 1, (g - 1) % 2 * BANK + j * P:(g - 1) % 2 * BANK + (j + 1) * P],
                               w_out[:, c * P:(c + 1) * P], c % per == 0, c % per == per - 1)
                    m.then_inc(T.sem, T.now((tag, "o", g - 1)))

        def moe_scalar(act, tag, func, bias):
            for g in range(tag_groups[tag]):
                act.wait_ge(T.sem, T.at((tag, "h", g)))
                if g >= 2:
                    act.wait_ge(V.sem, V.at((tag, "g", g - 2)))
                o = g % 2 * BANK
                if bias is None:
                    m = nc.scalar.activation(probs[:, 0, o:o + BANK], ps[:, g % 2, :], func)
                else:
                    for j in range(4):
                        m = nc.scalar.activation(probs[:, 0, o + j * P:o + (j + 1) * P], ps[:, g % 2, j * P:(j + 1) * P],
                                                 func, bias=bias[:, 4 * g + j:4 * g + j + 1])
                m.then_inc(A.sem, A.now((tag, "a", g)))

        def moe_vector(dve, tag, gated):
            for g in range(tag_groups[tag]):
                dve.wait_ge(A.sem, A.at((tag, "a", g)))
                if g >= 2:
                    dve.wait_ge(T.sem, T.at((tag, "o", g - 2)))
                o = g % 2 * BANK
                if gated:
                    m = nc.vector.tensor_tensor(probs[:, 1, o:o + BANK], probs[:, 0, o:o + BANK], ps[:, 2 + g % 2, :],
                                                ALU.mult)
                else:
                    m = nc.vector.tensor_copy(probs[:, 1, o:o + BANK], probs[:, 0, o:o + BANK])
                m.then_inc(V.sem, V.now((tag, "g", g)))

        G.plan("const")
        V.plan("prelude")

        @on("pool")
        def _(pool):
            nc.gpsimd.memset(half[:, 0:1], -0.5)
            nc.gpsimd.memset(half[:, 1:2], 0.5)
            nc.gpsimd.memset(one[:, :], 1.0)
            nc.gpsimd.memset(oneb[:, :], 1.0)
            nc.gpsimd.memset(vaug[:, :], 1.0)
            nc.gpsimd.memset(values[:, :, P:H * 9], 1.0).then_inc(G.sem, G.now("const"))

        @on("dve")
        def _(dve):
            loaded(dve, "const")
            nc.vector.tensor_copy(identb[:, :], ident)
            nc.vector.tensor_copy(picks[:, :].rearrange("p (k w) -> p k w", w=LW), bc(ident, 2, [P, P, LW]))
            nc.vector.tensor_copy(causalb[:, :], at["causal"]).then_inc(V.sem, V.now("prelude"))

        def l0x():
            tag = "l0x"
            start_plan(tag)
            V.plan("l0x.q")
            ctx_plan(tag, 1)
            V.plan("l0x.t")
            T.plan("l0x.row")
            V.plan("l0x.rowmax")
            A.plan("l0x.rowexp")
            V.plan("l0x.row")
            T.plan("l0x.batt")
            V.plan("l0x.batt")
            T.plan("l0x.bar")
            V.plan("l0x.bar")
            V.plan("l0x.hq")
            turn_plan("l0x.hq")
            V.plan("l0x.prod")
            T.plan("l0x.y")
            V.plan("l0x.x")
            s = small4

            @on("pe")
            def _(pe):
                loaded(pe, "const")
                start_tensor(pe, tag)

                def ready(pe, h):
                    loaded(pe, "ctxT")
                    pe.wait_ge(V.sem, V.at("l0x.q"))
                pe.wait_ge(G.sem, G.at("const"))
                loaded(pe, "ctx")
                ctx_tensor(pe, tag, 1, lambda h: tA[:, :], ctxT, lambda g, t: values[:, t, 0:P + 1],
                           lambda g: ps[:, 6, 0:P + 1], ready)
                pe.wait_ge(V.sem, V.at("l0x.t"))
                tr(ps[0:1, 7, 0:P], s[:, 2:3]).then_inc(T.sem, T.now("l0x.row"))
                pe.wait_ge(V.sem, V.at("l0x.row"))
                mm(ps[:, 7, 128:129], tC[0:1, :], one[0:1, 0:1]).then_inc(T.sem, T.now("l0x.batt"))
                pe.wait_ge(V.sem, V.at("l0x.batt"))
                mm(ps[:, 7, 130:131], xn[:, :], s[:, 8:9]).then_inc(T.sem, T.now("l0x.bar"))
                turn_tensor(pe, "l0x.hq", tB[:, :], "l0x.hq", 5)
                pe.wait_ge(V.sem, V.at("l0x.prod"))
                loaded(pe, "w_a")
                for i, f in enumerate((xnT, tD, tE, tF)):
                    m = mm(ps[:, 4, 0:P], f[:, :], at["w_l0x"][:, i * P:(i + 1) * P], i == 0, i == 3)
                m.then_inc(T.sem, T.now("l0x.y"))

            @on("dve")
            def _(dve):
                loaded(dve, "x")
                dve.wait_ge(G.sem, G.at("const"))
                loaded(dve, "rows")
                loaded(dve, "cols")
                start_vector(dve, tag, at["l0x_b"])
                dve.wait_ge(V.sem, V.at("l0x.xn.T"))
                nc.vector.tensor_scalar(tA[:, :], xnT[:, :], at["w3"], at["w2"], ALU.mult,
                                        ALU.add).then_inc(V.sem, V.now("l0x.q"))
                nc.vector.tensor_tensor_reduce(tC[:, :], xn[:, :], at["w1"], 1.0, 0.0, ALU.mult, ALU.add, s[:, 0:1])
                ctx_vector(dve, tag, 1, 1.0)
                vl(dve, nc.vector.tensor_tensor(s[:, 1:2], s[:, 0:1], at["b_sim"], ALU.add))
                nc.vector.tensor_tensor(s[:, 2:3], s[:, 1:2], nmax[:, 0:1],
                                        ALU.subtract).then_inc(V.sem, V.now("l0x.t"))
                dve.wait_ge(T.sem, T.at("l0x.row"))
                nc.vector.tensor_reduce(s[0:1, 4:5], ps[0:1, 7, 0:P], AX.X, ALU.max,
                                        negate=True).then_inc(V.sem, V.now("l0x.rowmax"))
                dve.wait_ge(A.sem, A.at("l0x.rowexp"))
                vl(dve, nc.vector.reciprocal(s[0:1, 6:7], s[0:1, 5:6]))
                nc.vector.tensor_scalar(tC[0:1, :], tC[0:1, :], s[0:1, 6:7], None,
                                        ALU.mult).then_inc(V.sem, V.now("l0x.row"))
                dve.wait_ge(T.sem, T.at("l0x.batt"))
                nc.vector.tensor_copy(s[:, 8:9], ps[:, 7, 128:129]).then_inc(V.sem, V.now("l0x.batt"))
                dve.wait_ge(T.sem, T.at("l0x.bar"))
                nc.vector.tensor_copy(s[:, 9:10], ps[:, 7, 130:131]).then_inc(V.sem, V.now("l0x.bar"))
                dve.wait_ge(T.sem, T.at((tag, "pv", 0, 3)))
                vl(dve, nc.vector.reciprocal(s[:, 10:11], ps[:, 6, P:P + 1]))
                nc.vector.tensor_scalar(tB[:, :], ps[:, 6, 0:P], s[:, 10:11], None,
                                        ALU.mult).then_inc(V.sem, V.now("l0x.hq"))
                turn_vector(dve, "l0x.hq", tD, 5)
                dve.wait_ge(V.sem, V.at("l0x.hq.T"))
                nc.vector.tensor_tensor(tE[:, :], xnT[:, :], tD[:, :], ALU.mult)
                nc.vector.tensor_scalar(tF[:, :], xnT[:, :], s[:, 9:10], None,
                                        ALU.mult).then_inc(V.sem, V.now("l0x.prod"))
                end_vector(dve, tag, ps[:, 4, 0:P], xb[:, :], "l0x.y")

            @on("act")
            def _(act):
                ctx_scalar(act, tag, 1, 1.0)
                act.wait_ge(V.sem, V.at("l0x.rowmax"))
                nc.scalar.activation(tC[0:1, :], ps[0:1, 7, 0:P], ACT.Exp, bias=s[0:1, 4:5],
                                     accum_out=s[0:1, 5:6]).then_inc(A.sem, A.now("l0x.rowexp"))

            @on("pool")
            def _(pool):
                norm_gpsimd(pool, tag)

        def l0a():
            tag = "l0a"
            start_plan(tag)
            T.plan("l0a.qkv")
            V.plan("l0a.v", "l0a.q", "l0a.k")
            turn_plan("l0a.q")
            T.plan("l0a.kv")
            V.plan("l0a.kv")
            T.plan("l0a.c")
            V.plan("l0a.c")
            T.plan("l0a.y")
            V.plan("l0a.x")

            @on("pe")
            def _(pe):
                start_tensor(pe, tag)
                pe.wait_ge(V.sem, V.at("l0a.xn.T"))
                for i, w in enumerate(("q", "k", "v")):
                    m = mm(ps[:, i, 0:P], xnT[:, :], at["w_l0a_" + w])
                m.then_inc(T.sem, T.now("l0a.qkv"))
                turn_tensor(pe, "l0a.q", tA[:, :], "l0a.q", 5)
                pe.wait_ge(V.sem, V.at("l0a.k"))
                mm(ps[:, 3, 0:P], tB[:, :], tC[:, :]).then_inc(T.sem, T.now("l0a.kv"))
                pe.wait_ge(V.sem, V.at("l0a.kv"))
                mm(ps[:, 4, 0:P], tD[:, :], tE[:, :]).then_inc(T.sem, T.now("l0a.c"))
                pe.wait_ge(V.sem, V.at("l0a.c"))
                mm(ps[:, 6, 0:P], tF[:, :], at["w_l0a_o"]).then_inc(T.sem, T.now("l0a.y"))

            def rotate(dve, src, bias, dst, name):
                vl(dve, nc.vector.tensor_tensor(tG[:, :], src, bias, ALU.add))
                g = tG[:, :].rearrange("p (n t) -> p n t", t=2)
                f = tF[:, :].rearrange("p (n t) -> p n t", t=2)
                sn = at["sin"].rearrange("p (n t) -> p n t", t=2)
                nc.vector.tensor_tensor(f[:, :, 0], g[:, :, 1], sn[:, :, 0], ALU.mult)
                nc.vector.tensor_tensor(f[:, :, 1], g[:, :, 0], sn[:, :, 1], ALU.mult)
                vl(dve, nc.vector.tensor_tensor(dst[:, :], tG[:, :], at["cos"], ALU.mult))
                nc.vector.tensor_tensor(dst[:, :], dst[:, :], tF[:, :], ALU.add).then_inc(V.sem, V.now(name))
                dve.wait_ge(V.sem, V.at(name))

            @on("dve")
            def _(dve):
                dve.wait_ge(V.sem, V.at("l0x.x"))
                start_vector(dve, tag, at["l0a_bo"])
                dve.wait_ge(T.sem, T.at("l0a.qkv"))
                nc.vector.tensor_tensor(tC[:, :], ps[:, 2, 0:P], at["l0a_bv"], ALU.add).then_inc(V.sem, V.now("l0a.v"))
                rotate(dve, ps[:, 0, 0:P], at["l0a_bq"], tA, "l0a.q")
                rotate(dve, ps[:, 1, 0:P], at["l0a_bk"], tB, "l0a.k")
                turn_vector(dve, "l0a.q", tE, 5)
                dve.wait_ge(T.sem, T.at("l0a.kv"))
                nc.vector.scalar_tensor_tensor(tD[:, :], ps[:, 3, 0:P], 1.0 / np.sqrt(8.0), at["bm8"], ALU.mult,
                                               ALU.mult).then_inc(V.sem, V.now("l0a.kv"))
                dve.wait_ge(T.sem, T.at("l0a.c"))
                nc.vector.tensor_copy(tF[:, :], ps[:, 4, 0:P]).then_inc(V.sem, V.now("l0a.c"))
                end_vector(dve, tag, ps[:, 6, 0:P], xb[:, :], "l0a.y")

            @on("pool")
            def _(pool):
                norm_gpsimd(pool, tag)

        def l0f():
            tag = "l0f"
            start_plan(tag)
            T.plan("l0f.qkv")
            V.plan("l0f.qkv")
            self_plan(tag)
            T.plan("l0f.mla")
            V.plan("l0f.mla")
            turn_plan("l0f.mla")
            T.plan("l0f.route")
            V.plan("l0f.rmax")
            A.plan("l0f.rexp")
            V.plan("l0f.comb")
            moe_plan(tag)
            V.plan("l0f.x")
            s = small4

            @on("pe")
            def _(pe):
                start_tensor(pe, tag)
                pe.wait_ge(V.sem, V.at("l0f.xn.T"))
                mm(ps[0:64, 4, 0:P], at["w_l0f_q"], xnT[:, :])
                mm(ps[0:64, 5, 0:P], at["w_l0f_k"], xnT[:, :])
                mm(ps[:, 6, 0:64], xnT[:, :], at["w_l0f_v"]).then_inc(T.sem, T.now("l0f.qkv"))
                pe.wait_ge(V.sem, V.at("l0f.qkv"))
                self_tensor(pe, tag, 64, 4, tC, probs[:, 0, :])
                pe.wait_ge(V.sem, V.at("l0f.o.T"))
                mm(ps[:, 7, 0:P], tB[0:64, :], at["w_l0f_o"][0:64, :]).then_inc(T.sem, T.now("l0f.mla"))
                turn_tensor(pe, "l0f.mla", tC[:, :], "l0f.mla", 6)
                pe.wait_ge(V.sem, V.at("l0f.mla.T"))
                mm(ps[:, 7, 0:E], tD[:, :], at["w_l0f_r"]).then_inc(T.sem, T.now("l0f.route"))
                loaded(pe, "w_l0f")
                moe_tensor(pe, tag, at["w_l0f.w1"], None, at["w_l0f.w2"], tD[:, :], 2)

            @on("dve")
            def _(dve):
                dve.wait_ge(V.sem, V.at("l0a.x"))
                start_vector(dve, tag, None)
                dve.wait_ge(T.sem, T.at("l0f.qkv"))
                nc.vector.tensor_scalar(tC[0:64, :], ps[0:64, 4, 0:P], at["l0f_qb"][0:64, :], None, ALU.add)
                vl(dve, nc.vector.tensor_scalar(tD[0:64, :], ps[0:64, 5, 0:P], at["l0f_kb"][0:64, :], None, ALU.add))
                va = vaug[:, 0:H * 5].rearrange("p (h w) -> p h w", h=H)
                nc.vector.tensor_tensor(va[:, :, 0:4], ps[:, 6, 0:64].rearrange("p (h w) -> p h w", h=H),
                                        at["l0f_vb"].rearrange("p (h w) -> p h w", h=H), ALU.add)
                spread_heads(probs[:, 0, :], tD, at["hm4"], 64).then_inc(V.sem, V.now("l0f.qkv"))
                self_vector(dve, tag, 64, 4)
                dve.wait_ge(T.sem, T.at("l0f.mla"))
                nc.vector.tensor_tensor(tC[:, :], ps[:, 7, 0:P], at["l0f_ob"], ALU.add).then_inc(V.sem, V.now("l0f.mla"))
                turn_vector(dve, "l0f.mla", tD, 6)
                route_vector(dve, "l0f", at["l0f_rb"])
                top2(dve, s[:, 16:24], s[:, 24:32])
                vl(dve, nc.vector.tensor_tensor_reduce(s[:, 32:40], s[:, 16:24], s[:, 24:32], 1.0, 0.0, ALU.mult,
                                                       ALU.add, s[:, 40:41]))
                vl(dve, nc.vector.tensor_scalar(s[:, 41:42], s[:, 40:41], 1e-8, None, ALU.add))
                vl(dve, nc.vector.reciprocal(s[:, 42:43], s[:, 41:42]))
                nc.vector.tensor_scalar(s[:, 48:56], s[:, 32:40], s[:, 42:43], 0.3, ALU.mult,
                                        ALU.mult).then_inc(V.sem, V.now("l0f.comb"))
                vl(dve, nc.vector.tensor_tensor(xb[:, :], xs[:, x_at[tag], :], xn[:, :], ALU.add))
                moe_vector(dve, tag, False)
                loaded(dve, "l0f_b2")
                mix_vector(dve, tag, s[:, 48:56], xb[:, :])

            @on("act")
            def _(act):
                self_scalar(act, tag, 0.5)
                route_scalar(act, "l0f")
                loaded(act, "cols")
                moe_scalar(act, tag, ACT.Gelu, at["l0f_b1"])

            @on("pool")
            def _(pool):
                norm_gpsimd(pool, tag)

        def route_vector(dve, tag, bias):
            s = small4
            dve.wait_ge(T.sem, T.at(tag + ".route"))
            vl(dve, nc.vector.tensor_tensor(s[:, 0:8], ps[:, 7, 0:E], bias, ALU.add))
            nc.vector.tensor_reduce(s[:, 8:9], s[:, 0:8], AX.X, ALU.max, negate=True).then_inc(V.sem, V.now(tag + ".rmax"))
            dve.wait_ge(A.sem, A.at(tag + ".rexp"))
            vl(dve, nc.vector.reciprocal(s[:, 10:11], s[:, 9:10]))
            vl(dve, nc.vector.tensor_scalar(s[:, 16:24], s[:, 0:8], s[:, 10:11], None, ALU.mult))

        def route_scalar(act, tag):
            s = small4
            act.wait_ge(V.sem, V.at(tag + ".rmax"))
            nc.scalar.activation(s[:, 0:8], s[:, 0:8], ACT.Exp, bias=s[:, 8:9],
                                 accum_out=s[:, 9:10]).then_inc(A.sem, A.now(tag + ".rexp"))

        def mix_vector(dve, tag, comb, base, biases=True):
            ng = tag_groups[tag]
            dve.wait_ge(T.sem, T.at((tag, "o", ng - 1)))
            if biases:
                nc.vector.tensor_tensor(probs[:, 0, 0:BANK], ps[:, 4, :], b2rows[:, 0:BANK], ALU.add)
                vl(dve, nc.vector.tensor_tensor(probs[:, 0, BANK:2 * BANK], ps[:, 5, :], b2rows[:, BANK:], ALU.add))
            src = base
            for e in range(E):
                last = e == E - 1
                dst = xs[:, 1 - x_at[tag], :] if last else (tE, tF)[e % 2][:, :]
                o = probs[:, 0, e * P:(e + 1) * P] if biases else ps[:, 4 + e // 4, (e % 4) * P:(e % 4 + 1) * P]
                m = nc.vector.scalar_tensor_tensor(dst, o, comb[:, e:e + 1], src, ALU.mult, ALU.add)
                if last:
                    m.then_inc(V.sem, V.now(tag + ".x"))
                else:
                    vl(dve, m)
                src = dst

        def kv_plan(tag):
            T.plan(*((tag, "kv", i) for i in range(8)))
            A.plan(*((tag, "k", i) for i in range(4)))
            V.plan(*((tag, "v", i) for i in range(4)))

        def kv_tensor(pe, tag, wk, wv):
            for b in range(NB):
                mm(ps[:, b, :], wk, ctxT[:, b * BANK:(b + 1) * BANK]).then_inc(T.sem, T.now((tag, "kv", b)))
            for b in range(4):
                pe.wait_ge(A.sem, A.at((tag, "k", b)))
                for j in range(4):
                    t = 4 * b + j
                    m = mm(ps[:, b, j * P:(j + 1) * P], ctxT[:, t * P:(t + 1) * P], wv)
                m.then_inc(T.sem, T.now((tag, "kv", 4 + b)))

        def kv_scalar(act, tag, bias):
            for b in range(NB):
                act.wait_ge(T.sem, T.at((tag, "kv", b)))
                o = keysT[:, b * BANK:(b + 1) * BANK]
                if bias is None:
                    m = nc.scalar.copy(o, ps[:, b, :])
                else:
                    m = nc.scalar.activation(o, ps[:, b, :], ACT.Identity, bias=bias)
                m.then_inc(A.sem, A.now((tag, "k", b)))

        def kv_vector(dve, tag, bias):
            for b in range(4):
                dve.wait_ge(T.sem, T.at((tag, "kv", 4 + b)))
                for j in range(4):
                    t = 4 * b + j
                    o = values[:, t, :].rearrange("p (h w) -> p h w", h=H)[:, :, 0:8]
                    i = ps[:, b, j * P:(j + 1) * P].rearrange("p (h w) -> p h w", h=H)
                    if bias is None:
                        m = nc.vector.tensor_copy(o, i)
                    else:
                        m = nc.vector.tensor_tensor(o, i, bias.rearrange("p (h w) -> p h w", h=H), ALU.add)
                m.then_inc(V.sem, V.now((tag, "v", b)))

        def cross(tag, before, w, scale, masked, q_bias, k_bias, v_bias, o_bias, pack):
            G.plan(tag + ".ones")
            kv_plan(tag)
            start_plan(tag)
            T.plan(tag + ".q")
            V.plan(tag + ".q")
            ctx_plan(tag, H)
            out_plan(tag)
            T.plan(tag + ".y")
            V.plan(tag + ".x")
            qbd = sbq[:, :]

            @on("pe")
            def _(pe):
                loaded(pe, pack)
                pe.wait_ge(V.sem, V.at(before))
                kv_tensor(pe, tag, w("k"), w("v"))
                start_tensor(pe, tag)
                pe.wait_ge(V.sem, V.at(tag + ".xn.T"))
                mm(ps[:, 7, 0:P], w("q"), xnT[:, :]).then_inc(T.sem, T.now(tag + ".q"))

                def ready(pe, h):
                    if h == 0:
                        pe.wait_ge(V.sem, V.at(tag + ".q"))
                        pe.wait_ge(A.sem, A.at((tag, "k", 3)))
                ctx_tensor(pe, tag, H, lambda h: qbd[:, h * P:(h + 1) * P], keysT,
                           lambda g, t: values[:, t, 9 * g:9 * g + 9], lambda g: U[:, 9 * g:9 * g + 9], ready,
                           maskb if masked else None)
                turn_tensor(pe, tag + ".o", tA[:, :], tag + ".o", 5)
                pe.wait_ge(V.sem, V.at(tag + ".o.T"))
                mm(ps[:, 7, 0:P], tB[:, :], w("o")).then_inc(T.sem, T.now(tag + ".y"))

            @on("dve")
            def _(dve):
                dve.wait_ge(V.sem, V.at(before))
                dve.wait_ge(G.sem, G.at(tag + ".ones"))
                kv_vector(dve, tag, v_bias)
                start_vector(dve, tag, o_bias)
                dve.wait_ge(T.sem, T.at(tag + ".q"))
                if masked:
                    vl(dve, nc.vector.tensor_scalar(tC[:, :], ps[:, 7, 0:P], q_bias, seen[:, 2:3], ALU.add, ALU.mult))
                else:
                    vl(dve, nc.vector.tensor_copy(tC[:, :], ps[:, 7, 0:P]))
                spread_heads(qbd, tC, at["hm8"], P).then_inc(V.sem, V.now(tag + ".q"))
                ctx_vector(dve, tag, H, scale)
                dve.wait_ge(T.sem, T.at((tag, "pv", H - 1, 3)))
                out_vector(dve, tag, P, 8)
                end_vector(dve, tag, ps[:, 7, 0:P], xb[:, :], tag + ".y")

            @on("act")
            def _(act):
                loaded(act, "cols")
                kv_scalar(act, tag, k_bias)
                ctx_scalar(act, tag, H, scale)

            @on("pool")
            def _(pool):
                pool.wait_ge(V.sem, V.at(before))
                nc.gpsimd.memset(values[:, :, :], 1.0).then_inc(G.sem, G.now(tag + ".ones"))
                norm_gpsimd(pool, tag)

        def l1a():
            tag = "l1a"
            start_plan(tag)
            T.plan("l1a.qkv")
            V.plan("l1a.qkv")
            T.plan("l1a.kv")
            V.plan("l1a.kv")
            T.plan("l1a.num")
            V.plan("l1a.o")
            turn_plan("l1a.o")
            T.plan("l1a.y")
            V.plan("l1a.x")

            @on("pe")
            def _(pe):
                start_tensor(pe, tag)
                pe.wait_ge(V.sem, V.at("l1a.xn.T"))
                w = at["w_l1a_qkv"]
                mm(ps[:, 0, 0:P], w[:, 0:P], xnT[:, :])
                mm(ps[:, 1, 0:P], xnT[:, :], w[:, P:2 * P])
                mm(ps[:, 2, 0:P], xnT[:, :], w[:, 2 * P:3 * P]).then_inc(T.sem, T.now("l1a.qkv"))
                pe.wait_ge(V.sem, V.at("l1a.qkv"))
                mm(ps[:, 3, 0:P], tB[:, :], tC[:, :])
                mm(ps[:, 4, 0:P], tB[:, :], one[:, :]).then_inc(T.sem, T.now("l1a.kv"))
                pe.wait_ge(V.sem, V.at("l1a.kv"))
                mm(ps[:, 5, 0:P], tA[:, :], tD[:, :])
                mm(ps[:, 6, 0:P], tA[:, :], tE[:, :]).then_inc(T.sem, T.now("l1a.num"))
                turn_tensor(pe, "l1a.o", tF[:, :], "l1a.o", 7)
                pe.wait_ge(V.sem, V.at("l1a.o.T"))
                mm(ps[:, 0, 0:P], tG[:, :], at["w_l1a_p"]).then_inc(T.sem, T.now("l1a.y"))

            @on("dve")
            def _(dve):
                dve.wait_ge(V.sem, V.at("l1x.x"))
                start_vector(dve, tag, at["l1a_b"])
                dve.wait_ge(T.sem, T.at("l1a.qkv"))
                nc.vector.tensor_scalar(tA[:, :], ps[:, 0, 0:P], 0.0, None, ALU.max)
                nc.vector.tensor_scalar(tB[:, :], ps[:, 1, 0:P], 0.0, None, ALU.max)
                nc.vector.tensor_scalar(tC[:, :], ps[:, 2, 0:P], 0.0, None, ALU.max).then_inc(V.sem, V.now("l1a.qkv"))
                dve.wait_ge(T.sem, T.at("l1a.kv"))
                nc.vector.tensor_tensor(tD[:, :], ps[:, 3, 0:P], at["bm4"], ALU.mult)
                nc.vector.tensor_tensor(tE[:, :], ps[:, 4, 0:P], at["bm4"], ALU.mult).then_inc(V.sem, V.now("l1a.kv"))
                dve.wait_ge(T.sem, T.at("l1a.num"))
                vl(dve, nc.vector.tensor_scalar(tG[:, :], ps[:, 6, 0:P], 1e-15, None, ALU.add))
                vl(dve, nc.vector.reciprocal(tF[:, :], tG[:, :]))
                nc.vector.tensor_tensor(tF[:, :], ps[:, 5, 0:P], tF[:, :], ALU.mult).then_inc(V.sem, V.now("l1a.o"))
                turn_vector(dve, "l1a.o", tG, 7)
                end_vector(dve, tag, ps[:, 0, 0:P], xb[:, :], "l1a.y")

            @on("pool")
            def _(pool):
                norm_gpsimd(pool, tag)

        TREES = ("q", "k", "v", "f")

        def tree_plan(i):
            n = TREES[i]
            T.plan(("fm", n))
            V.plan(("fm", n))
            for g in range(9):
                if g < 8:
                    T.plan(("fa", n, g))
                    A.plan(("fr", n, g))
                    V.plan(("fh", n, g))
                if g:
                    T.plan(("fo", n, g - 1))

        def tree_tensor(pe, i, xT, turned):
            n = TREES[i]
            loaded(pe, "w_" + n)
            o = ps[:, 4 + i % 4, 0:P]
            w1, w2 = at[f"w_{n}.w1"], at[f"w_{n}.w2"]
            mask = paths[:, i % 3, :]
            tr(ps[:, 0, 0:P], mask[:, 0:P])
            tr(ps[:, 0, P:2 * P], mask[:, P:2 * P]).then_inc(T.sem, T.now(("fm", n)))
            pe.wait_ge(V.sem, V.at(("fm", n)))
            loaded(pe, "ffb2")
            for c in range(2):
                b2 = ffb2[:, (2 * i + c) * P:(2 * i + c + 1) * P]
                if turned:
                    mm(o, b2, maskT[:, c, :], c == 0, False)
                else:
                    mm(o, maskT[:, c, :], b2, c == 0, False)
            for g in range(9):
                if g < 8:
                    if g >= 2:
                        pe.wait_ge(A.sem, A.at(("fr", n, g - 2)))
                        pe.wait_ge(V.sem, V.at(("fh", n, g - 2)))
                    for j in range(4):
                        c = 4 * g + j
                        mm(ps[:, g % 2, j * P:(j + 1) * P], w1[:, c * P:(c + 1) * P], xT)
                    for j in range(4):
                        c = 4 * g + j
                        pick = picks[:, (c % 16) * P:(c % 16 + 1) * P]
                        m = mm(ps[:, 2 + g % 2, j * P:(j + 1) * P], pick, maskTb[:, c // 16, :])
                    m.then_inc(T.sem, T.now(("fa", n, g)))
                if g:
                    pe.wait_ge(V.sem, V.at(("fh", n, g - 1)))
                    for j in range(4):
                        c = 4 * (g - 1) + j
                        h = probs[:, 1, (g - 1) % 2 * BANK + j * P:(g - 1) % 2 * BANK + (j + 1) * P]
                        w = w2[:, c * P:(c + 1) * P]
                        m = mm(o, w, h, False, c == CH - 1) if turned else mm(o, h, w, False, c == CH - 1)
                    m.then_inc(T.sem, T.now(("fo", n, g - 1)))

        def tree_scalar(act, i, func):
            n = TREES[i]
            for g in range(8):
                act.wait_ge(T.sem, T.at(("fa", n, g)))
                if g >= 2:
                    act.wait_ge(V.sem, V.at(("fh", n, g - 2)))
                o = g % 2 * BANK
                for j in range(4):
                    c = 4 * g + j
                    m = nc.scalar.activation(probs[:, 0, o + j * P:o + (j + 1) * P], ps[:, g % 2, j * P:(j + 1) * P],
                                             func, bias=at["fff_b1"][:, i * CH + c:i * CH + c + 1])
                m.then_inc(A.sem, A.now(("fr", n, g)))

        def tree_vector(dve, i):
            n = TREES[i]
            dve.wait_ge(T.sem, T.at(("fm", n)))
            nc.vector.tensor_copy(maskT[:, :, :].rearrange("p a b -> p (a b)"), ps[:, 0, 0:2 * P])
            nc.vector.tensor_copy(maskTb[:, :, :].rearrange("p a b -> p (a b)"),
                                  ps[:, 0, 0:2 * P]).then_inc(V.sem, V.now(("fm", n)))
            for g in range(8):
                dve.wait_ge(A.sem, A.at(("fr", n, g)))
                if g >= 2:
                    dve.wait_ge(T.sem, T.at(("fo", n, g - 2)))
                o = g % 2 * BANK
                nc.vector.tensor_tensor(probs[:, 1, o:o + BANK], probs[:, 0, o:o + BANK], ps[:, 2 + g % 2, :],
                                        ALU.mult).then_inc(V.sem, V.now(("fh", n, g)))

        def walk_vector(dve, first, count, name):
            ways = keysT[:, 0:count * 2 * LEAVES].rearrange("p (n k s) -> p n k s", n=count, s=2)
            for j in range(count):
                i = first + j
                vl(dve, nc.vector.tensor_tensor(probs[:, 0, j * NODES:(j + 1) * NODES], logits(j),
                                                nbias[:, i * NODES:(i + 1) * NODES], ALU.add))
            lg = probs[:, 0, 0:count * NODES].rearrange("p (n k) -> p n k", n=count)
            nc.vector.tensor_scalar(ways[:, :, 0:NODES, 0], lg, 0.0, None, ALU.is_le)
            vl(dve, nc.vector.tensor_scalar(ways[:, :, 0:NODES, 1], lg, 0.0, None, ALU.is_gt))
            cur = ways[:, :, 0, :]
            for d in range(1, DEPTH):
                w = 2 ** d
                dst = paths[:, 0:count, :] if d == DEPTH - 1 else \
                    levels[:, d % 2, 0:count * 2 * w].rearrange("p (n k) -> p n k", n=count)
                for j in range(count):
                    m = nc.vector.tensor_tensor(dst[:, j].rearrange("p (k s) -> p k s", s=2),
                                                bc(cur[:, j], 2, [P, w, 2]), ways[:, j, w - 1:2 * w - 1, :], ALU.mult)
                    if j < count - 1:
                        continue
                    if d == DEPTH - 1:
                        m.then_inc(V.sem, V.now(name))
                    else:
                        vl(dve, m)
                cur = dst

        def logits(j):
            return ps[:, 1 + j // 2, (j % 2) * 256:(j % 2) * 256 + NODES]

        def l1f():
            tag = "l1f"
            norm_plan("l1f")
            V.plan("l1f.sd")
            G.plan("l1f.sd")
            V.plan("l1f.xx")
            G.plan("l1f.xx")
            V.plan("l1f.xh")
            turn_plan("l1f.xh")
            T.plan("l1f.nodes")
            V.plan("l1f.paths")
            for i in range(3):
                tree_plan(i)
            V.plan("l1f.qkv")
            T.plan("l1f.s")
            V.plan("l1f.m")
            A.plan("l1f.p")
            V.plan("l1f.p")
            turn_plan("l1f.p")
            T.plan("l1f.av")
            V.plan("l1f.y")
            turn_plan("l1f.y")
            T.plan("l1f.nodef")
            V.plan("l1f.pathf")
            tree_plan(3)
            V.plan("l1f.x")
            s = small4

            @on("pe")
            def _(pe):
                turn_tensor(pe, "l1f.xh", tA[:, :], "l1f.xh")
                pe.wait_ge(V.sem, V.at("l1f.xh.T"))
                loaded(pe, "node")
                for j in range(3):
                    m = mm(logits(j), xnT[:, :], nodew[:, j * NODES:(j + 1) * NODES])
                m.then_inc(T.sem, T.now("l1f.nodes"))
                pe.wait_ge(V.sem, V.at("l1f.paths"))
                tree_tensor(pe, 0, xnT[:, :], True)
                tree_tensor(pe, 1, xnT[:, :], True)
                tree_tensor(pe, 2, xnT[:, :], False)
                pe.wait_ge(V.sem, V.at("l1f.qkv"))
                mm(ps[:, 0, 0:P], tC[:, :], tD[:, :]).then_inc(T.sem, T.now("l1f.s"))
                turn_tensor(pe, "l1f.p", tF[:, :], "l1f.p", 7)
                pe.wait_ge(V.sem, V.at("l1f.p.T"))
                mm(ps[:, 1, 0:P], tG[:, :], tE[:, :]).then_inc(T.sem, T.now("l1f.av"))
                turn_tensor(pe, "l1f.y", tB[:, :], "l1f.y", 7)
                pe.wait_ge(V.sem, V.at("l1f.y.T"))
                mm(logits(0), xnT[:, :], nodew[:, 3 * NODES:4 * NODES]).then_inc(T.sem, T.now("l1f.nodef"))
                pe.wait_ge(V.sem, V.at("l1f.pathf"))
                tree_tensor(pe, 3, xnT[:, :], False)

            @on("dve")
            def _(dve):
                dve.wait_ge(V.sem, V.at("l1a.x"))
                norm_vector(dve, "l1f", xs[:, x_at[tag], :])
                dve.wait_ge(V.sem, V.at("l1f.xn"))
                vl(dve, nc.vector.bn_stats(st[:, :], xn[:, :]))
                vl(dve, nc.vector.bn_aggr(mv[:, 0:2], st[:, :]))
                nc.vector.tensor_scalar(mv[:, 2:3], mv[:, 1:2], P / (P - 1.0), None,
                                        ALU.mult).then_inc(V.sem, V.now("l1f.sd"))
                dve.wait_ge(G.sem, G.at("l1f.sd"))
                nc.vector.tensor_scalar(mv[:, 2:3], mv[:, 3:4], 1e-5, None, ALU.add).then_inc(V.sem, V.now("l1f.xx"))
                dve.wait_ge(G.sem, G.at("l1f.xx"))
                nc.vector.tensor_scalar(tA[:, :], xn[:, :], mv[:, 0:1], mv[:, 3:4], ALU.subtract,
                                        ALU.mult).then_inc(V.sem, V.now("l1f.xh"))
                turn_vector(dve, "l1f.xh", xnT)
                loaded(dve, "node")
                dve.wait_ge(T.sem, T.at("l1f.nodes"))
                walk_vector(dve, 0, 3, "l1f.paths")
                for i in range(3):
                    tree_vector(dve, i)
                dve.wait_ge(T.sem, T.at(("fo", "v", 7)))
                nc.vector.tensor_copy(tC[:, :], ps[:, 4, 0:P])
                nc.vector.tensor_copy(tD[:, :], ps[:, 5, 0:P])
                nc.vector.tensor_copy(tE[:, :], ps[:, 6, 0:P]).then_inc(V.sem, V.now("l1f.qkv"))
                dve.wait_ge(T.sem, T.at("l1f.s"))
                vl(dve, nc.vector.tensor_reduce(s[:, 0:1], ps[:, 0, 0:P], AX.X, ALU.max))
                nc.vector.tensor_scalar(s[:, 1:2], s[:, 0:1], -1.0 / np.sqrt(float(P)), None,
                                        ALU.mult).then_inc(V.sem, V.now("l1f.m"))
                dve.wait_ge(A.sem, A.at("l1f.p"))
                vl(dve, nc.vector.reciprocal(s[:, 3:4], s[:, 2:3]))
                nc.vector.tensor_scalar(tF[:, :], tF[:, :], s[:, 3:4], None, ALU.mult).then_inc(V.sem, V.now("l1f.p"))
                turn_vector(dve, "l1f.p", tG, 7)
                dve.wait_ge(T.sem, T.at("l1f.av"))
                nc.vector.tensor_tensor(tB[:, :], ps[:, 1, 0:P], tA[:, :], ALU.add).then_inc(V.sem, V.now("l1f.y"))
                turn_vector(dve, "l1f.y", xnT, 7)
                vl(dve, nc.vector.tensor_tensor(xb[:, :], xs[:, x_at[tag], :], tB[:, :], ALU.add))
                dve.wait_ge(T.sem, T.at("l1f.nodef"))
                walk_vector(dve, 3, 1, "l1f.pathf")
                tree_vector(dve, 3)
                end_vector(dve, tag, ps[:, 7, 0:P], xb[:, :], ("fo", "f", 7))

            @on("act")
            def _(act):
                for i in range(3):
                    tree_scalar(act, i, ACT.Relu)
                act.wait_ge(V.sem, V.at("l1f.m"))
                nc.scalar.activation(tF[:, :], ps[:, 0, 0:P], ACT.Exp, bias=s[:, 1:2], scale=float(1.0 / np.sqrt(P)),
                                     accum_out=s[:, 2:3]).then_inc(A.sem, A.now("l1f.p"))
                tree_scalar(act, 3, ACT.Gelu)

            @on("pool")
            def _(pool):
                norm_gpsimd(pool, "l1f")
                pool.wait_ge(V.sem, V.at("l1f.sd"))
                nc.gpsimd.tensor_tensor(mv[:, 3:4], mv[:, 2:3], half[:, 1:2], ALU.pow).then_inc(G.sem, G.now("l1f.sd"))
                pool.wait_ge(V.sem, V.at("l1f.xx"))
                nc.gpsimd.tensor_tensor(mv[:, 3:4], mv[:, 2:3], half[:, 0:1], ALU.pow).then_inc(G.sem, G.now("l1f.xx"))

        def l2a():
            tag = "l2a"
            start_plan(tag)
            T.plan("l2a.qkv")
            V.plan("l2a.qkv")
            self_plan(tag)
            T.plan("l2a.y")
            V.plan("l2a.x")

            @on("pe")
            def _(pe):
                start_tensor(pe, tag)
                loaded(pe, "bias")
                for g in range(4):
                    mm(ps[:, g, :], at["flip"], biases[:, g * BANK:(g + 1) * BANK], True, False)
                pe.wait_ge(V.sem, V.at("l2a.xn.T"))
                w = at["w_b.l2a_qkv"]
                mm(ps[:, 4, 0:P], w[:, 0:P], xnT[:, :])
                mm(ps[:, 5, 0:P], w[:, P:2 * P], xnT[:, :])
                mm(ps[:, 6, 0:P], xnT[:, :], w[:, 2 * P:3 * P]).then_inc(T.sem, T.now("l2a.qkv"))
                pe.wait_ge(V.sem, V.at("l2a.qkv"))
                self_tensor(pe, tag, P, 8, tC, probs[:, 0, :], True)
                pe.wait_ge(V.sem, V.at("l2a.o.T"))
                mm(ps[:, 7, 0:P], tB[:, :], at["w_b.l2a_o"]).then_inc(T.sem, T.now("l2a.y"))

            @on("dve")
            def _(dve):
                dve.wait_ge(V.sem, V.at("l2x.x"))
                start_vector(dve, tag, None)
                dve.wait_ge(T.sem, T.at("l2a.qkv"))
                nc.vector.tensor_scalar(tC[:, :], ps[:, 4, 0:P], float(8 ** -0.5), None, ALU.mult)
                vl(dve, nc.vector.tensor_copy(tD[:, :], ps[:, 5, 0:P]))
                va = vaug[:, :].rearrange("p (h w) -> p h w", h=H)
                nc.vector.tensor_copy(va[:, :, 0:8], ps[:, 6, 0:P].rearrange("p (h w) -> p h w", h=H))
                nc.vector.memset(va[:, :, 8], 1.0)
                spread_heads(probs[:, 0, :], tD, at["hm8"], P).then_inc(V.sem, V.now("l2a.qkv"))
                self_vector(dve, tag, P, 8)
                end_vector(dve, tag, ps[:, 7, 0:P], xs[:, x_at[tag], :], "l2a.y")

            @on("act")
            def _(act):
                self_scalar(act, tag, 1.0)

            @on("pool")
            def _(pool):
                norm_gpsimd(pool, tag)

        def l2f():
            tag = "l2f"
            norm_plan("l2f")
            norm_plan("l2f1")
            V.plan("l2f1.h")
            turn_plan("l2f1.h")
            T.plan("l2f.qkv")
            V.plan("l2f.qkv")
            self_plan(tag)
            T.plan("l2f.ap")
            V.plan("l2f.x1")
            norm_plan("l2f2")
            V.plan("l2f2.h")
            turn_plan("l2f2.h")
            T.plan("l2f.route")
            V.plan("l2f.rmax")
            A.plan("l2f.rexp")
            V.plan("l2f.mask")
            T.plan("l2f.rank")
            moe_plan(tag)
            V.plan("l2f.eo")
            V.plan(*(("l2f.perm", e) for e in range(E)))
            T.plan("l2f.y")
            V.plan("l2f.x")
            s = small4

            @on("pe")
            def _(pe):
                pe.wait_ge(V.sem, V.at("l2f.xn"))
                for g in range(4):
                    mm(ps[:, g, :], identb[:, :], bc(causalb[:, :], 1, [P, 4, P]), True, False)
                turn_tensor(pe, "l2f1.h", tA[:, :], "l2f1.h")
                pe.wait_ge(V.sem, V.at("l2f1.h.T"))
                w = at["w_b.l2f_qkv"]
                mm(ps[:, 4, 0:P], w[:, 0:P], xnT[:, :])
                mm(ps[:, 5, 0:P], w[:, P:2 * P], xnT[:, :])
                mm(ps[:, 6, 0:P], xnT[:, :], w[:, 2 * P:3 * P]).then_inc(T.sem, T.now("l2f.qkv"))
                pe.wait_ge(V.sem, V.at("l2f.qkv"))
                self_tensor(pe, tag, P, 8, tC, probs[:, 0, :], True)
                pe.wait_ge(V.sem, V.at("l2f.o.T"))
                mm(ps[:, 7, 0:P], tB[:, :], at["w_b.l2f_p"]).then_inc(T.sem, T.now("l2f.ap"))
                turn_tensor(pe, "l2f2.h", tB[:, :], "l2f2.h", 6)
                pe.wait_ge(V.sem, V.at("l2f2.h.T"))
                mm(ps[:, 7, 0:E], xnT[:, :], at["w_b.l2f_g"]).then_inc(T.sem, T.now("l2f.route"))
                pe.wait_ge(V.sem, V.at("l2f.mask"))
                mm(ps[:, 7, 0:E], at["tri"], s[:, 24:32]).then_inc(T.sem, T.now("l2f.rank"))
                loaded(pe, "w_l2f")
                moe_tensor(pe, tag, at["w_l2f.w1"], None, at["w_l2f.w2"], xnT[:, :], 4)
                pe.wait_ge(V.sem, V.at("l2f.eo"))
                for e in range(E):
                    pe.wait_ge(V.sem, V.at(("l2f.perm", e)))
                    m = mm(ps[:, 6, 0:P], perm[:, e * P:(e + 1) * P], probs[:, 0, e * P:(e + 1) * P], e == 0, e == E - 1)
                m.then_inc(T.sem, T.now("l2f.y"))

            def affine(dve, ready, name, dst, scale, bias):
                dve.wait_ge(V.sem, V.at(ready))
                vl(dve, nc.vector.tensor_tensor(dst[:, :], xn[:, :], scale, ALU.mult))
                nc.vector.tensor_tensor(dst[:, :], dst[:, :], bias, ALU.add).then_inc(V.sem, V.now(name))

            @on("dve")
            def _(dve):
                dve.wait_ge(V.sem, V.at("l2a.x"))
                norm_vector(dve, "l2f", xs[:, x_at[tag], :])
                dve.wait_ge(V.sem, V.at("l2f.xn"))
                vl(dve, nc.vector.tensor_copy(tE[:, :], xn[:, :]))
                norm_vector(dve, "l2f1", tE[:, :])
                nc.vector.tensor_tensor(xb[:, :], tE[:, :], at["l2f_ap"], ALU.add)
                affine(dve, "l2f1.xn", "l2f1.h", tA, at["ln1_s"], at["ln1_b"])
                turn_vector(dve, "l2f1.h", xnT)
                dve.wait_ge(T.sem, T.at("l2f.qkv"))
                nc.vector.tensor_scalar(tC[:, :], ps[:, 4, 0:P], at["l2f_bq"], float(8 ** -0.5), ALU.add, ALU.mult)
                vl(dve, nc.vector.tensor_scalar(tD[:, :], ps[:, 5, 0:P], at["l2f_bk"], None, ALU.add))
                va = vaug[:, :].rearrange("p (h w) -> p h w", h=H)
                nc.vector.tensor_tensor(va[:, :, 0:8], ps[:, 6, 0:P].rearrange("p (h w) -> p h w", h=H),
                                        at["l2f_bv"].rearrange("p (h w) -> p h w", h=H), ALU.add)
                spread_heads(probs[:, 0, :], tD, at["hm8"], P).then_inc(V.sem, V.now("l2f.qkv"))
                self_vector(dve, tag, P, 8)
                dve.wait_ge(T.sem, T.at("l2f.ap"))
                nc.vector.tensor_tensor(tG[:, :], ps[:, 7, 0:P], xb[:, :], ALU.add).then_inc(V.sem, V.now("l2f.x1"))
                dve.wait_ge(V.sem, V.at("l2f.x1"))
                norm_vector(dve, "l2f2", tG[:, :])
                nc.vector.tensor_tensor(xb[:, :], xs[:, x_at[tag], :], tG[:, :], ALU.add)
                affine(dve, "l2f2.xn", "l2f2.h", tB, at["ln2_s"], at["ln2_b"])
                turn_vector(dve, "l2f2.h", xnT, 6)
                route_vector(dve, "l2f", at["l2f_gb"])
                top2(dve, s[:, 16:24], s[:, 24:32])
                nc.vector.tensor_tensor(s[:, 32:40], s[:, 16:24], s[:, 24:32], ALU.mult).then_inc(V.sem, V.now("l2f.mask"))
                dve.wait_ge(T.sem, T.at("l2f.rank"))
                vl(dve, nc.vector.tensor_copy(s[:, 40:48], ps[:, 7, 0:E]))
                moe_vector(dve, tag, False)
                loaded(dve, "l2f_b2")
                dve.wait_ge(T.sem, T.at((tag, "o", tag_groups[tag] - 1)))
                nc.vector.tensor_tensor(probs[:, 0, 0:BANK], ps[:, 4, :], b2rows[:, 0:BANK], ALU.add)
                nc.vector.tensor_tensor(probs[:, 0, BANK:2 * BANK], ps[:, 5, :], b2rows[:, BANK:],
                                        ALU.add).then_inc(V.sem, V.now("l2f.eo"))
                for e in range(E):
                    nc.vector.tensor_scalar(perm[:, e * P:(e + 1) * P], at["iota1"], s[:, 40 + e:41 + e],
                                            s[:, 32 + e:33 + e], ALU.is_equal,
                                            ALU.mult).then_inc(V.sem, V.now(("l2f.perm", e)))
                end_vector(dve, tag, ps[:, 6, 0:P], xb[:, :], "l2f.y")

            @on("act")
            def _(act):
                self_scalar(act, tag, 1.0)
                route_scalar(act, "l2f")
                moe_scalar(act, tag, ACT.Gelu_apprx_tanh, at["l2f_bfc"])

            @on("pool")
            def _(pool):
                norm_gpsimd(pool, "l2f")
                norm_gpsimd(pool, "l2f1")
                norm_gpsimd(pool, "l2f2")

        def l3x():
            tag = "l3x"
            start_plan(tag)
            T.plan("l3x.q")
            V.plan("l3x.q")
            T.plan("l3x.qk")
            V.plan("l3x.qk")
            G.plan("l3x.ones", "l3a.wide")
            for h in range(H + 1):
                if h < H:
                    T.plan((tag, "s", h))
                    V.plan((tag, "m", h))
                if h:
                    g = h - 1
                    T.plan((tag, "t", g, 0), (tag, "t", g, 1), (tag, "pv", g, 0), (tag, "t", g, 2),
                           (tag, "pv", g, 1), (tag, "t", g, 3), (tag, "pv", g, 2), (tag, "pv", g, 3))
                    A.plan((tag, "e", g, 0), (tag, "e", g, 1))
                    V.plan((tag, "e", g, 2), (tag, "e", g, 3), ("l3x.u", g))
                if h < H:
                    A.plan((tag, "exp", h))
            for c in range(4):
                T.plan(("l3x.ut", c))
                V.plan(("l3x.ut", c))
            T.plan("l3x.o")
            V.plan("l3x.o")
            T.plan("l3x.1")
            V.plan("l3x.1")
            T.plan("l3x.2")
            V.plan("l3x.2")
            norm_plan("l3xo")
            V.plan("l3x.x")
            us = uheads

            @on("pe")
            def _(pe):
                start_tensor(pe, tag)
                pe.wait_ge(V.sem, V.at("l3x.xn.T"))
                for c in range(8):
                    m = mm(ps[:, c // 4, (c % 4) * P:(c % 4 + 1) * P], at["w_b.l3x_q"][:, c * P:(c + 1) * P], xnT[:, :])
                m.then_inc(T.sem, T.now("l3x.q"))
                pe.wait_ge(V.sem, V.at("l3x.q"))
                for h in range(H):
                    r = 64 * (h % 2)
                    c = h // 2
                    m = mm(ps[:, 2 + 2 * (h % 2) + c // 4, (c % 4) * P:(c % 4 + 1) * P],
                           at["w_b.l3x_k"][r:r + 64, c * P:(c + 1) * P], qheads[r:r + 64, c * P:(c + 1) * P])
                m.then_inc(T.sem, T.now("l3x.qk"))

                def ready(pe, h):
                    if h == 0:
                        pe.wait_ge(V.sem, V.at("l3x.qk"))
                        loaded(pe, "ctx2")
                        pe.wait_ge(G.sem, G.at("l3x.ones"))

                def free(pe, g):
                    if g >= 2:
                        pe.wait_ge(V.sem, V.at(("l3x.u", g - 2)))
                ctx_tensor(pe, tag, H, lambda h: sbq[:, h * P:(h + 1) * P], ctxT, lambda g, t: values[:, t, 0:P + 1],
                           lambda g: ps[:, 6 + g % 2, 0:P + 1], ready, None, free)
                pe.wait_ge(V.sem, V.at(("l3x.u", H - 1)))
                for c in range(4):
                    for j in range(4):
                        h = 4 * c + j
                        m = tr(ps[:, c, j * P:(j + 1) * P], us[:, h * P:(h + 1) * P])
                    m.then_inc(T.sem, T.now(("l3x.ut", c)))
                for h in range(H):
                    if h % 4 == 0:
                        pe.wait_ge(V.sem, V.at(("l3x.ut", h // 4)))
                    r = 64 * (h % 2)
                    c = h // 2
                    m = mm(ps[r:r + 64, 4 + c // 4, (c % 4) * P:(c % 4 + 1) * P],
                           at["w_b.l3x_v"][:, h * 64:(h + 1) * 64], sbq[:, h * P:(h + 1) * P])
                m.then_inc(T.sem, T.now("l3x.o"))
                pe.wait_ge(V.sem, V.at("l3x.o"))
                for c in range(8):
                    m = mm(ps[:, 6, 0:P], at["w_b.l3x_o1"][:, c * P:(c + 1) * P], qheads[:, c * P:(c + 1) * P],
                           c == 0, c == 7)
                m.then_inc(T.sem, T.now("l3x.1"))
                pe.wait_ge(V.sem, V.at("l3x.1"))
                mm(ps[:, 7, 0:P], tA[:, :], at["w_b.l3x_o2"]).then_inc(T.sem, T.now("l3x.2"))

            @on("dve")
            def _(dve):
                dve.wait_ge(V.sem, V.at("l2f.x"))
                start_vector(dve, tag, None)
                dve.wait_ge(T.sem, T.at("l3x.q"))
                nc.vector.tensor_copy(qheads[:, :], ps[:, 0:2, :].rearrange("p a b -> p (a b)")).then_inc(
                    V.sem, V.now("l3x.q"))
                dve.wait_ge(T.sem, T.at("l3x.qk"))
                q4 = sbq[:, :].rearrange("p (c s n) -> p c s n", s=2, n=P)
                nc.vector.tensor_copy(q4[:, :, 0, :], ps[:, 2:4, :].rearrange("p a (b n) -> p (a b) n", n=P))
                nc.vector.tensor_copy(q4[:, :, 1, :], ps[:, 4:6, :].rearrange("p a (b n) -> p (a b) n", n=P)).then_inc(
                    V.sem, V.now("l3x.qk"))

                def after(dve, g):
                    dve.wait_ge(T.sem, T.at((tag, "pv", g, 3)))
                    vl(dve, nc.vector.reciprocal(small2[:, g:g + 1], ps[:, 6 + g % 2, P:P + 1]))
                    nc.vector.tensor_scalar(us[:, g * P:(g + 1) * P], ps[:, 6 + g % 2, 0:P], small2[:, g:g + 1], None,
                                            ALU.mult).then_inc(V.sem, V.now(("l3x.u", g)))
                ctx_vector(dve, tag, H, 0.125, after)
                for c in range(4):
                    dve.wait_ge(T.sem, T.at(("l3x.ut", c)))
                    nc.vector.tensor_copy(sbq[:, c * BANK:(c + 1) * BANK], ps[:, c, :]).then_inc(
                        V.sem, V.now(("l3x.ut", c)))
                dve.wait_ge(T.sem, T.at("l3x.o"))
                nc.vector.tensor_copy(qheads[:, :], ps[:, 4:6, :].rearrange("p a b -> p (a b)")).then_inc(
                    V.sem, V.now("l3x.o"))
                dve.wait_ge(T.sem, T.at("l3x.1"))
                nc.vector.tensor_scalar(tA[:, :], ps[:, 6, 0:P], 0.0, None, ALU.max).then_inc(V.sem, V.now("l3x.1"))
                dve.wait_ge(T.sem, T.at("l3x.2"))
                nc.vector.tensor_copy(tB[:, :], ps[:, 7, 0:P]).then_inc(V.sem, V.now("l3x.2"))
                dve.wait_ge(V.sem, V.at("l3x.2"))
                norm_vector(dve, "l3xo", tB[:, :])
                dve.wait_ge(V.sem, V.at("l3xo.xn"))
                vl(dve, nc.vector.tensor_tensor(tC[:, :], xn[:, :], at["l3x_g"], ALU.mult))
                nc.vector.tensor_tensor(xs[:, 1 - x_at[tag], :], tC[:, :], xs[:, x_at[tag], :], ALU.add).then_inc(
                    V.sem, V.now("l3x.x"))

            @on("act")
            def _(act):
                ctx_scalar(act, tag, H, 0.125)

            @on("pool")
            def _(pool):
                norm_gpsimd(pool, tag)
                pool.wait_ge(loads["ctx2"], 16)
                nc.gpsimd.memset(values[:, :, P:P + 1], 1.0).then_inc(G.sem, G.now("l3x.ones"))
                loaded(pool, "w_c")
                for name, dst in (("k", keysT[:, 0:8 * P]), ("q", shared[:, 8 * P:])):
                    nc.gpsimd.tensor_copy(dst.rearrange("p (a b) -> p a b", b=8), bc(at["w_c." + name], 2, [P, P, 8]))
                for h in range(H):
                    m = nc.gpsimd.tensor_copy(
                        keysT[:, 8 * P + 64 * h:8 * P + 64 * h + 64].rearrange("p (a b) -> p a b", a=8),
                        bc(at["w_c.v"][:, 8 * h:8 * h + 8], 1, [P, 8, 8]))
                m.then_inc(G.sem, G.now("l3a.wide"))
                norm_gpsimd(pool, "l3xo")

        def l3a():
            tag = "l3a"
            V.plan("l3a.var", "l3a.xn")
            turn_plan("l3a.xn")
            T.plan("l3a.m1", "l3a.kvq")
            V.plan("l3a.m1")
            T.plan("l3a.z")
            V.plan("l3a.nb")
            A.plan("l3a.k", "l3a.q", "l3a.z")
            V.plan("l3a.s")
            T.plan("l3a.s")
            V.plan("l3a.st")
            T.plan("l3a.y0")
            V.plan("l3a.y0")
            turn_plan("l3a.y")
            T.plan("l3a.p")
            V.plan("l3a.ss")
            V.plan("l3a.yn")
            turn_plan("l3a.yn")
            T.plan("l3a.fc")
            V.plan("l3a.fc")
            T.plan("l3a.cp")
            V.plan("l3a.x")
            s = small4
            n8 = 8 * P
            kx, qx, st8, dx = (probs[:, 0, 0:n8], probs[:, 0, n8:], probs[:, 1, 0:n8], probs[:, 1, n8:])
            ux = sbq[:, 0:n8]
            wide_k, wide_v, wide_q = keysT[:, 0:n8], keysT[:, n8:], shared[:, n8:]
            G.plan("l3a.rstd", "l3a.sel", "l3a.rs")

            @on("pe")
            def _(pe):
                start_tensor(pe, tag)
                pe.wait_ge(V.sem, V.at("l3a.xn.T"))
                loaded(pe, "w_c")
                pe.wait_ge(G.sem, G.at("l3a.wide"))
                mm(ps[0:32, 6, 0:P], at["w_c.m1"], xnT[:, :]).then_inc(T.sem, T.now("l3a.m1"))
                for j in range(8):
                    o, b = (j % 4) * P, j // 4
                    mm(ps[:, b, o:o + P], wide_k[:, j * P:(j + 1) * P], xnT[:, :])
                    mm(ps[:, 2 + b, o:o + P], wide_v[:, j * P:(j + 1) * P], xnT[:, :])
                    m = mm(ps[:, 4 + b, o:o + P], wide_q[:, j * P:(j + 1) * P], xnT[:, :])
                m.then_inc(T.sem, T.now("l3a.kvq"))
                pe.wait_ge(V.sem, V.at("l3a.m1"))
                mm(ps[0:H, 7, 0:P], at["w_c.m2"][0:32, :], tA[0:32, :]).then_inc(T.sem, T.now("l3a.z"))
                pe.wait_ge(V.sem, V.at("l3a.s"))
                pe.wait_ge(G.sem, G.at("l3a.sel"))
                for j in range(8):
                    m = mm(ps[:, 6 + j // 4, (j % 4) * P:(j % 4 + 1) * P],
                           probsT[0:H, j // 4, (j % 4) * P:(j % 4 + 1) * P], tC[0:H, :])
                m.then_inc(T.sem, T.now("l3a.s"))
                pe.wait_ge(V.sem, V.at("l3a.st"))
                for j in range(8):
                    m = mm(ps[:, 0, 16 * j:16 * j + 16], st8[:, j * P:(j + 1) * P], at["gather"])
                m.then_inc(T.sem, T.now("l3a.y0"))
                turn_tensor(pe, "l3a.y", tA[:, :], "l3a.y0", 5)
                pe.wait_ge(V.sem, V.at("l3a.y.T"))
                mm(ps[:, 4, 0:P], tB[:, :], at["w_c.p"]).then_inc(T.sem, T.now("l3a.p"))
                turn_tensor(pe, "l3a.yn", tE[:, :], "l3a.yn", 5)
                pe.wait_ge(V.sem, V.at("l3a.yn.T"))
                for c in range(4):
                    m = mm(ps[:, 6, c * P:(c + 1) * P], at["w_c.fc"][:, c * P:(c + 1) * P], tF[:, :])
                m.then_inc(T.sem, T.now("l3a.fc"))
                pe.wait_ge(V.sem, V.at("l3a.fc"))
                for c in range(4):
                    m = mm(ps[:, 7, 0:P], probs[:, 0, c * P:(c + 1) * P], at["w_c.cp"][:, c * P:(c + 1) * P], c == 0, c == 3)
                m.then_inc(T.sem, T.now("l3a.cp"))

            @on("dve")
            def _(dve):
                dve.wait_ge(V.sem, V.at("l3x.x"))
                start_vector(dve, tag, None)
                dve.wait_ge(T.sem, T.at("l3a.m1"))
                nc.vector.tensor_scalar(tA[0:32, :], ps[0:32, 6, 0:P], at["l3a_bm1"][0:32, :], 0.0, ALU.add,
                                        ALU.max).then_inc(V.sem, V.now("l3a.m1"))
                nc.vector.tensor_scalar(s[0:H, 0:1], at["l3a_bm2"][0:H, :], -1.0, None,
                                        ALU.mult).then_inc(V.sem, V.now("l3a.nb"))
                dve.wait_ge(A.sem, A.at("l3a.z"))
                vl(dve, nc.vector.tensor_scalar(tD[0:H, :], tB[0:H, :], 1.0, None, ALU.add))
                nc.vector.reciprocal(tC[0:H, :], tD[0:H, :]).then_inc(V.sem, V.now("l3a.s"))
                dve.wait_ge(T.sem, T.at("l3a.s"))
                dve.wait_ge(A.sem, A.at("l3a.k"))
                kv = ps[:, 2:4, :].rearrange("p a b -> p (a b)")
                sp8 = ps[:, 6:8, :].rearrange("p a b -> p (a b)")
                vl(dve, nc.vector.tensor_tensor(ux, kx, kv, ALU.mult))
                nc.vector.tensor_tensor(ux, ux, sp8, ALU.mult)
                vl(dve, nc.vector.tensor_scalar(dx, sp8, -1.0, 1.0, ALU.mult, ALU.add))
                vl(dve, nc.vector.memset(dx.rearrange("p (j t) -> p j t", t=P)[:, :, 0:1], 0.0))
                vl(dve, nc.vector.tensor_tensor_scan(st8, dx, ux, 0.0, ALU.mult, ALU.add))
                dve.wait_ge(A.sem, A.at("l3a.q"))
                nc.vector.tensor_tensor(st8, st8, qx, ALU.mult).then_inc(V.sem, V.now("l3a.st"))
                dve.wait_ge(T.sem, T.at("l3a.y0"))
                nc.vector.tensor_copy(tA[:, :], ps[:, 0, 0:P]).then_inc(V.sem, V.now("l3a.y0"))
                turn_vector(dve, "l3a.y", tB, 5)
                dve.wait_ge(T.sem, T.at("l3a.p"))
                vl(dve, nc.vector.tensor_copy(tC[:, :], ps[:, 4, 0:P]))
                vl(dve, nc.vector.tensor_tensor_reduce(tD[:, :], tC[:, :], tC[:, :], 1.0, 0.0, ALU.mult, ALU.add, s[:, 1:2]))
                nc.vector.tensor_scalar(mv[:, 2:3], s[:, 1:2], 1.0 / P, float(np.finfo(np.float32).eps), ALU.mult,
                                        ALU.add).then_inc(V.sem, V.now("l3a.ss"))
                dve.wait_ge(G.sem, G.at("l3a.rs"))
                nc.vector.tensor_scalar(tE[:, :], tC[:, :], mv[:, 3:4], None, ALU.mult).then_inc(V.sem, V.now("l3a.yn"))
                nc.vector.tensor_tensor(xb[:, :], tC[:, :], xs[:, x_at[tag], :], ALU.add)
                turn_vector(dve, "l3a.yn", tF, 5)
                dve.wait_ge(T.sem, T.at("l3a.fc"))
                vl(dve, nc.vector.tensor_scalar(probs[:, 0, BANK:2 * BANK], ps[:, 6, :], 0.0, None, ALU.max))
                nc.vector.tensor_tensor(probs[:, 0, 0:BANK], probs[:, 0, BANK:2 * BANK], probs[:, 0, BANK:2 * BANK],
                                        ALU.mult).then_inc(V.sem, V.now("l3a.fc"))
                end_vector(dve, tag, ps[:, 7, 0:P], xb[:, :], "l3a.cp")

            @on("act")
            def _(act):
                act.wait_ge(T.sem, T.at("l3a.kvq"))
                nc.scalar.copy(kx, ps[:, 0:2, :].rearrange("p a b -> p (a b)")).then_inc(A.sem, A.now("l3a.k"))
                nc.scalar.copy(qx, ps[:, 4:6, :].rearrange("p a b -> p (a b)")).then_inc(A.sem, A.now("l3a.q"))
                act.wait_ge(T.sem, T.at("l3a.z"))
                act.wait_ge(V.sem, V.at("l3a.nb"))
                nc.scalar.activation(tB[0:H, :], ps[0:H, 7, 0:P], ACT.Exp, bias=s[0:H, 0:1],
                                     scale=-1.0).then_inc(A.sem, A.now("l3a.z"))

            @on("pool")
            def _(pool):
                norm_gpsimd(pool, tag)
                nc.gpsimd.tensor_copy(probsT[0:H, 0:2, :].rearrange("p a (h n) -> p (a h) n", n=64),
                                      bc(ident[0:H, 0:H], 2, [H, H, 64])).then_inc(G.sem, G.now("l3a.sel"))
                pool.wait_ge(V.sem, V.at("l3a.ss"))
                nc.gpsimd.tensor_tensor(mv[:, 3:4], mv[:, 2:3], half[:, 0:1], ALU.pow).then_inc(G.sem, G.now("l3a.rs"))

        def l3f():
            tag = "l3f"
            start_plan(tag)
            T.plan("l3f.conf")
            V.plan("l3f.conf")
            A.plan("l3f.conf")
            V.plan("l3f.bm")
            A.plan("l3f.w")
            V.plan("l3f.comb")
            moe_plan(tag)
            V.plan("l3f.x")
            s = small4

            @on("pe")
            def _(pe):
                start_tensor(pe, tag)
                pe.wait_ge(V.sem, V.at("l3f.xn.T"))
                mm(ps[:, 7, 0:E], xnT[:, :], at["w_c.conf"]).then_inc(T.sem, T.now("l3f.conf"))
                loaded(pe, "w_l3f")
                loaded(pe, "w_l3d")
                moe_tensor(pe, tag, at["w_l3f.gate"], at["w_l3f.up"], at["w_l3d.down"], xnT[:, :], 4)

            @on("dve")
            def _(dve):
                dve.wait_ge(V.sem, V.at("l3a.x"))
                start_vector(dve, tag, None)
                dve.wait_ge(T.sem, T.at("l3f.conf"))
                nc.vector.tensor_tensor(s[:, 0:8], ps[:, 7, 0:E], at["conf_b"], ALU.add).then_inc(V.sem, V.now("l3f.conf"))
                dve.wait_ge(A.sem, A.at("l3f.conf"))
                vl(dve, nc.vector.tensor_scalar(s[:, 8:16], s[:, 8:16], 1.0, None, ALU.add))
                vl(dve, nc.vector.reciprocal(s[:, 8:16], s[:, 8:16]))
                vl(dve, nc.vector.tensor_tensor(s[:, 16:24], s[:, 8:16], at["wealth"], ALU.mult))
                nc.vector.tensor_reduce(s[:, 40:41], s[:, 16:24], AX.X, ALU.max, negate=True).then_inc(V.sem, V.now("l3f.bm"))
                top2(dve, s[:, 16:24], s[:, 24:32])
                dve.wait_ge(A.sem, A.at("l3f.w"))
                vl(dve, nc.vector.tensor_tensor_reduce(s[:, 32:40], s[:, 0:8], s[:, 24:32], 1.0, 0.0, ALU.mult, ALU.add,
                                                       s[:, 41:42]))
                vl(dve, nc.vector.reciprocal(s[:, 42:43], s[:, 41:42]))
                nc.vector.tensor_scalar(s[:, 48:56], s[:, 32:40], s[:, 42:43], None, ALU.mult).then_inc(
                    V.sem, V.now("l3f.comb"))
                dve.wait_ge(V.sem, V.at("l3f.comb"))
                moe_vector(dve, tag, True)
                mix_vector(dve, tag, s[:, 48:56], xs[:, x_at[tag], :], False)

            @on("act")
            def _(act):
                act.wait_ge(V.sem, V.at("l3f.conf"))
                nc.scalar.activation(s[:, 8:16], s[:, 0:8], ACT.Exp, scale=-1.0).then_inc(A.sem, A.now("l3f.conf"))
                act.wait_ge(V.sem, V.at("l3f.bm"))
                nc.scalar.activation(s[:, 0:8], s[:, 16:24], ACT.Exp, bias=s[:, 40:41]).then_inc(A.sem, A.now("l3f.w"))
                moe_scalar(act, tag, ACT.Silu, None)

            @on("pool")
            def _(pool):
                norm_gpsimd(pool, tag)

        def hidden():
            V.plan("mask.any")
            T.plan("mask.any")
            V.plan("mask")

            @on("pe")
            def _(pe):
                pe.wait_ge(V.sem, V.at("mask.any"))
                mm(ps[:, 7, 300:301], one[0:1, :], seen[0:1, 1:2]).then_inc(T.sem, T.now("mask.any"))

            @on("dve")
            def _(dve):
                loaded(dve, "mask")
                dve.wait_ge(G.sem, G.at("const"))
                z = probsT[0:1, :, :].rearrange("p a b -> p (a b)")
                vl(dve, nc.vector.tensor_scalar(z, keysT[0:1, :].bitcast(I32), 0.0, None, ALU.is_equal))
                vl(dve, nc.vector.tensor_reduce(seen[0:1, 0:1], z, AX.X, ALU.min))
                nc.vector.tensor_scalar(seen[0:1, 1:2], seen[0:1, 0:1], -1.0, 1.0, ALU.mult,
                                        ALU.add).then_inc(V.sem, V.now("mask.any"))
                dve.wait_ge(V.sem, V.at("mask.any"))
                nc.vector.tensor_scalar(maskb[:, :], z, seen[0:1, 1:2], HIDDEN, ALU.mult, ALU.mult)
                dve.wait_ge(T.sem, T.at("mask.any"))
                nc.vector.tensor_copy(seen[:, 2:3], ps[:, 7, 300:301]).then_inc(V.sem, V.now("mask"))

        def distance():
            T.plan("d.1", "d.2", "d.3")
            V.plan("d.1", "d.2", "d.3")

            @on("pe")
            def _(pe):
                loaded(pe, "w_a")
                pe.wait_ge(V.sem, V.at("mask"))
                mm(ps[0:4, 7, 0:64], at["w_coeff"][0:64, :], at["ramp"][0:64, :]).then_inc(T.sem, T.now("d.1"))
                pe.wait_ge(V.sem, V.at("d.1"))
                mm(ps[0:64, 7, 64:64 + H], tC[0:4, 0:64], at["w_wpos"][0:4, :]).then_inc(T.sem, T.now("d.2"))
                pe.wait_ge(V.sem, V.at("d.2"))
                mm(ps[0:H, 7, 128:128 + 255], tD[0:64, 0:H], at["dist"][0:64, :]).then_inc(T.sem, T.now("d.3"))

            @on("dve")
            def _(dve):
                dve.wait_ge(T.sem, T.at("d.1"))
                nc.vector.tensor_copy(tC[0:4, 0:64], ps[0:4, 7, 0:64]).then_inc(V.sem, V.now("d.1"))
                dve.wait_ge(T.sem, T.at("d.2"))
                nc.vector.tensor_copy(tD[0:64, 0:H], ps[0:64, 7, 64:64 + H]).then_inc(V.sem, V.now("d.2"))
                dve.wait_ge(T.sem, T.at("d.3"))
                nc.vector.tensor_copy(dists[:, :], ps[0:H, 7, 128:128 + 255]).then_inc(V.sem, V.now("d.3"))

        paths = sbq[:, 0:3 * LEAVES].rearrange("p (n k) -> p n k", n=3)
        levels = sbq[:, 3 * LEAVES:3 * LEAVES + 2 * 3 * P].rearrange("p (a k) -> p a k", a=2)
        biases = shared[:, :]
        qheads = shared[:, 0:8 * P]
        dists = sb("dists", [H, 255])
        perm = sbq[:, 0:E * P]
        uheads = region[:, 2 * REG + width(W_L3D):2 * REG + width(W_L3D) + H * P]

        hidden()
        distance()
        l0x()
        l0a()
        l0f()
        cross("l1x", "l0f.x", lambda n: at["w_l1x_" + n], float(1.0 / np.sqrt(P)), True, at["l1x_bq"], at["l1x_bk"],
              at["l1x_bv"], at["l1x_bo"], "w_a")
        l1a()
        l1f()
        cross("l2x", "l1f.x", lambda n: at["w_b.l2x_" + n], float(1.0 / np.sqrt(8.0)), False, None, None, None,
              at["l2x_b"], "w_b")
        l2a()
        l2f()
        l3x()
        l3a()
        l3f()

        @on("sp")
        def _(sp):
            sp.wait_ge(V.sem, V.at("l3f.x"))
            nc.sync.dma_start(out, xs[:, 1 - x_at["l3f"], :]).then_inc(stored, 16)
            if dbg is not None:
                sp.wait_ge(dbg_stored, 16 * len(STAGES))
            sp.wait_ge(stored, 16)

        if dbg is not None:
            dbg_stored = sem("dbg_stored")
            orig = list(parts["pool"])
            parts["pool"] = orig[0:1]
            for k, (f, n) in enumerate(zip(orig[1:], STAGES)):
                def dump(pool, n=n, k=k):
                    pool.wait_ge(V.sem, V.at(n + ".x"))
                    nc.gpsimd.dma_start(dbg[k], xs[:, 1 - x_at[n], :]).then_inc(dbg_stored, 16)
                    pool.wait_ge(dbg_stored, 16 * (k + 1))
                parts["pool"] += [f, dump]
            for i, n in enumerate(STAGES[:-1]):
                pass

        block = ctx.enter_context(nc.Block())

        @block.tensor
        def _(pe):
            for part in parts["pe"]:
                part(pe)

        @block.vector
        def _(dve):
            for part in parts["dve"]:
                part(dve)

        @block.scalar
        def _(act):
            for part in parts["act"]:
                part(act)

        @block.gpsimd
        def _(pool):
            for part in parts["pool"]:
                part(pool)

        @block.sync
        def _(sp):
            for part in parts["sp"]:
                part(sp)




def constants():
    i = np.arange(P)
    f = np.float32
    c = {"ident": np.eye(P, dtype=f), "causal": np.where(i[None, :] <= i[:, None], 0.0, HIDDEN).astype(f)}
    freq = (f(1.0) / np.power(f(10000.0), np.arange(0, 8, 2, dtype=f))).astype(f)
    angle = (i.astype(f)[:, None] * freq[None, :]).astype(f)
    c["cos"] = np.tile(np.repeat(np.cos(angle), 2, axis=1), (1, H))
    sin = np.stack([-np.sin(angle), np.sin(angle)], axis=2).reshape(P, 8)
    c["sin"] = np.tile(sin, (1, H))
    c["tri"] = (i[:, None] <= i[None, :])
    c["iota1"] = np.tile(i[None, :] + 1.0, (P, 1))
    c["hm8"] = (i[:, None] // 8 == np.arange(H)[None, :])
    c["hm4"] = (i[:, None] // 4 == np.arange(H)[None, :])
    c["bm8"] = (i[:, None] // 8 == i[None, :] // 8)
    c["bm4"] = (i[:, None] // 4 == i[None, :] // 4)
    e = np.arange(E)
    c["before"] = np.tile((e[None, :] < e[:, None]).reshape(1, E * E), (P, 1))
    c["gather"] = ((i[:, None] // 64 == np.arange(16)[None, :] // 8) & (i[:, None] % 8 == np.arange(16)[None, :] % 8))
    c["flip"] = (i[:, None] + i[None, :] == P - 1)
    r = np.arange(64)
    ramp = np.linspace(0.0, 1.0, 64).astype(f)
    lag = r[None, :] - r[:, None]
    c["ramp"] = np.concatenate([np.where(lag >= 0, ramp[np.clip(lag, 0, 63)], 0.0), np.zeros((64, 64))])
    far = (np.abs(np.arange(255) - 127).astype(f) / f(P - 1)).astype(f)
    step = np.clip(np.round(far * f(63)), 0, 63)
    c["dist"] = (i[:, None] == step[None, :])
    return np.concatenate([c[n].astype(f).reshape(P, w) for n, w in CONST], axis=1)


def packed(inputs):
    a = {k: np.asarray(v) for k, v in inputs.items()}

    def tall(m):
        n = m.shape[0] // P
        return m.reshape(n, P, -1).transpose(1, 0, 2).reshape(P, -1)

    def col(v, n=P):
        return np.concatenate([v.reshape(-1, 1), np.zeros((P - v.size, 1), v.dtype)]) if v.size < P else v.reshape(-1, P).T

    def pad(m):
        return np.concatenate([m, np.zeros((P - m.shape[0], m.shape[1]), m.dtype)])

    def side(parts, pack):
        got = [np.ascontiguousarray(p).reshape(P, -1) for p in parts]
        assert [g.shape[1] for g in got] == [w for _, w in pack], [(g.shape[1], n, w) for g, (n, w) in zip(got, pack)]
        return np.ascontiguousarray(np.concatenate(got, axis=1))

    ws = a["L0_xattn_w_sim"]
    d = {"const": constants()}
    d["x"] = a["x"].reshape(P, P)
    ctx = a["ctx_1024"].reshape(CTX, P)
    d["ctxT"] = np.ascontiguousarray(ctx.T)
    d["ctx"] = np.ascontiguousarray(ctx.reshape(KT_N, P, P).transpose(1, 0, 2))
    d["mask"] = a["mask_Bx1x1xS2_if1"].reshape(1, CTX)
    b1 = [a[f"L1_ffn_{t}_b1"].reshape(CH, P).T for t in "qkvf"]
    bq = a["L2_ffn_b_qkv"]
    d["cols"] = side([col(ws[P:2 * P]), col(ws[2 * P:]), col(a["L0_ffn_q_b"].reshape(H, 8)[:, :4].reshape(-1)),
                      col(a["L0_ffn_k_b"]), a["L0_ffn_b1"].reshape(16, P).T, col(a["L1_xattn_bq"]), col(a["L1_xattn_bk"]),
                      np.concatenate(b1, axis=1), col(bq[0:P]), col(bq[P:2 * P]), a["L2_ffn_b_fc"].reshape(32, P).T,
                      col(a["L3_attn_bm1"]), col(a["L3_attn_bm2"])], COLS)
    rows = [a["L0_xattn_b_sim"], ws[0:P], a["L0_xattn_b_qv"], a["L0_attn_bq"], a["L0_attn_bk"], a["L0_attn_bv"],
            a["L0_attn_bo"], a["L0_ffn_v_b"], a["L0_ffn_o_b"], a["L0_ffn_router_b"], a["L1_xattn_bv"], a["L1_xattn_bo"],
            a["L1_attn_proj_bias"], a["L2_xattn_b_o"], a["L2_ffn_ln1_scale"], a["L2_ffn_ln1_bias"], bq[2 * P:],
            a["L2_ffn_b_attnproj"], a["L2_ffn_ln2_scale"], a["L2_ffn_ln2_bias"], a["L2_ffn_b_gate"],
            a["L3_xattn_gamma"], a["L3_ffn_conf_b"], a["L3_ffn_wealth"]]
    assert [r.size for r in rows] == [w for _, w in ROWS]
    d["rows"] = np.concatenate([r.reshape(-1) for r in rows])
    d["w_a"] = side([tall(a["L0_xattn_W_qv"]), a["L0_attn_Wq"], a["L0_attn_Wk"], a["L0_attn_Wv"], a["L0_attn_Wo"],
                     a["L0_ffn_q_w"].reshape(P, H, 8)[:, :, :4], a["L0_ffn_k_w"], a["L0_ffn_v_w"], a["L0_ffn_o_w"], a["L0_ffn_router_w"],
                     a["L1_xattn_Wq"].T, a["L1_xattn_Wk"].T, a["L1_xattn_Wv"].T, a["L1_xattn_Wo"].T,
                     a["L1_attn_qkv_weight"].T, a["L1_attn_proj_weight"].T, pad(a["L2_attn_coeffs"][:, :64].T),
                     pad(a["L2_attn_Wpos"].T)], W_A)
    d["w_l0f"] = side([a["L0_ffn_w1"].transpose(1, 0, 2).reshape(P, -1), tall(a["L0_ffn_w2"].reshape(-1, P))], W_L0F)
    d["l0f_b2"] = a["L0_ffn_b2"].reshape(-1)
    for t in "qkvf":
        d["w_" + t] = side([a[f"L1_ffn_{t}_w1"].transpose(1, 0, 2).reshape(P, -1),
                            tall(a[f"L1_ffn_{t}_w2"].reshape(-1, P))], W_FFF)
    d["node"] = np.concatenate([a[f"L1_ffn_{t}_nw"].T for t in "qkvf"], axis=1)
    d["nbias"] = np.concatenate([a[f"L1_ffn_{t}_nb"] for t in "qkvf"])
    d["ffb2"] = np.concatenate([tall(a[f"L1_ffn_{t}_b2"]) for t in "qkvf"], axis=1)
    wkv = a["L3_xattn_w_kv"]
    d["w_b"] = side([a["L2_xattn_W_q"], a["L2_xattn_W_k"], a["L2_xattn_W_v"], a["L2_xattn_W_o"], a["L2_attn_Wqkv"].T,
                     a["L2_attn_Wout"].T, a["L2_ffn_w_qkv"], a["L2_ffn_w_attnproj"], a["L2_ffn_w_gate"],
                     a["L3_xattn_w_q"], tall(np.ascontiguousarray(wkv[:, :8 * P].T)), wkv[:, 8 * P:],
                     tall(a["L3_xattn_w_out1"]), a["L3_xattn_w_out2"]], W_B)
    d["w_c"] = side([a["L3_attn_Wq"].T, a["L3_attn_Wk"].T, a["L3_attn_Wv"].T, a["L3_attn_Wm1"].T,
                     pad(a["L3_attn_Wm2"].T), a["L3_attn_Wproj"].T, a["L3_attn_Wfc"].T,
                     tall(np.ascontiguousarray(a["L3_attn_Wcp"].T)), a["L3_ffn_conf_w"].T], W_C)
    d["w_l2f"] = side([a["L2_ffn_w_fc"].transpose(1, 0, 2).reshape(P, -1), tall(a["L2_ffn_w_fcproj"].reshape(-1, P))],
                      W_L2F)
    d["l2f_b2"] = a["L2_ffn_b_fcproj"].reshape(-1)
    d["w_l3f"] = side([a["L3_ffn_gate_w"].transpose(2, 0, 1).reshape(P, -1),
                       a["L3_ffn_up_w"].transpose(2, 0, 1).reshape(P, -1)], W_L3F)
    d["w_l3d"] = side([tall(np.ascontiguousarray(a["L3_ffn_down_w"].transpose(0, 2, 1)).reshape(-1, P))], W_L3D)
    return {k: np.ascontiguousarray(v) for k, v in d.items()}


def kernel(**inputs):
    from concourse import bacc
    from concourse.bass_utils import run_bass_kernel_spmd

    arrays = packed(inputs)
    nc = bacc.Bacc("TRN2", target_bir_lowering=False, num_devices=1)
    dram = {}
    for n, v in arrays.items():
        dram[n] = nc.dram_tensor("in_" + n, v.shape, mybir.dt.from_np(v.dtype), kind="ExternalInput").ap()
    out = nc.dram_tensor("out_0", (P, P), F32, kind="ExternalOutput").ap()
    scratch = nc.dram_tensor("distance_rows", (H, 255), F32).ap()
    dbg = nc.dram_tensor("dbg", (len(STAGES), P, P), F32, kind="ExternalOutput").ap() if DEBUG else None
    build(nc, dram, out, scratch, dbg)
    r = run_bass_kernel_spmd(nc, [{"in_" + n: v for n, v in arrays.items()}], core_ids=[0])
    return r.results[0]["out_0"].reshape(1, P, P)
```

```python
from contextlib import ExitStack

import numpy as np

import concourse.bass as bass
from concourse import mybir

F32 = mybir.dt.float32
BF16 = mybir.dt.bfloat16
F32R = mybir.dt.float32r
I32 = mybir.dt.int32
ALU = mybir.AluOpType
ACT = mybir.ActivationFunctionType
AX = mybir.AxisListType

P = 128
CTX = 2048
KT_N = CTX // P
BANK = 512
NB = CTX // BANK
H = 16
E = 8
LEAVES = 256
NODES = LEAVES - 1
DEPTH = 8
LW = 16
CH = LEAVES * LW // P
EPS = 1e-5
HIDDEN = -1e30

CONST = [("ident", P), ("causal", P), ("cos", P), ("sin", P), ("tri", P), ("iota1", P), ("hm8", H),
         ("hm4", H), ("bm8", P), ("bm4", P), ("before", E * E), ("gather", 16), ("flip", P), ("hm32", 4), ("strip", 2 * P - 8),
         ("ramp", 64), ("dist", 255)]
COLS = [("w2", 1), ("w3", 1), ("l0f_qb", 1), ("l0f_kb", 1), ("l0f_b1", 16), ("l1x_bq", 4), ("l1x_bk", 1),
        ("fff_b1", 4 * CH), ("l2f_bq", 1), ("l2f_bk", 1), ("l2f_bfc", 32), ("l3a_bm1", 1), ("l3a_bm2", 1)]
ROWS = [("b_sim", 1), ("w1", P), ("l0x_b", P), ("l0a_bq", P), ("l0a_bk", P), ("l0a_bv", P), ("l0a_bo", P),
        ("l0f_vb", 64), ("l0f_ob", P), ("l0f_rb", E), ("l1x_bv", P), ("l1x_bo", P), ("l1a_b", P),
        ("l2x_b", P), ("ln1_s", P), ("ln1_b", P), ("l2f_bv", P), ("l2f_ap", P), ("ln2_s", P), ("ln2_b", P),
        ("l2f_gb", E), ("l3x_g", P), ("conf_b", E), ("wealth", E)]
W_A = [("l0x", 4 * P), ("l0a_q", P), ("l0a_k", P), ("l0a_v", P), ("l0a_o", P),
       ("l0f_q", 64), ("l0f_k", 64), ("l0f_v", 64), ("l0f_o", P), ("l0f_r", E),
       ("l1x_q", 4 * P), ("l1x_k", P), ("l1x_v", P), ("l1x_o", P),
       ("l1a_qkv", 3 * P), ("l1a_p", P), ("coeff", 4), ("wpos", H)]
W_L0F = [("w1", E * 2 * P), ("w2", E * 2 * P)]
W_FFF = [("w1", LEAVES * LW), ("w2", LEAVES * LW)]
W_B = [("l2x_q", 4 * P), ("l2x_k", P), ("l2x_v", P), ("l2x_o", P), ("l2a_qkv", 3 * P), ("l2a_o", P),
       ("l2f_qkv", 3 * P), ("l2f_p", P), ("l2f_g", E), ("l3x_q", 8 * P), ("l3x_k", 8 * P), ("l3x_v", 8 * P),
       ("l3x_o1", 8 * P), ("l3x_o2", P)]
W_C = [("q", P), ("k", P), ("v", P), ("m1", 32), ("m2", H), ("p", P), ("fc", 4 * P), ("cp", 4 * P), ("conf", E)]
W_L2F = [("w1", E * 4 * P), ("w2", E * 4 * P)]
W_L3F = [("gate", E * 4 * P), ("up", E * 4 * P)]
W_L3D = [("down", E * 4 * P)]
PACKS = {"const": CONST, "cols": COLS, "w_a": W_A, "w_l0f": W_L0F, "w_q": W_FFF, "w_k": W_FFF, "w_v": W_FFF,
         "w_f": W_FFF, "w_b": W_B, "w_c": W_C, "w_l2f": W_L2F, "w_l3f": W_L3F, "w_l3d": W_L3D}
STAGES = ("l0x", "l0a", "l0f", "l1x", "l1a", "l1f", "l2x", "l2a", "l2f", "l3x", "l3a", "l3f")
DEBUG = False


def width(pack):
    return sum(n for _, n in pack)


class Steps:

    def __init__(self, sem):
        self.sem, self.order, self.value, self.taken = sem, [], {}, 0

    def plan(self, *names):
        for n in names:
            assert n not in self.value, n
            self.order.append(n)
            self.value[n] = len(self.order)

    def at(self, name):
        return self.value[name]

    def now(self, name):
        assert self.order[self.taken] == name, (self.order[self.taken], name)
        self.taken += 1
        return 1


def build(nc, dram, out, scratch, dbg=None):
    ctx = ExitStack()
    with ctx:
        def sb(name, shape, dt=F32):
            return ctx.enter_context(nc.sbuf_tensor(name, shape, dt))

        def sem(name):
            return ctx.enter_context(nc.semaphore(name))

        ps = ctx.enter_context(nc.psum_tensor("banks", [P, 8, BANK], F32))
        tiles = {n: sb("p_" + n, [P, width(PACKS[n])]) for n in ("const", "cols", "w_a")}
        rows_t = sb("p_rows", [P, width(ROWS)])
        REG = 2 * LEAVES * LW
        region_at = -(-nc.sbuf_base // 32) * 32
        region = sb("region", [P, 3 * REG])
        ctxT = sb("ctxT", [P, CTX])
        keysT = sb("keysT", [P, CTX])
        values = sb("values", [P, KT_N, P])
        probs = sb("probs", [P, 2, CTX])
        probsT = sb("probsT", [P, 4, BANK])
        xs = sb("xs", [P, 2, P])
        xb = sb("xb", [P, P])
        xn = sb("xn", [P, P])
        xnT = sb("xnT", [P, P])
        tA = sb("tA", [P, P])
        tB = sb("tB", [P, P])
        tC = sb("tC", [P, P])
        tD = sb("tD", [P, P])
        tE = sb("tE", [P, P])
        tF = sb("tF", [P, P])
        tG = sb("tG", [P, P])
        st = sb("st", [P, 6])
        mv = sb("mv", [P, 4])
        half = sb("half", [P, 2])
        one = sb("one", [P, P])
        oneb = sb("oneb", [P, P], BF16)
        identb = sb("identb", [P, P], BF16)
        picks = sb("picks", [P, 16 * P], BF16)
        causalb = sb("causalb", [P, P], BF16)
        small = sb("small", [P, 64])
        small2 = sb("small2", [P, 64])
        small3 = sb("small3", [P, 64])
        small4 = sb("small4", [P, 64])
        seen = sb("seen", [P, 4])
        nmax = sb("nmax", [P, H])
        wsum = sb("wsum", [P, 2, H])
        vaug = sb("vaug", [P, H * 9])
        maskb = sb("maskb", [1, CTX], BF16)
        ffb2 = values[:, :, :].rearrange("p a b -> p (a b)")[:, 0:8 * P]
        shared = sb("shared", [P, 16 * P])
        nodew = shared[:, 0:4 * NODES]
        nbias = shared[:, 8 * P:8 * P + 4 * NODES]
        maskTb = sb("maskTb", [P, 2, P], BF16)
        maskT = sb("maskT", [P, 2, P])
        U = ps[:, 6, :]
        at = {}
        for n, pack in (*((n, PACKS[n]) for n in tiles), ("rows", ROWS)):
            base = rows_t if n == "rows" else tiles[n]
            o = 0
            for name, w in pack:
                at[name if n != "w_a" else "w_" + name] = base[:, o:o + w]
                o += w

        def inside(base, pack):
            o = base
            for name, w in PACKS[pack]:
                at[pack + "." + name] = region[:, o:o + w]
                o += w
            return o

        for i, t in enumerate(("w_q", "w_k", "w_v")):
            inside(i * REG, t)
        inside(0, "w_f")
        inside(2 * REG, "w_l0f")
        inside(0, "w_l2f")
        assert inside(inside(REG, "w_b"), "w_c") <= 2 * REG
        inside(0, "w_l3f")
        inside(2 * REG, "w_l3d")
        sbq_at = -(-nc.sbuf_base // 32) * 32
        sbq = sb("sbq", [P, CTX])

        def over(name, shape, offset):
            return nc.alloc_sbuf_tensor_at(name, shape, F32R, offset=offset)

        keys_r = {"l1x": over("keys_l1x", [P, 4, CTX], region_at + 4 * REG),
                  "l2x": over("keys_l2x", [P, 4, CTX], region_at + 8 * REG)}
        query_r = over("query_r", [P, CTX], sbq_at)
        query_lo = over("query_lo", [P, CTX], region_at + 8 * REG)
        ctx_hi = over("ctx_hi", [P, CTX], region_at + 8 * REG + 4 * CTX)
        ctx_lo = over("ctx_lo", [P, CTX], region_at + 8 * REG + 8 * CTX)
        w_vo = region[:, 2 * REG + 3 * CTX:3 * REG]
        b2rows = sbq[:, 8 * P:]
        ident = at["ident"]

        T, V, A, G = (Steps(sem(n)) for n in ("tensor_steps", "vector_steps", "scalar_steps", "gpsimd_steps"))
        v_link, a_link, g_link = sem("vector_link"), sem("scalar_link"), sem("gpsimd_link")
        loads = {n: sem("loaded_" + n) for n in
                 ("x", "const", "cols", "rows", "w_a", "ctxT", "ctx", "mask", "w_l0f", "l0f_b2", "node", "ffb2", "w_q",
                  "w_k", "w_v", "w_f", "w_b", "w_c", "w_l2f", "l2f_b2", "w_l3f", "w_l3d", "ctx2", "bias", "keys_l1x", "keys_l2x")}
        load_n = {}
        stored = sem("stored")
        bias_out = sem("bias_stored")
        linked = {"v": 0, "a": 0, "g": 0}

        def vl(dve, ins):
            linked["v"] += 1
            ins.then_inc(v_link, 1)
            dve.wait_ge(v_link, linked["v"])

        def al(act, ins):
            linked["a"] += 1
            ins.then_inc(a_link, 1)
            act.wait_ge(a_link, linked["a"])

        def gl(pool, ins):
            linked["g"] += 1
            ins.then_inc(g_link, 1)
            pool.wait_ge(g_link, linked["g"])

        parts = {"pe": [], "dve": [], "act": [], "pool": [], "sp": []}

        def on(engine):
            def add(f):
                parts[engine].append(f)
                return f
            return add

        def mm(o, lhsT, rhs, start=True, stop=True):
            return nc.tensor.matmul(o, lhsT, rhs, start=start, stop=stop)

        def tr(o, i, n=P):
            return nc.tensor.transpose(o, i, ident[0:n, 0:n])

        def bc(ap, axis, shape):
            return ap.unsqueeze(axis).broadcast_to(shape)

        x_at = {n: i % 2 for i, n in enumerate(STAGES)}

        def stack_keys(sp, tag, low):
            sp.wait_ge(A.sem, A.at((tag, "k", 3)))
            sp.wait_ge(V.sem, V.at((tag, "k", 3)))
            for t in range(4):
                for part in range(4):
                    src = (keysT[:, :] if part < 2 else low)[32 * t:32 * t + 32, :]
                    load("keys_" + tag, keys_r[tag][32 * part:32 * part + 32, t, :].bitcast(F32), src)

        def load(name, dst, src):
            load_n[name] = load_n.get(name, 0) + 16
            nc.sync.dma_start(dst, src).then_inc(loads[name], 16)

        def loaded(eng, name):
            eng.wait_ge(loads[name], {"node": 32, "keys_l1x": 256, "keys_l2x": 256}.get(name, 16))

        @on("sp")
        def _(sp):
            load("x", xs[:, 0, :], dram["x"])
            load("mask", keysT[0:1, :].bitcast(I32), dram["mask"])
            load("const", tiles["const"][:, :], dram["const"])
            load("cols", tiles["cols"][:, :], dram["cols"])
            load("rows", rows_t[:, :], dram["rows"].partition_broadcast(P))
            load("ctxT", ctxT[:, :], dram["ctxT"])
            load("ctx", values[:, :, 0:P], dram["ctx"])
            load("w_a", tiles["w_a"][:, :], dram["w_a"])
            load("w_l0f", region[:, 2 * REG:2 * REG + width(W_L0F)], dram["w_l0f"])
            load("l0f_b2", b2rows, dram["l0f_b2"].partition_broadcast(P))
            load("w_q", region[:, 0:REG], dram["w_q"])
            stack_keys(sp, "l1x", shared)
            sp.wait_ge(V.sem, V.at("d.3"))
            nc.sync.dma_start(scratch, dists[:, :]).then_inc(bias_out, 16)
            sp.wait_ge(V.sem, V.at("l0f.x"))
            load("w_v", region[:, 2 * REG:3 * REG], dram["w_v"])
            sp.wait_ge(loads["keys_l1x"], 256)
            load("node", nodew, dram["node"])
            load("node", nbias, dram["nbias"].partition_broadcast(P))
            sp.wait_ge(V.sem, V.at("l1x.o"))
            load("w_k", region[:, REG:2 * REG], dram["w_k"])
            load("ffb2", ffb2, dram["ffb2"])
            sp.wait_ge(T.sem, T.at(("fo", "q", 7)))
            load("w_f", region[:, 0:REG], dram["w_f"])
            sp.wait_ge(T.sem, T.at(("fo", "k", 7)))
            load("w_b", region[:, REG:REG + width(W_B)], dram["w_b"])
            load("w_c", region[:, REG + width(W_B):REG + width(W_B) + width(W_C)], dram["w_c"])
            sp.wait_ge(T.sem, T.at(("fo", "v", 7)))
            stack_keys(sp, "l2x", probsT[:, :, :].rearrange("p a b -> p (a b)"))
            sp.wait_ge(T.sem, T.at(("fo", "f", 7)))
            load("w_l2f", region[:, 0:REG], dram["w_l2f"])
            sp.wait_ge(bias_out, 16)
            sp.wait_ge(V.sem, V.at("l1f.x"))
            hankel = bass.AP(scratch.tensor, 0, [[1, P], [255, H], [1, P]])
            load("bias", biases.rearrange("p (h t) -> p h t", h=H), hankel)
            sp.wait_ge(V.sem, V.at("l2x.o"))
            load("ctx2", values[:, :, 0:P], dram["ctx"])
            load("l2f_b2", b2rows, dram["l2f_b2"].partition_broadcast(P))
            sp.wait_ge(V.sem, V.at("l2f.x"))
            load("w_l3f", region[:, 0:REG], dram["w_l3f"])
            sp.wait_ge(T.sem, T.at(("l3x", "w", H - 1)))
            load("w_l3d", region[:, 2 * REG:2 * REG + width(W_L3D)], dram["w_l3d"])

        def norm_plan(tag):
            V.plan(tag + ".var", tag + ".xn")
            G.plan(tag + ".rstd")

        def norm_vector(dve, tag, src, eps=EPS):
            vl(dve, nc.vector.bn_stats(st[:, :], src))
            vl(dve, nc.vector.bn_aggr(mv[:, 0:2], st[:, :]))
            nc.vector.tensor_scalar(mv[:, 2:3], mv[:, 1:2], eps, None, ALU.add).then_inc(V.sem, V.now(tag + ".var"))
            dve.wait_ge(G.sem, G.at(tag + ".rstd"))
            nc.vector.tensor_scalar(xn[:, :], src, mv[:, 0:1], mv[:, 3:4], ALU.subtract,
                                    ALU.mult).then_inc(V.sem, V.now(tag + ".xn"))

        def norm_gpsimd(pool, tag):
            pool.wait_ge(V.sem, V.at(tag + ".var"))
            nc.gpsimd.tensor_tensor(mv[:, 3:4], mv[:, 2:3], half[:, 0:1], ALU.pow).then_inc(G.sem, G.now(tag + ".rstd"))

        def turn_plan(tag):
            T.plan(tag + ".turned")
            V.plan(tag + ".T")

        def turn_tensor(pe, tag, src, ready, bank=7, n=P):
            pe.wait_ge(V.sem, V.at(ready))
            tr(ps[0:n, bank, 0:P], src, P).then_inc(T.sem, T.now(tag + ".turned"))

        def turn_vector(dve, tag, dst, bank=7, n=P):
            dve.wait_ge(T.sem, T.at(tag + ".turned"))
            nc.vector.tensor_copy(dst[0:n, :], ps[0:n, bank, 0:P]).then_inc(V.sem, V.now(tag + ".T"))

        def start_vector(dve, tag, bias):
            norm_vector(dve, tag, xs[:, x_at[tag], :])
            if bias is not None:
                nc.vector.tensor_tensor(xb[:, :], xs[:, x_at[tag], :], bias, ALU.add)
            turn_vector(dve, tag + ".xn", xnT)

        def start_tensor(pe, tag):
            turn_tensor(pe, tag + ".xn", xn[:, :], tag + ".xn")

        def start_plan(tag):
            norm_plan(tag)
            turn_plan(tag + ".xn")

        def end_vector(dve, tag, src, base, ready):
            dve.wait_ge(T.sem, T.at(ready))
            nc.vector.tensor_tensor(xs[:, 1 - x_at[tag], :], src, base, ALU.add).then_inc(V.sem, V.now(tag + ".x"))

        def ctx_plan(tag, nh, folded=False):
            T.plan((tag, "s", 0, 0), (tag, "s", 0, 1))
            V.plan((tag, "m", 0))
            for g in range(nh):
                more = g + 1 < nh
                if more:
                    T.plan((tag, "s", g + 1, 0))
                if g:
                    T.plan((tag, "pv", g - 1, 2), (tag, "pv", g - 1, 3))
                if folded and g >= 2:
                    T.plan((tag, "w", g - 2))
                T.plan((tag, "t", g, 0), (tag, "t", g, 1))
                if more:
                    T.plan((tag, "s", g + 1, 1))
                T.plan((tag, "pv", g, 0), (tag, "t", g, 2), (tag, "pv", g, 1), (tag, "t", g, 3))
                A.plan((tag, "x", g, 0), (tag, "x", g, 1), (tag, "e", g, 0), (tag, "e", g, 1))
                if more:
                    V.plan((tag, "m", g + 1))
                V.plan((tag, "e", g, 2), (tag, "e", g, 3))
                if folded and g:
                    V.plan((tag, "u", g - 1))
                if folded and g >= 2:
                    V.plan((tag, "a", g - 2))
                if nh == H and not folded and g and g % 4 == 0:
                    V.plan((tag, "g", g // 4 - 1))
            T.plan((tag, "pv", nh - 1, 2), (tag, "pv", nh - 1, 3))
            if folded:
                T.plan((tag, "w", nh - 2), (tag, "w", nh - 1))
                V.plan((tag, "u", nh - 1), (tag, "a", nh - 2), (tag, "a", nh - 1))

        def evacuated(eng, tag, g, c):
            steps = A if c < 2 else V
            eng.wait_ge(steps.sem, steps.at((tag, "e", g, c)))

        def ctx_tensor(pe, tag, nh, score, weigh_tile, between=None):
            def scores(h, half):
                if h:
                    pe.wait_ge(A.sem, A.at((tag, "x", h - 1, half)))
                for b in (2 * half, 2 * half + 1):
                    m = score(h, b)
                m.then_inc(T.sem, T.now((tag, "s", h, half)))

            def turn(g, c):
                pe.wait_ge(A.sem, A.at((tag, "x", g, c // 2)))
                n = 4 * g + c - 2
                if n >= 0:
                    evacuated(pe, tag, n // 4, n % 4)
                for j in range(4):
                    m = tr(ps[:, 4 + c % 2, j * P:(j + 1) * P], probs[:, g % 2, (4 * c + j) * P:(4 * c + j + 1) * P])
                m.then_inc(T.sem, T.now((tag, "t", g, c)))

            def weigh(g, c):
                evacuated(pe, tag, g, c)
                for j in range(4):
                    m = weigh_tile(g, 4 * c + j, probsT[:, c, j * P:(j + 1) * P])
                m.then_inc(T.sem, T.now((tag, "pv", g, c)))

            scores(0, 0)
            scores(0, 1)
            for g in range(nh):
                if g + 1 < nh:
                    scores(g + 1, 0)
                if g:
                    weigh(g - 1, 2)
                    weigh(g - 1, 3)
                if between is not None and g >= 2:
                    between(pe, g - 2)
                turn(g, 0)
                turn(g, 1)
                if g + 1 < nh:
                    scores(g + 1, 1)
                weigh(g, 0)
                turn(g, 2)
                weigh(g, 1)
                turn(g, 3)
            weigh(nh - 1, 2)
            weigh(nh - 1, 3)
            if between is not None:
                between(pe, nh - 2)
                between(pe, nh - 1)

        def evacuate(eng, tag, g, c):
            eng.wait_ge(T.sem, T.at((tag, "t", g, c)))
            if g:
                eng.wait_ge(T.sem, T.at((tag, "pv", g - 1, c)))
            if c < 2:
                nc.scalar.copy(probsT[:, c, :], ps[:, 4 + c % 2, :]).then_inc(A.sem, A.now((tag, "e", g, c)))
            else:
                nc.vector.tensor_copy(probsT[:, c, :], ps[:, 4 + c % 2, :]).then_inc(V.sem, V.now((tag, "e", g, c)))

        def ctx_vector(dve, tag, nh, scale, after=None):
            def largest(h):
                for half in range(2):
                    dve.wait_ge(T.sem, T.at((tag, "s", h, half)))
                    m = nc.vector.tensor_reduce(small[:, half:half + 1], ps[:, 2 * half:2 * half + 2, :], AX.XY, ALU.max)
                vl(dve, m)
                nc.vector.tensor_scalar(nmax[:, h:h + 1], small[:, 0:1], small[:, 1:2], -scale, ALU.max,
                                        ALU.mult).then_inc(V.sem, V.now((tag, "m", h)))

            largest(0)
            for g in range(nh):
                if g + 1 < nh:
                    largest(g + 1)
                evacuate(dve, tag, g, 2)
                evacuate(dve, tag, g, 3)
                if after is not None:
                    after(dve, g)

        def ctx_scalar(act, tag, nh, scale):
            for g in range(nh):
                act.wait_ge(V.sem, V.at((tag, "m", g)))
                if g >= 2:
                    act.wait_ge(T.sem, T.at((tag, "t", g - 2, 3)))
                for half in range(2):
                    o = half * 2 * BANK
                    nc.scalar.activation(probs[:, g % 2, o:o + 2 * BANK],
                                         ps[:, 2 * half:2 * half + 2, :].rearrange("p a b -> p (a b)"), ACT.Exp,
                                         bias=nmax[:, g:g + 1], scale=scale,
                                         accum_out=wsum[:, half, g:g + 1]).then_inc(A.sem, A.now((tag, "x", g, half)))
                evacuate(act, tag, g, 0)
                evacuate(act, tag, g, 1)

        def sums_vector(dve, tag, nh, dst):
            dve.wait_ge(A.sem, A.at((tag, "x", nh - 1, 1)))
            vl(dve, nc.vector.tensor_tensor(small3[:, 0:nh], wsum[:, 0, 0:nh], wsum[:, 1, 0:nh], ALU.add))
            return nc.vector.reciprocal(dst, small3[:, 0:nh])

        def self_plan(tag):
            T.plan(*((tag, "s", g) for g in range(4)))
            V.plan(*((tag, "sub", g) for g in range(4)))
            A.plan(*((tag, "exp", g) for g in range(4)))
            T.plan((tag, "t", 0), (tag, "t", 1), (tag, "t", 2), (tag, "t", 3), tag + ".U")
            V.plan(*((tag, "e", g) for g in range(4)))
            out_plan(tag)

        def out_plan(tag):
            V.plan(tag + ".o")
            turn_plan(tag + ".o")

        def self_tensor(pe, tag, n, hd, qT, kbd, first=None):
            for g in range(4):
                mm(ps[:, g, :], qT[0:n, :], kbd[0:n, g * BANK:(g + 1) * BANK], first is None,
                   True).then_inc(T.sem, T.now((tag, "s", g)))
            for g in range(4):
                pe.wait_ge(A.sem, A.at((tag, "exp", g)))
                if g >= 2:
                    pe.wait_ge(V.sem, V.at((tag, "e", g - 2)))
                for j in range(4):
                    m = tr(ps[:, 4 + g % 2, j * P:(j + 1) * P], probs[:, 1, (4 * g + j) * P:(4 * g + j + 1) * P])
                m.then_inc(T.sem, T.now((tag, "t", g)))
            w = hd + 1
            for g in range(4):
                pe.wait_ge(V.sem, V.at((tag, "e", g)))
                for j in range(4):
                    h = 4 * g + j
                    m = mm(U[:, h * w:(h + 1) * w], probsT[:, g, j * P:(j + 1) * P], vaug[:, h * w:(h + 1) * w])
            m.then_inc(T.sem, T.now(tag + ".U"))
            turn_tensor(pe, tag + ".o", tA[:, 0:n], tag + ".o", 5, n)

        def self_vector(dve, tag, n, hd):
            for g in range(4):
                dve.wait_ge(T.sem, T.at((tag, "s", g)))
                s = ps[:, g, :].rearrange("p (h t) -> p h t", h=4)
                vl(dve, nc.vector.tensor_reduce(nmax[:, 4 * g:4 * g + 4], s, AX.X, ALU.max))
                nc.vector.tensor_tensor(probs[:, 1, g * BANK:(g + 1) * BANK].rearrange("p (h t) -> p h t", h=4), s,
                                        bc(nmax[:, 4 * g:4 * g + 4], 2, [P, 4, P]),
                                        ALU.subtract).then_inc(V.sem, V.now((tag, "sub", g)))
            for g in range(4):
                dve.wait_ge(T.sem, T.at((tag, "t", g)))
                nc.vector.tensor_copy(probsT[:, g, :], ps[:, 4 + g % 2, :]).then_inc(V.sem, V.now((tag, "e", g)))
            dve.wait_ge(T.sem, T.at(tag + ".U"))
            out_vector(dve, tag, n, hd)

        def out_vector(dve, tag, n, hd):
            u = U[:, 0:H * (hd + 1)].rearrange("p (h w) -> p h w", h=H)
            vl(dve, nc.vector.reciprocal(small[:, 0:H], u[:, :, hd]))
            nc.vector.tensor_tensor(tA[:, 0:n].rearrange("p (h w) -> p h w", h=H), u[:, :, 0:hd],
                                    bc(small[:, 0:H], 2, [P, H, hd]), ALU.mult).then_inc(V.sem, V.now(tag + ".o"))
            turn_vector(dve, tag + ".o", tB, 5, n)

        def self_scalar(act, tag, scale):
            for g in range(4):
                act.wait_ge(V.sem, V.at((tag, "sub", g)))
                p = probs[:, 1, g * BANK:(g + 1) * BANK]
                nc.scalar.activation(p, p, ACT.Exp, scale=scale).then_inc(A.sem, A.now((tag, "exp", g)))

        def spread_heads(dst, src, heads, n):
            return nc.vector.tensor_tensor(dst.rearrange("p (h t) -> p h t", h=H)[0:n], bc(src[0:n, :], 1, [n, H, P]),
                                           bc(heads[0:n, :], 2, [n, H, P]), ALU.mult)

        def top2(dve, vals, mask):
            mine, other = bc(vals, 2, [P, E, E]), bc(vals, 1, [P, E, E])
            v3 = small2[:, :].rearrange("p (a b) -> p a b", a=E)
            w3 = small3[:, :].rearrange("p (a b) -> p a b", a=E)
            nc.vector.tensor_tensor(w3, other, mine, ALU.is_gt)
            vl(dve, nc.vector.tensor_tensor(v3, other, mine, ALU.is_ge))
            vl(dve, nc.vector.tensor_tensor(small2[:, :], small2[:, :], at["before"], ALU.mult))
            vl(dve, nc.vector.tensor_tensor(small2[:, :], small2[:, :], small3[:, :], ALU.max))
            vl(dve, nc.vector.tensor_reduce(small3[:, 0:E], v3, AX.X, ALU.add))
            vl(dve, nc.vector.tensor_scalar(mask, small3[:, 0:E], 1.5, None, ALU.is_lt))

        def moe_plan(tag):
            for g in range(tag_groups[tag] + 1):
                if g < tag_groups[tag]:
                    T.plan((tag, "h", g))
                    A.plan((tag, "a", g))
                    V.plan((tag, "g", g))
                if g:
                    T.plan((tag, "o", g - 1))

        tag_groups = {"l0f": 4, "l2f": 8, "l3f": 8}

        def moe_tensor(pe, tag, w_in, w_gate, w_out, xT, per):
            ng = tag_groups[tag]
            for g in range(ng + 1):
                if g < ng:
                    if g >= 2:
                        pe.wait_ge(V.sem, V.at((tag, "g", g - 2)))
                    for j in range(4):
                        c = 4 * g + j
                        m = mm(ps[:, g % 2, j * P:(j + 1) * P], w_in[:, c * P:(c + 1) * P], xT)
                        if w_gate is not None:
                            m = mm(ps[:, 2 + g % 2, j * P:(j + 1) * P], w_gate[:, c * P:(c + 1) * P], xT)
                    m.then_inc(T.sem, T.now((tag, "h", g)))
                if g:
                    pe.wait_ge(V.sem, V.at((tag, "g", g - 1)))
                    for j in range(4):
                        c = 4 * (g - 1) + j
                        e = c // per
                        m = mm(ps[:, 4 + e // 4, (e % 4) * P:(e % 4 + 1) * P],
                               probs[:, 1, (g - 1) % 2 * BANK + j * P:(g - 1) % 2 * BANK + (j + 1) * P],
                               w_out[:, c * P:(c + 1) * P], c % per == 0, c % per == per - 1)
                    m.then_inc(T.sem, T.now((tag, "o", g - 1)))

        def moe_scalar(act, tag, func, bias):
            for g in range(tag_groups[tag]):
                act.wait_ge(T.sem, T.at((tag, "h", g)))
                if g >= 2:
                    act.wait_ge(V.sem, V.at((tag, "g", g - 2)))
                o = g % 2 * BANK
                if bias is None:
                    m = nc.scalar.activation(probs[:, 0, o:o + BANK], ps[:, g % 2, :], func)
                else:
                    for j in range(4):
                        m = nc.scalar.activation(probs[:, 0, o + j * P:o + (j + 1) * P], ps[:, g % 2, j * P:(j + 1) * P],
                                                 func, bias=bias[:, 4 * g + j:4 * g + j + 1])
                m.then_inc(A.sem, A.now((tag, "a", g)))

        def moe_vector(dve, tag, gated):
            for g in range(tag_groups[tag]):
                dve.wait_ge(A.sem, A.at((tag, "a", g)))
                if g >= 2:
                    dve.wait_ge(T.sem, T.at((tag, "o", g - 2)))
                o = g % 2 * BANK
                if gated:
                    m = nc.vector.tensor_tensor(probs[:, 1, o:o + BANK], probs[:, 0, o:o + BANK], ps[:, 2 + g % 2, :],
                                                ALU.mult)
                else:
                    m = nc.vector.tensor_copy(probs[:, 1, o:o + BANK], probs[:, 0, o:o + BANK])
                m.then_inc(V.sem, V.now((tag, "g", g)))

        G.plan("const")
        V.plan("prelude")

        @on("pool")
        def _(pool):
            nc.gpsimd.memset(half[:, 0:1], -0.5)
            nc.gpsimd.memset(half[:, 1:2], 0.5)
            nc.gpsimd.memset(one[:, :], 1.0)
            nc.gpsimd.memset(oneb[:, :], 1.0)
            nc.gpsimd.memset(vaug[:, :], 1.0).then_inc(G.sem, G.now("const"))

        @on("dve")
        def _(dve):
            loaded(dve, "const")
            nc.vector.tensor_copy(identb[:, :], ident)
            nc.vector.tensor_copy(picks[:, :].rearrange("p (k w) -> p k w", w=LW), bc(ident, 2, [P, P, LW]))
            nc.vector.tensor_copy(causalb[:, :], at["causal"]).then_inc(V.sem, V.now("prelude"))

        def l0x():
            tag = "l0x"
            start_plan(tag)
            V.plan("l0x.q")
            ctx_plan(tag, 1)
            V.plan("l0x.t")
            T.plan("l0x.row")
            V.plan("l0x.rowmax")
            A.plan("l0x.rowexp")
            V.plan("l0x.row")
            T.plan("l0x.batt")
            V.plan("l0x.batt")
            T.plan("l0x.bar")
            V.plan("l0x.bar")
            V.plan("l0x.rd")
            T.plan("l0x.rd")
            V.plan("l0x.prod")
            keys_plan("l1x")
            T.plan("l0x.y")
            V.plan("l0x.x")
            s = small4

            @on("pe")
            def _(pe):
                loaded(pe, "const")
                start_tensor(pe, tag)

                def ready(pe, h):
                    loaded(pe, "ctxT")
                    pe.wait_ge(V.sem, V.at("l0x.q"))
                loaded(pe, "ctx")
                ready(pe, 0)
                ctx_tensor(pe, tag, 1, lambda h, b: mm(ps[:, b, :], tA[:, :], ctxT[:, b * BANK:(b + 1) * BANK]),
                           lambda g, t, p: mm(ps[:, 6, 0:P], values[:, t, 0:P], p, t == 0, t == KT_N - 1))
                pe.wait_ge(V.sem, V.at("l0x.t"))
                tr(ps[0:1, 7, 0:P], s[:, 2:3]).then_inc(T.sem, T.now("l0x.row"))
                pe.wait_ge(V.sem, V.at("l0x.row"))
                mm(ps[:, 7, 128:129], tC[0:1, :], one[0:1, 0:1]).then_inc(T.sem, T.now("l0x.batt"))
                pe.wait_ge(V.sem, V.at("l0x.batt"))
                mm(ps[:, 7, 130:131], xn[:, :], s[:, 8:9]).then_inc(T.sem, T.now("l0x.bar"))
                pe.wait_ge(V.sem, V.at("l0x.rd"))
                mm(ps[:, 5, 0:P], tB[:, :], ident).then_inc(T.sem, T.now("l0x.rd"))
                keys_tensor(pe, "l1x", at["w_l1x_k"], 0)
                pe.wait_ge(V.sem, V.at("l0x.prod"))
                loaded(pe, "w_a")
                for i, f in enumerate((xnT, tD, tE, tF)):
                    m = mm(ps[:, 4, 0:P], f[:, :], at["w_l0x"][:, i * P:(i + 1) * P], i == 0, i == 3)
                m.then_inc(T.sem, T.now("l0x.y"))

            @on("dve")
            def _(dve):
                loaded(dve, "x")
                dve.wait_ge(G.sem, G.at("const"))
                loaded(dve, "rows")
                loaded(dve, "cols")
                start_vector(dve, tag, at["l0x_b"])
                dve.wait_ge(V.sem, V.at("l0x.xn.T"))
                nc.vector.tensor_scalar(tA[:, :], xnT[:, :], at["w3"], at["w2"], ALU.mult,
                                        ALU.add).then_inc(V.sem, V.now("l0x.q"))
                nc.vector.tensor_tensor_reduce(tC[:, :], xn[:, :], at["w1"], 1.0, 0.0, ALU.mult, ALU.add, s[:, 0:1])
                ctx_vector(dve, tag, 1, 1.0)
                vl(dve, nc.vector.tensor_tensor(s[:, 1:2], s[:, 0:1], at["b_sim"], ALU.add))
                nc.vector.tensor_tensor(s[:, 2:3], s[:, 1:2], nmax[:, 0:1],
                                        ALU.subtract).then_inc(V.sem, V.now("l0x.t"))
                dve.wait_ge(T.sem, T.at("l0x.row"))
                nc.vector.tensor_reduce(s[0:1, 4:5], ps[0:1, 7, 0:P], AX.X, ALU.max,
                                        negate=True).then_inc(V.sem, V.now("l0x.rowmax"))
                dve.wait_ge(A.sem, A.at("l0x.rowexp"))
                vl(dve, nc.vector.reciprocal(s[0:1, 6:7], s[0:1, 5:6]))
                nc.vector.tensor_scalar(tC[0:1, :], tC[0:1, :], s[0:1, 6:7], None,
                                        ALU.mult).then_inc(V.sem, V.now("l0x.row"))
                dve.wait_ge(T.sem, T.at("l0x.batt"))
                nc.vector.tensor_copy(s[:, 8:9], ps[:, 7, 128:129]).then_inc(V.sem, V.now("l0x.batt"))
                dve.wait_ge(T.sem, T.at("l0x.bar"))
                nc.vector.tensor_copy(s[:, 9:10], ps[:, 7, 130:131]).then_inc(V.sem, V.now("l0x.bar"))
                vl(dve, sums_vector(dve, tag, 1, s[:, 10:11]))
                nc.vector.tensor_scalar(tB[:, :], one[:, :], s[:, 10:11], None,
                                        ALU.mult).then_inc(V.sem, V.now("l0x.rd"))
                dve.wait_ge(T.sem, T.at("l0x.rd"))
                vl(dve, nc.vector.tensor_copy(tE[:, :], ps[:, 5, 0:P]))
                vl(dve, nc.vector.tensor_tensor(tD[:, :], ps[:, 6, 0:P], tE[:, :], ALU.mult))
                nc.vector.tensor_tensor(tE[:, :], xnT[:, :], tD[:, :], ALU.mult)
                nc.vector.tensor_scalar(tF[:, :], xnT[:, :], s[:, 9:10], None,
                                        ALU.mult).then_inc(V.sem, V.now("l0x.prod"))
                keys_vector(dve, "l1x", at["l1x_bk"], 0, shared)
                end_vector(dve, tag, ps[:, 4, 0:P], xb[:, :], "l0x.y")

            @on("act")
            def _(act):
                ctx_scalar(act, tag, 1, 1.0)
                act.wait_ge(V.sem, V.at("l0x.rowmax"))
                nc.scalar.activation(tC[0:1, :], ps[0:1, 7, 0:P], ACT.Exp, bias=s[0:1, 4:5],
                                     accum_out=s[0:1, 5:6]).then_inc(A.sem, A.now("l0x.rowexp"))
                keys_scalar(act, "l1x", at["l1x_bk"], 0)

            @on("pool")
            def _(pool):
                norm_gpsimd(pool, tag)

        def l0a():
            tag = "l0a"
            start_plan(tag)
            T.plan("l0a.qkv")
            V.plan("l0a.v", "l0a.q", "l0a.k")
            turn_plan("l0a.q")
            T.plan("l0a.kv")
            V.plan("l0a.kv")
            T.plan("l0a.c")
            V.plan("l0a.c")
            T.plan("l0a.y")
            V.plan("l0a.x")

            @on("pe")
            def _(pe):
                start_tensor(pe, tag)
                pe.wait_ge(V.sem, V.at("l0a.xn.T"))
                for i, w in enumerate(("q", "k", "v")):
                    m = mm(ps[:, i, 0:P], xnT[:, :], at["w_l0a_" + w])
                m.then_inc(T.sem, T.now("l0a.qkv"))
                turn_tensor(pe, "l0a.q", tA[:, :], "l0a.q", 5)
                pe.wait_ge(V.sem, V.at("l0a.k"))
                mm(ps[:, 3, 0:P], tB[:, :], tC[:, :]).then_inc(T.sem, T.now("l0a.kv"))
                pe.wait_ge(V.sem, V.at("l0a.kv"))
                mm(ps[:, 4, 0:P], tD[:, :], tE[:, :]).then_inc(T.sem, T.now("l0a.c"))
                pe.wait_ge(V.sem, V.at("l0a.c"))
                mm(ps[:, 6, 0:P], tF[:, :], at["w_l0a_o"]).then_inc(T.sem, T.now("l0a.y"))

            def rotate(dve, src, bias, dst, name):
                vl(dve, nc.vector.tensor_tensor(tG[:, :], src, bias, ALU.add))
                g = tG[:, :].rearrange("p (n t) -> p n t", t=2)
                f = tF[:, :].rearrange("p (n t) -> p n t", t=2)
                sn = at["sin"].rearrange("p (n t) -> p n t", t=2)
                nc.vector.tensor_tensor(f[:, :, 0], g[:, :, 1], sn[:, :, 0], ALU.mult)
                nc.vector.tensor_tensor(f[:, :, 1], g[:, :, 0], sn[:, :, 1], ALU.mult)
                vl(dve, nc.vector.tensor_tensor(dst[:, :], tG[:, :], at["cos"], ALU.mult))
                nc.vector.tensor_tensor(dst[:, :], dst[:, :], tF[:, :], ALU.add).then_inc(V.sem, V.now(name))
                dve.wait_ge(V.sem, V.at(name))

            @on("dve")
            def _(dve):
                dve.wait_ge(V.sem, V.at("l0x.x"))
                start_vector(dve, tag, at["l0a_bo"])
                dve.wait_ge(T.sem, T.at("l0a.qkv"))
                nc.vector.tensor_tensor(tC[:, :], ps[:, 2, 0:P], at["l0a_bv"], ALU.add).then_inc(V.sem, V.now("l0a.v"))
                rotate(dve, ps[:, 0, 0:P], at["l0a_bq"], tA, "l0a.q")
                rotate(dve, ps[:, 1, 0:P], at["l0a_bk"], tB, "l0a.k")
                turn_vector(dve, "l0a.q", tE, 5)
                dve.wait_ge(T.sem, T.at("l0a.kv"))
                nc.vector.scalar_tensor_tensor(tD[:, :], ps[:, 3, 0:P], 1.0 / np.sqrt(8.0), at["bm8"], ALU.mult,
                                               ALU.mult).then_inc(V.sem, V.now("l0a.kv"))
                dve.wait_ge(T.sem, T.at("l0a.c"))
                nc.vector.tensor_copy(tF[:, :], ps[:, 4, 0:P]).then_inc(V.sem, V.now("l0a.c"))
                end_vector(dve, tag, ps[:, 6, 0:P], xb[:, :], "l0a.y")

            @on("pool")
            def _(pool):
                norm_gpsimd(pool, tag)

        def l0f():
            tag = "l0f"
            start_plan(tag)
            T.plan("l0f.qkv")
            V.plan("l0f.qkv")
            self_plan(tag)
            T.plan("l0f.mla")
            V.plan("l0f.mla")
            turn_plan("l0f.mla")
            T.plan("l0f.route")
            V.plan("l0f.rmax")
            A.plan("l0f.rexp")
            V.plan("l0f.comb")
            moe_plan(tag)
            V.plan("l0f.x")
            s = small4

            @on("pe")
            def _(pe):
                start_tensor(pe, tag)
                pe.wait_ge(V.sem, V.at("l0f.xn.T"))
                mm(ps[0:64, 4, 0:P], at["w_l0f_q"], xnT[:, :])
                mm(ps[0:64, 5, 0:P], at["w_l0f_k"], xnT[:, :])
                mm(ps[:, 6, 0:64], xnT[:, :], at["w_l0f_v"]).then_inc(T.sem, T.now("l0f.qkv"))
                pe.wait_ge(V.sem, V.at("l0f.qkv"))
                self_tensor(pe, tag, 64, 4, tC, probs[:, 0, :])
                pe.wait_ge(V.sem, V.at("l0f.o.T"))
                mm(ps[:, 7, 0:P], tB[0:64, :], at["w_l0f_o"][0:64, :]).then_inc(T.sem, T.now("l0f.mla"))
                turn_tensor(pe, "l0f.mla", tC[:, :], "l0f.mla", 6)
                pe.wait_ge(V.sem, V.at("l0f.mla.T"))
                mm(ps[:, 7, 0:E], tD[:, :], at["w_l0f_r"]).then_inc(T.sem, T.now("l0f.route"))
                loaded(pe, "w_l0f")
                moe_tensor(pe, tag, at["w_l0f.w1"], None, at["w_l0f.w2"], tD[:, :], 2)

            @on("dve")
            def _(dve):
                dve.wait_ge(V.sem, V.at("l0a.x"))
                start_vector(dve, tag, None)
                dve.wait_ge(T.sem, T.at("l0f.qkv"))
                nc.vector.tensor_scalar(tC[0:64, :], ps[0:64, 4, 0:P], at["l0f_qb"][0:64, :], None, ALU.add)
                vl(dve, nc.vector.tensor_scalar(tD[0:64, :], ps[0:64, 5, 0:P], at["l0f_kb"][0:64, :], None, ALU.add))
                va = vaug[:, 0:H * 5].rearrange("p (h w) -> p h w", h=H)
                nc.vector.tensor_tensor(va[:, :, 0:4], ps[:, 6, 0:64].rearrange("p (h w) -> p h w", h=H),
                                        at["l0f_vb"].rearrange("p (h w) -> p h w", h=H), ALU.add)
                spread_heads(probs[:, 0, :], tD, at["hm4"], 64).then_inc(V.sem, V.now("l0f.qkv"))
                self_vector(dve, tag, 64, 4)
                dve.wait_ge(T.sem, T.at("l0f.mla"))
                nc.vector.tensor_tensor(tC[:, :], ps[:, 7, 0:P], at["l0f_ob"], ALU.add).then_inc(V.sem, V.now("l0f.mla"))
                turn_vector(dve, "l0f.mla", tD, 6)
                route_vector(dve, "l0f", at["l0f_rb"])
                top2(dve, s[:, 16:24], s[:, 24:32])
                vl(dve, nc.vector.tensor_tensor_reduce(s[:, 32:40], s[:, 16:24], s[:, 24:32], 1.0, 0.0, ALU.mult,
                                                       ALU.add, s[:, 40:41]))
                vl(dve, nc.vector.tensor_scalar(s[:, 41:42], s[:, 40:41], 1e-8, None, ALU.add))
                vl(dve, nc.vector.reciprocal(s[:, 42:43], s[:, 41:42]))
                nc.vector.tensor_scalar(s[:, 48:56], s[:, 32:40], s[:, 42:43], 0.3, ALU.mult,
                                        ALU.mult).then_inc(V.sem, V.now("l0f.comb"))
                vl(dve, nc.vector.tensor_tensor(xb[:, :], xs[:, x_at[tag], :], xn[:, :], ALU.add))
                moe_vector(dve, tag, False)
                loaded(dve, "l0f_b2")
                mix_vector(dve, tag, s[:, 48:56], xb[:, :])

            @on("act")
            def _(act):
                self_scalar(act, tag, 0.5)
                route_scalar(act, "l0f")
                loaded(act, "cols")
                moe_scalar(act, tag, ACT.Gelu, at["l0f_b1"])

            @on("pool")
            def _(pool):
                norm_gpsimd(pool, tag)

        def route_vector(dve, tag, bias):
            s = small4
            dve.wait_ge(T.sem, T.at(tag + ".route"))
            vl(dve, nc.vector.tensor_tensor(s[:, 0:8], ps[:, 7, 0:E], bias, ALU.add))
            nc.vector.tensor_reduce(s[:, 8:9], s[:, 0:8], AX.X, ALU.max, negate=True).then_inc(V.sem, V.now(tag + ".rmax"))
            dve.wait_ge(A.sem, A.at(tag + ".rexp"))
            vl(dve, nc.vector.reciprocal(s[:, 10:11], s[:, 9:10]))
            vl(dve, nc.vector.tensor_scalar(s[:, 16:24], s[:, 0:8], s[:, 10:11], None, ALU.mult))

        def route_scalar(act, tag):
            s = small4
            act.wait_ge(V.sem, V.at(tag + ".rmax"))
            nc.scalar.activation(s[:, 0:8], s[:, 0:8], ACT.Exp, bias=s[:, 8:9],
                                 accum_out=s[:, 9:10]).then_inc(A.sem, A.now(tag + ".rexp"))

        def mix_vector(dve, tag, comb, base, biases=True):
            ng = tag_groups[tag]
            dve.wait_ge(T.sem, T.at((tag, "o", ng - 1)))
            if biases:
                nc.vector.tensor_tensor(probs[:, 0, 0:BANK], ps[:, 4, :], b2rows[:, 0:BANK], ALU.add)
                vl(dve, nc.vector.tensor_tensor(probs[:, 0, BANK:2 * BANK], ps[:, 5, :], b2rows[:, BANK:], ALU.add))
            src = base
            for e in range(E):
                last = e == E - 1
                dst = xs[:, 1 - x_at[tag], :] if last else (tE, tF)[e % 2][:, :]
                o = probs[:, 0, e * P:(e + 1) * P] if biases else ps[:, 4 + e // 4, (e % 4) * P:(e % 4 + 1) * P]
                m = nc.vector.scalar_tensor_tensor(dst, o, comb[:, e:e + 1], src, ALU.mult, ALU.add)
                if last:
                    m.then_inc(V.sem, V.now(tag + ".x"))
                else:
                    vl(dve, m)
                src = dst

        def keys_plan(tag):
            T.plan(*((tag, "kp", b) for b in range(NB)))
            A.plan(*((tag, "k", b) for b in range(NB)))
            V.plan(*((tag, "k", b) for b in range(NB)))

        def keys_tensor(pe, tag, wk, bank):
            for b in range(NB):
                mm(ps[:, bank + b, :], wk, ctxT[:, b * BANK:(b + 1) * BANK]).then_inc(T.sem, T.now((tag, "kp", b)))

        def keys_scalar(act, tag, bias, bank):
            for b in range(NB):
                act.wait_ge(T.sem, T.at((tag, "kp", b)))
                o = keysT[:, b * BANK:(b + 1) * BANK].bitcast(F32R)
                if bias is None:
                    m = nc.scalar.copy(o, ps[:, bank + b, :])
                else:
                    m = nc.scalar.activation(o, ps[:, bank + b, :], ACT.Identity, bias=bias)
                m.then_inc(A.sem, A.now((tag, "k", b)))

        def keys_vector(dve, tag, bias, bank, low):
            for b in range(NB):
                dve.wait_ge(A.sem, A.at((tag, "k", b)))
                o = low[:, b * BANK:(b + 1) * BANK]
                hi = keysT[:, b * BANK:(b + 1) * BANK]
                if bias is None:
                    m = nc.vector.tensor_tensor(o, ps[:, bank + b, :], hi, ALU.subtract)
                else:
                    m = nc.vector.scalar_tensor_tensor(o, ps[:, bank + b, :], bias, hi, ALU.add, ALU.subtract)
                m.then_inc(V.sem, V.now((tag, "k", b)))

        def values_tensor(pe, tag, wv):
            for b in range(4):
                for j in range(4):
                    t = 4 * b + j
                    m = mm(ps[:, b, j * P:(j + 1) * P], ctxT[:, t * P:(t + 1) * P], wv)
                m.then_inc(T.sem, T.now((tag, "vp", b)))

        def values_vector(dve, tag, bias):
            for b in range(4):
                dve.wait_ge(T.sem, T.at((tag, "vp", b)))
                o = values[:, 4 * b:4 * b + 4, 0:P]
                i = ps[:, b, :].rearrange("p (t n) -> p t n", n=P)
                if bias is None:
                    m = nc.vector.tensor_copy(o, i)
                else:
                    m = nc.vector.tensor_tensor(o, i, bc(bias, 1, [P, 4, P]), ALU.add)
                m.then_inc(V.sem, V.now((tag, "v", b)))

        def cross(tag, before, w, scale, masked, q_bias, v_bias, o_bias, pack):
            T.plan(*((tag, "vp", b) for b in range(4)))
            start_plan(tag)
            V.plan(*((tag, "v", b) for b in range(4)))
            T.plan(tag + ".q")
            V.plan(tag + ".qs", *((tag, "q", t) for t in range(4)), (tag, "zero"))
            ctx_plan(tag, H)
            V.plan(tag + ".rd", (tag, "g", 3), tag + ".rdT")
            T.plan(tag + ".rd", tag + ".o")
            V.plan(tag + ".o")
            T.plan(tag + ".y")
            V.plan(tag + ".x")
            keys = keys_r[tag]

            @on("pe")
            def _(pe):
                loaded(pe, pack)
                pe.wait_ge(V.sem, V.at(before))
                values_tensor(pe, tag, w("v"))
                start_tensor(pe, tag)
                pe.wait_ge(V.sem, V.at(tag + ".xn.T"))
                for t in range(4):
                    m = mm(ps[:, 6, t * P:(t + 1) * P], w("q")[:, t * P:(t + 1) * P], xnT[:, :])
                m.then_inc(T.sem, T.now(tag + ".q"))
                loaded(pe, "keys_" + tag)
                pe.wait_ge(V.sem, V.at((tag, "zero")))

                def score(h, b):
                    if h % 4 == 0 and b == 0:
                        pe.wait_ge(V.sem, V.at((tag, "q", h // 4)))
                    m = mm(ps[:, b, :], query_r[:, h * P:(h + 1) * P], keys[:, h // 4, b * BANK:(b + 1) * BANK],
                           True, not masked)
                    if masked:
                        m = mm(ps[:, b, :], oneb[0:1, :], maskb[:, b * BANK:(b + 1) * BANK], False, True)
                    return m

                def weigh_tile(g, t, p):
                    j = t % 4
                    if g >= 8 and g % 4 == 0 and t == 0:
                        pe.wait_ge(V.sem, V.at((tag, "g", g // 4 - 2)))
                    return mm(ps[32 * j:32 * j + 8, 6 + g // 4 % 2, (g % 4) * P:(g % 4 + 1) * P],
                              values[:, t, 8 * g:8 * g + 8], p, t < 4, t >= KT_N - 4)

                def fold(gs):
                    for g in gs:
                        pe.wait_ge(V.sem, V.at((tag, "g", g // 4)))
                        m = mm(ps[:, 6, 0:P], at["strip"][:, 120 - 8 * g:248 - 8 * g], keysT[:, g * P:(g + 1) * P],
                               g == 0, g == H - 1)
                    return m
                ctx_tensor(pe, tag, H, score, weigh_tile)
                fold(range(12))
                pe.wait_ge(V.sem, V.at(tag + ".rd"))
                mm(ps[:, 5, 0:P], tA[:, :], ident).then_inc(T.sem, T.now(tag + ".rd"))
                fold(range(12, H)).then_inc(T.sem, T.now(tag + ".o"))
                pe.wait_ge(V.sem, V.at(tag + ".o"))
                mm(ps[:, 4, 0:P], tB[:, :], w("o")).then_inc(T.sem, T.now(tag + ".y"))

            @on("dve")
            def _(dve):
                dve.wait_ge(V.sem, V.at(before))
                start_vector(dve, tag, o_bias)
                values_vector(dve, tag, v_bias)
                dve.wait_ge(T.sem, T.at(tag + ".q"))
                full = probs[:, 1, 0:BANK]
                hi = probs[:, 1, BANK:2 * BANK]
                if masked:
                    for t in range(4):
                        m = nc.vector.tensor_scalar(full[:, t * P:(t + 1) * P], ps[:, 6, t * P:(t + 1) * P],
                                                    q_bias[:, t:t + 1], seen[:, 2:3], ALU.add, ALU.mult)
                else:
                    m = nc.vector.tensor_copy(full, ps[:, 6, :])
                vl(dve, m)
                vl(dve, nc.vector.tensor_copy(hi.bitcast(F32R), full))
                for p in (32, 96):
                    m = nc.vector.tensor_tensor(hi[p:p + 32, :], full[p:p + 32, :], hi[p:p + 32, :], ALU.subtract)
                m.then_inc(V.sem, V.now(tag + ".qs"))
                dve.wait_ge(V.sem, V.at(tag + ".qs"))
                for t in range(4):
                    nc.vector.tensor_tensor(query_r[:, 4 * t * P:4 * (t + 1) * P].rearrange("p (h n) -> p h n", h=4),
                                            bc(hi[:, t * P:(t + 1) * P], 1, [P, 4, P]), bc(at["hm32"], 2, [P, 4, P]),
                                            ALU.mult).then_inc(V.sem, V.now((tag, "q", t)))
                nc.vector.memset(ps[:, 6:8, :], 0.0).then_inc(V.sem, V.now((tag, "zero")))

                def after(dve, g):
                    if g % 4 == 0 and g:
                        gather(dve, g // 4 - 1)

                def gather(dve, n):
                    dve.wait_ge(T.sem, T.at((tag, "pv", 4 * n + 3, 3)))
                    nc.vector.tensor_copy(keysT[:, n * BANK:(n + 1) * BANK], ps[:, 6 + n % 2, :]).then_inc(
                        V.sem, V.now((tag, "g", n)))
                ctx_vector(dve, tag, H, scale, after)
                vl(dve, sums_vector(dve, tag, H, small[:, 16:32]))
                nc.vector.tensor_copy(tA[:, :].rearrange("p (h w) -> p h w", h=H),
                                      bc(small[:, 16:32], 2, [P, H, 8])).then_inc(V.sem, V.now(tag + ".rd"))
                gather(dve, 3)
                dve.wait_ge(T.sem, T.at(tag + ".rd"))
                nc.vector.tensor_copy(tC[:, :], ps[:, 5, 0:P]).then_inc(V.sem, V.now(tag + ".rdT"))
                dve.wait_ge(V.sem, V.at(tag + ".rdT"))
                dve.wait_ge(T.sem, T.at(tag + ".o"))
                nc.vector.tensor_tensor(tB[:, :], ps[:, 6, 0:P], tC[:, :], ALU.mult).then_inc(V.sem, V.now(tag + ".o"))
                end_vector(dve, tag, ps[:, 4, 0:P], xb[:, :], tag + ".y")

            @on("act")
            def _(act):
                ctx_scalar(act, tag, H, scale)

            @on("pool")
            def _(pool):
                norm_gpsimd(pool, tag)

        def l1a():
            tag = "l1a"
            start_plan(tag)
            T.plan("l1a.qkv")
            V.plan("l1a.qkv")
            T.plan("l1a.kv")
            V.plan("l1a.kv")
            T.plan("l1a.num")
            V.plan("l1a.o")
            turn_plan("l1a.o")
            T.plan("l1a.y")
            V.plan("l1a.x")

            @on("pe")
            def _(pe):
                start_tensor(pe, tag)
                pe.wait_ge(V.sem, V.at("l1a.xn.T"))
                w = at["w_l1a_qkv"]
                mm(ps[:, 0, 0:P], w[:, 0:P], xnT[:, :])
                mm(ps[:, 1, 0:P], xnT[:, :], w[:, P:2 * P])
                mm(ps[:, 2, 0:P], xnT[:, :], w[:, 2 * P:3 * P]).then_inc(T.sem, T.now("l1a.qkv"))
                pe.wait_ge(V.sem, V.at("l1a.qkv"))
                mm(ps[:, 3, 0:P], tB[:, :], tC[:, :])
                mm(ps[:, 4, 0:P], tB[:, :], one[:, :]).then_inc(T.sem, T.now("l1a.kv"))
                pe.wait_ge(V.sem, V.at("l1a.kv"))
                mm(ps[:, 5, 0:P], tA[:, :], tD[:, :])
                mm(ps[:, 6, 0:P], tA[:, :], tE[:, :]).then_inc(T.sem, T.now("l1a.num"))
                turn_tensor(pe, "l1a.o", tF[:, :], "l1a.o", 7)
                pe.wait_ge(V.sem, V.at("l1a.o.T"))
                mm(ps[:, 0, 0:P], tG[:, :], at["w_l1a_p"]).then_inc(T.sem, T.now("l1a.y"))

            @on("dve")
            def _(dve):
                dve.wait_ge(V.sem, V.at("l1x.x"))
                start_vector(dve, tag, at["l1a_b"])
                dve.wait_ge(T.sem, T.at("l1a.qkv"))
                nc.vector.tensor_scalar(tA[:, :], ps[:, 0, 0:P], 0.0, None, ALU.max)
                nc.vector.tensor_scalar(tB[:, :], ps[:, 1, 0:P], 0.0, None, ALU.max)
                nc.vector.tensor_scalar(tC[:, :], ps[:, 2, 0:P], 0.0, None, ALU.max).then_inc(V.sem, V.now("l1a.qkv"))
                dve.wait_ge(T.sem, T.at("l1a.kv"))
                nc.vector.tensor_tensor(tD[:, :], ps[:, 3, 0:P], at["bm4"], ALU.mult)
                nc.vector.tensor_tensor(tE[:, :], ps[:, 4, 0:P], at["bm4"], ALU.mult).then_inc(V.sem, V.now("l1a.kv"))
                dve.wait_ge(T.sem, T.at("l1a.num"))
                vl(dve, nc.vector.tensor_scalar(tG[:, :], ps[:, 6, 0:P], 1e-15, None, ALU.add))
                vl(dve, nc.vector.reciprocal(tF[:, :], tG[:, :]))
                nc.vector.tensor_tensor(tF[:, :], ps[:, 5, 0:P], tF[:, :], ALU.mult).then_inc(V.sem, V.now("l1a.o"))
                turn_vector(dve, "l1a.o", tG, 7)
                end_vector(dve, tag, ps[:, 0, 0:P], xb[:, :], "l1a.y")

            @on("pool")
            def _(pool):
                norm_gpsimd(pool, tag)

        TREES = ("q", "k", "v", "f")

        def tree_plan(i):
            n = TREES[i]
            T.plan(("fm", n))
            V.plan(("fm", n))
            for g in range(9):
                if g < 8:
                    T.plan(("fa", n, g))
                    A.plan(("fr", n, g))
                    V.plan(("fh", n, g))
                if g:
                    T.plan(("fo", n, g - 1))

        def tree_tensor(pe, i, xT, turned):
            n = TREES[i]
            loaded(pe, "w_" + n)
            o = ps[:, 4 + i % 4, 0:P]
            w1, w2 = at[f"w_{n}.w1"], at[f"w_{n}.w2"]
            mask = paths[:, i % 3, :]
            tr(ps[:, 0, 0:P], mask[:, 0:P])
            tr(ps[:, 0, P:2 * P], mask[:, P:2 * P]).then_inc(T.sem, T.now(("fm", n)))
            pe.wait_ge(V.sem, V.at(("fm", n)))
            loaded(pe, "ffb2")
            for c in range(2):
                b2 = ffb2[:, (2 * i + c) * P:(2 * i + c + 1) * P]
                if turned:
                    mm(o, b2, maskT[:, c, :], c == 0, False)
                else:
                    mm(o, maskT[:, c, :], b2, c == 0, False)
            for g in range(9):
                if g < 8:
                    if g >= 2:
                        pe.wait_ge(A.sem, A.at(("fr", n, g - 2)))
                        pe.wait_ge(V.sem, V.at(("fh", n, g - 2)))
                    for j in range(4):
                        c = 4 * g + j
                        mm(ps[:, g % 2, j * P:(j + 1) * P], w1[:, c * P:(c + 1) * P], xT)
                    for j in range(4):
                        c = 4 * g + j
                        pick = picks[:, (c % 16) * P:(c % 16 + 1) * P]
                        m = mm(ps[:, 2 + g % 2, j * P:(j + 1) * P], pick, maskTb[:, c // 16, :])
                    m.then_inc(T.sem, T.now(("fa", n, g)))
                if g:
                    pe.wait_ge(V.sem, V.at(("fh", n, g - 1)))
                    for j in range(4):
                        c = 4 * (g - 1) + j
                        h = probs[:, 1, (g - 1) % 2 * BANK + j * P:(g - 1) % 2 * BANK + (j + 1) * P]
                        w = w2[:, c * P:(c + 1) * P]
                        m = mm(o, w, h, False, c == CH - 1) if turned else mm(o, h, w, False, c == CH - 1)
                    m.then_inc(T.sem, T.now(("fo", n, g - 1)))

        def tree_scalar(act, i, func):
            n = TREES[i]
            for g in range(8):
                act.wait_ge(T.sem, T.at(("fa", n, g)))
                if g >= 2:
                    act.wait_ge(V.sem, V.at(("fh", n, g - 2)))
                o = g % 2 * BANK
                for j in range(4):
                    c = 4 * g + j
                    m = nc.scalar.activation(probs[:, 0, o + j * P:o + (j + 1) * P], ps[:, g % 2, j * P:(j + 1) * P],
                                             func, bias=at["fff_b1"][:, i * CH + c:i * CH + c + 1])
                m.then_inc(A.sem, A.now(("fr", n, g)))

        def tree_vector(dve, i):
            n = TREES[i]
            dve.wait_ge(T.sem, T.at(("fm", n)))
            nc.vector.tensor_copy(maskT[:, :, :].rearrange("p a b -> p (a b)"), ps[:, 0, 0:2 * P])
            nc.vector.tensor_copy(maskTb[:, :, :].rearrange("p a b -> p (a b)"),
                                  ps[:, 0, 0:2 * P]).then_inc(V.sem, V.now(("fm", n)))
            for g in range(8):
                dve.wait_ge(A.sem, A.at(("fr", n, g)))
                if g >= 2:
                    dve.wait_ge(T.sem, T.at(("fo", n, g - 2)))
                o = g % 2 * BANK
                nc.vector.tensor_tensor(probs[:, 1, o:o + BANK], probs[:, 0, o:o + BANK], ps[:, 2 + g % 2, :],
                                        ALU.mult).then_inc(V.sem, V.now(("fh", n, g)))

        def walk_vector(dve, first, count, name):
            ways = probs[:, 1, 0:count * 2 * LEAVES].rearrange("p (n k s) -> p n k s", n=count, s=2)
            for j in range(count):
                i = first + j
                vl(dve, nc.vector.tensor_tensor(probs[:, 0, j * NODES:(j + 1) * NODES], logits(j),
                                                nbias[:, i * NODES:(i + 1) * NODES], ALU.add))
            lg = probs[:, 0, 0:count * NODES].rearrange("p (n k) -> p n k", n=count)
            nc.vector.tensor_scalar(ways[:, :, 0:NODES, 0], lg, 0.0, None, ALU.is_le)
            vl(dve, nc.vector.tensor_scalar(ways[:, :, 0:NODES, 1], lg, 0.0, None, ALU.is_gt))
            cur = ways[:, :, 0, :]
            for d in range(1, DEPTH):
                w = 2 ** d
                dst = paths[:, 0:count, :] if d == DEPTH - 1 else \
                    levels[:, d % 2, 0:count * 2 * w].rearrange("p (n k) -> p n k", n=count)
                for j in range(count):
                    m = nc.vector.tensor_tensor(dst[:, j].rearrange("p (k s) -> p k s", s=2),
                                                bc(cur[:, j], 2, [P, w, 2]), ways[:, j, w - 1:2 * w - 1, :], ALU.mult)
                    if j < count - 1:
                        continue
                    if d == DEPTH - 1:
                        m.then_inc(V.sem, V.now(name))
                    else:
                        vl(dve, m)
                cur = dst

        def logits(j):
            return ps[:, 1 + j // 2, (j % 2) * 256:(j % 2) * 256 + NODES]

        def l1f():
            tag = "l1f"
            norm_plan("l1f")
            V.plan("l1f.sd")
            G.plan("l1f.sd")
            V.plan("l1f.xx")
            G.plan("l1f.xx")
            V.plan("l1f.xh")
            turn_plan("l1f.xh")
            T.plan("l1f.nodes")
            V.plan("l1f.paths")
            for i in range(3):
                tree_plan(i)
            V.plan("l1f.qkv")
            T.plan("l1f.s")
            V.plan("l1f.m")
            A.plan("l1f.p")
            V.plan("l1f.p")
            turn_plan("l1f.p")
            T.plan("l1f.av")
            V.plan("l1f.y")
            turn_plan("l1f.y")
            T.plan("l1f.nodef")
            V.plan("l1f.pathf")
            keys_plan("l2x")
            tree_plan(3)
            V.plan("l1f.x")
            s = small4

            @on("pe")
            def _(pe):
                turn_tensor(pe, "l1f.xh", tA[:, :], "l1f.xh")
                pe.wait_ge(V.sem, V.at("l1f.xh.T"))
                loaded(pe, "node")
                for j in range(3):
                    m = mm(logits(j), xnT[:, :], nodew[:, j * NODES:(j + 1) * NODES])
                m.then_inc(T.sem, T.now("l1f.nodes"))
                pe.wait_ge(V.sem, V.at("l1f.paths"))
                tree_tensor(pe, 0, xnT[:, :], True)
                tree_tensor(pe, 1, xnT[:, :], True)
                tree_tensor(pe, 2, xnT[:, :], False)
                pe.wait_ge(V.sem, V.at("l1f.qkv"))
                mm(ps[:, 0, 0:P], tC[:, :], tD[:, :]).then_inc(T.sem, T.now("l1f.s"))
                turn_tensor(pe, "l1f.p", tF[:, :], "l1f.p", 7)
                pe.wait_ge(V.sem, V.at("l1f.p.T"))
                mm(ps[:, 1, 0:P], tG[:, :], tE[:, :]).then_inc(T.sem, T.now("l1f.av"))
                turn_tensor(pe, "l1f.y", tB[:, :], "l1f.y", 7)
                pe.wait_ge(V.sem, V.at("l1f.y.T"))
                mm(logits(0), xnT[:, :], nodew[:, 3 * NODES:4 * NODES]).then_inc(T.sem, T.now("l1f.nodef"))
                loaded(pe, "w_b")
                keys_tensor(pe, "l2x", at["w_b.l2x_k"], 2)
                pe.wait_ge(V.sem, V.at("l1f.pathf"))
                pe.wait_ge(V.sem, V.at(("l2x", "k", 3)))
                tree_tensor(pe, 3, xnT[:, :], False)

            @on("dve")
            def _(dve):
                dve.wait_ge(V.sem, V.at("l1a.x"))
                norm_vector(dve, "l1f", xs[:, x_at[tag], :])
                dve.wait_ge(V.sem, V.at("l1f.xn"))
                vl(dve, nc.vector.bn_stats(st[:, :], xn[:, :]))
                vl(dve, nc.vector.bn_aggr(mv[:, 0:2], st[:, :]))
                nc.vector.tensor_scalar(mv[:, 2:3], mv[:, 1:2], P / (P - 1.0), None,
                                        ALU.mult).then_inc(V.sem, V.now("l1f.sd"))
                dve.wait_ge(G.sem, G.at("l1f.sd"))
                nc.vector.tensor_scalar(mv[:, 2:3], mv[:, 3:4], 1e-5, None, ALU.add).then_inc(V.sem, V.now("l1f.xx"))
                dve.wait_ge(G.sem, G.at("l1f.xx"))
                nc.vector.tensor_scalar(tA[:, :], xn[:, :], mv[:, 0:1], mv[:, 3:4], ALU.subtract,
                                        ALU.mult).then_inc(V.sem, V.now("l1f.xh"))
                turn_vector(dve, "l1f.xh", xnT)
                loaded(dve, "node")
                dve.wait_ge(T.sem, T.at("l1f.nodes"))
                walk_vector(dve, 0, 3, "l1f.paths")
                for i in range(3):
                    tree_vector(dve, i)
                dve.wait_ge(T.sem, T.at(("fo", "v", 7)))
                nc.vector.tensor_copy(tC[:, :], ps[:, 4, 0:P])
                nc.vector.tensor_copy(tD[:, :], ps[:, 5, 0:P])
                nc.vector.tensor_copy(tE[:, :], ps[:, 6, 0:P]).then_inc(V.sem, V.now("l1f.qkv"))
                dve.wait_ge(T.sem, T.at("l1f.s"))
                vl(dve, nc.vector.tensor_reduce(s[:, 0:1], ps[:, 0, 0:P], AX.X, ALU.max))
                nc.vector.tensor_scalar(s[:, 1:2], s[:, 0:1], -1.0 / np.sqrt(float(P)), None,
                                        ALU.mult).then_inc(V.sem, V.now("l1f.m"))
                dve.wait_ge(A.sem, A.at("l1f.p"))
                vl(dve, nc.vector.reciprocal(s[:, 3:4], s[:, 2:3]))
                nc.vector.tensor_scalar(tF[:, :], tF[:, :], s[:, 3:4], None, ALU.mult).then_inc(V.sem, V.now("l1f.p"))
                turn_vector(dve, "l1f.p", tG, 7)
                dve.wait_ge(T.sem, T.at("l1f.av"))
                nc.vector.tensor_tensor(tB[:, :], ps[:, 1, 0:P], tA[:, :], ALU.add).then_inc(V.sem, V.now("l1f.y"))
                turn_vector(dve, "l1f.y", xnT, 7)
                vl(dve, nc.vector.tensor_tensor(xb[:, :], xs[:, x_at[tag], :], tB[:, :], ALU.add))
                dve.wait_ge(T.sem, T.at("l1f.nodef"))
                walk_vector(dve, 3, 1, "l1f.pathf")
                keys_vector(dve, "l2x", None, 2, probsT[:, :, :].rearrange("p a b -> p (a b)"))
                tree_vector(dve, 3)
                end_vector(dve, tag, ps[:, 7, 0:P], xb[:, :], ("fo", "f", 7))

            @on("act")
            def _(act):
                for i in range(3):
                    tree_scalar(act, i, ACT.Relu)
                act.wait_ge(V.sem, V.at("l1f.m"))
                nc.scalar.activation(tF[:, :], ps[:, 0, 0:P], ACT.Exp, bias=s[:, 1:2], scale=float(1.0 / np.sqrt(P)),
                                     accum_out=s[:, 2:3]).then_inc(A.sem, A.now("l1f.p"))
                keys_scalar(act, "l2x", None, 2)
                tree_scalar(act, 3, ACT.Gelu)

            @on("pool")
            def _(pool):
                norm_gpsimd(pool, "l1f")
                pool.wait_ge(V.sem, V.at("l1f.sd"))
                nc.gpsimd.tensor_tensor(mv[:, 3:4], mv[:, 2:3], half[:, 1:2], ALU.pow).then_inc(G.sem, G.now("l1f.sd"))
                pool.wait_ge(V.sem, V.at("l1f.xx"))
                nc.gpsimd.tensor_tensor(mv[:, 3:4], mv[:, 2:3], half[:, 0:1], ALU.pow).then_inc(G.sem, G.now("l1f.xx"))

        def l2a():
            tag = "l2a"
            start_plan(tag)
            T.plan("l2a.qkv")
            V.plan("l2a.qkv")
            G.plan("l3x.split")
            self_plan(tag)
            T.plan("l2a.y")
            V.plan("l2a.x")

            @on("pe")
            def _(pe):
                start_tensor(pe, tag)
                loaded(pe, "bias")
                for g in range(4):
                    mm(ps[:, g, :], at["flip"], biases[:, g * BANK:(g + 1) * BANK], True, False)
                pe.wait_ge(V.sem, V.at("l2a.xn.T"))
                w = at["w_b.l2a_qkv"]
                mm(ps[:, 4, 0:P], w[:, 0:P], xnT[:, :])
                mm(ps[:, 5, 0:P], w[:, P:2 * P], xnT[:, :])
                mm(ps[:, 6, 0:P], xnT[:, :], w[:, 2 * P:3 * P]).then_inc(T.sem, T.now("l2a.qkv"))
                pe.wait_ge(V.sem, V.at("l2a.qkv"))
                self_tensor(pe, tag, P, 8, tC, probs[:, 0, :], True)
                pe.wait_ge(V.sem, V.at("l2a.o.T"))
                mm(ps[:, 7, 0:P], tB[:, :], at["w_b.l2a_o"]).then_inc(T.sem, T.now("l2a.y"))

            @on("dve")
            def _(dve):
                dve.wait_ge(V.sem, V.at("l2x.x"))
                start_vector(dve, tag, None)
                dve.wait_ge(T.sem, T.at("l2a.qkv"))
                nc.vector.tensor_scalar(tC[:, :], ps[:, 4, 0:P], float(8 ** -0.5), None, ALU.mult)
                vl(dve, nc.vector.tensor_copy(tD[:, :], ps[:, 5, 0:P]))
                va = vaug[:, :].rearrange("p (h w) -> p h w", h=H)
                nc.vector.tensor_copy(va[:, :, 0:8], ps[:, 6, 0:P].rearrange("p (h w) -> p h w", h=H))
                nc.vector.memset(va[:, :, 8], 1.0)
                spread_heads(probs[:, 0, :], tD, at["hm8"], P).then_inc(V.sem, V.now("l2a.qkv"))
                self_vector(dve, tag, P, 8)
                end_vector(dve, tag, ps[:, 7, 0:P], xs[:, x_at[tag], :], "l2a.y")

            @on("act")
            def _(act):
                self_scalar(act, tag, 1.0)

            @on("pool")
            def _(pool):
                norm_gpsimd(pool, tag)
                gl(pool, nc.gpsimd.tensor_copy(ctx_hi[:, :], ctxT[:, :]))
                nc.gpsimd.tensor_tensor(ctx_lo[:, :], ctxT[:, :], ctx_hi[:, :].bitcast(F32),
                                        ALU.subtract).then_inc(G.sem, G.now("l3x.split"))

        def l2f():
            tag = "l2f"
            T.plan("l3x.vo")
            A.plan("l3x.vo")
            norm_plan("l2f")
            norm_plan("l2f1")
            V.plan("l2f1.h")
            turn_plan("l2f1.h")
            T.plan("l2f.qkv")
            V.plan("l2f.qkv")
            self_plan(tag)
            T.plan("l2f.ap")
            V.plan("l2f.x1")
            norm_plan("l2f2")
            V.plan("l2f2.h")
            turn_plan("l2f2.h")
            T.plan("l2f.route")
            V.plan("l2f.rmax")
            A.plan("l2f.rexp")
            V.plan("l2f.mask")
            T.plan("l2f.rank")
            moe_plan(tag)
            V.plan("l2f.eo")
            V.plan(*(("l2f.perm", e) for e in range(E)))
            T.plan("l2f.y")
            V.plan("l2f.x")
            s = small4

            @on("pe")
            def _(pe):
                pe.wait_ge(V.sem, V.at("l2a.x"))
                for h in range(H):
                    r = 64 * (h % 2)
                    c = h // 2
                    m = mm(ps[:, 4 + 2 * (h % 2) + c // 4, (c % 4) * P:(c % 4 + 1) * P],
                           at["w_b.l3x_v"][r:r + 64, c * P:(c + 1) * P], at["w_b.l3x_o1"][r:r + 64, c * P:(c + 1) * P])
                m.then_inc(T.sem, T.now("l3x.vo"))
                for g in range(4):
                    mm(ps[:, g, :], identb[:, :], bc(causalb[:, :], 1, [P, 4, P]), True, False)
                pe.wait_ge(A.sem, A.at("l3x.vo"))
                turn_tensor(pe, "l2f1.h", tA[:, :], "l2f1.h")
                pe.wait_ge(V.sem, V.at("l2f1.h.T"))
                w = at["w_b.l2f_qkv"]
                mm(ps[:, 4, 0:P], w[:, 0:P], xnT[:, :])
                mm(ps[:, 5, 0:P], w[:, P:2 * P], xnT[:, :])
                mm(ps[:, 6, 0:P], xnT[:, :], w[:, 2 * P:3 * P]).then_inc(T.sem, T.now("l2f.qkv"))
                pe.wait_ge(V.sem, V.at("l2f.qkv"))
                self_tensor(pe, tag, P, 8, tC, probs[:, 0, :], True)
                pe.wait_ge(V.sem, V.at("l2f.o.T"))
                mm(ps[:, 7, 0:P], tB[:, :], at["w_b.l2f_p"]).then_inc(T.sem, T.now("l2f.ap"))
                turn_tensor(pe, "l2f2.h", tB[:, :], "l2f2.h", 6)
                pe.wait_ge(V.sem, V.at("l2f2.h.T"))
                mm(ps[:, 7, 0:E], xnT[:, :], at["w_b.l2f_g"]).then_inc(T.sem, T.now("l2f.route"))
                pe.wait_ge(V.sem, V.at("l2f.mask"))
                mm(ps[:, 7, 0:E], at["tri"], s[:, 24:32]).then_inc(T.sem, T.now("l2f.rank"))
                loaded(pe, "w_l2f")
                moe_tensor(pe, tag, at["w_l2f.w1"], None, at["w_l2f.w2"], xnT[:, :], 4)
                pe.wait_ge(V.sem, V.at("l2f.eo"))
                for e in range(E):
                    pe.wait_ge(V.sem, V.at(("l2f.perm", e)))
                    m = mm(ps[:, 6, 0:P], perm[:, e * P:(e + 1) * P], probs[:, 0, e * P:(e + 1) * P], e == 0, e == E - 1)
                m.then_inc(T.sem, T.now("l2f.y"))

            def affine(dve, ready, name, dst, scale, bias):
                dve.wait_ge(V.sem, V.at(ready))
                vl(dve, nc.vector.tensor_tensor(dst[:, :], xn[:, :], scale, ALU.mult))
                nc.vector.tensor_tensor(dst[:, :], dst[:, :], bias, ALU.add).then_inc(V.sem, V.now(name))

            @on("dve")
            def _(dve):
                dve.wait_ge(V.sem, V.at("l2a.x"))
                norm_vector(dve, "l2f", xs[:, x_at[tag], :])
                dve.wait_ge(V.sem, V.at("l2f.xn"))
                vl(dve, nc.vector.tensor_copy(tE[:, :], xn[:, :]))
                norm_vector(dve, "l2f1", tE[:, :])
                nc.vector.tensor_tensor(xb[:, :], tE[:, :], at["l2f_ap"], ALU.add)
                affine(dve, "l2f1.xn", "l2f1.h", tA, at["ln1_s"], at["ln1_b"])
                turn_vector(dve, "l2f1.h", xnT)
                dve.wait_ge(T.sem, T.at("l2f.qkv"))
                nc.vector.tensor_scalar(tC[:, :], ps[:, 4, 0:P], at["l2f_bq"], float(8 ** -0.5), ALU.add, ALU.mult)
                vl(dve, nc.vector.tensor_scalar(tD[:, :], ps[:, 5, 0:P], at["l2f_bk"], None, ALU.add))
                va = vaug[:, :].rearrange("p (h w) -> p h w", h=H)
                nc.vector.tensor_tensor(va[:, :, 0:8], ps[:, 6, 0:P].rearrange("p (h w) -> p h w", h=H),
                                        at["l2f_bv"].rearrange("p (h w) -> p h w", h=H), ALU.add)
                spread_heads(probs[:, 0, :], tD, at["hm8"], P).then_inc(V.sem, V.now("l2f.qkv"))
                self_vector(dve, tag, P, 8)
                dve.wait_ge(T.sem, T.at("l2f.ap"))
                nc.vector.tensor_tensor(tG[:, :], ps[:, 7, 0:P], xb[:, :], ALU.add).then_inc(V.sem, V.now("l2f.x1"))
                dve.wait_ge(V.sem, V.at("l2f.x1"))
                norm_vector(dve, "l2f2", tG[:, :])
                nc.vector.tensor_tensor(xb[:, :], xs[:, x_at[tag], :], tG[:, :], ALU.add)
                affine(dve, "l2f2.xn", "l2f2.h", tB, at["ln2_s"], at["ln2_b"])
                turn_vector(dve, "l2f2.h", xnT, 6)
                route_vector(dve, "l2f", at["l2f_gb"])
                top2(dve, s[:, 16:24], s[:, 24:32])
                nc.vector.tensor_tensor(s[:, 32:40], s[:, 16:24], s[:, 24:32], ALU.mult).then_inc(V.sem, V.now("l2f.mask"))
                dve.wait_ge(T.sem, T.at("l2f.rank"))
                vl(dve, nc.vector.tensor_copy(s[:, 40:48], ps[:, 7, 0:E]))
                moe_vector(dve, tag, False)
                loaded(dve, "l2f_b2")
                dve.wait_ge(T.sem, T.at((tag, "o", tag_groups[tag] - 1)))
                nc.vector.tensor_tensor(probs[:, 0, 0:BANK], ps[:, 4, :], b2rows[:, 0:BANK], ALU.add)
                nc.vector.tensor_tensor(probs[:, 0, BANK:2 * BANK], ps[:, 5, :], b2rows[:, BANK:],
                                        ALU.add).then_inc(V.sem, V.now("l2f.eo"))
                for e in range(E):
                    nc.vector.tensor_scalar(perm[:, e * P:(e + 1) * P], at["iota1"], s[:, 40 + e:41 + e],
                                            s[:, 32 + e:33 + e], ALU.is_equal,
                                            ALU.mult).then_inc(V.sem, V.now(("l2f.perm", e)))
                end_vector(dve, tag, ps[:, 6, 0:P], xb[:, :], "l2f.y")

            @on("act")
            def _(act):
                act.wait_ge(T.sem, T.at("l3x.vo"))
                w4 = w_vo.rearrange("p (c s n) -> p c s n", s=2, n=P)
                for i in range(2):
                    m = nc.scalar.copy(w4[:, :, i, :], ps[:, 4 + 2 * i:6 + 2 * i, :].rearrange("p a (b n) -> p (a b) n", n=P))
                m.then_inc(A.sem, A.now("l3x.vo"))
                self_scalar(act, tag, 1.0)
                route_scalar(act, "l2f")
                moe_scalar(act, tag, ACT.Gelu_apprx_tanh, at["l2f_bfc"])

            @on("pool")
            def _(pool):
                norm_gpsimd(pool, "l2f")
                norm_gpsimd(pool, "l2f1")
                norm_gpsimd(pool, "l2f2")

        def l3x():
            tag = "l3x"
            start_plan(tag)
            T.plan("l3x.q")
            V.plan("l3x.q")
            T.plan("l3x.qk")
            A.plan("l3x.qhi")
            V.plan("l3x.qlo")
            G.plan("l3a.wide")
            ctx_plan(tag, H, True)
            V.plan("l3x.1")
            turn_plan("l3x.1")
            T.plan("l3x.2")
            V.plan("l3x.2")
            norm_plan("l3xo")
            V.plan("l3x.x")

            def by_parity(ap, i):
                return ap.rearrange("p (c s n) -> p c s n", s=2, n=P)[:, :, i, :]

            def queries(i):
                return ps[:, 2 + 2 * i:4 + 2 * i, :].rearrange("p a (b n) -> p (a b) n", n=P)

            @on("pe")
            def _(pe):
                start_tensor(pe, tag)
                pe.wait_ge(V.sem, V.at("l3x.xn.T"))
                for c in range(8):
                    m = mm(ps[:, c // 4, (c % 4) * P:(c % 4 + 1) * P], at["w_b.l3x_q"][:, c * P:(c + 1) * P], xnT[:, :])
                m.then_inc(T.sem, T.now("l3x.q"))
                pe.wait_ge(V.sem, V.at("l3x.q"))
                for h in range(H):
                    r = 64 * (h % 2)
                    c = h // 2
                    m = mm(ps[:, 2 + 2 * (h % 2) + c // 4, (c % 4) * P:(c % 4 + 1) * P],
                           at["w_b.l3x_k"][r:r + 64, c * P:(c + 1) * P], qheads[r:r + 64, c * P:(c + 1) * P])
                m.then_inc(T.sem, T.now("l3x.qk"))
                pe.wait_ge(A.sem, A.at("l3x.qhi"))
                pe.wait_ge(V.sem, V.at("l3x.qlo"))
                pe.wait_ge(G.sem, G.at("l3x.split"))
                loaded(pe, "ctx2")

                def score(h, b):
                    hi, lo = query_r[:, h * P:(h + 1) * P], query_lo[:, h * P:(h + 1) * P]
                    c = slice(b * BANK, (b + 1) * BANK)
                    mm(ps[:, b, :], hi, ctx_hi[:, c], True, False)
                    mm(ps[:, b, :], hi, ctx_lo[:, c], False, False)
                    return mm(ps[:, b, :], lo, ctx_hi[:, c], False, True)

                def weigh_tile(g, t, p):
                    if g >= 2 and t == 0:
                        pe.wait_ge(V.sem, V.at((tag, "u", g - 2)))
                        if g >= 3:
                            pe.wait_ge(V.sem, V.at((tag, "a", g - 3)))
                    return mm(ps[:, 6 + g % 2, 0:P], values[:, t, 0:P], p, t == 0, t == KT_N - 1)

                def output(pe, g):
                    pe.wait_ge(V.sem, V.at((tag, "u", g)))
                    mm(ps[:, 6 + (g + 1) % 2, P:2 * P], (tD, tE)[g % 2][:, :],
                       w_vo[:, g * P:(g + 1) * P]).then_inc(T.sem, T.now((tag, "w", g)))
                ctx_tensor(pe, tag, H, score, weigh_tile, output)
                turn_tensor(pe, "l3x.1", tA[:, :], "l3x.1", 4)
                pe.wait_ge(V.sem, V.at("l3x.1.T"))
                mm(ps[:, 5, 0:P], tB[:, :], at["w_b.l3x_o2"]).then_inc(T.sem, T.now("l3x.2"))

            @on("dve")
            def _(dve):
                dve.wait_ge(V.sem, V.at("l2f.x"))
                start_vector(dve, tag, None)
                dve.wait_ge(T.sem, T.at("l3x.q"))
                nc.vector.tensor_copy(qheads[:, :], ps[:, 0:2, :].rearrange("p a b -> p (a b)")).then_inc(
                    V.sem, V.now("l3x.q"))
                dve.wait_ge(A.sem, A.at("l3x.qhi"))
                for i in range(2):
                    m = nc.vector.tensor_tensor(by_parity(query_lo[:, :], i), queries(i),
                                                by_parity(query_r[:, :].bitcast(F32), i), ALU.subtract)
                m.then_inc(V.sem, V.now("l3x.qlo"))

                def take(g, ready):
                    dve.wait_ge(T.sem, T.at(ready))
                    nc.vector.tensor_copy((tD, tE)[g % 2][:, :], ps[:, 6 + g % 2, 0:P]).then_inc(
                        V.sem, V.now((tag, "u", g)))

                def add(g):
                    vl(dve, nc.vector.tensor_tensor(small3[:, g:g + 1], wsum[:, 0, g:g + 1], wsum[:, 1, g:g + 1], ALU.add))
                    vl(dve, nc.vector.reciprocal(small2[:, g:g + 1], small3[:, g:g + 1]))
                    dve.wait_ge(T.sem, T.at((tag, "w", g)))
                    o = ps[:, 6 + (g + 1) % 2, P:2 * P]
                    if g:
                        m = nc.vector.scalar_tensor_tensor(tF[:, :], o, small2[:, g:g + 1], tF[:, :], ALU.mult, ALU.add)
                    else:
                        m = nc.vector.tensor_scalar(tF[:, :], o, small2[:, g:g + 1], None, ALU.mult)
                    m.then_inc(V.sem, V.now((tag, "a", g)))

                def after(dve, g):
                    if g:
                        take(g - 1, (tag, "w", g - 2) if g >= 2 else (tag, "pv", g - 1, 3))
                    if g >= 2:
                        add(g - 2)
                ctx_vector(dve, tag, H, 0.125, after)
                take(H - 1, (tag, "w", H - 2))
                add(H - 2)
                dve.wait_ge(V.sem, V.at((tag, "a", H - 2)))
                add(H - 1)
                dve.wait_ge(V.sem, V.at((tag, "a", H - 1)))
                nc.vector.tensor_scalar(tA[:, :], tF[:, :], 0.0, None, ALU.max).then_inc(V.sem, V.now("l3x.1"))
                turn_vector(dve, "l3x.1", tB, 4)
                dve.wait_ge(T.sem, T.at("l3x.2"))
                nc.vector.tensor_copy(tC[:, :], ps[:, 5, 0:P]).then_inc(V.sem, V.now("l3x.2"))
                dve.wait_ge(V.sem, V.at("l3x.2"))
                norm_vector(dve, "l3xo", tC[:, :])
                dve.wait_ge(V.sem, V.at("l3xo.xn"))
                vl(dve, nc.vector.tensor_tensor(tD[:, :], xn[:, :], at["l3x_g"], ALU.mult))
                nc.vector.tensor_tensor(xs[:, 1 - x_at[tag], :], tD[:, :], xs[:, x_at[tag], :], ALU.add).then_inc(
                    V.sem, V.now("l3x.x"))

            @on("act")
            def _(act):
                act.wait_ge(T.sem, T.at("l3x.qk"))
                for i in range(2):
                    m = nc.scalar.copy(by_parity(query_r[:, :], i), queries(i))
                m.then_inc(A.sem, A.now("l3x.qhi"))
                ctx_scalar(act, tag, H, 0.125)

            @on("pool")
            def _(pool):
                norm_gpsimd(pool, tag)
                loaded(pool, "w_c")
                for name, dst in (("k", keysT[:, 0:8 * P]), ("q", shared[:, 8 * P:])):
                    nc.gpsimd.tensor_copy(dst.rearrange("p (a b) -> p a b", b=8), bc(at["w_c." + name], 2, [P, P, 8]))
                for h in range(H):
                    m = nc.gpsimd.tensor_copy(
                        keysT[:, 8 * P + 64 * h:8 * P + 64 * h + 64].rearrange("p (a b) -> p a b", a=8),
                        bc(at["w_c.v"][:, 8 * h:8 * h + 8], 1, [P, 8, 8]))
                m.then_inc(G.sem, G.now("l3a.wide"))
                norm_gpsimd(pool, "l3xo")

        def l3a():
            tag = "l3a"
            V.plan("l3a.var", "l3a.xn")
            turn_plan("l3a.xn")
            T.plan("l3a.m1", "l3a.kvq")
            V.plan("l3a.m1")
            T.plan("l3a.z")
            V.plan("l3a.nb")
            A.plan("l3a.k", "l3a.q", "l3a.z")
            V.plan("l3a.s")
            T.plan("l3a.s")
            V.plan("l3a.st")
            T.plan("l3a.y0")
            V.plan("l3a.y0")
            turn_plan("l3a.y")
            T.plan("l3a.p")
            V.plan("l3a.ss")
            V.plan("l3a.yn")
            turn_plan("l3a.yn")
            T.plan("l3a.fc")
            V.plan("l3a.fc")
            T.plan("l3a.cp")
            V.plan("l3a.x")
            s = small4
            n8 = 8 * P
            kx, qx, st8, dx = (probs[:, 0, 0:n8], probs[:, 0, n8:], probs[:, 1, 0:n8], probs[:, 1, n8:])
            ux = sbq[:, 0:n8]
            wide_k, wide_v, wide_q = keysT[:, 0:n8], keysT[:, n8:], shared[:, n8:]
            G.plan("l3a.rstd", "l3a.sel", "l3a.rs")

            @on("pe")
            def _(pe):
                start_tensor(pe, tag)
                pe.wait_ge(V.sem, V.at("l3a.xn.T"))
                loaded(pe, "w_c")
                pe.wait_ge(G.sem, G.at("l3a.wide"))
                mm(ps[0:32, 6, 0:P], at["w_c.m1"], xnT[:, :]).then_inc(T.sem, T.now("l3a.m1"))
                for j in range(8):
                    o, b = (j % 4) * P, j // 4
                    mm(ps[:, b, o:o + P], wide_k[:, j * P:(j + 1) * P], xnT[:, :])
                    mm(ps[:, 2 + b, o:o + P], wide_v[:, j * P:(j + 1) * P], xnT[:, :])
                    m = mm(ps[:, 4 + b, o:o + P], wide_q[:, j * P:(j + 1) * P], xnT[:, :])
                m.then_inc(T.sem, T.now("l3a.kvq"))
                pe.wait_ge(V.sem, V.at("l3a.m1"))
                mm(ps[0:H, 7, 0:P], at["w_c.m2"][0:32, :], tA[0:32, :]).then_inc(T.sem, T.now("l3a.z"))
                pe.wait_ge(V.sem, V.at("l3a.s"))
                pe.wait_ge(G.sem, G.at("l3a.sel"))
                for j in range(8):
                    m = mm(ps[:, 6 + j // 4, (j % 4) * P:(j % 4 + 1) * P],
                           probsT[0:H, j // 4, (j % 4) * P:(j % 4 + 1) * P], tC[0:H, :])
                m.then_inc(T.sem, T.now("l3a.s"))
                pe.wait_ge(V.sem, V.at("l3a.st"))
                for j in range(8):
                    m = mm(ps[:, 0, 16 * j:16 * j + 16], st8[:, j * P:(j + 1) * P], at["gather"])
                m.then_inc(T.sem, T.now("l3a.y0"))
                turn_tensor(pe, "l3a.y", tA[:, :], "l3a.y0", 5)
                pe.wait_ge(V.sem, V.at("l3a.y.T"))
                mm(ps[:, 4, 0:P], tB[:, :], at["w_c.p"]).then_inc(T.sem, T.now("l3a.p"))
                turn_tensor(pe, "l3a.yn", tE[:, :], "l3a.yn", 5)
                pe.wait_ge(V.sem, V.at("l3a.yn.T"))
                for c in range(4):
                    m = mm(ps[:, 6, c * P:(c + 1) * P], at["w_c.fc"][:, c * P:(c + 1) * P], tF[:, :])
                m.then_inc(T.sem, T.now("l3a.fc"))
                pe.wait_ge(V.sem, V.at("l3a.fc"))
                for c in range(4):
                    m = mm(ps[:, 7, 0:P], probs[:, 0, c * P:(c + 1) * P], at["w_c.cp"][:, c * P:(c + 1) * P], c == 0, c == 3)
                m.then_inc(T.sem, T.now("l3a.cp"))

            @on("dve")
            def _(dve):
                dve.wait_ge(V.sem, V.at("l3x.x"))
                start_vector(dve, tag, None)
                dve.wait_ge(T.sem, T.at("l3a.m1"))
                nc.vector.tensor_scalar(tA[0:32, :], ps[0:32, 6, 0:P], at["l3a_bm1"][0:32, :], 0.0, ALU.add,
                                        ALU.max).then_inc(V.sem, V.now("l3a.m1"))
                nc.vector.tensor_scalar(s[0:H, 0:1], at["l3a_bm2"][0:H, :], -1.0, None,
                                        ALU.mult).then_inc(V.sem, V.now("l3a.nb"))
                dve.wait_ge(A.sem, A.at("l3a.z"))
                vl(dve, nc.vector.tensor_scalar(tD[0:H, :], tB[0:H, :], 1.0, None, ALU.add))
                nc.vector.reciprocal(tC[0:H, :], tD[0:H, :]).then_inc(V.sem, V.now("l3a.s"))
                dve.wait_ge(T.sem, T.at("l3a.s"))
                dve.wait_ge(A.sem, A.at("l3a.k"))
                kv = ps[:, 2:4, :].rearrange("p a b -> p (a b)")
                sp8 = ps[:, 6:8, :].rearrange("p a b -> p (a b)")
                vl(dve, nc.vector.tensor_tensor(ux, kx, kv, ALU.mult))
                nc.vector.tensor_tensor(ux, ux, sp8, ALU.mult)
                vl(dve, nc.vector.tensor_scalar(dx, sp8, -1.0, 1.0, ALU.mult, ALU.add))
                vl(dve, nc.vector.memset(dx.rearrange("p (j t) -> p j t", t=P)[:, :, 0:1], 0.0))
                vl(dve, nc.vector.tensor_tensor_scan(st8, dx, ux, 0.0, ALU.mult, ALU.add))
                dve.wait_ge(A.sem, A.at("l3a.q"))
                nc.vector.tensor_tensor(st8, st8, qx, ALU.mult).then_inc(V.sem, V.now("l3a.st"))
                dve.wait_ge(T.sem, T.at("l3a.y0"))
                nc.vector.tensor_copy(tA[:, :], ps[:, 0, 0:P]).then_inc(V.sem, V.now("l3a.y0"))
                turn_vector(dve, "l3a.y", tB, 5)
                dve.wait_ge(T.sem, T.at("l3a.p"))
                vl(dve, nc.vector.tensor_copy(tC[:, :], ps[:, 4, 0:P]))
                vl(dve, nc.vector.tensor_tensor_reduce(tD[:, :], tC[:, :], tC[:, :], 1.0, 0.0, ALU.mult, ALU.add, s[:, 1:2]))
                nc.vector.tensor_scalar(mv[:, 2:3], s[:, 1:2], 1.0 / P, float(np.finfo(np.float32).eps), ALU.mult,
                                        ALU.add).then_inc(V.sem, V.now("l3a.ss"))
                dve.wait_ge(G.sem, G.at("l3a.rs"))
                nc.vector.tensor_scalar(tE[:, :], tC[:, :], mv[:, 3:4], None, ALU.mult).then_inc(V.sem, V.now("l3a.yn"))
                nc.vector.tensor_tensor(xb[:, :], tC[:, :], xs[:, x_at[tag], :], ALU.add)
                turn_vector(dve, "l3a.yn", tF, 5)
                dve.wait_ge(T.sem, T.at("l3a.fc"))
                vl(dve, nc.vector.tensor_scalar(probs[:, 0, BANK:2 * BANK], ps[:, 6, :], 0.0, None, ALU.max))
                nc.vector.tensor_tensor(probs[:, 0, 0:BANK], probs[:, 0, BANK:2 * BANK], probs[:, 0, BANK:2 * BANK],
                                        ALU.mult).then_inc(V.sem, V.now("l3a.fc"))
                end_vector(dve, tag, ps[:, 7, 0:P], xb[:, :], "l3a.cp")

            @on("act")
            def _(act):
                act.wait_ge(T.sem, T.at("l3a.kvq"))
                nc.scalar.copy(kx, ps[:, 0:2, :].rearrange("p a b -> p (a b)")).then_inc(A.sem, A.now("l3a.k"))
                nc.scalar.copy(qx, ps[:, 4:6, :].rearrange("p a b -> p (a b)")).then_inc(A.sem, A.now("l3a.q"))
                act.wait_ge(T.sem, T.at("l3a.z"))
                act.wait_ge(V.sem, V.at("l3a.nb"))
                nc.scalar.activation(tB[0:H, :], ps[0:H, 7, 0:P], ACT.Exp, bias=s[0:H, 0:1],
                                     scale=-1.0).then_inc(A.sem, A.now("l3a.z"))

            @on("pool")
            def _(pool):
                norm_gpsimd(pool, tag)
                nc.gpsimd.tensor_copy(probsT[0:H, 0:2, :].rearrange("p a (h n) -> p (a h) n", n=64),
                                      bc(ident[0:H, 0:H], 2, [H, H, 64])).then_inc(G.sem, G.now("l3a.sel"))
                pool.wait_ge(V.sem, V.at("l3a.ss"))
                nc.gpsimd.tensor_tensor(mv[:, 3:4], mv[:, 2:3], half[:, 0:1], ALU.pow).then_inc(G.sem, G.now("l3a.rs"))

        def l3f():
            tag = "l3f"
            start_plan(tag)
            T.plan("l3f.conf")
            V.plan("l3f.conf")
            A.plan("l3f.conf")
            V.plan("l3f.bm")
            A.plan("l3f.w")
            V.plan("l3f.comb")
            moe_plan(tag)
            V.plan("l3f.x")
            s = small4

            @on("pe")
            def _(pe):
                start_tensor(pe, tag)
                pe.wait_ge(V.sem, V.at("l3f.xn.T"))
                mm(ps[:, 7, 0:E], xnT[:, :], at["w_c.conf"]).then_inc(T.sem, T.now("l3f.conf"))
                loaded(pe, "w_l3f")
                loaded(pe, "w_l3d")
                moe_tensor(pe, tag, at["w_l3f.gate"], at["w_l3f.up"], at["w_l3d.down"], xnT[:, :], 4)

            @on("dve")
            def _(dve):
                dve.wait_ge(V.sem, V.at("l3a.x"))
                start_vector(dve, tag, None)
                dve.wait_ge(T.sem, T.at("l3f.conf"))
                nc.vector.tensor_tensor(s[:, 0:8], ps[:, 7, 0:E], at["conf_b"], ALU.add).then_inc(V.sem, V.now("l3f.conf"))
                dve.wait_ge(A.sem, A.at("l3f.conf"))
                vl(dve, nc.vector.tensor_scalar(s[:, 8:16], s[:, 8:16], 1.0, None, ALU.add))
                vl(dve, nc.vector.reciprocal(s[:, 8:16], s[:, 8:16]))
                vl(dve, nc.vector.tensor_tensor(s[:, 16:24], s[:, 8:16], at["wealth"], ALU.mult))
                nc.vector.tensor_reduce(s[:, 40:41], s[:, 16:24], AX.X, ALU.max, negate=True).then_inc(V.sem, V.now("l3f.bm"))
                top2(dve, s[:, 16:24], s[:, 24:32])
                dve.wait_ge(A.sem, A.at("l3f.w"))
                vl(dve, nc.vector.tensor_tensor_reduce(s[:, 32:40], s[:, 0:8], s[:, 24:32], 1.0, 0.0, ALU.mult, ALU.add,
                                                       s[:, 41:42]))
                vl(dve, nc.vector.reciprocal(s[:, 42:43], s[:, 41:42]))
                nc.vector.tensor_scalar(s[:, 48:56], s[:, 32:40], s[:, 42:43], None, ALU.mult).then_inc(
                    V.sem, V.now("l3f.comb"))
                dve.wait_ge(V.sem, V.at("l3f.comb"))
                moe_vector(dve, tag, True)
                mix_vector(dve, tag, s[:, 48:56], xs[:, x_at[tag], :], False)

            @on("act")
            def _(act):
                act.wait_ge(V.sem, V.at("l3f.conf"))
                nc.scalar.activation(s[:, 8:16], s[:, 0:8], ACT.Exp, scale=-1.0).then_inc(A.sem, A.now("l3f.conf"))
                act.wait_ge(V.sem, V.at("l3f.bm"))
                nc.scalar.activation(s[:, 0:8], s[:, 16:24], ACT.Exp, bias=s[:, 40:41]).then_inc(A.sem, A.now("l3f.w"))
                moe_scalar(act, tag, ACT.Silu, None)

            @on("pool")
            def _(pool):
                norm_gpsimd(pool, tag)

        def hidden():
            V.plan("mask.any")
            T.plan("mask.any")
            V.plan("mask")

            @on("pe")
            def _(pe):
                pe.wait_ge(V.sem, V.at("mask.any"))
                mm(ps[:, 7, 300:301], one[0:1, :], seen[0:1, 1:2]).then_inc(T.sem, T.now("mask.any"))

            @on("dve")
            def _(dve):
                loaded(dve, "mask")
                dve.wait_ge(G.sem, G.at("const"))
                z = probsT[0:1, :, :].rearrange("p a b -> p (a b)")
                vl(dve, nc.vector.tensor_scalar(z, keysT[0:1, :].bitcast(I32), 0.0, None, ALU.is_equal))
                vl(dve, nc.vector.tensor_reduce(seen[0:1, 0:1], z, AX.X, ALU.min))
                nc.vector.tensor_scalar(seen[0:1, 1:2], seen[0:1, 0:1], -1.0, 1.0, ALU.mult,
                                        ALU.add).then_inc(V.sem, V.now("mask.any"))
                dve.wait_ge(V.sem, V.at("mask.any"))
                nc.vector.tensor_scalar(maskb[:, :], z, seen[0:1, 1:2], HIDDEN, ALU.mult, ALU.mult)
                dve.wait_ge(T.sem, T.at("mask.any"))
                nc.vector.tensor_copy(seen[:, 2:3], ps[:, 7, 300:301]).then_inc(V.sem, V.now("mask"))

        def distance():
            T.plan("d.1", "d.2", "d.3")
            V.plan("d.1", "d.2", "d.3")

            @on("pe")
            def _(pe):
                loaded(pe, "w_a")
                pe.wait_ge(V.sem, V.at("mask"))
                mm(ps[0:4, 7, 0:64], at["w_coeff"][0:64, :], at["ramp"][0:64, :]).then_inc(T.sem, T.now("d.1"))
                pe.wait_ge(V.sem, V.at("d.1"))
                mm(ps[0:64, 7, 64:64 + H], tC[0:4, 0:64], at["w_wpos"][0:4, :]).then_inc(T.sem, T.now("d.2"))
                pe.wait_ge(V.sem, V.at("d.2"))
                mm(ps[0:H, 7, 128:128 + 255], tD[0:64, 0:H], at["dist"][0:64, :]).then_inc(T.sem, T.now("d.3"))

            @on("dve")
            def _(dve):
                dve.wait_ge(T.sem, T.at("d.1"))
                nc.vector.tensor_copy(tC[0:4, 0:64], ps[0:4, 7, 0:64]).then_inc(V.sem, V.now("d.1"))
                dve.wait_ge(T.sem, T.at("d.2"))
                nc.vector.tensor_copy(tD[0:64, 0:H], ps[0:64, 7, 64:64 + H]).then_inc(V.sem, V.now("d.2"))
                dve.wait_ge(T.sem, T.at("d.3"))
                nc.vector.tensor_copy(dists[:, :], ps[0:H, 7, 128:128 + 255]).then_inc(V.sem, V.now("d.3"))

        paths = sbq[:, 0:3 * LEAVES].rearrange("p (n k) -> p n k", n=3)
        levels = sbq[:, 3 * LEAVES:3 * LEAVES + 2 * 3 * P].rearrange("p (a k) -> p a k", a=2)
        biases = shared[:, :]
        qheads = shared[:, 0:8 * P]
        dists = sb("dists", [H, 255])
        perm = sbq[:, 0:E * P]

        hidden()
        distance()
        l0x()
        l0a()
        l0f()
        cross("l1x", "l0f.x", lambda n: at["w_l1x_" + n], float(1.0 / np.sqrt(P)), True, at["l1x_bq"], at["l1x_bv"],
              at["l1x_bo"], "w_a")
        l1a()
        l1f()
        cross("l2x", "l1f.x", lambda n: at["w_b.l2x_" + n], float(1.0 / np.sqrt(8.0)), False, None, None,
              at["l2x_b"], "w_b")
        l2a()
        l2f()
        l3x()
        l3a()
        l3f()

        @on("sp")
        def _(sp):
            sp.wait_ge(V.sem, V.at("l3f.x"))
            nc.sync.dma_start(out, xs[:, 1 - x_at["l3f"], :]).then_inc(stored, 16)
            if dbg is not None:
                sp.wait_ge(dbg_stored, 16 * len(STAGES))
            sp.wait_ge(stored, 16)

        if dbg is not None:
            dbg_stored = sem("dbg_stored")
            orig = list(parts["pool"])
            parts["pool"] = orig[0:1]
            for k, (f, n) in enumerate(zip(orig[1:], STAGES)):
                def dump(pool, n=n, k=k):
                    pool.wait_ge(V.sem, V.at(n + ".x"))
                    nc.gpsimd.dma_start(dbg[k], xs[:, 1 - x_at[n], :]).then_inc(dbg_stored, 16)
                    pool.wait_ge(dbg_stored, 16 * (k + 1))
                parts["pool"] += [f, dump]
            for i, n in enumerate(STAGES[:-1]):
                pass

        block = ctx.enter_context(nc.Block())

        @block.tensor
        def _(pe):
            for part in parts["pe"]:
                part(pe)

        @block.vector
        def _(dve):
            for part in parts["dve"]:
                part(dve)

        @block.scalar
        def _(act):
            for part in parts["act"]:
                part(act)

        @block.gpsimd
        def _(pool):
            for part in parts["pool"]:
                part(pool)

        @block.sync
        def _(sp):
            for part in parts["sp"]:
                part(sp)




def constants():
    i = np.arange(P)
    f = np.float32
    c = {"ident": np.eye(P, dtype=f), "causal": np.where(i[None, :] <= i[:, None], 0.0, HIDDEN).astype(f)}
    freq = (f(1.0) / np.power(f(10000.0), np.arange(0, 8, 2, dtype=f))).astype(f)
    angle = (i.astype(f)[:, None] * freq[None, :]).astype(f)
    c["cos"] = np.tile(np.repeat(np.cos(angle), 2, axis=1), (1, H))
    sin = np.stack([-np.sin(angle), np.sin(angle)], axis=2).reshape(P, 8)
    c["sin"] = np.tile(sin, (1, H))
    c["tri"] = (i[:, None] <= i[None, :])
    c["iota1"] = np.tile(i[None, :] + 1.0, (P, 1))
    c["hm8"] = (i[:, None] // 8 == np.arange(H)[None, :])
    c["hm4"] = (i[:, None] // 4 == np.arange(H)[None, :])
    c["bm8"] = (i[:, None] // 8 == i[None, :] // 8)
    c["bm4"] = (i[:, None] // 4 == i[None, :] // 4)
    e = np.arange(E)
    c["before"] = np.tile((e[None, :] < e[:, None]).reshape(1, E * E), (P, 1))
    c["gather"] = ((i[:, None] // 64 == np.arange(16)[None, :] // 8) & (i[:, None] % 8 == np.arange(16)[None, :] % 8))
    c["hm32"] = ((i[:, None] % 32) // 8 == np.arange(4)[None, :])
    c["strip"] = ((np.arange(2 * P - 8)[None, :] == 120 + i[:, None] % 32) & (i[:, None] % 32 < 8))
    c["flip"] = (i[:, None] + i[None, :] == P - 1)
    r = np.arange(64)
    ramp = np.linspace(0.0, 1.0, 64).astype(f)
    lag = r[None, :] - r[:, None]
    c["ramp"] = np.concatenate([np.where(lag >= 0, ramp[np.clip(lag, 0, 63)], 0.0), np.zeros((64, 64))])
    far = (np.abs(np.arange(255) - 127).astype(f) / f(P - 1)).astype(f)
    step = np.clip(np.round(far * f(63)), 0, 63)
    c["dist"] = (i[:, None] == step[None, :])
    return np.concatenate([c[n].astype(f).reshape(P, w) for n, w in CONST], axis=1)


def packed(inputs):
    a = {k: np.asarray(v) for k, v in inputs.items()}

    def tall(m):
        n = m.shape[0] // P
        return m.reshape(n, P, -1).transpose(1, 0, 2).reshape(P, -1)

    def col(v, n=P):
        return np.concatenate([v.reshape(-1, 1), np.zeros((P - v.size, 1), v.dtype)]) if v.size < P else v.reshape(-1, P).T

    def pad(m):
        return np.concatenate([m, np.zeros((P - m.shape[0], m.shape[1]), m.dtype)])

    def side(parts, pack):
        got = [np.ascontiguousarray(p).reshape(P, -1) for p in parts]
        assert [g.shape[1] for g in got] == [w for _, w in pack], [(g.shape[1], n, w) for g, (n, w) in zip(got, pack)]
        return np.ascontiguousarray(np.concatenate(got, axis=1))

    def fourfold(m):
        return np.tile(m.reshape(-1, 4, 1, 32), (1, 1, 4, 1)).reshape(m.shape[0], 4 * P)

    ws = a["L0_xattn_w_sim"]
    d = {"const": constants()}
    d["x"] = a["x"].reshape(P, P)
    ctx = a["ctx_1024"].reshape(CTX, P)
    d["ctxT"] = np.ascontiguousarray(ctx.T)
    d["ctx"] = np.ascontiguousarray(ctx.reshape(KT_N, P, P).transpose(1, 0, 2))
    d["mask"] = a["mask_Bx1x1xS2_if1"].reshape(1, CTX)
    b1 = [a[f"L1_ffn_{t}_b1"].reshape(CH, P).T for t in "qkvf"]
    bq = a["L2_ffn_b_qkv"]
    d["cols"] = side([col(ws[P:2 * P]), col(ws[2 * P:]), col(a["L0_ffn_q_b"].reshape(H, 8)[:, :4].reshape(-1)),
                      col(a["L0_ffn_k_b"]), a["L0_ffn_b1"].reshape(16, P).T, fourfold(a["L1_xattn_bq"].reshape(1, P)).reshape(4, P).T, col(a["L1_xattn_bk"]),
                      np.concatenate(b1, axis=1), col(bq[0:P]), col(bq[P:2 * P]), a["L2_ffn_b_fc"].reshape(32, P).T,
                      col(a["L3_attn_bm1"]), col(a["L3_attn_bm2"])], COLS)
    rows = [a["L0_xattn_b_sim"], ws[0:P], a["L0_xattn_b_qv"], a["L0_attn_bq"], a["L0_attn_bk"], a["L0_attn_bv"],
            a["L0_attn_bo"], a["L0_ffn_v_b"], a["L0_ffn_o_b"], a["L0_ffn_router_b"], a["L1_xattn_bv"], a["L1_xattn_bo"],
            a["L1_attn_proj_bias"], a["L2_xattn_b_o"], a["L2_ffn_ln1_scale"], a["L2_ffn_ln1_bias"], bq[2 * P:],
            a["L2_ffn_b_attnproj"], a["L2_ffn_ln2_scale"], a["L2_ffn_ln2_bias"], a["L2_ffn_b_gate"],
            a["L3_xattn_gamma"], a["L3_ffn_conf_b"], a["L3_ffn_wealth"]]
    assert [r.size for r in rows] == [w for _, w in ROWS]
    d["rows"] = np.concatenate([r.reshape(-1) for r in rows])
    d["w_a"] = side([tall(a["L0_xattn_W_qv"]), a["L0_attn_Wq"], a["L0_attn_Wk"], a["L0_attn_Wv"], a["L0_attn_Wo"],
                     a["L0_ffn_q_w"].reshape(P, H, 8)[:, :, :4], a["L0_ffn_k_w"], a["L0_ffn_v_w"], a["L0_ffn_o_w"], a["L0_ffn_router_w"],
                     fourfold(a["L1_xattn_Wq"].T), a["L1_xattn_Wk"].T, a["L1_xattn_Wv"].T, a["L1_xattn_Wo"].T,
                     a["L1_attn_qkv_weight"].T, a["L1_attn_proj_weight"].T, pad(a["L2_attn_coeffs"][:, :64].T),
                     pad(a["L2_attn_Wpos"].T)], W_A)
    d["w_l0f"] = side([a["L0_ffn_w1"].transpose(1, 0, 2).reshape(P, -1), tall(a["L0_ffn_w2"].reshape(-1, P))], W_L0F)
    d["l0f_b2"] = a["L0_ffn_b2"].reshape(-1)
    for t in "qkvf":
        d["w_" + t] = side([a[f"L1_ffn_{t}_w1"].transpose(1, 0, 2).reshape(P, -1),
                            tall(a[f"L1_ffn_{t}_w2"].reshape(-1, P))], W_FFF)
    d["node"] = np.concatenate([a[f"L1_ffn_{t}_nw"].T for t in "qkvf"], axis=1)
    d["nbias"] = np.concatenate([a[f"L1_ffn_{t}_nb"] for t in "qkvf"])
    d["ffb2"] = np.concatenate([tall(a[f"L1_ffn_{t}_b2"]) for t in "qkvf"], axis=1)
    wkv = a["L3_xattn_w_kv"]
    d["w_b"] = side([fourfold(a["L2_xattn_W_q"]), a["L2_xattn_W_k"], a["L2_xattn_W_v"], a["L2_xattn_W_o"], a["L2_attn_Wqkv"].T,
                     a["L2_attn_Wout"].T, a["L2_ffn_w_qkv"], a["L2_ffn_w_attnproj"], a["L2_ffn_w_gate"],
                     a["L3_xattn_w_q"], tall(np.ascontiguousarray(wkv[:, :8 * P].T)), tall(np.ascontiguousarray(wkv[:, 8 * P:].T)),
                     tall(a["L3_xattn_w_out1"]), a["L3_xattn_w_out2"]], W_B)
    d["w_c"] = side([a["L3_attn_Wq"].T, a["L3_attn_Wk"].T, a["L3_attn_Wv"].T, a["L3_attn_Wm1"].T,
                     pad(a["L3_attn_Wm2"].T), a["L3_attn_Wproj"].T, a["L3_attn_Wfc"].T,
                     tall(np.ascontiguousarray(a["L3_attn_Wcp"].T)), a["L3_ffn_conf_w"].T], W_C)
    d["w_l2f"] = side([a["L2_ffn_w_fc"].transpose(1, 0, 2).reshape(P, -1), tall(a["L2_ffn_w_fcproj"].reshape(-1, P))],
                      W_L2F)
    d["l2f_b2"] = a["L2_ffn_b_fcproj"].reshape(-1)
    d["w_l3f"] = side([a["L3_ffn_gate_w"].transpose(2, 0, 1).reshape(P, -1),
                       a["L3_ffn_up_w"].transpose(2, 0, 1).reshape(P, -1)], W_L3F)
    d["w_l3d"] = side([tall(np.ascontiguousarray(a["L3_ffn_down_w"].transpose(0, 2, 1)).reshape(-1, P))], W_L3D)
    return {k: np.ascontiguousarray(v) for k, v in d.items()}


def kernel(**inputs):
    from concourse import bacc
    from concourse.bass_utils import run_bass_kernel_spmd

    arrays = packed(inputs)
    nc = bacc.Bacc("TRN2", target_bir_lowering=False, num_devices=1)
    dram = {}
    for n, v in arrays.items():
        dram[n] = nc.dram_tensor("in_" + n, v.shape, mybir.dt.from_np(v.dtype), kind="ExternalInput").ap()
    out = nc.dram_tensor("out_0", (P, P), F32, kind="ExternalOutput").ap()
    scratch = nc.dram_tensor("distance_rows", (H, 255), F32).ap()
    dbg = nc.dram_tensor("dbg", (len(STAGES), P, P), F32, kind="ExternalOutput").ap() if DEBUG else None
    build(nc, dram, out, scratch, dbg)
    r = run_bass_kernel_spmd(nc, [{"in_" + n: v for n, v in arrays.items()}], core_ids=[0])
    return r.results[0]["out_0"].reshape(1, P, P)
```

```python
from contextlib import ExitStack

import numpy as np

import concourse.bass as bass
from concourse import mybir

F32 = mybir.dt.float32
BF16 = mybir.dt.bfloat16
F32R = mybir.dt.float32r
I32 = mybir.dt.int32
ALU = mybir.AluOpType
ACT = mybir.ActivationFunctionType
AX = mybir.AxisListType

P = 128
CTX = 2048
KT_N = CTX // P
BANK = 512
NB = CTX // BANK
H = 16
E = 8
LEAVES = 256
NODES = LEAVES - 1
DEPTH = 8
LW = 16
LEAF1 = LW * P + LW
LEAF = LEAF1 + LW * P + P
WARM = 30
EPS = 1e-5
HIDDEN = -2.0 ** 99

FIRST = [("ident", P)]
CONST = [("causal", P), ("cos", P), ("sin", P), ("tri", P), ("iota1", P), ("hm8", H),
         ("hm4", H), ("bm8", P), ("bm4", P), ("before", E * E), ("gather", 15 * 16),
         ("flip", P), ("hm32", 4), ("hm32m", 4), ("strip", 2 * P - 8),
         ("ramp", 64), ("dist", 255), ("leaf", LEAVES),
         ("place", 224), ("places", 224)]
COLS = [("w2", 1), ("w3", 1), ("l0f_qb", 1), ("l0f_kb", 1), ("l0f_b1", 16), ("l1x_bq", 4), ("l1x_bk", 1),
        ("l1x_bv", 1),
        ("l2f_bq", 1), ("l2f_bk", 1), ("l2f_bfc", 32), ("l3a_bm1", 1), ("l3a_bm2", 1)]
ROWS = [("b_sim", 1), ("w1", P), ("l0x_b", P), ("l0a_bq", P), ("l0a_bk", P), ("l0a_bv", P), ("l0a_bo", P),
        ("l0f_vb", P), ("l0f_ob", P), ("l0f_rb", E), ("l1x_bo", P), ("l1a_b", P),
        ("l2x_b", P), ("ln1_s", P), ("ln1_b", P), ("l2f_bv", P), ("l2f_ap", P), ("ln2_s", P), ("ln2_b", P),
        ("l2f_gb", E), ("l3x_g", P), ("conf_b", E), ("wealth", E)]
W_A = [("l0x", 4 * P), ("l0a_q", P), ("l0a_k", P), ("l0a_v", P), ("l0a_o", P),
       ("l0f_q", 64), ("l0f_k", 64), ("l0f_v", P), ("l0f_o", P), ("l0f_r", E),
       ("l1x_q", 4 * P), ("l1x_k", P), ("l1x_v", P), ("l1x_o", P),
       ("l1a_qkv", 3 * P), ("l1a_p", P), ("coeff", 4), ("wpos", H)]
W_L0F = [("w1", E * 2 * P), ("w2", E * 2 * P)]
W_B = [("l2x_q", 4 * P), ("l2x_k", P), ("l2x_v", P), ("l2x_o", P), ("l2a_qkv", 3 * P), ("l2a_o", P),
       ("l2f_qkv", 3 * P), ("l2f_p", P), ("l2f_g", E), ("l3x_q", 8 * P), ("l3x_k", 8 * P), ("l3x_v", 8 * P),
       ("l3x_o1", 8 * P), ("l3x_o2", P)]
W_C = [("q", P), ("k", P), ("v", P), ("m1", 32), ("m2", H), ("p", P), ("fc", 4 * P), ("cp", 4 * P), ("conf", E)]
W_L2F = [("w1", E * 4 * P), ("w2", E * 4 * P)]
W_L3F = [("gate", E * 4 * P), ("up", E * 4 * P)]
W_L3D = [("down", E * 4 * P)]
PACKS = {"first": FIRST, "const": CONST, "cols": COLS, "w_a": W_A, "w_l0f": W_L0F, "w_b": W_B, "w_c": W_C,
         "w_l2f": W_L2F, "w_l3f": W_L3F, "w_l3d": W_L3D}
STAGES = ("l0x", "l0a", "l0f", "l1x", "l1a", "l1f", "l2x", "l2a", "l2f", "l3x", "l3a", "l3f")


def width(pack):
    return sum(n for _, n in pack)


class Steps:

    def __init__(self, sem):
        self.sem, self.order, self.value, self.taken = sem, [], {}, 0

    def plan(self, *names):
        for n in names:
            assert n not in self.value, n
            self.order.append(n)
            self.value[n] = len(self.order)

    def at(self, name):
        return self.value[name]

    def now(self, name):
        assert self.order[self.taken] == name, (self.order[self.taken], name)
        self.taken += 1
        return 1


def build(nc, dram, out, scratch):
    ctx = ExitStack()
    with ctx:
        def sb(name, shape, dt=F32):
            return ctx.enter_context(nc.sbuf_tensor(name, shape, dt))

        def sem(name):
            return ctx.enter_context(nc.semaphore(name))

        ps = ctx.enter_context(nc.psum_tensor("banks", [P, 8, BANK], F32))
        tiles = {n: sb("p_" + n, [P, width(PACKS[n])]) for n in ("first", "const", "cols", "w_a")}
        rows_t = sb("p_rows", [P, width(ROWS)])
        REG = 8192
        region_at = -(-nc.sbuf_base // 32) * 32
        region = sb("region", [P, 3 * REG])
        ctxT = sb("ctxT", [P, CTX])
        keysT = sb("keysT", [P, CTX])
        values_at = -(-nc.sbuf_base // 32) * 32
        values_t = sb("values", [P, CTX + 32])
        probs = sb("probs", [P, 2, CTX])
        probsT_at = -(-nc.sbuf_base // 32) * 32
        probsT = sb("probsT", [P, 4, BANK])
        xs = sb("xs", [P, 2, P])
        xb = sb("xb", [P, P])
        xn = sb("xn", [P, P])
        xnT = sb("xnT", [P, P])
        tA = sb("tA", [P, P])
        tB = sb("tB", [P, P])
        tC = sb("tC", [P, P])
        tD = sb("tD", [P, P])
        tE = sb("tE", [P, P])
        tF = sb("tF", [P, P])
        tG = sb("tG", [P, P])
        st = sb("st", [P, 6])
        mv = sb("mv", [P, 4])
        half = sb("half", [P, 2])
        one = sb("one", [P, P])
        identb = sb("identb", [P, P], BF16)
        leaf_at = sb("leaf_at", [P, 4])
        leaf_no = sb("leaf_no", [P, 4], mybir.dt.uint32)
        causalb = sb("causalb", [P, P], BF16)
        small = sb("small", [P, 64])
        small2 = sb("small2", [P, 64])
        small3 = sb("small3", [P, 64])
        small4 = sb("small4", [P, 64])
        seen = sb("seen", [P, 4])
        nmax = sb("nmax", [P, H])
        wsum = sb("wsum", [P, NB, H])
        vaug = sb("vaug", [P, H * 9 + 32])
        values = values_t[:, 0:CTX].rearrange("p (t n) -> p t n", n=P)
        shared = sb("shared", [P, 16 * P])
        nodew = shared[:, 0:4 * NODES]
        nbias = shared[:, 8 * P:8 * P + 4 * NODES]
        U = ps[:, 6, :]
        at = {}
        for n, pack in (*((n, PACKS[n]) for n in tiles), ("rows", ROWS)):
            base = rows_t if n == "rows" else tiles[n]
            o = 0
            for name, w in pack:
                at[name if n != "w_a" else "w_" + name] = base[:, o:o + w]
                o += w

        def inside(base, pack):
            o = base
            for name, w in PACKS[pack]:
                at[pack + "." + name] = region[:, o:o + w]
                o += w
            return o

        leaves = {n: region[:, o:o + LEAF] for n, o in (("q", 0), ("v", LEAF), ("k", 2 * REG), ("f", 0))}
        w_b_at = 2 * REG - width(W_B) - width(W_C)
        assert w_b_at >= max(2 * LEAF, REG)
        inside(2 * REG, "w_l0f")
        inside(0, "w_l2f")
        inside(inside(w_b_at, "w_b"), "w_c")
        inside(0, "w_l3f")
        inside(2 * REG, "w_l3d")
        sbq_at = -(-nc.sbuf_base // 32) * 32
        sbq = sb("sbq", [P, CTX])

        def over(name, shape, offset):
            return nc.alloc_sbuf_tensor_at(name, shape, F32R, offset=offset)

        keys_r = {"l1x": over("keys_l1x", [P, 4, CTX], region_at + 4 * REG),
                  "l2x": over("keys_l2x", [P, 4, CTX], region_at + 8 * REG)}
        query_r = over("query_r", [P, CTX], sbq_at)
        query_lo = over("query_lo", [P, CTX], region_at + 8 * REG)
        ctx_hi = over("ctx_hi", [P, CTX], region_at + 8 * REG + 4 * CTX)
        ctx_lo = over("ctx_lo", [P, CTX], region_at + 8 * REG + 8 * CTX)
        rows_hi = over("rows_hi", [P, CTX], probsT_at)
        rows_lo = over("rows_lo", [P, CTX], values_at)
        weights_hi = over("weights_hi", [P, KT_N, 2, P], region_at)
        weights_lo = over("weights_lo", [P, KT_N, 2, P], region_at + 4 * 2 * CTX)
        w_vo = region[:, 2 * REG + 3 * CTX:3 * REG]
        b2rows = sbq[:, 8 * P:]
        ident = at["ident"]

        T, V, A, G = (Steps(sem(n)) for n in ("tensor_steps", "vector_steps", "scalar_steps", "gpsimd_steps"))
        v_link, a_link, g_link = sem("vector_link"), sem("scalar_link"), sem("gpsimd_link")
        loads = {n: sem("loaded_" + n) for n in
                 ("x", "first", "const", "cols", "rows", "w_a", "ctxT", "ctx", "mask", "w_l0f", "l0f_b2", "node",
                  *("leaf1_" + t for t in "qkvf"),
                  *("leaf2_" + t for t in "qkvf"), "w_b", "w_c", "w_l2f", "l2f_b2", "w_l3f", "w_l3d", "ctx2", "bias", "keys_l1x", "keys_l2x")}
        load_n = {}
        stored = sem("stored")
        bias_out = sem("bias_stored")
        linked = {"v": 0, "a": 0, "g": 0}

        def vl(dve, ins):
            linked["v"] += 1
            ins.then_inc(v_link, 1)
            dve.wait_ge(v_link, linked["v"])

        def al(act, ins):
            linked["a"] += 1
            ins.then_inc(a_link, 1)
            act.wait_ge(a_link, linked["a"])

        def gl(pool, ins):
            linked["g"] += 1
            ins.then_inc(g_link, 1)
            pool.wait_ge(g_link, linked["g"])

        parts = {"pe": [], "dve": [], "act": [], "pool": [], "sp": []}

        def on(engine):
            def add(f):
                parts[engine].append(f)
                return f
            return add

        def mm(o, lhsT, rhs, start=True, stop=True):
            return nc.tensor.matmul(o, lhsT, rhs, start=start, stop=stop)

        def tr(o, i, n=P):
            return nc.tensor.transpose(o, i, ident[0:n, 0:n])

        def bc(ap, axis, shape):
            return ap.unsqueeze(axis).broadcast_to(shape)

        x_at = {n: i % 2 for i, n in enumerate(STAGES)}

        def stack_keys(sp, tag, high):
            sp.wait_ge(A.sem, A.at((tag, "k", 3)))
            sp.wait_ge(G.sem, G.at((tag, "low")))
            for t in range(4):
                for part in range(3 if tag == "l1x" else 4):
                    src = (high if part < 2 else keysT[:, :])[32 * t:32 * t + 32, :]
                    load("keys_" + tag, keys_r[tag][32 * part:32 * part + 32, t, :].bitcast(F32), src)
                if tag == "l1x":
                    if t:
                        load("keys_" + tag, keys_r[tag][96:97, t, :].bitcast(F32), keys_r[tag][96:97, 0, :].bitcast(F32))
                    load("keys_" + tag, keys_r[tag][97:128, t, :].bitcast(F32), keysT[1:32, :])

        def load(name, dst, src):
            load_n[name] = load_n.get(name, 0) + 16
            nc.sync.dma_start(dst, src).then_inc(loads[name], 16)

        def loaded(eng, name):
            eng.wait_ge(loads[name], {"node": 32, "keys_l1x": 19 * 16, "keys_l2x": 256}.get(name, 16))

        @on("sp")
        def _(sp):
            load("x", xs[:, 0, :], dram["x"])
            load("first", tiles["first"][:, :], dram["first"])
            load("mask", keysT[96:97, :].bitcast(I32), dram["mask"])
            load("cols", tiles["cols"][:, :], dram["cols"])
            load("ctxT", ctxT[:, :], dram["ctxT"])
            load("rows", rows_t[:, :], dram["rows"].partition_broadcast(P))
            load("ctx", values, dram["ctx"])
            load("w_a", tiles["w_a"][:, :], dram["w_a"])
            load("const", tiles["const"][:, :], dram["const"])
            load("w_l0f", region[:, 2 * REG:2 * REG + width(W_L0F)], dram["w_l0f"])
            load("l0f_b2", b2rows, dram["l0f_b2"].partition_broadcast(P))
            sp.wait_ge(V.sem, V.at("d.3"))
            nc.sync.dma_start(scratch, dists[:, :]).then_inc(bias_out, 16)
            stack_keys(sp, "l1x", shared[:, :])
            loaded(sp, "keys_l1x")
            load("node", nodew, dram["node"])
            load("node", nbias, dram["nbias"].partition_broadcast(P))
            sp.wait_ge(V.sem, V.at("l1x.o"))
            load("w_b", region[:, w_b_at:w_b_at + width(W_B)], dram["w_b"])
            load("w_c", region[:, w_b_at + width(W_B):2 * REG], dram["w_c"])
            sp.wait_ge(T.sem, T.at(("o", "k")))
            stack_keys(sp, "l2x", probsT[:, :, :].rearrange("p a b -> p (a b)"))
            sp.wait_ge(T.sem, T.at(("o", "f")))
            load("w_l2f", region[:, 0:REG], dram["w_l2f"])
            sp.wait_ge(bias_out, 16)
            sp.wait_ge(V.sem, V.at("l1f.x"))
            hankel = bass.AP(scratch.tensor, 0, [[1, P], [255, H], [1, P]])
            load("bias", biases.rearrange("p (h t) -> p h t", h=H), hankel)
            sp.wait_ge(V.sem, V.at("l2x.o"))
            load("ctx2", values[:, :, 0:P], dram["ctx"])
            load("l2f_b2", b2rows, dram["l2f_b2"].partition_broadcast(P))
            sp.wait_ge(T.sem, T.at(("l3x", "pv", H // 2 - 1, 3)))
            load("w_l3f", region[:, 0:REG], dram["w_l3f"])
            sp.wait_ge(T.sem, T.at(("l3x", "w", H - 1)))
            load("w_l3d", region[:, 2 * REG:2 * REG + width(W_L3D)], dram["w_l3d"])

        def norm_plan(tag):
            V.plan(tag + ".var", tag + ".xn")
            G.plan(tag + ".rstd")

        def norm_vector(dve, tag, src, eps=EPS):
            vl(dve, nc.vector.bn_stats(st[:, :], src))
            vl(dve, nc.vector.bn_aggr(mv[:, 0:2], st[:, :]))
            nc.vector.tensor_scalar(mv[:, 2:3], mv[:, 1:2], eps, None, ALU.add).then_inc(V.sem, V.now(tag + ".var"))
            dve.wait_ge(G.sem, G.at(tag + ".rstd"))
            nc.vector.tensor_scalar(xn[:, :], src, mv[:, 0:1], mv[:, 3:4], ALU.subtract,
                                    ALU.mult).then_inc(V.sem, V.now(tag + ".xn"))

        def norm_gpsimd(pool, tag):
            pool.wait_ge(V.sem, V.at(tag + ".var"))
            nc.gpsimd.tensor_tensor(mv[:, 3:4], mv[:, 2:3], half[:, 0:1], ALU.pow).then_inc(G.sem, G.now(tag + ".rstd"))

        def turn_plan(tag):
            T.plan(tag + ".turned")
            V.plan(tag + ".T")

        def turn_tensor(pe, tag, src, ready, bank=7, n=P):
            pe.wait_ge(V.sem, V.at(ready))
            tr(ps[0:n, bank, 0:P], src, P).then_inc(T.sem, T.now(tag + ".turned"))

        def turn_vector(dve, tag, dst, bank=7, n=P):
            dve.wait_ge(T.sem, T.at(tag + ".turned"))
            nc.vector.tensor_copy(dst[0:n, :], ps[0:n, bank, 0:P]).then_inc(V.sem, V.now(tag + ".T"))

        def start_vector(dve, tag, bias):
            norm_vector(dve, tag, xs[:, x_at[tag], :])
            if bias is not None:
                nc.vector.tensor_tensor(xb[:, :], xs[:, x_at[tag], :], bias, ALU.add)
            turn_vector(dve, tag + ".xn", xnT)

        def start_tensor(pe, tag):
            turn_tensor(pe, tag + ".xn", xn[:, :], tag + ".xn")

        def start_plan(tag):
            norm_plan(tag)
            turn_plan(tag + ".xn")

        def end_vector(dve, tag, src, base, ready):
            dve.wait_ge(T.sem, T.at(ready))
            nc.vector.tensor_tensor(xs[:, 1 - x_at[tag], :], src, base, ALU.add).then_inc(V.sem, V.now(tag + ".x"))

        RING = 5
        SCALAR_TURNS = 2
        QUARTERS = range(NB)

        def ring(h, b):
            return ps[:, (NB * h + b) % RING, :]

        def ctx_plan(tag, nh):
            T.plan(*((tag, "s", 0, b) for b in QUARTERS))
            V.plan((tag, "m", 0))
            for g in range(nh):
                more = g + 1 < nh
                if more:
                    T.plan(*((tag, "s", g + 1, b) for b in (0, 1)))
                T.plan((tag, "t", g, 0))
                if more:
                    T.plan((tag, "s", g + 1, 2))
                T.plan((tag, "t", g, 1))
                if more:
                    T.plan((tag, "s", g + 1, 3))
                if g:
                    T.plan((tag, "pv", g - 1, 2), (tag, "pv", g - 1, 3))
                T.plan((tag, "t", g, 2), (tag, "pv", g, 0), (tag, "t", g, 3), (tag, "pv", g, 1))
                A.plan(*((tag, "x", g, b) for b in QUARTERS), *((tag, "e", g, c) for c in range(SCALAR_TURNS)))
                if more:
                    V.plan((tag, "m", g + 1))
                if nh == H and g and g % 4 == 0:
                    V.plan((tag, "g", g // 4 - 1))
                V.plan(*((tag, "e", g, c) for c in range(SCALAR_TURNS, NB)))
            T.plan((tag, "pv", nh - 1, 2), (tag, "pv", nh - 1, 3))

        def evacuated(eng, tag, g, c):
            steps = A if c < SCALAR_TURNS else V
            eng.wait_ge(steps.sem, steps.at((tag, "e", g, c)))

        def ctx_tensor(pe, tag, nh, score, weigh_tile, last=None):
            def scores(h, *quarters):
                if h == nh:
                    return
                for b in quarters:
                    n = NB * h + b - RING
                    if n >= 0:
                        pe.wait_ge(A.sem, A.at((tag, "x", n // NB, n % NB)))
                    score(h, b).then_inc(T.sem, T.now((tag, "s", h, b)))

            def turn(g, c):
                pe.wait_ge(A.sem, A.at((tag, "x", g, c)))
                n = 4 * g + c - 2
                if n >= 0:
                    evacuated(pe, tag, n // 4, n % 4)
                for j in range(4):
                    m = tr(ps[:, 5 + c % 2, j * P:(j + 1) * P], probs[:, g % 2, (4 * c + j) * P:(4 * c + j + 1) * P])
                m.then_inc(T.sem, T.now((tag, "t", g, c)))

            def weigh(g, c):
                evacuated(pe, tag, g, c)
                for j in range(4):
                    m = weigh_tile(g, 4 * c + j, probsT[:, c, j * P:(j + 1) * P])
                m.then_inc(T.sem, T.now((tag, "pv", g, c)))

            scores(0, *QUARTERS)
            for g in range(nh):
                scores(g + 1, 0, 1)
                turn(g, 0)
                scores(g + 1, 2)
                turn(g, 1)
                scores(g + 1, 3)
                if g:
                    weigh(g - 1, 2)
                    weigh(g - 1, 3)
                if g == nh - 1 and last is not None:
                    last()
                turn(g, 2)
                weigh(g, 0)
                turn(g, 3)
                weigh(g, 1)
            weigh(nh - 1, 2)
            weigh(nh - 1, 3)

        def evacuate(eng, tag, g, c):
            eng.wait_ge(T.sem, T.at((tag, "t", g, c)))
            if g:
                eng.wait_ge(T.sem, T.at((tag, "pv", g - 1, c)))
            if c < SCALAR_TURNS:
                nc.scalar.copy(probsT[:, c, :], ps[:, 5 + c % 2, :]).then_inc(A.sem, A.now((tag, "e", g, c)))
            else:
                nc.vector.tensor_copy(probsT[:, c, :], ps[:, 5 + c % 2, :]).then_inc(V.sem, V.now((tag, "e", g, c)))

        def ctx_vector(dve, tag, nh, scale, between=None):
            def largest(h):
                for b in QUARTERS:
                    dve.wait_ge(T.sem, T.at((tag, "s", h, b)))
                    m = nc.vector.tensor_reduce(small[:, b:b + 1], ring(h, b), AX.X, ALU.max)
                vl(dve, m)
                vl(dve, nc.vector.tensor_reduce(small[:, 4:5], small[:, 0:NB], AX.X, ALU.max))
                nc.vector.tensor_scalar(nmax[:, h:h + 1], small[:, 4:5], scale, None, ALU.mult).then_inc(
                    V.sem, V.now((tag, "m", h)))

            largest(0)
            for g in range(nh):
                if g + 1 < nh:
                    largest(g + 1)
                if between is not None:
                    between(dve, g)
                for c in range(SCALAR_TURNS, NB):
                    evacuate(dve, tag, g, c)

        def ctx_scalar(act, tag, nh, scale):
            for g in range(nh):
                act.wait_ge(V.sem, V.at((tag, "m", g)))
                if g >= 2:
                    act.wait_ge(T.sem, T.at((tag, "t", g - 2, 3)))
                for b in QUARTERS:
                    nc.scalar.activation(probs[:, g % 2, b * BANK:(b + 1) * BANK], ring(g, b), ACT.Exp,
                                         bias=nmax[:, g:g + 1], scale=scale,
                                         accum_out=wsum[:, b, g:g + 1]).then_inc(A.sem, A.now((tag, "x", g, b)))
                for c in range(SCALAR_TURNS):
                    evacuate(act, tag, g, c)

        def sums_vector(dve, tag, nh, dst):
            dve.wait_ge(A.sem, A.at((tag, "x", nh - 1, NB - 1)))
            vl(dve, nc.vector.tensor_reduce(small3[:, 0:nh], wsum[:, :, 0:nh].rearrange("p b h -> p h b"), AX.X, ALU.add))
            return nc.vector.reciprocal(dst, small3[:, 0:nh])

        def self_plan(tag):
            T.plan(*((tag, "s", g) for g in range(4)))
            V.plan(*((tag, "sub", g) for g in range(4)))
            A.plan(*((tag, "exp", g) for g in range(4)))
            T.plan((tag, "t", 0), (tag, "t", 1), (tag, "t", 2), (tag, "t", 3), tag + ".U", tag + ".fold")
            V.plan((tag, "e", 0), (tag, "e", 2), tag + ".gathered", tag + ".o")
            A.plan((tag, "e", 1), (tag, "e", 3))

        def taken(eng, tag, g):
            steps = A if g % 2 else V
            eng.wait_ge(steps.sem, steps.at((tag, "e", g)))

        def self_tensor(pe, tag, n, qT, kbd, first=None):
            for g in range(4):
                if g == 2:
                    pe.wait_ge(G.sem, G.at(tag + ".spread"))
                mm(ps[:, g, :], qT[0:n, :], kbd[0:n, g * BANK:(g + 1) * BANK], first is None,
                   True).then_inc(T.sem, T.now((tag, "s", g)))
            for g in range(4):
                pe.wait_ge(A.sem, A.at((tag, "exp", g)))
                if g >= 2:
                    taken(pe, tag, g - 2)
                for j in range(4):
                    m = tr(ps[:, 4 + g % 2, j * P:(j + 1) * P], probs[:, 1, (4 * g + j) * P:(4 * g + j + 1) * P])
                m.then_inc(T.sem, T.now((tag, "t", g)))
            for g in range(4):
                taken(pe, tag, g)
                for j in range(4):
                    v = 9 * (4 * g + j)
                    m = mm(ps[32 * j:32 * j + 32, 6, g * P:(g + 1) * P], vaug[:, v:v + 32], probsT[:, g, j * P:(j + 1) * P])
            m.then_inc(T.sem, T.now(tag + ".U"))
            pe.wait_ge(V.sem, V.at(tag + ".gathered"))
            for bank, const in ((4, "place"), (5, "places")):
                for g in range(4):
                    m = mm(ps[:, bank, 0:P], at[const][:, 96 - 32 * g:224 - 32 * g], probs[:, 1, g * P:(g + 1) * P],
                           g == 0, g == 3)
            m.then_inc(T.sem, T.now(tag + ".fold"))

        def self_vector(dve, tag, scale):
            for g in range(4):
                dve.wait_ge(T.sem, T.at((tag, "s", g)))
                s = ps[:, g, :].rearrange("p (h t) -> p h t", h=4)
                m4 = nmax[:, 4 * g:4 * g + 4]
                if g % 2:
                    vl(dve, nc.vector.tensor_reduce(m4, s, AX.X, ALU.max))
                    nc.vector.tensor_scalar(m4, m4, -scale, None, ALU.mult).then_inc(V.sem, V.now((tag, "sub", g)))
                    continue
                vl(dve, nc.vector.tensor_reduce(m4, s, AX.X, ALU.max))
                nc.vector.tensor_tensor(probs[:, 1, g * BANK:(g + 1) * BANK].rearrange("p (h t) -> p h t", h=4), s,
                                        bc(nmax[:, 4 * g:4 * g + 4], 2, [P, 4, P]),
                                        ALU.subtract).then_inc(V.sem, V.now((tag, "sub", g)))
            for g in (0, 2):
                dve.wait_ge(T.sem, T.at((tag, "t", g)))
                nc.vector.tensor_copy(probsT[:, g, :], ps[:, 4 + g % 2, :]).then_inc(V.sem, V.now((tag, "e", g)))
            dve.wait_ge(T.sem, T.at(tag + ".U"))
            nc.vector.tensor_copy(probs[:, 1, 0:BANK], U).then_inc(V.sem, V.now(tag + ".gathered"))
            dve.wait_ge(T.sem, T.at(tag + ".fold"))
            vl(dve, nc.vector.reciprocal(tA[:, :], ps[:, 5, 0:P]))
            nc.vector.tensor_tensor(tB[:, :], ps[:, 4, 0:P], tA[:, :], ALU.mult).then_inc(V.sem, V.now(tag + ".o"))

        def self_scalar(act, tag, scale):
            for g in range(4):
                act.wait_ge(V.sem, V.at((tag, "sub", g)))
                p = probs[:, 1, g * BANK:(g + 1) * BANK]
                if g % 2:
                    for j in range(4):
                        h = 4 * g + j
                        m = nc.scalar.activation(probs[:, 1, h * P:(h + 1) * P], ps[:, g, j * P:(j + 1) * P], ACT.Exp,
                                                 scale=scale, bias=nmax[:, h:h + 1])
                else:
                    m = nc.scalar.activation(p, p, ACT.Exp, scale=scale)
                m.then_inc(A.sem, A.now((tag, "exp", g)))
            for g in (1, 3):
                act.wait_ge(T.sem, T.at((tag, "t", g)))
                nc.scalar.copy(probsT[:, g, :], ps[:, 4 + g % 2, :]).then_inc(A.sem, A.now((tag, "e", g)))

        def spread_heads(engine, dst, src, heads, n, i):
            hs = slice(8 * i, 8 * i + 8)
            return engine.tensor_tensor(dst.rearrange("p (h t) -> p h t", h=H)[0:n, hs], bc(src[0:n, :], 1, [n, 8, P]),
                                        bc(heads[0:n, hs], 2, [n, 8, P]), ALU.mult)

        def spread_gpsimd(pool, tag, heads, n):
            pool.wait_ge(V.sem, V.at(tag + ".keys"))
            spread_heads(nc.gpsimd, probs[:, 0, :], tD, heads, n, 1).then_inc(G.sem, G.now(tag + ".spread"))

        def top2(dve, vals, mask):
            mine, other = bc(vals, 2, [P, E, E]), bc(vals, 1, [P, E, E])
            v3 = small2[:, :].rearrange("p (a b) -> p a b", a=E)
            w3 = small3[:, :].rearrange("p (a b) -> p a b", a=E)
            nc.vector.tensor_tensor(w3, other, mine, ALU.is_gt)
            vl(dve, nc.vector.tensor_tensor(v3, other, mine, ALU.is_ge))
            vl(dve, nc.vector.tensor_tensor(small2[:, :], small2[:, :], at["before"], ALU.mult))
            vl(dve, nc.vector.tensor_tensor(small2[:, :], small2[:, :], small3[:, :], ALU.max))
            vl(dve, nc.vector.tensor_reduce(small3[:, 0:E], v3, AX.X, ALU.add))
            vl(dve, nc.vector.tensor_scalar(mask, small3[:, 0:E], 1.5, None, ALU.is_lt))

        def moe_plan(tag, midway=()):
            for g in range(tag_groups[tag] + 1):
                if g < tag_groups[tag]:
                    T.plan((tag, "h", g))
                    A.plan((tag, "a", g))
                if g == 4:
                    T.plan(*midway)
                if g:
                    T.plan((tag, "o", g - 1))

        tag_groups = {"l0f": 4, "l2f": 8, "l3f": 8}

        def moe_tensor(pe, tag, w_in, w_gate, w_out, xT, per, midway=None):
            ng = tag_groups[tag]

            def made(g):
                if w_gate is None:
                    pe.wait_ge(A.sem, A.at((tag, "a", g)))
                else:
                    pe.wait_ge(V.sem, V.at((tag, "g", g)))
            for g in range(ng + 1):
                if g < ng:
                    if g >= 2:
                        made(g - 2)
                    for j in range(4):
                        c = 4 * g + j
                        m = mm(ps[:, g % 2, j * P:(j + 1) * P], w_in[:, c * P:(c + 1) * P], xT)
                        if w_gate is not None:
                            m = mm(ps[:, 2 + g % 2, j * P:(j + 1) * P], w_gate[:, c * P:(c + 1) * P], xT)
                    m.then_inc(T.sem, T.now((tag, "h", g)))
                if g == 4 and midway is not None:
                    midway(pe)
                if g:
                    made(g - 1)
                    for j in range(4):
                        c = 4 * (g - 1) + j
                        e = c // per
                        m = mm(ps[:, 4 + e // 4, (e % 4) * P:(e % 4 + 1) * P],
                               probs[:, 1, (g - 1) % 2 * BANK + j * P:(g - 1) % 2 * BANK + (j + 1) * P],
                               w_out[:, c * P:(c + 1) * P], c % per == 0, c % per == per - 1)
                    m.then_inc(T.sem, T.now((tag, "o", g - 1)))

        def moe_scalar(act, tag, func, bias):
            for g in range(tag_groups[tag]):
                act.wait_ge(T.sem, T.at((tag, "h", g)))
                o = g % 2 * BANK
                if bias is None:
                    if g >= 2:
                        act.wait_ge(V.sem, V.at((tag, "g", g - 2)))
                    m = nc.scalar.activation(probs[:, 0, o:o + BANK], ps[:, g % 2, :], func)
                else:
                    if g >= 2:
                        act.wait_ge(T.sem, T.at((tag, "o", g - 2)))
                    for j in range(4):
                        m = nc.scalar.activation(probs[:, 1, o + j * P:o + (j + 1) * P], ps[:, g % 2, j * P:(j + 1) * P],
                                                 func, bias=bias[:, 4 * g + j:4 * g + j + 1])
                m.then_inc(A.sem, A.now((tag, "a", g)))

        def gate_vector(dve, tag, g):
            dve.wait_ge(A.sem, A.at((tag, "a", g)))
            if g >= 2:
                dve.wait_ge(T.sem, T.at((tag, "o", g - 2)))
            o = g % 2 * BANK
            nc.vector.tensor_tensor(probs[:, 1, o:o + BANK], probs[:, 0, o:o + BANK], ps[:, 2 + g % 2, :],
                                    ALU.mult).then_inc(V.sem, V.now((tag, "g", g)))

        G.plan("const")

        @on("pool")
        def _(pool):
            nc.gpsimd.memset(half[:, 0:1], -0.5)
            nc.gpsimd.memset(half[:, 1:2], 0.5)
            nc.gpsimd.memset(one[:, :], 1.0)
            nc.gpsimd.memset(values_t[:, CTX:], 0.0)
            nc.gpsimd.memset(vaug[:, H * 9:], 0.0)
            nc.gpsimd.memset(vaug[:, 0:H * 9], 1.0).then_inc(G.sem, G.now("const"))

        def hidden_vector(dve):
            loaded(dve, "mask")
            z = probsT[96:97, :, :].rearrange("p a b -> p (a b)")
            vl(dve, nc.vector.tensor_scalar(z, keysT[96:97, :].bitcast(I32), 0.0, None, ALU.is_equal))
            vl(dve, nc.vector.tensor_reduce(seen[96:97, 0:1], z, AX.X, ALU.min))
            nc.vector.tensor_scalar(seen[96:97, 1:2], seen[96:97, 0:1], -1.0, 1.0, ALU.mult,
                                    ALU.add).then_inc(V.sem, V.now("mask.any"))
            dve.wait_ge(V.sem, V.at("mask.any"))
            nc.vector.tensor_scalar(keys_r["l1x"][96:97, 0, :], z, seen[96:97, 1:2], HIDDEN, ALU.mult,
                                    ALU.mult).then_inc(V.sem, V.now("mask.row"))

        ramped, steps = probs[0:4, 0, 0:64], probs[0:64, 0, 64:64 + H]

        def distance_tensor(pe, i):
            if i == 1:
                loaded(pe, "const")
                mm(ps[0:4, 5, 256:320], at["w_coeff"][0:64, :], at["ramp"][0:64, :]).then_inc(T.sem, T.now("d.1"))
                return
            pe.wait_ge(V.sem, V.at(f"d.{i - 1}"))
            if i == 2:
                mm(ps[0:64, 6, 256:256 + H], ramped, at["w_wpos"][0:4, :]).then_inc(T.sem, T.now("d.2"))
            else:
                mm(ps[0:H, 7, 128:128 + 255], steps, at["dist"][0:64, :]).then_inc(T.sem, T.now("d.3"))

        def distance_vector(dve, i):
            dve.wait_ge(T.sem, T.at(f"d.{i}"))
            o, src = ((ramped, ps[0:4, 5, 256:320]), (steps, ps[0:64, 6, 256:256 + H]),
                      (dists[:, :], ps[0:H, 7, 128:128 + 255]))[i - 1]
            nc.vector.tensor_copy(o, src).then_inc(V.sem, V.now(f"d.{i}"))

        def l0x():
            tag = "l0x"
            start_plan(tag)
            V.plan("l0x.q", "mask.any", "mask.row")
            G.plan("prelude")
            ctx_plan(tag, 1)
            V.plan("l0x.t")
            T.plan("l0x.row")
            V.plan("l0x.rowmax")
            A.plan("l0x.rowexp")
            V.plan("l0x.row")
            T.plan("l0x.batt")
            V.plan("l0x.batt")
            T.plan("l0x.bar")
            V.plan("l0x.bar")
            V.plan("l0x.rd")
            T.plan("l0x.rd")
            V.plan("l0x.prod")
            T.plan("d.1", "l0x.y")
            V.plan("d.1", "l0x.x")
            s = small4

            @on("pe")
            def _(pe):
                loaded(pe, "first")
                start_tensor(pe, tag)
                loaded(pe, "ctxT")
                pe.wait_ge(V.sem, V.at("l0x.q"))

                def weigh_tile(g, t, p):
                    if t == 0:
                        loaded(pe, "ctx")
                    return mm(ps[:, 7, 0:P], values[:, t, 0:P], p, t == 0, t == KT_N - 1)
                ctx_tensor(pe, tag, 1, lambda h, b: mm(ring(h, b), tA[:, :], ctxT[:, b * BANK:(b + 1) * BANK]),
                           weigh_tile)
                pe.wait_ge(V.sem, V.at("l0x.t"))
                tr(ps[0:1, 0, 0:P], s[:, 2:3]).then_inc(T.sem, T.now("l0x.row"))
                pe.wait_ge(V.sem, V.at("l0x.row"))
                mm(ps[:, 0, 128:129], tC[0:1, :], one[0:1, 0:1]).then_inc(T.sem, T.now("l0x.batt"))
                pe.wait_ge(V.sem, V.at("l0x.batt"))
                mm(ps[:, 0, 130:131], xn[:, :], s[:, 8:9]).then_inc(T.sem, T.now("l0x.bar"))
                pe.wait_ge(V.sem, V.at("l0x.rd"))
                mm(ps[:, 5, 0:P], tB[:, :], ident).then_inc(T.sem, T.now("l0x.rd"))
                pe.wait_ge(V.sem, V.at("l0x.prod"))
                loaded(pe, "w_a")
                distance_tensor(pe, 1)
                for i, f in enumerate((xnT, tD, tE, tF)):
                    m = mm(ps[:, 4, 0:P], f[:, :], at["w_l0x"][:, i * P:(i + 1) * P], i == 0, i == 3)
                m.then_inc(T.sem, T.now("l0x.y"))

            @on("dve")
            def _(dve):
                loaded(dve, "x")
                dve.wait_ge(G.sem, G.at("const"))
                start_vector(dve, tag, None)
                loaded(dve, "cols")
                dve.wait_ge(V.sem, V.at("l0x.xn.T"))
                nc.vector.tensor_scalar(tA[:, :], xnT[:, :], at["w3"], at["w2"], ALU.mult,
                                        ALU.add).then_inc(V.sem, V.now("l0x.q"))
                hidden_vector(dve)
                loaded(dve, "rows")
                nc.vector.tensor_tensor(xb[:, :], xs[:, x_at[tag], :], at["l0x_b"], ALU.add)
                nc.vector.tensor_tensor_reduce(tC[:, :], xn[:, :], at["w1"], 1.0, 0.0, ALU.mult, ALU.add, s[:, 0:1])
                ctx_vector(dve, tag, 1, -1.0)
                vl(dve, nc.vector.tensor_tensor(s[:, 1:2], s[:, 0:1], at["b_sim"], ALU.add))
                nc.vector.tensor_tensor(s[:, 2:3], s[:, 1:2], nmax[:, 0:1],
                                        ALU.subtract).then_inc(V.sem, V.now("l0x.t"))
                dve.wait_ge(T.sem, T.at("l0x.row"))
                nc.vector.tensor_reduce(s[0:1, 4:5], ps[0:1, 0, 0:P], AX.X, ALU.max,
                                        negate=True).then_inc(V.sem, V.now("l0x.rowmax"))
                dve.wait_ge(A.sem, A.at("l0x.rowexp"))
                vl(dve, nc.vector.reciprocal(s[0:1, 6:7], s[0:1, 5:6]))
                nc.vector.tensor_scalar(tC[0:1, :], tC[0:1, :], s[0:1, 6:7], None,
                                        ALU.mult).then_inc(V.sem, V.now("l0x.row"))
                dve.wait_ge(T.sem, T.at("l0x.batt"))
                nc.vector.tensor_copy(s[:, 8:9], ps[:, 0, 128:129]).then_inc(V.sem, V.now("l0x.batt"))
                dve.wait_ge(T.sem, T.at("l0x.bar"))
                nc.vector.tensor_copy(s[:, 9:10], ps[:, 0, 130:131]).then_inc(V.sem, V.now("l0x.bar"))
                vl(dve, sums_vector(dve, tag, 1, s[:, 10:11]))
                nc.vector.tensor_scalar(tB[:, :], one[:, :], s[:, 10:11], None,
                                        ALU.mult).then_inc(V.sem, V.now("l0x.rd"))
                dve.wait_ge(T.sem, T.at("l0x.rd"))
                vl(dve, nc.vector.tensor_copy(tE[:, :], ps[:, 5, 0:P]))
                vl(dve, nc.vector.tensor_tensor(tD[:, :], ps[:, 7, 0:P], tE[:, :], ALU.mult))
                nc.vector.tensor_tensor(tE[:, :], xnT[:, :], tD[:, :], ALU.mult)
                nc.vector.tensor_scalar(tF[:, :], xnT[:, :], s[:, 9:10], None,
                                        ALU.mult).then_inc(V.sem, V.now("l0x.prod"))
                distance_vector(dve, 1)
                end_vector(dve, tag, ps[:, 4, 0:P], xb[:, :], "l0x.y")

            @on("act")
            def _(act):
                ctx_scalar(act, tag, 1, 1.0)
                act.wait_ge(V.sem, V.at("l0x.rowmax"))
                nc.scalar.activation(tC[0:1, :], ps[0:1, 0, 0:P], ACT.Exp, bias=s[0:1, 4:5],
                                     accum_out=s[0:1, 5:6]).then_inc(A.sem, A.now("l0x.rowexp"))

            @on("pool")
            def _(pool):
                norm_gpsimd(pool, tag)
                loaded(pool, "first")
                loaded(pool, "const")
                nc.gpsimd.tensor_copy(identb[:, :], ident)
                nc.gpsimd.tensor_copy(causalb[:, :], at["causal"]).then_inc(G.sem, G.now("prelude"))

        def l0a():
            tag = "l0a"
            start_plan(tag)
            T.plan("d.2", "l0a.qkv", "mask.any", "d.3")
            V.plan("d.2", "l0a.v", "mask", "l0a.q", "l0a.k", "d.3")
            turn_plan("l0a.q")
            T.plan("l0a.kv")
            V.plan("l0a.kv")
            T.plan("l0a.c")
            V.plan("l0a.c")
            T.plan("l0a.y")
            V.plan("l0a.x")

            @on("pe")
            def _(pe):
                start_tensor(pe, tag)
                distance_tensor(pe, 2)
                pe.wait_ge(V.sem, V.at("l0a.xn.T"))
                for i, w in enumerate(("q", "k", "v")):
                    m = mm(ps[:, i, 0:P], xnT[:, :], at["w_l0a_" + w])
                m.then_inc(T.sem, T.now("l0a.qkv"))
                mm(ps[:, 5, 300:301], one[96:97, :], seen[96:97, 1:2]).then_inc(T.sem, T.now("mask.any"))
                distance_tensor(pe, 3)
                turn_tensor(pe, "l0a.q", tA[:, :], "l0a.q", 5)
                pe.wait_ge(V.sem, V.at("l0a.k"))
                mm(ps[:, 3, 0:P], tB[:, :], tC[:, :]).then_inc(T.sem, T.now("l0a.kv"))
                pe.wait_ge(V.sem, V.at("l0a.kv"))
                mm(ps[:, 4, 0:P], tD[:, :], tE[:, :]).then_inc(T.sem, T.now("l0a.c"))
                pe.wait_ge(V.sem, V.at("l0a.c"))
                mm(ps[:, 6, 0:P], tF[:, :], at["w_l0a_o"]).then_inc(T.sem, T.now("l0a.y"))

            def rotate(dve, src, bias, dst, name):
                vl(dve, nc.vector.tensor_tensor(tG[:, :], src, bias, ALU.add))
                g = tG[:, :].rearrange("p (n t) -> p n t", t=2)
                f = tF[:, :].rearrange("p (n t) -> p n t", t=2)
                sn = at["sin"].rearrange("p (n t) -> p n t", t=2)
                nc.vector.tensor_tensor(f[:, :, 0], g[:, :, 1], sn[:, :, 0], ALU.mult)
                nc.vector.tensor_tensor(f[:, :, 1], g[:, :, 0], sn[:, :, 1], ALU.mult)
                vl(dve, nc.vector.tensor_tensor(dst[:, :], tG[:, :], at["cos"], ALU.mult))
                nc.vector.tensor_tensor(dst[:, :], dst[:, :], tF[:, :], ALU.add).then_inc(V.sem, V.now(name))
                dve.wait_ge(V.sem, V.at(name))

            @on("dve")
            def _(dve):
                dve.wait_ge(V.sem, V.at("l0x.x"))
                loaded(dve, "const")
                start_vector(dve, tag, at["l0a_bo"])
                distance_vector(dve, 2)
                dve.wait_ge(T.sem, T.at("l0a.qkv"))
                nc.vector.tensor_tensor(tC[:, :], ps[:, 2, 0:P], at["l0a_bv"], ALU.add).then_inc(V.sem, V.now("l0a.v"))
                dve.wait_ge(T.sem, T.at("mask.any"))
                vl(dve, nc.vector.tensor_copy(seen[:, 2:3], ps[:, 5, 300:301]))
                nc.vector.tensor_scalar(seen[:, 0:1], seen[:, 2:3], float(1.0 / np.sqrt(P)), None, ALU.mult)
                nc.vector.tensor_scalar(seen[:, 3:4], seen[:, 2:3], float(-1.0 / np.sqrt(P)), None,
                                        ALU.mult).then_inc(V.sem, V.now("mask"))
                rotate(dve, ps[:, 0, 0:P], at["l0a_bq"], tA, "l0a.q")
                rotate(dve, ps[:, 1, 0:P], at["l0a_bk"], tB, "l0a.k")
                distance_vector(dve, 3)
                turn_vector(dve, "l0a.q", tE, 5)
                dve.wait_ge(T.sem, T.at("l0a.kv"))
                nc.vector.scalar_tensor_tensor(tD[:, :], ps[:, 3, 0:P], 1.0 / np.sqrt(8.0), at["bm8"], ALU.mult,
                                               ALU.mult).then_inc(V.sem, V.now("l0a.kv"))
                dve.wait_ge(T.sem, T.at("l0a.c"))
                nc.vector.tensor_copy(tF[:, :], ps[:, 4, 0:P]).then_inc(V.sem, V.now("l0a.c"))
                end_vector(dve, tag, ps[:, 6, 0:P], xb[:, :], "l0a.y")

            @on("pool")
            def _(pool):
                norm_gpsimd(pool, tag)

        def l0f():
            tag = "l0f"
            keys_plan("l1x")
            start_plan(tag)
            T.plan("l0f.qkv")
            V.plan("l0f.keys", "l0f.qkv")
            G.plan("l0f.spread", ("l1x", "low"))
            values_plan("l1x")
            self_plan(tag)
            T.plan("l0f.mla")
            V.plan("l0f.mla")
            turn_plan("l0f.mla")
            T.plan("l0f.route")
            V.plan("l0f.rmax")
            A.plan("l0f.rexp")
            V.plan("l0f.comb")
            moe_plan(tag)
            V.plan("l0f.x")
            s = small4

            @on("pe")
            def _(pe):
                keys_tensor(pe, "l1x", at["w_l1x_k"], (0, 1, 2, 3))
                start_tensor(pe, tag)
                pe.wait_ge(V.sem, V.at("l0f.xn.T"))
                mm(ps[0:64, 4, 0:P], at["w_l0f_q"], xnT[:, :])
                mm(ps[0:64, 5, 0:P], at["w_l0f_k"], xnT[:, :])
                mm(ps[:, 6, 0:P], xnT[:, :], at["w_l0f_v"]).then_inc(T.sem, T.now("l0f.qkv"))
                values_tensor(pe, "l1x", at["w_l1x_v"], (0, 1, 2, 3), tuple(("k", b) for b in range(4)))
                pe.wait_ge(V.sem, V.at("l0f.qkv"))
                pe.wait_ge(A.sem, A.at(("l1x", "v", 3)))
                self_tensor(pe, tag, 64, tC, probs[:, 0, :])
                pe.wait_ge(V.sem, V.at("l0f.o"))
                mm(ps[:, 7, 0:P], tB[:, :], at["w_l0f_o"]).then_inc(T.sem, T.now("l0f.mla"))
                turn_tensor(pe, "l0f.mla", tC[:, :], "l0f.mla", 6)
                pe.wait_ge(V.sem, V.at("l0f.mla.T"))
                mm(ps[:, 7, 0:E], tD[:, :], at["w_l0f_r"]).then_inc(T.sem, T.now("l0f.route"))
                loaded(pe, "w_l0f")
                moe_tensor(pe, tag, at["w_l0f.w1"], None, at["w_l0f.w2"], tD[:, :], 2)

            @on("dve")
            def _(dve):
                dve.wait_ge(V.sem, V.at("l0a.x"))
                start_vector(dve, tag, None)
                dve.wait_ge(T.sem, T.at("l0f.qkv"))
                nc.vector.tensor_scalar(tC[0:64, :], ps[0:64, 4, 0:P], at["l0f_qb"][0:64, :], None, ALU.add)
                nc.vector.tensor_scalar(tD[0:64, :], ps[0:64, 5, 0:P], at["l0f_kb"][0:64, :], None,
                                        ALU.add).then_inc(V.sem, V.now("l0f.keys"))
                dve.wait_ge(V.sem, V.at("l0f.keys"))
                va = vaug[:, 0:H * 9].rearrange("p (h w) -> p h w", h=H)
                nc.vector.tensor_tensor(va[:, :, 0:8], ps[:, 6, 0:P].rearrange("p (h w) -> p h w", h=H),
                                        at["l0f_vb"].rearrange("p (h w) -> p h w", h=H), ALU.add)
                spread_heads(nc.vector, probs[:, 0, :], tD, at["hm4"], 64, 0).then_inc(V.sem, V.now("l0f.qkv"))
                self_vector(dve, tag, 0.5)
                dve.wait_ge(T.sem, T.at("l0f.mla"))
                nc.vector.tensor_tensor(tC[:, :], ps[:, 7, 0:P], at["l0f_ob"], ALU.add).then_inc(V.sem, V.now("l0f.mla"))
                turn_vector(dve, "l0f.mla", tD, 6)
                route_vector(dve, "l0f", at["l0f_rb"])
                top2(dve, s[:, 16:24], s[:, 24:32])
                vl(dve, nc.vector.tensor_tensor_reduce(s[:, 32:40], s[:, 16:24], s[:, 24:32], 1.0, 0.0, ALU.mult,
                                                       ALU.add, s[:, 40:41]))
                vl(dve, nc.vector.tensor_scalar(s[:, 41:42], s[:, 40:41], 1e-8, None, ALU.add))
                vl(dve, nc.vector.reciprocal(s[:, 42:43], s[:, 41:42]))
                nc.vector.tensor_scalar(s[:, 48:56], s[:, 32:40], s[:, 42:43], 0.3, ALU.mult,
                                        ALU.mult).then_inc(V.sem, V.now("l0f.comb"))
                vl(dve, nc.vector.tensor_tensor(xb[:, :], xs[:, x_at[tag], :], xn[:, :], ALU.add))
                loaded(dve, "l0f_b2")
                mix_vector(dve, tag, s[:, 48:56], xb[:, :])

            @on("act")
            def _(act):
                loaded(act, "cols")
                keys_scalar(act, "l1x", at["l1x_bk"], (0, 1, 2, 3), shared[:, :])
                values_scalar(act, "l1x", (0, 1, 2, 3))
                self_scalar(act, tag, 0.5)
                route_scalar(act, "l0f")
                moe_scalar(act, tag, ACT.Gelu, at["l0f_b1"])

            @on("pool")
            def _(pool):
                norm_gpsimd(pool, tag)
                spread_gpsimd(pool, tag, at["hm4"], 64)
                keys_gpsimd(pool, "l1x", shared)

        def route_vector(dve, tag, bias):
            s = small4
            dve.wait_ge(T.sem, T.at(tag + ".route"))
            vl(dve, nc.vector.tensor_tensor(s[:, 0:8], ps[:, 7, 0:E], bias, ALU.add))
            nc.vector.tensor_reduce(s[:, 8:9], s[:, 0:8], AX.X, ALU.max, negate=True).then_inc(V.sem, V.now(tag + ".rmax"))
            dve.wait_ge(A.sem, A.at(tag + ".rexp"))
            vl(dve, nc.vector.reciprocal(s[:, 10:11], s[:, 9:10]))
            vl(dve, nc.vector.tensor_scalar(s[:, 16:24], s[:, 0:8], s[:, 10:11], None, ALU.mult))

        def route_scalar(act, tag):
            s = small4
            act.wait_ge(V.sem, V.at(tag + ".rmax"))
            nc.scalar.activation(s[:, 0:8], s[:, 0:8], ACT.Exp, bias=s[:, 8:9],
                                 accum_out=s[:, 9:10]).then_inc(A.sem, A.now(tag + ".rexp"))

        def mix_vector(dve, tag, comb, base, biases=True):
            ng = tag_groups[tag]
            dve.wait_ge(T.sem, T.at((tag, "o", ng - 1)))
            if biases:
                nc.vector.tensor_tensor(probs[:, 0, 0:BANK], ps[:, 4, :], b2rows[:, 0:BANK], ALU.add)
                vl(dve, nc.vector.tensor_tensor(probs[:, 0, BANK:2 * BANK], ps[:, 5, :], b2rows[:, BANK:], ALU.add))
            src = base
            for e in range(E):
                last = e == E - 1
                dst = xs[:, 1 - x_at[tag], :] if last else (tE, tF)[e % 2][:, :]
                o = probs[:, 0, e * P:(e + 1) * P] if biases else ps[:, 4 + e // 4, (e % 4) * P:(e % 4 + 1) * P]
                m = nc.vector.scalar_tensor_tensor(dst, o, comb[:, e:e + 1], src, ALU.mult, ALU.add)
                if last:
                    m.then_inc(V.sem, V.now(tag + ".x"))
                else:
                    vl(dve, m)
                src = dst

        def keys_plan(tag):
            T.plan(*((tag, "kp", b) for b in range(NB)))
            A.plan(*((tag, "k", b) for b in range(NB)))

        def keys_tensor(pe, tag, wk, banks):
            for b in range(NB):
                mm(ps[:, banks[b], :], wk, ctxT[:, b * BANK:(b + 1) * BANK]).then_inc(T.sem, T.now((tag, "kp", b)))

        def keys_scalar(act, tag, bias, banks, high):
            for b in range(NB):
                act.wait_ge(T.sem, T.at((tag, "kp", b)))
                for o in (keysT[:, b * BANK:(b + 1) * BANK], high[:, b * BANK:(b + 1) * BANK].bitcast(F32R)):
                    if bias is None:
                        m = nc.scalar.copy(o, ps[:, banks[b], :])
                    else:
                        m = nc.scalar.activation(o, ps[:, banks[b], :], ACT.Identity, bias=bias)
                m.then_inc(A.sem, A.now((tag, "k", b)))

        def keys_gpsimd(pool, tag, high):
            pool.wait_ge(A.sem, A.at((tag, "k", NB - 1)))
            nc.gpsimd.tensor_tensor(keysT[:, :], keysT[:, :], high[:, :], ALU.subtract).then_inc(G.sem, G.now((tag, "low")))

        def values_plan(tag):
            T.plan(*((tag, "vp", b) for b in range(4)))
            A.plan(*((tag, "v", b) for b in range(4)))

        def values_tensor(pe, tag, wv, banks, after):
            for b in range(4):
                if after[b] is not None:
                    pe.wait_ge(A.sem, A.at((tag,) + after[b]))
                for j in range(4):
                    t = 4 * b + j
                    m = mm(ps[:, banks[b], j * P:(j + 1) * P], ctxT[:, t * P:(t + 1) * P], wv)
                m.then_inc(T.sem, T.now((tag, "vp", b)))

        def values_scalar(act, tag, banks):
            for b in range(4):
                act.wait_ge(T.sem, T.at((tag, "vp", b)))
                nc.scalar.copy(values_t[:, b * BANK:(b + 1) * BANK], ps[:, banks[b], :]).then_inc(
                    A.sem, A.now((tag, "v", b)))

        def cross(tag, before, w, scale, masked, q_bias, v_bias, o_bias, pack):
            if masked:
                V.plan(tag + ".ones")
            start_plan(tag)
            T.plan(tag + ".q")
            A.plan(tag + ".qhi")
            V.plan(tag + ".qs", (tag, "q", 0))
            G.plan(*((tag, "q", t) for t in range(1, 4)))
            ctx_plan(tag, H)
            V.plan(tag + ".rd", (tag, "g", 3), tag + ".rdT")
            T.plan(tag + ".rd", tag + ".o")
            V.plan(tag + ".o")
            T.plan(tag + ".y")
            V.plan(tag + ".x")
            keys = keys_r[tag]
            hi = keysT[:, 3 * BANK:]
            heads = at["hm32m" if masked else "hm32"]

            def spread(engine, t):
                return engine.tensor_tensor(query_r[:, 4 * t * P:4 * (t + 1) * P].rearrange("p (h n) -> p h n", h=4),
                                            bc(hi[:, t * P:(t + 1) * P], 1, [P, 4, P]), bc(heads, 2, [P, 4, P]), ALU.mult)

            @on("pe")
            def _(pe):
                loaded(pe, pack)
                start_tensor(pe, tag)
                pe.wait_ge(V.sem, V.at(tag + ".xn.T"))
                for t in range(4):
                    m = mm(ps[:, 4, t * P:(t + 1) * P], w("q")[:, t * P:(t + 1) * P], xnT[:, :])
                m.then_inc(T.sem, T.now(tag + ".q"))
                loaded(pe, "keys_" + tag)

                def score(h, b):
                    if h % 4 == 0 and b == 0:
                        queries = G if h else V
                        pe.wait_ge(queries.sem, queries.at((tag, "q", h // 4)))
                    return mm(ring(h, b), query_r[:, h * P:(h + 1) * P], keys[:, h // 4, b * BANK:(b + 1) * BANK])

                def weigh_tile(g, t, p):
                    j = t % 4
                    if g and g % 4 == 0 and t == 0:
                        pe.wait_ge(V.sem, V.at((tag, "g", g // 4 - 1)))
                    v = t * P + 8 * g
                    return mm(ps[32 * j:32 * j + 32, 7, (g % 4) * P:(g % 4 + 1) * P],
                              values_t[:, v:v + 32], p, t < 4, t >= KT_N - 4)

                def fold(gs):
                    for g in gs:
                        pe.wait_ge(V.sem, V.at((tag, "g", g // 4)))
                        m = mm(ps[:, 4, 0:P], at["strip"][:, 120 - 8 * g:248 - 8 * g], keysT[:, g * P:(g + 1) * P],
                               g == 0, g == H - 1)
                    return m

                assert (NB * H) % RING == 4
                ctx_tensor(pe, tag, H, score, weigh_tile, lambda: fold(range(12)))
                pe.wait_ge(V.sem, V.at(tag + ".rd"))
                mm(ps[:, 5, 0:P], tA[:, :], ident).then_inc(T.sem, T.now(tag + ".rd"))
                fold(range(12, H)).then_inc(T.sem, T.now(tag + ".o"))
                pe.wait_ge(V.sem, V.at(tag + ".o"))
                mm(ps[:, 3, 0:P], tB[:, :], w("o")).then_inc(T.sem, T.now(tag + ".y"))

            @on("dve")
            def _(dve):
                dve.wait_ge(V.sem, V.at(before))
                if masked:
                    loaded(dve, "keys_" + tag)
                    nc.vector.memset(hi[96:128, :], 1.0).then_inc(V.sem, V.now(tag + ".ones"))
                start_vector(dve, tag, o_bias)
                dve.wait_ge(A.sem, A.at(tag + ".qhi"))
                low = hi[32:64, :]
                if masked:
                    for t in range(4):
                        c = slice(t * P, (t + 1) * P)
                        m = nc.vector.scalar_tensor_tensor(low[:, c], ps[32:64, 4, c], q_bias[32:64, t:t + 1], low[:, c],
                                                           ALU.add, ALU.subtract)
                else:
                    nc.vector.tensor_tensor(low, ps[32:64, 4, :], low, ALU.subtract)
                    m = nc.vector.tensor_tensor(hi[96:128, :], ps[96:128, 4, :], hi[96:128, :], ALU.subtract)
                m.then_inc(V.sem, V.now(tag + ".qs"))
                dve.wait_ge(V.sem, V.at(tag + ".qs"))
                spread(nc.vector, 0).then_inc(V.sem, V.now((tag, "q", 0)))

                def between(dve, g):
                    if g % 4 == 0 and g:
                        gather(dve, g // 4 - 1)

                def gather(dve, n):
                    dve.wait_ge(T.sem, T.at((tag, "pv", 4 * n + 3, 3)))
                    nc.vector.tensor_copy(keysT[:, n * BANK:(n + 1) * BANK], ps[:, 7, :]).then_inc(
                        V.sem, V.now((tag, "g", n)))
                ctx_vector(dve, tag, H, seen[:, 3:4] if masked else -scale, between)
                vl(dve, sums_vector(dve, tag, H, small[:, 16:32]))
                nc.vector.tensor_copy(tA[:, :].rearrange("p (h w) -> p h w", h=H),
                                      bc(small[:, 16:32], 2, [P, H, 8])).then_inc(V.sem, V.now(tag + ".rd"))
                gather(dve, 3)
                dve.wait_ge(T.sem, T.at(tag + ".rd"))
                nc.vector.tensor_copy(tC[:, :], ps[:, 5, 0:P]).then_inc(V.sem, V.now(tag + ".rdT"))
                dve.wait_ge(V.sem, V.at(tag + ".rdT"))
                dve.wait_ge(T.sem, T.at(tag + ".o"))
                m = nc.vector.tensor_tensor(tB[:, :], ps[:, 4, 0:P], tC[:, :], ALU.mult)
                if v_bias is not None:
                    vl(dve, m)
                    m = nc.vector.tensor_scalar(tB[:, :], tB[:, :], v_bias, None, ALU.add)
                m.then_inc(V.sem, V.now(tag + ".o"))
                end_vector(dve, tag, ps[:, 3, 0:P], xb[:, :], tag + ".y")

            @on("act")
            def _(act):
                act.wait_ge(T.sem, T.at(tag + ".q"))
                loaded(act, "keys_" + tag)
                if masked:
                    for t in range(4):
                        c = slice(t * P, (t + 1) * P)
                        m = nc.scalar.activation(hi[0:96, c].bitcast(F32R), ps[0:96, 4, c], ACT.Identity,
                                                 bias=q_bias[0:96, t:t + 1])
                else:
                    m = nc.scalar.copy(hi.bitcast(F32R), ps[:, 4, :])
                m.then_inc(A.sem, A.now(tag + ".qhi"))
                ctx_scalar(act, tag, H, seen[:, 0:1] if masked else scale)

            @on("pool")
            def _(pool):
                norm_gpsimd(pool, tag)
                pool.wait_ge(V.sem, V.at(tag + ".qs"))
                for t in range(1, 4):
                    spread(nc.gpsimd, t).then_inc(G.sem, G.now((tag, "q", t)))

        def l1a():
            tag = "l1a"
            start_plan(tag)
            T.plan("l1a.qkv")
            V.plan("l1a.qkv")
            T.plan("l1a.kv")
            V.plan("l1a.kv")
            T.plan("l1a.num")
            V.plan("l1a.o")
            turn_plan("l1a.o")
            T.plan("l1a.y")
            V.plan("l1a.x")

            @on("pe")
            def _(pe):
                start_tensor(pe, tag)
                pe.wait_ge(V.sem, V.at("l1a.xn.T"))
                w = at["w_l1a_qkv"]
                mm(ps[:, 0, 0:P], w[:, 0:P], xnT[:, :])
                mm(ps[:, 1, 0:P], xnT[:, :], w[:, P:2 * P])
                mm(ps[:, 2, 0:P], xnT[:, :], w[:, 2 * P:3 * P]).then_inc(T.sem, T.now("l1a.qkv"))
                pe.wait_ge(V.sem, V.at("l1a.qkv"))
                mm(ps[:, 3, 0:P], tB[:, :], tC[:, :])
                mm(ps[:, 4, 0:P], tB[:, :], one[:, :]).then_inc(T.sem, T.now("l1a.kv"))
                pe.wait_ge(V.sem, V.at("l1a.kv"))
                mm(ps[:, 5, 0:P], tA[:, :], tD[:, :])
                mm(ps[:, 6, 0:P], tA[:, :], tE[:, :]).then_inc(T.sem, T.now("l1a.num"))
                turn_tensor(pe, "l1a.o", tF[:, :], "l1a.o", 7)
                pe.wait_ge(V.sem, V.at("l1a.o.T"))
                mm(ps[:, 0, 0:P], tG[:, :], at["w_l1a_p"]).then_inc(T.sem, T.now("l1a.y"))

            @on("dve")
            def _(dve):
                dve.wait_ge(V.sem, V.at("l1x.x"))
                start_vector(dve, tag, at["l1a_b"])
                dve.wait_ge(T.sem, T.at("l1a.qkv"))
                nc.vector.tensor_scalar(tA[:, :], ps[:, 0, 0:P], 0.0, None, ALU.max)
                nc.vector.tensor_scalar(tB[:, :], ps[:, 1, 0:P], 0.0, None, ALU.max)
                nc.vector.tensor_scalar(tC[:, :], ps[:, 2, 0:P], 0.0, None, ALU.max).then_inc(V.sem, V.now("l1a.qkv"))
                dve.wait_ge(T.sem, T.at("l1a.kv"))
                nc.vector.tensor_tensor(tD[:, :], ps[:, 3, 0:P], at["bm4"], ALU.mult)
                nc.vector.tensor_tensor(tE[:, :], ps[:, 4, 0:P], at["bm4"], ALU.mult).then_inc(V.sem, V.now("l1a.kv"))
                dve.wait_ge(T.sem, T.at("l1a.num"))
                vl(dve, nc.vector.tensor_scalar(tG[:, :], ps[:, 6, 0:P], 1e-15, None, ALU.add))
                vl(dve, nc.vector.reciprocal(tF[:, :], tG[:, :]))
                nc.vector.tensor_tensor(tF[:, :], ps[:, 5, 0:P], tF[:, :], ALU.mult).then_inc(V.sem, V.now("l1a.o"))
                turn_vector(dve, "l1a.o", tG, 7)
                end_vector(dve, tag, ps[:, 0, 0:P], xb[:, :], "l1a.y")

            @on("pool")
            def _(pool):
                norm_gpsimd(pool, tag)

        TREES = ("q", "k", "v", "f")

        def tree_plan(n, func=False):
            if func:
                V.plan(("hb", n))
                A.plan(("hf", n))
            else:
                V.plan(("h", n))
            V.plan(("p", n, 0), ("p", n, 1))
            A.plan(("p", n, 2), ("p", n, 3))
            T.plan(("o", n))

        def tree_gather(pool, n):
            i = TREES.index(n)
            for layer, dst in ((1, leaves[n][:, 0:LEAF1]), (2, leaves[n][:, LEAF1:LEAF])):
                nc.gpsimd.indirect_dma_start(dst, None, dram[f"tree{layer}_{n}"], bass.IndirectOffsetOnAxis(
                    leaf_no[:, i:i + 1], 0)).then_inc(loads[f"leaf{layer}_{n}"], 16)

        def units(n):
            i = TREES.index(n)
            return small3[:, LW * i:LW * (i + 1)]

        def second(n, c):
            return leaves[n][:, LEAF1 + 4 * c * P:LEAF1 + 4 * (c + 1) * P]

        def tree_tensor(pe, n, turned):
            o = ps[:, 4 + TREES.index(n), 0:P]
            loaded(pe, "leaf1_" + n)
            for _ in range(WARM):
                mm(ps[:, 0, 0:P], identb[:, :], identb[:, :])
            for c in range(4):
                made = A if c >= 2 else V
                pe.wait_ge(made.sem, made.at(("p", n, c)))
                for j in range(5 if c == 3 else 4):
                    w = second(n, c)[:, j * P:(j + 1) * P] if j < 4 else leaves[n][:, LEAF - P:LEAF]
                    if turned:
                        m = mm(o, w, ident, c == j == 0, j == 4)
                    else:
                        m = mm(o, ident, w, c == j == 0, j == 4)
            m.then_inc(T.sem, T.now(("o", n)))

        def tree_vector(dve, n, x, func=False):
            loaded(dve, "leaf1_" + n)
            h = units(n)
            w1 = leaves[n]
            for j in range(LW):
                w = w1[:, j * P:(j + 1) * P]
                m = nc.vector.tensor_tensor_reduce(w, x, w, 1.0, 0.0, ALU.mult, ALU.add, h[:, j:j + 1])
            vl(dve, m)
            m = nc.vector.tensor_tensor(h, h, w1[:, LW * P:LEAF1], ALU.add)
            if func:
                m.then_inc(V.sem, V.now(("hb", n)))
                dve.wait_ge(A.sem, A.at(("hf", n)))
            else:
                vl(dve, m)
                nc.vector.tensor_scalar(h, h, 0.0, None, ALU.max).then_inc(V.sem, V.now(("h", n)))
                dve.wait_ge(V.sem, V.at(("h", n)))
            loaded(dve, "leaf2_" + n)
            for c in range(2):
                w = second(n, c).rearrange("p (j n) -> p j n", n=P)
                nc.vector.tensor_tensor(w, w, bc(h[:, 4 * c:4 * c + 4], 2, [P, 4, P]), ALU.mult).then_inc(
                    V.sem, V.now(("p", n, c)))

        def tree_scalar(act, n, func=None):
            h = units(n)
            if func is None:
                act.wait_ge(V.sem, V.at(("h", n)))
            else:
                act.wait_ge(V.sem, V.at(("hb", n)))
                nc.scalar.activation(h, h, func).then_inc(A.sem, A.now(("hf", n)))
                act.wait_ge(A.sem, A.at(("hf", n)))
            loaded(act, "leaf2_" + n)
            for c in range(2, 4):
                for j in range(4):
                    w = second(n, c)[:, j * P:(j + 1) * P]
                    m = nc.scalar.activation(w, w, ACT.Copy, scale=h[:, 4 * c + j:4 * c + j + 1])
                m.then_inc(A.sem, A.now(("p", n, c)))

        def walk_vector(dve, first, count, name, place=0):
            ways = probs[:, 1, 0:count * 2 * LEAVES].rearrange("p (n k s) -> p n k s", n=count, s=2)
            for j in range(count):
                i = first + j
                vl(dve, nc.vector.tensor_tensor(probs[:, 0, j * NODES:(j + 1) * NODES], logits(place + j),
                                                nbias[:, i * NODES:(i + 1) * NODES], ALU.add))
            lg = probs[:, 0, 0:count * NODES].rearrange("p (n k) -> p n k", n=count)
            nc.vector.tensor_scalar(ways[:, :, 0:NODES, 0], lg, 0.0, None, ALU.is_le)
            vl(dve, nc.vector.tensor_scalar(ways[:, :, 0:NODES, 1], lg, 0.0, None, ALU.is_gt))
            cur = ways[:, :, 0, :]
            for d in range(1, DEPTH):
                w = 2 ** d
                dst = paths[:, 0:count, :] if d == DEPTH - 1 else \
                    levels[:, d % 2, 0:count * 2 * w].rearrange("p (n k) -> p n k", n=count)
                for j in range(count):
                    m = nc.vector.tensor_tensor(dst[:, j].rearrange("p (k s) -> p k s", s=2),
                                                bc(cur[:, j], 2, [P, w, 2]), ways[:, j, w - 1:2 * w - 1, :], ALU.mult)
                    if j < count - 1:
                        continue
                    vl(dve, m)
                cur = dst
            for j in range(count):
                m = nc.vector.tensor_tensor_reduce(paths[:, j, :], paths[:, j, :], at["leaf"], 1.0, 0.0, ALU.mult,
                                                   ALU.add, leaf_at[:, first + j:first + j + 1])
            vl(dve, m)
            nc.vector.tensor_copy(leaf_no[:, first:first + count], leaf_at[:, first:first + count]).then_inc(
                V.sem, V.now(name))

        def logits(j):
            return ps[:, 1 + j // 2, (j % 2) * 256:(j % 2) * 256 + NODES]

        def l1f():
            tag = "l1f"
            norm_plan("l1f")
            V.plan("l1f.sd")
            G.plan("l1f.sd")
            V.plan("l1f.xx")
            G.plan("l1f.xx")
            V.plan("l1f.xh")
            turn_plan("l1f.xh")
            T.plan("l1f.nodes")
            keys_plan("l2x")
            values_plan("l2x")
            V.plan("l1f.pathq", "l1f.paths")
            G.plan(("l2x", "low"))
            for n in "qkv":
                tree_plan(n)
            V.plan("l1f.qkv")
            T.plan("l1f.s")
            V.plan("l1f.m")
            A.plan("l1f.p")
            V.plan("l1f.p")
            turn_plan("l1f.p")
            T.plan("l1f.av")
            V.plan("l1f.y")
            turn_plan("l1f.y")
            T.plan("l1f.nodef")
            V.plan("l1f.pathf")
            tree_plan("f", True)
            V.plan("l1f.x")
            s = small4

            @on("pe")
            def _(pe):
                pe.wait_ge(G.sem, G.at("prelude"))
                turn_tensor(pe, "l1f.xh", tA[:, :], "l1f.xh")
                pe.wait_ge(V.sem, V.at("l1f.xh.T"))
                loaded(pe, "node")
                for j in range(3):
                    m = mm(logits(j), xnT[:, :], nodew[:, j * NODES:(j + 1) * NODES])
                m.then_inc(T.sem, T.now("l1f.nodes"))
                loaded(pe, "w_b")
                keys_tensor(pe, "l2x", at["w_b.l2x_k"], (3, 4, 5, 6))
                values_tensor(pe, "l2x", at["w_b.l2x_v"], (7, 3, 4, 5), (None, ("k", 0), ("k", 1), ("k", 2)))
                pe.wait_ge(A.sem, A.at(("l2x", "v", 3)))
                tree_tensor(pe, "q", True)
                tree_tensor(pe, "k", True)
                tree_tensor(pe, "v", False)
                pe.wait_ge(V.sem, V.at("l1f.qkv"))
                mm(ps[:, 0, 0:P], tC[:, :], tD[:, :]).then_inc(T.sem, T.now("l1f.s"))
                turn_tensor(pe, "l1f.p", tF[:, :], "l1f.p", 7)
                pe.wait_ge(V.sem, V.at("l1f.p.T"))
                mm(ps[:, 1, 0:P], tG[:, :], tE[:, :]).then_inc(T.sem, T.now("l1f.av"))
                turn_tensor(pe, "l1f.y", tB[:, :], "l1f.y", 7)
                pe.wait_ge(V.sem, V.at("l1f.y.T"))
                mm(logits(0), xnT[:, :], nodew[:, 3 * NODES:4 * NODES]).then_inc(T.sem, T.now("l1f.nodef"))
                tree_tensor(pe, "f", False)

            @on("dve")
            def _(dve):
                dve.wait_ge(V.sem, V.at("l1a.x"))
                norm_vector(dve, "l1f", xs[:, x_at[tag], :])
                dve.wait_ge(V.sem, V.at("l1f.xn"))
                vl(dve, nc.vector.bn_stats(st[:, :], xn[:, :]))
                vl(dve, nc.vector.bn_aggr(mv[:, 0:2], st[:, :]))
                nc.vector.tensor_scalar(mv[:, 2:3], mv[:, 1:2], P / (P - 1.0), None,
                                        ALU.mult).then_inc(V.sem, V.now("l1f.sd"))
                dve.wait_ge(G.sem, G.at("l1f.sd"))
                nc.vector.tensor_scalar(mv[:, 2:3], mv[:, 3:4], 1e-5, None, ALU.add).then_inc(V.sem, V.now("l1f.xx"))
                dve.wait_ge(G.sem, G.at("l1f.xx"))
                nc.vector.tensor_scalar(tA[:, :], xn[:, :], mv[:, 0:1], mv[:, 3:4], ALU.subtract,
                                        ALU.mult).then_inc(V.sem, V.now("l1f.xh"))
                turn_vector(dve, "l1f.xh", xnT)
                loaded(dve, "node")
                dve.wait_ge(T.sem, T.at("l1f.nodes"))
                walk_vector(dve, 0, 1, "l1f.pathq")
                dve.wait_ge(V.sem, V.at("l1f.pathq"))
                walk_vector(dve, 1, 2, "l1f.paths", 1)
                for n in "qkv":
                    tree_vector(dve, n, tA[:, :])
                dve.wait_ge(T.sem, T.at(("o", "v")))
                nc.vector.tensor_copy(tC[:, :], ps[:, 4, 0:P])
                nc.vector.tensor_copy(tD[:, :], ps[:, 5, 0:P])
                nc.vector.tensor_copy(tE[:, :], ps[:, 6, 0:P]).then_inc(V.sem, V.now("l1f.qkv"))
                dve.wait_ge(T.sem, T.at("l1f.s"))
                vl(dve, nc.vector.tensor_reduce(s[:, 0:1], ps[:, 0, 0:P], AX.X, ALU.max))
                nc.vector.tensor_scalar(s[:, 1:2], s[:, 0:1], -1.0 / np.sqrt(float(P)), None,
                                        ALU.mult).then_inc(V.sem, V.now("l1f.m"))
                dve.wait_ge(A.sem, A.at("l1f.p"))
                vl(dve, nc.vector.reciprocal(s[:, 3:4], s[:, 2:3]))
                nc.vector.tensor_scalar(tF[:, :], tF[:, :], s[:, 3:4], None, ALU.mult).then_inc(V.sem, V.now("l1f.p"))
                turn_vector(dve, "l1f.p", tG, 7)
                dve.wait_ge(T.sem, T.at("l1f.av"))
                nc.vector.tensor_tensor(tB[:, :], ps[:, 1, 0:P], tA[:, :], ALU.add).then_inc(V.sem, V.now("l1f.y"))
                turn_vector(dve, "l1f.y", xnT, 7)
                vl(dve, nc.vector.tensor_tensor(xb[:, :], xs[:, x_at[tag], :], tB[:, :], ALU.add))
                dve.wait_ge(T.sem, T.at("l1f.nodef"))
                walk_vector(dve, 3, 1, "l1f.pathf")
                tree_vector(dve, "f", tB[:, :], True)
                end_vector(dve, tag, ps[:, 7, 0:P], xb[:, :], ("o", "f"))

            @on("act")
            def _(act):
                keys_scalar(act, "l2x", None, (3, 4, 5, 6), probsT[:, :, :].rearrange("p a b -> p (a b)"))
                values_scalar(act, "l2x", (7, 3, 4, 5))
                for n in "qkv":
                    tree_scalar(act, n)
                act.wait_ge(V.sem, V.at("l1f.m"))
                nc.scalar.activation(tF[:, :], ps[:, 0, 0:P], ACT.Exp, bias=s[:, 1:2], scale=float(1.0 / np.sqrt(P)),
                                     accum_out=s[:, 2:3]).then_inc(A.sem, A.now("l1f.p"))
                tree_scalar(act, "f", ACT.Gelu)

            @on("pool")
            def _(pool):
                norm_gpsimd(pool, "l1f")
                pool.wait_ge(V.sem, V.at("l1f.sd"))
                nc.gpsimd.tensor_tensor(mv[:, 3:4], mv[:, 2:3], half[:, 1:2], ALU.pow).then_inc(G.sem, G.now("l1f.sd"))
                pool.wait_ge(V.sem, V.at("l1f.xx"))
                nc.gpsimd.tensor_tensor(mv[:, 3:4], mv[:, 2:3], half[:, 0:1], ALU.pow).then_inc(G.sem, G.now("l1f.xx"))
                pool.wait_ge(V.sem, V.at("l1f.pathq"))
                tree_gather(pool, "q")
                pool.wait_ge(V.sem, V.at("l1f.paths"))
                tree_gather(pool, "k")
                tree_gather(pool, "v")
                keys_gpsimd(pool, "l2x", probsT[:, :, :].rearrange("p a b -> p (a b)"))
                pool.wait_ge(V.sem, V.at("l1f.pathf"))
                pool.wait_ge(T.sem, T.at(("o", "q")))
                tree_gather(pool, "f")

        def l2a():
            tag = "l2a"
            start_plan(tag)
            T.plan("l2a.qkv")
            V.plan("l2a.keys", "l2a.qkv")
            G.plan("l2a.spread", "l3x.split")
            self_plan(tag)
            T.plan("l2a.y")
            V.plan("l2a.x")

            @on("pe")
            def _(pe):
                start_tensor(pe, tag)
                pe.wait_ge(V.sem, V.at("l2a.xn.T"))
                w = at["w_b.l2a_qkv"]
                mm(ps[:, 4, 0:P], w[:, 0:P], xnT[:, :])
                mm(ps[:, 5, 0:P], w[:, P:2 * P], xnT[:, :])
                mm(ps[:, 6, 0:P], xnT[:, :], w[:, 2 * P:3 * P]).then_inc(T.sem, T.now("l2a.qkv"))
                loaded(pe, "bias")
                for g in range(4):
                    mm(ps[:, g, :], at["flip"], biases[:, g * BANK:(g + 1) * BANK], True, False)
                pe.wait_ge(V.sem, V.at("l2a.qkv"))
                self_tensor(pe, tag, P, tC, probs[:, 0, :], True)
                pe.wait_ge(V.sem, V.at("l2a.o"))
                mm(ps[:, 7, 0:P], tB[:, :], at["w_b.l2a_o"]).then_inc(T.sem, T.now("l2a.y"))

            @on("dve")
            def _(dve):
                dve.wait_ge(V.sem, V.at("l2x.x"))
                start_vector(dve, tag, None)
                dve.wait_ge(T.sem, T.at("l2a.qkv"))
                nc.vector.tensor_scalar(tC[:, :], ps[:, 4, 0:P], float(8 ** -0.5), None, ALU.mult)
                nc.vector.tensor_copy(tD[:, :], ps[:, 5, 0:P]).then_inc(V.sem, V.now("l2a.keys"))
                dve.wait_ge(V.sem, V.at("l2a.keys"))
                va = vaug[:, 0:H * 9].rearrange("p (h w) -> p h w", h=H)
                nc.vector.tensor_copy(va[:, :, 0:8], ps[:, 6, 0:P].rearrange("p (h w) -> p h w", h=H))
                spread_heads(nc.vector, probs[:, 0, :], tD, at["hm8"], P, 0).then_inc(V.sem, V.now("l2a.qkv"))
                self_vector(dve, tag, 1.0)
                end_vector(dve, tag, ps[:, 7, 0:P], xs[:, x_at[tag], :], "l2a.y")

            @on("act")
            def _(act):
                self_scalar(act, tag, 1.0)

            @on("pool")
            def _(pool):
                norm_gpsimd(pool, tag)
                spread_gpsimd(pool, tag, at["hm8"], P)
                gl(pool, nc.gpsimd.tensor_copy(ctx_hi[:, :], ctxT[:, :]))
                nc.gpsimd.tensor_tensor(ctx_lo[:, :], ctxT[:, :], ctx_hi[:, :].bitcast(F32),
                                        ALU.subtract).then_inc(G.sem, G.now("l3x.split"))

        def l2f():
            tag = "l2f"
            T.plan("l3x.vo")
            A.plan("l3x.vo")
            norm_plan("l2f")
            norm_plan("l2f1")
            V.plan("l2f1.h")
            turn_plan("l2f1.h")
            T.plan("l2f.qkv")
            V.plan("l2f.keys", "l2f.qkv")
            G.plan("l2f.spread")
            self_plan(tag)
            T.plan("l2f.ap")
            V.plan("l2f.x1")
            norm_plan("l2f2")
            G.plan("l3x.rows")
            V.plan("l2f2.h")
            turn_plan("l2f2.h")
            T.plan("l2f.route")
            V.plan("l2f.rmax")
            A.plan("l2f.rexp")
            V.plan("l2f.mask")
            moe_plan(tag, midway=("l2f.rank",))
            V.plan(*(("l2f.perm", e) for e in range(E)))
            V.plan("l2f.eo")
            T.plan("l2f.y")
            V.plan("l2f.x")
            s = small4

            @on("pe")
            def _(pe):
                pe.wait_ge(G.sem, G.at("prelude"))
                pe.wait_ge(V.sem, V.at("l2a.x"))
                for h in range(H):
                    r = 64 * (h % 2)
                    c = h // 2
                    m = mm(ps[:, 4 + 2 * (h % 2) + c // 4, (c % 4) * P:(c % 4 + 1) * P],
                           at["w_b.l3x_v"][r:r + 64, c * P:(c + 1) * P], at["w_b.l3x_o1"][r:r + 64, c * P:(c + 1) * P])
                m.then_inc(T.sem, T.now("l3x.vo"))
                turn_tensor(pe, "l2f1.h", tA[:, :], "l2f1.h", 3)
                pe.wait_ge(V.sem, V.at("l2f1.h.T"))
                pe.wait_ge(A.sem, A.at("l3x.vo"))
                w = at["w_b.l2f_qkv"]
                mm(ps[:, 4, 0:P], w[:, 0:P], xnT[:, :])
                mm(ps[:, 5, 0:P], w[:, P:2 * P], xnT[:, :])
                mm(ps[:, 6, 0:P], xnT[:, :], w[:, 2 * P:3 * P]).then_inc(T.sem, T.now("l2f.qkv"))
                for g in range(4):
                    mm(ps[:, g, :], identb[:, :], bc(causalb[:, :], 1, [P, 4, P]), True, False)
                pe.wait_ge(V.sem, V.at("l2f.qkv"))
                self_tensor(pe, tag, P, tC, probs[:, 0, :], True)
                pe.wait_ge(V.sem, V.at("l2f.o"))
                mm(ps[:, 7, 0:P], tB[:, :], at["w_b.l2f_p"]).then_inc(T.sem, T.now("l2f.ap"))
                turn_tensor(pe, "l2f2.h", tB[:, :], "l2f2.h", 6)
                pe.wait_ge(V.sem, V.at("l2f2.h.T"))
                mm(ps[:, 7, 0:E], xnT[:, :], at["w_b.l2f_g"]).then_inc(T.sem, T.now("l2f.route"))
                loaded(pe, "w_l2f")

                def rank(pe):
                    pe.wait_ge(V.sem, V.at("l2f.mask"))
                    mm(ps[:, 7, 0:E], at["tri"], s[:, 24:32]).then_inc(T.sem, T.now("l2f.rank"))
                moe_tensor(pe, tag, at["w_l2f.w1"], None, at["w_l2f.w2"], xnT[:, :], 4, rank)
                pe.wait_ge(V.sem, V.at("l2f.eo"))
                for e in range(E):
                    pe.wait_ge(V.sem, V.at(("l2f.perm", e)))
                    m = mm(ps[:, 6, 0:P], perm[:, e * P:(e + 1) * P], probs[:, 0, e * P:(e + 1) * P], e == 0, e == E - 1)
                m.then_inc(T.sem, T.now("l2f.y"))

            def affine(dve, ready, name, dst, scale, bias):
                dve.wait_ge(V.sem, V.at(ready))
                vl(dve, nc.vector.tensor_tensor(dst[:, :], xn[:, :], scale, ALU.mult))
                nc.vector.tensor_tensor(dst[:, :], dst[:, :], bias, ALU.add).then_inc(V.sem, V.now(name))

            @on("dve")
            def _(dve):
                dve.wait_ge(V.sem, V.at("l2a.x"))
                norm_vector(dve, "l2f", xs[:, x_at[tag], :])
                dve.wait_ge(V.sem, V.at("l2f.xn"))
                vl(dve, nc.vector.tensor_copy(tE[:, :], xn[:, :]))
                norm_vector(dve, "l2f1", tE[:, :])
                nc.vector.tensor_tensor(xb[:, :], tE[:, :], at["l2f_ap"], ALU.add)
                affine(dve, "l2f1.xn", "l2f1.h", tA, at["ln1_s"], at["ln1_b"])
                turn_vector(dve, "l2f1.h", xnT, 3)
                dve.wait_ge(T.sem, T.at("l2f.qkv"))
                nc.vector.tensor_scalar(tC[:, :], ps[:, 4, 0:P], at["l2f_bq"], float(8 ** -0.5), ALU.add, ALU.mult)
                nc.vector.tensor_scalar(tD[:, :], ps[:, 5, 0:P], at["l2f_bk"], None,
                                        ALU.add).then_inc(V.sem, V.now("l2f.keys"))
                dve.wait_ge(V.sem, V.at("l2f.keys"))
                va = vaug[:, 0:H * 9].rearrange("p (h w) -> p h w", h=H)
                nc.vector.tensor_tensor(va[:, :, 0:8], ps[:, 6, 0:P].rearrange("p (h w) -> p h w", h=H),
                                        at["l2f_bv"].rearrange("p (h w) -> p h w", h=H), ALU.add)
                spread_heads(nc.vector, probs[:, 0, :], tD, at["hm8"], P, 0).then_inc(V.sem, V.now("l2f.qkv"))
                self_vector(dve, tag, 1.0)
                dve.wait_ge(T.sem, T.at("l2f.ap"))
                nc.vector.tensor_tensor(tG[:, :], ps[:, 7, 0:P], xb[:, :], ALU.add).then_inc(V.sem, V.now("l2f.x1"))
                dve.wait_ge(V.sem, V.at("l2f.x1"))
                norm_vector(dve, "l2f2", tG[:, :])
                nc.vector.tensor_tensor(xb[:, :], xs[:, x_at[tag], :], tG[:, :], ALU.add)
                affine(dve, "l2f2.xn", "l2f2.h", tB, at["ln2_s"], at["ln2_b"])
                turn_vector(dve, "l2f2.h", xnT, 6)
                route_vector(dve, "l2f", at["l2f_gb"])
                top2(dve, s[:, 16:24], s[:, 24:32])
                nc.vector.tensor_tensor(s[:, 32:40], s[:, 16:24], s[:, 24:32], ALU.mult).then_inc(V.sem, V.now("l2f.mask"))
                dve.wait_ge(T.sem, T.at("l2f.rank"))
                vl(dve, nc.vector.tensor_copy(s[:, 40:48], ps[:, 7, 0:E]))
                loaded(dve, "l2f_b2")
                for e in range(E):
                    nc.vector.tensor_scalar(perm[:, e * P:(e + 1) * P], at["iota1"], s[:, 40 + e:41 + e],
                                            s[:, 32 + e:33 + e], ALU.is_equal,
                                            ALU.mult).then_inc(V.sem, V.now(("l2f.perm", e)))
                dve.wait_ge(T.sem, T.at((tag, "o", tag_groups[tag] - 1)))
                nc.vector.tensor_tensor(probs[:, 0, 0:BANK], ps[:, 4, :], b2rows[:, 0:BANK], ALU.add)
                nc.vector.tensor_tensor(probs[:, 0, BANK:2 * BANK], ps[:, 5, :], b2rows[:, BANK:],
                                        ALU.add).then_inc(V.sem, V.now("l2f.eo"))
                end_vector(dve, tag, ps[:, 6, 0:P], xb[:, :], "l2f.y")

            @on("act")
            def _(act):
                act.wait_ge(T.sem, T.at("l3x.vo"))
                w4 = w_vo.rearrange("p (c s n) -> p c s n", s=2, n=P)
                for i in range(2):
                    m = nc.scalar.copy(w4[:, :, i, :], ps[:, 4 + 2 * i:6 + 2 * i, :].rearrange("p a (b n) -> p (a b) n", n=P))
                m.then_inc(A.sem, A.now("l3x.vo"))
                self_scalar(act, tag, 1.0)
                route_scalar(act, "l2f")
                moe_scalar(act, tag, ACT.Gelu_apprx_tanh, at["l2f_bfc"])

            @on("pool")
            def _(pool):
                norm_gpsimd(pool, "l2f")
                norm_gpsimd(pool, "l2f1")
                spread_gpsimd(pool, tag, at["hm8"], P)
                norm_gpsimd(pool, "l2f2")
                loaded(pool, "ctx2")
                gl(pool, nc.gpsimd.tensor_copy(rows_hi[:, :], values_t[:, 0:CTX]))
                nc.gpsimd.tensor_tensor(rows_lo[:, :], values_t[:, 0:CTX], rows_hi[:, :].bitcast(F32),
                                        ALU.subtract).then_inc(G.sem, G.now("l3x.rows"))

        def l3x():
            tag = "l3x"
            start_plan(tag)
            T.plan("l3x.q")
            V.plan(("l3x.q", 0), ("l3x.q", 1))
            T.plan(("l3x.qk", 0))
            A.plan(("l3x.qhi", 0))
            V.plan(("l3x.qlo", 0))
            G.plan("l3a.wide")
            T.plan((tag, "s", 0, 0), (tag, "s", 0, 1), ("l3x.qk", 1))
            V.plan((tag, "m", 0))
            A.plan((tag, "x", 0, 0), (tag, "x", 0, 1), ("l3x.qhi", 1))
            V.plan(("l3x.qlo", 1))
            for g in range(H):
                more = g + 1 < H
                if more:
                    T.plan((tag, "s", g + 1, 0))
                T.plan((tag, "t", g, 0), (tag, "t", g, 1))
                if more:
                    T.plan((tag, "s", g + 1, 1))
                T.plan((tag, "t", g, 2), (tag, "t", g, 3))
                if g % 2 and g >= 3:
                    T.plan((tag, "w", g - 3), (tag, "w", g - 2))
                late = g % 2 == 0 and g >= 2
                if g % 2:
                    T.plan(*((tag, "pv", g // 2, c) for c in range(3)))
                if late:
                    T.plan((tag, "pv", g // 2 - 1, 3))
                A.plan(*((tag, "e", g, c) for c in range(3 if late else 4)))
                if more:
                    A.plan((tag, "x", g + 1, 0), (tag, "x", g + 1, 1))
                if late:
                    A.plan((tag, "e", g, 3))
                V.plan((tag, "e", g, 0), (tag, "e", g, 1))
                if more:
                    V.plan((tag, "m", g + 1))
                V.plan((tag, "e", g, 2))
                if late:
                    V.plan((tag, "u", g // 2 - 1))
                V.plan((tag, "e", g, 3))
                if g % 2 and g >= 3:
                    V.plan((tag, "a", g - 3), (tag, "a", g - 2))
            V.plan((tag, "u", H // 2 - 1))
            T.plan((tag, "pv", H // 2 - 1, 3), (tag, "w", H - 2), (tag, "w", H - 1))
            V.plan((tag, "a", H - 2), (tag, "a", H - 1))
            V.plan("l3x.1")
            turn_plan("l3x.1")
            T.plan("l3x.2")
            V.plan("l3x.2")
            norm_plan("l3xo")
            V.plan("l3x.x")

            def by_parity(ap, n, i):
                return ap.rearrange("p (n c s q) -> p n c s q", n=2, s=2, q=P)[:, n, :, i, :]

            pair = shared[:, 0:2 * P]

            def sides(g, c, of):
                return of[:, 4 * c:4 * c + 4, g % 2, :]

            def queries(n, i):
                return ps[:, 4 + 2 * n + i, :].rearrange("p (c q) -> p c q", q=P)

            def against_context(n):
                for h in range(8 * n, 8 * n + 8):
                    r = 64 * (h % 2)
                    c = h // 2
                    m = mm(ps[:, 4 + 2 * n + h % 2, (c % 4) * P:(c % 4 + 1) * P],
                           at["w_b.l3x_k"][r:r + 64, c * P:(c + 1) * P], qheads[r:r + 64, c * P:(c + 1) * P])
                m.then_inc(T.sem, T.now(("l3x.qk", n)))

            def high(act, n):
                act.wait_ge(T.sem, T.at(("l3x.qk", n)))
                for i in range(2):
                    m = nc.scalar.copy(by_parity(query_r[:, :], n, i), queries(n, i))
                m.then_inc(A.sem, A.now(("l3x.qhi", n)))

            def rest(dve, n):
                dve.wait_ge(A.sem, A.at(("l3x.qhi", n)))
                for i in range(2):
                    m = nc.vector.tensor_tensor(by_parity(query_lo[:, :], n, i), queries(n, i),
                                                by_parity(query_r[:, :].bitcast(F32), n, i), ALU.subtract)
                m.then_inc(V.sem, V.now(("l3x.qlo", n)))

            @on("pe")
            def _(pe):
                start_tensor(pe, tag)
                pe.wait_ge(V.sem, V.at("l3x.xn.T"))
                for c in range(8):
                    m = mm(ps[:, 6 + c // 4, (c % 4) * P:(c % 4 + 1) * P], at["w_b.l3x_q"][:, c * P:(c + 1) * P], xnT[:, :])
                m.then_inc(T.sem, T.now("l3x.q"))
                pe.wait_ge(V.sem, V.at(("l3x.q", 0)))
                against_context(0)
                pe.wait_ge(V.sem, V.at(("l3x.qlo", 0)))
                pe.wait_ge(G.sem, G.at("l3x.split"))
                loaded(pe, "ctx2")

                def score(h, b):
                    hi, lo = query_r[:, h * P:(h + 1) * P], query_lo[:, h * P:(h + 1) * P]
                    c = slice(b * BANK, (b + 1) * BANK)
                    mm(ps[:, b, :], hi, ctx_hi[:, c], True, False)
                    mm(ps[:, b, :], hi, ctx_lo[:, c], False, False)
                    return mm(ps[:, b, :], lo, ctx_hi[:, c], False, True)

                def scores(h, half):
                    if h:
                        pe.wait_ge(A.sem, A.at((tag, "x", h - 1, half)))
                    for b in (2 * half, 2 * half + 1):
                        m = score(h, b)
                    m.then_inc(T.sem, T.now((tag, "s", h, half)))

                def turn(g, c):
                    pe.wait_ge(A.sem, A.at((tag, "x", g, c // 2)))
                    n = 4 * g + c - 2
                    if n >= 0:
                        pe.wait_ge(V.sem, V.at((tag, "e", n // 4, n % 4)))
                    for j in range(4):
                        m = tr(ps[:, 4 + c % 2, j * P:(j + 1) * P], probs[:, g % 2, (4 * c + j) * P:(4 * c + j + 1) * P])
                    m.then_inc(T.sem, T.now((tag, "t", g, c)))

                def weigh(p, cs):
                    if p == 0 and 0 in cs:
                        pe.wait_ge(V.sem, V.at(("l3x.qlo", 1)))
                    if p >= 2 and 0 in cs:
                        pe.wait_ge(V.sem, V.at((tag, "a", 2 * p - 3)))
                    o = ps[:, 6 + p % 2, 0:2 * P]
                    for c in cs:
                        pe.wait_ge(V.sem, V.at((tag, "e", 2 * p + 1, c)))
                        for t in range(4 * c, 4 * c + 4):
                            hi, lo = (of[:, t, :, :].rearrange("p a b -> p (a b)") for of in (weights_hi, weights_lo))
                            rhi, rlo = rows_hi[:, t * P:(t + 1) * P], rows_lo[:, t * P:(t + 1) * P]
                            mm(o, rhi, hi, t == 0, False)
                            mm(o, rhi, lo, False, False)
                            m = mm(o, rlo, hi, False, t == KT_N - 1)
                        m.then_inc(T.sem, T.now((tag, "pv", p, c)))

                def output(p):
                    pe.wait_ge(V.sem, V.at((tag, "u", p)))
                    for i in range(2):
                        h = 2 * p + i
                        mm(ps[:, 6 + p % 2, (2 + i) * P:(3 + i) * P], pair[:, i * P:(i + 1) * P],
                           w_vo[:, h * P:(h + 1) * P]).then_inc(T.sem, T.now((tag, "w", h)))

                scores(0, 0)
                scores(0, 1)
                pe.wait_ge(V.sem, V.at(("l3x.q", 1)))
                against_context(1)
                pe.wait_ge(G.sem, G.at("l3x.rows"))
                for g in range(H):
                    if g + 1 < H:
                        scores(g + 1, 0)
                    turn(g, 0)
                    turn(g, 1)
                    if g + 1 < H:
                        scores(g + 1, 1)
                    turn(g, 2)
                    turn(g, 3)
                    if g % 2 and g >= 3:
                        output(g // 2 - 1)
                    if g % 2:
                        weigh(g // 2, (0, 1, 2))
                    elif g:
                        weigh(g // 2 - 1, (3,))
                weigh(H // 2 - 1, (3,))
                output(H // 2 - 1)
                turn_tensor(pe, "l3x.1", tA[:, :], "l3x.1", 4)
                pe.wait_ge(V.sem, V.at("l3x.1.T"))
                mm(ps[:, 5, 0:P], tB[:, :], at["w_b.l3x_o2"]).then_inc(T.sem, T.now("l3x.2"))

            @on("dve")
            def _(dve):
                dve.wait_ge(V.sem, V.at("l2f.x"))
                start_vector(dve, tag, None)
                dve.wait_ge(T.sem, T.at("l3x.q"))
                for n in range(2):
                    nc.vector.tensor_copy(qheads[:, n * BANK:(n + 1) * BANK], ps[:, 6 + n, :]).then_inc(
                        V.sem, V.now(("l3x.q", n)))
                rest(dve, 0)

                def largest(h, half):
                    dve.wait_ge(T.sem, T.at((tag, "s", h, half)))
                    return nc.vector.tensor_reduce(small[:, half:half + 1], ps[:, 2 * half:2 * half + 2, :], AX.XY, ALU.max)

                def shift(h):
                    vl(dve, largest(h, 1))
                    nc.vector.tensor_scalar(nmax[:, h:h + 1], small[:, 0:1], small[:, 1:2], -0.125, ALU.max,
                                            ALU.mult).then_inc(V.sem, V.now((tag, "m", h)))

                def low(g, c):
                    dve.wait_ge(A.sem, A.at((tag, "e", g, c)))
                    nc.vector.tensor_tensor(sides(g, c, weights_lo), ps[:, 4 + c % 2, :].rearrange("p (a b) -> p a b", a=4),
                                            sides(g, c, weights_hi).bitcast(F32), ALU.subtract).then_inc(
                                                V.sem, V.now((tag, "e", g, c)))

                def take(p):
                    dve.wait_ge(T.sem, T.at((tag, "pv", p, 3)))
                    nc.vector.tensor_copy(pair, ps[:, 6 + p % 2, 0:2 * P]).then_inc(V.sem, V.now((tag, "u", p)))

                def add(p):
                    two = slice(2 * p, 2 * p + 2)
                    vl(dve, nc.vector.tensor_tensor(small3[:, two], wsum[:, 0, two], wsum[:, 1, two], ALU.add))
                    vl(dve, nc.vector.reciprocal(small2[:, two], small3[:, two]))
                    for i in range(2):
                        g = 2 * p + i
                        dve.wait_ge(T.sem, T.at((tag, "w", 2 * p + 1)))
                        o = ps[:, 6 + p % 2, (2 + i) * P:(3 + i) * P]
                        if g:
                            dve.wait_ge(V.sem, V.at((tag, "a", g - 1)))
                            m = nc.vector.scalar_tensor_tensor(tF[:, :], o, small2[:, g:g + 1], tF[:, :], ALU.mult, ALU.add)
                        else:
                            m = nc.vector.tensor_scalar(tF[:, :], o, small2[:, g:g + 1], None, ALU.mult)
                        m.then_inc(V.sem, V.now((tag, "a", g)))

                largest(0, 0)
                shift(0)
                rest(dve, 1)
                for g in range(H):
                    if g + 1 < H:
                        largest(g + 1, 0)
                    low(g, 0)
                    low(g, 1)
                    if g + 1 < H:
                        shift(g + 1)
                    low(g, 2)
                    if g % 2 == 0 and g >= 2:
                        take(g // 2 - 1)
                    low(g, 3)
                    if g % 2 and g >= 3:
                        add(g // 2 - 1)
                take(H // 2 - 1)
                add(H // 2 - 1)
                dve.wait_ge(V.sem, V.at((tag, "a", H - 1)))
                nc.vector.tensor_scalar(tA[:, :], tF[:, :], 0.0, None, ALU.max).then_inc(V.sem, V.now("l3x.1"))
                turn_vector(dve, "l3x.1", tB, 4)
                dve.wait_ge(T.sem, T.at("l3x.2"))
                nc.vector.tensor_copy(tC[:, :], ps[:, 5, 0:P]).then_inc(V.sem, V.now("l3x.2"))
                dve.wait_ge(V.sem, V.at("l3x.2"))
                norm_vector(dve, "l3xo", tC[:, :])
                dve.wait_ge(V.sem, V.at("l3xo.xn"))
                vl(dve, nc.vector.tensor_tensor(tD[:, :], xn[:, :], at["l3x_g"], ALU.mult))
                nc.vector.tensor_tensor(xs[:, 1 - x_at[tag], :], tD[:, :], xs[:, x_at[tag], :], ALU.add).then_inc(
                    V.sem, V.now("l3x.x"))

            @on("act")
            def _(act):
                high(act, 0)

                def weight(g):
                    act.wait_ge(V.sem, V.at((tag, "m", g)))
                    if g >= 2:
                        act.wait_ge(T.sem, T.at((tag, "t", g - 2, 3)))
                    for half in range(2):
                        o = half * 2 * BANK
                        nc.scalar.activation(probs[:, g % 2, o:o + 2 * BANK],
                                             ps[:, 2 * half:2 * half + 2, :].rearrange("p a b -> p (a b)"), ACT.Exp,
                                             bias=nmax[:, g:g + 1], scale=0.125,
                                             accum_out=wsum[:, half, g:g + 1]).then_inc(A.sem, A.now((tag, "x", g, half)))
                weight(0)
                high(act, 1)
                for g in range(H):
                    for c in range(4):
                        if c == 3 and g % 2 == 0 and 2 <= g < H - 1:
                            weight(g + 1)
                        act.wait_ge(T.sem, T.at((tag, "t", g, c)))
                        if g >= 2:
                            act.wait_ge(T.sem, T.at((tag, "pv", g // 2 - 1, c)))
                        nc.scalar.copy(sides(g, c, weights_hi), ps[:, 4 + c % 2, :].rearrange(
                            "p (a b) -> p a b", a=4)).then_inc(A.sem, A.now((tag, "e", g, c)))
                    if g + 1 < H and (g % 2 or g == 0):
                        weight(g + 1)

            @on("pool")
            def _(pool):
                norm_gpsimd(pool, tag)
                loaded(pool, "w_c")
                for name, dst in (("k", keysT[:, 0:8 * P]), ("q", shared[:, 8 * P:])):
                    nc.gpsimd.tensor_copy(dst.rearrange("p (a b) -> p a b", b=8), bc(at["w_c." + name], 2, [P, P, 8]))
                for h in range(H):
                    m = nc.gpsimd.tensor_copy(
                        keysT[:, 8 * P + 64 * h:8 * P + 64 * h + 64].rearrange("p (a b) -> p a b", a=8),
                        bc(at["w_c.v"][:, 8 * h:8 * h + 8], 1, [P, 8, 8]))
                m.then_inc(G.sem, G.now("l3a.wide"))
                norm_gpsimd(pool, "l3xo")

        def l3a():
            tag = "l3a"
            V.plan("l3a.var", "l3a.xn")
            turn_plan("l3a.xn")
            T.plan("l3a.m1")
            V.plan("l3a.m1")
            T.plan("l3a.z", "l3a.kvq")
            V.plan("l3a.nb")
            A.plan("l3a.z", "l3a.k", "l3a.q")
            V.plan("l3a.s", "l3a.kv")
            T.plan("l3a.s")
            V.plan(("l3a.st", 0), ("l3a.st", 1))
            T.plan("l3a.y")
            V.plan("l3a.y")
            T.plan("l3a.p")
            V.plan("l3a.ss")
            V.plan("l3a.yn")
            turn_plan("l3a.yn")
            T.plan("l3a.fc")
            V.plan("l3a.fc")
            T.plan("l3a.cp")
            V.plan("l3a.x")
            s = small4
            n8 = 8 * P
            kx, qx, st8, dx = (probs[:, 0, 0:n8], probs[:, 0, n8:], probs[:, 1, 0:n8], probs[:, 1, n8:])
            ux = sbq[:, 0:n8]
            wide_k, wide_v, wide_q = keysT[:, 0:n8], keysT[:, n8:], shared[:, n8:]
            G.plan("l3a.rstd", "l3a.sel", "l3a.rs")

            @on("pe")
            def _(pe):
                start_tensor(pe, tag)
                pe.wait_ge(V.sem, V.at("l3a.xn.T"))
                loaded(pe, "w_c")
                pe.wait_ge(G.sem, G.at("l3a.wide"))
                mm(ps[0:32, 6, 0:P], at["w_c.m1"], xnT[:, :]).then_inc(T.sem, T.now("l3a.m1"))
                for j in range(8):
                    o, b = (j % 4) * P, j // 4
                    mm(ps[:, b, o:o + P], wide_k[:, j * P:(j + 1) * P], xnT[:, :])
                    mm(ps[:, 2 + b, o:o + P], wide_v[:, j * P:(j + 1) * P], xnT[:, :])
                    m = mm(ps[:, 4 + b, o:o + P], wide_q[:, j * P:(j + 1) * P], xnT[:, :])
                    if j == 1:
                        pe.wait_ge(V.sem, V.at("l3a.m1"))
                        mm(ps[0:H, 7, 0:P], at["w_c.m2"][0:32, :], tA[0:32, :]).then_inc(T.sem, T.now("l3a.z"))
                m.then_inc(T.sem, T.now("l3a.kvq"))
                pe.wait_ge(V.sem, V.at("l3a.s"))
                pe.wait_ge(G.sem, G.at("l3a.sel"))
                for j in range(8):
                    m = mm(ps[:, 6 + j // 4, (j % 4) * P:(j % 4 + 1) * P],
                           probsT[0:H, j // 4, (j % 4) * P:(j % 4 + 1) * P], tC[0:H, :])
                m.then_inc(T.sem, T.now("l3a.s"))
                for j in range(8):
                    if j % 4 == 0:
                        pe.wait_ge(V.sem, V.at(("l3a.st", j // 4)))
                    m = mm(ps[:, 0, 0:P], at["gather"][:, 112 - 16 * j:240 - 16 * j], st8[:, j * P:(j + 1) * P], j == 0, j == 7)
                m.then_inc(T.sem, T.now("l3a.y"))
                pe.wait_ge(V.sem, V.at("l3a.y"))
                mm(ps[:, 4, 0:P], tB[:, :], at["w_c.p"]).then_inc(T.sem, T.now("l3a.p"))
                turn_tensor(pe, "l3a.yn", tE[:, :], "l3a.yn", 5)
                pe.wait_ge(V.sem, V.at("l3a.yn.T"))
                for c in range(4):
                    m = mm(ps[:, 6, c * P:(c + 1) * P], at["w_c.fc"][:, c * P:(c + 1) * P], tF[:, :])
                m.then_inc(T.sem, T.now("l3a.fc"))
                pe.wait_ge(V.sem, V.at("l3a.fc"))
                for c in range(4):
                    m = mm(ps[:, 7, 0:P], probs[:, 0, c * P:(c + 1) * P], at["w_c.cp"][:, c * P:(c + 1) * P], c == 0, c == 3)
                m.then_inc(T.sem, T.now("l3a.cp"))

            @on("dve")
            def _(dve):
                dve.wait_ge(V.sem, V.at("l3x.x"))
                start_vector(dve, tag, None)
                dve.wait_ge(T.sem, T.at("l3a.m1"))
                nc.vector.tensor_scalar(tA[0:32, :], ps[0:32, 6, 0:P], at["l3a_bm1"][0:32, :], 0.0, ALU.add,
                                        ALU.max).then_inc(V.sem, V.now("l3a.m1"))
                nc.vector.tensor_scalar(s[0:H, 0:1], at["l3a_bm2"][0:H, :], -1.0, None,
                                        ALU.mult).then_inc(V.sem, V.now("l3a.nb"))
                dve.wait_ge(A.sem, A.at("l3a.z"))
                vl(dve, nc.vector.tensor_scalar(tD[0:H, :], tB[0:H, :], 1.0, None, ALU.add))
                nc.vector.reciprocal(tC[0:H, :], tD[0:H, :]).then_inc(V.sem, V.now("l3a.s"))
                dve.wait_ge(A.sem, A.at("l3a.k"))
                kv = ps[:, 2:4, :].rearrange("p a b -> p (a b)")
                sp8 = ps[:, 6:8, :].rearrange("p a b -> p (a b)")
                nc.vector.tensor_tensor(ux, kx, kv, ALU.mult).then_inc(V.sem, V.now("l3a.kv"))
                dve.wait_ge(V.sem, V.at("l3a.kv"))
                dve.wait_ge(T.sem, T.at("l3a.s"))
                nc.vector.tensor_tensor(ux, ux, sp8, ALU.mult)
                vl(dve, nc.vector.tensor_scalar(dx, sp8, -1.0, 1.0, ALU.mult, ALU.add))
                vl(dve, nc.vector.memset(dx.rearrange("p (j t) -> p j t", t=P)[:, :, 0:1], 0.0))
                vl(dve, nc.vector.tensor_tensor_scan(st8, dx, ux, 0.0, ALU.mult, ALU.add))
                dve.wait_ge(A.sem, A.at("l3a.q"))
                for i in range(2):
                    c = slice(i * BANK, (i + 1) * BANK)
                    nc.vector.tensor_tensor(st8[:, c], st8[:, c], qx[:, c], ALU.mult).then_inc(V.sem, V.now(("l3a.st", i)))
                dve.wait_ge(T.sem, T.at("l3a.y"))
                nc.vector.tensor_copy(tB[:, :], ps[:, 0, 0:P]).then_inc(V.sem, V.now("l3a.y"))
                dve.wait_ge(T.sem, T.at("l3a.p"))
                vl(dve, nc.vector.tensor_copy(tC[:, :], ps[:, 4, 0:P]))
                vl(dve, nc.vector.tensor_tensor_reduce(tD[:, :], tC[:, :], tC[:, :], 1.0, 0.0, ALU.mult, ALU.add, s[:, 1:2]))
                nc.vector.tensor_scalar(mv[:, 2:3], s[:, 1:2], 1.0 / P, float(np.finfo(np.float32).eps), ALU.mult,
                                        ALU.add).then_inc(V.sem, V.now("l3a.ss"))
                dve.wait_ge(G.sem, G.at("l3a.rs"))
                nc.vector.tensor_scalar(tE[:, :], tC[:, :], mv[:, 3:4], None, ALU.mult).then_inc(V.sem, V.now("l3a.yn"))
                nc.vector.tensor_tensor(xb[:, :], tC[:, :], xs[:, x_at[tag], :], ALU.add)
                turn_vector(dve, "l3a.yn", tF, 5)
                dve.wait_ge(T.sem, T.at("l3a.fc"))
                vl(dve, nc.vector.tensor_scalar(probs[:, 0, BANK:2 * BANK], ps[:, 6, :], 0.0, None, ALU.max))
                nc.vector.tensor_tensor(probs[:, 0, 0:BANK], probs[:, 0, BANK:2 * BANK], probs[:, 0, BANK:2 * BANK],
                                        ALU.mult).then_inc(V.sem, V.now("l3a.fc"))
                end_vector(dve, tag, ps[:, 7, 0:P], xb[:, :], "l3a.cp")

            @on("act")
            def _(act):
                act.wait_ge(T.sem, T.at("l3a.z"))
                act.wait_ge(V.sem, V.at("l3a.nb"))
                nc.scalar.activation(tB[0:H, :], ps[0:H, 7, 0:P], ACT.Exp, bias=s[0:H, 0:1],
                                     scale=-1.0).then_inc(A.sem, A.now("l3a.z"))
                act.wait_ge(T.sem, T.at("l3a.kvq"))
                nc.scalar.copy(kx, ps[:, 0:2, :].rearrange("p a b -> p (a b)")).then_inc(A.sem, A.now("l3a.k"))
                nc.scalar.copy(qx, ps[:, 4:6, :].rearrange("p a b -> p (a b)")).then_inc(A.sem, A.now("l3a.q"))

            @on("pool")
            def _(pool):
                norm_gpsimd(pool, tag)
                nc.gpsimd.tensor_copy(probsT[0:H, 0:2, :].rearrange("p a (h n) -> p (a h) n", n=64),
                                      bc(ident[0:H, 0:H], 2, [H, H, 64])).then_inc(G.sem, G.now("l3a.sel"))
                pool.wait_ge(V.sem, V.at("l3a.ss"))
                nc.gpsimd.tensor_tensor(mv[:, 3:4], mv[:, 2:3], half[:, 0:1], ALU.pow).then_inc(G.sem, G.now("l3a.rs"))

        def l3f():
            tag = "l3f"
            start_plan(tag)
            T.plan("l3f.conf")
            V.plan("l3f.conf")
            A.plan("l3f.conf")
            V.plan("l3f.bm")
            A.plan("l3f.w")
            V.plan(*((tag, "g", g) for g in range(tag_groups[tag])), "l3f.comb")
            moe_plan(tag)
            V.plan("l3f.x")
            s = small4

            @on("pe")
            def _(pe):
                start_tensor(pe, tag)
                pe.wait_ge(V.sem, V.at("l3f.xn.T"))
                mm(ps[:, 7, 0:E], xnT[:, :], at["w_c.conf"]).then_inc(T.sem, T.now("l3f.conf"))
                loaded(pe, "w_l3f")
                loaded(pe, "w_l3d")
                moe_tensor(pe, tag, at["w_l3f.gate"], at["w_l3f.up"], at["w_l3d.down"], xnT[:, :], 4)

            @on("dve")
            def _(dve):
                dve.wait_ge(V.sem, V.at("l3a.x"))
                start_vector(dve, tag, None)
                dve.wait_ge(T.sem, T.at("l3f.conf"))
                nc.vector.tensor_tensor(s[:, 0:8], ps[:, 7, 0:E], at["conf_b"], ALU.add).then_inc(V.sem, V.now("l3f.conf"))
                dve.wait_ge(A.sem, A.at("l3f.conf"))
                vl(dve, nc.vector.tensor_scalar(s[:, 8:16], s[:, 8:16], 1.0, None, ALU.add))
                vl(dve, nc.vector.reciprocal(s[:, 8:16], s[:, 8:16]))
                vl(dve, nc.vector.tensor_tensor(s[:, 16:24], s[:, 8:16], at["wealth"], ALU.mult))
                nc.vector.tensor_reduce(s[:, 40:41], s[:, 16:24], AX.X, ALU.max, negate=True).then_inc(V.sem, V.now("l3f.bm"))
                gate_vector(dve, tag, 0)
                gate_vector(dve, tag, 1)
                top2(dve, s[:, 16:24], s[:, 24:32])
                for g in range(2, tag_groups[tag]):
                    gate_vector(dve, tag, g)
                dve.wait_ge(A.sem, A.at("l3f.w"))
                vl(dve, nc.vector.tensor_tensor_reduce(s[:, 32:40], s[:, 0:8], s[:, 24:32], 1.0, 0.0, ALU.mult, ALU.add,
                                                       s[:, 41:42]))
                vl(dve, nc.vector.reciprocal(s[:, 42:43], s[:, 41:42]))
                nc.vector.tensor_scalar(s[:, 48:56], s[:, 32:40], s[:, 42:43], None, ALU.mult).then_inc(
                    V.sem, V.now("l3f.comb"))
                dve.wait_ge(V.sem, V.at("l3f.comb"))
                mix_vector(dve, tag, s[:, 48:56], xs[:, x_at[tag], :], False)

            @on("act")
            def _(act):
                act.wait_ge(V.sem, V.at("l3f.conf"))
                nc.scalar.activation(s[:, 8:16], s[:, 0:8], ACT.Exp, scale=-1.0).then_inc(A.sem, A.now("l3f.conf"))
                act.wait_ge(V.sem, V.at("l3f.bm"))
                nc.scalar.activation(s[:, 0:8], s[:, 16:24], ACT.Exp, bias=s[:, 40:41]).then_inc(A.sem, A.now("l3f.w"))
                moe_scalar(act, tag, ACT.Silu, None)

            @on("pool")
            def _(pool):
                norm_gpsimd(pool, tag)

        paths = sbq[:, 0:3 * LEAVES].rearrange("p (n k) -> p n k", n=3)
        levels = sbq[:, 3 * LEAVES:3 * LEAVES + 2 * 3 * P].rearrange("p (a k) -> p a k", a=2)
        biases = shared[:, :]
        qheads = shared[:, 0:8 * P]
        dists = sb("dists", [H, 255])
        perm = sbq[:, 0:E * P]

        l0x()
        l0a()
        l0f()
        cross("l1x", "l0f.x", lambda n: at["w_l1x_" + n], float(1.0 / np.sqrt(P)), True, at["l1x_bq"], at["l1x_bv"],
              at["l1x_bo"], "w_a")
        l1a()
        l1f()
        cross("l2x", "l1f.x", lambda n: at["w_b.l2x_" + n], float(1.0 / np.sqrt(8.0)), False, None, None,
              at["l2x_b"], "w_b")
        l2a()
        l2f()
        l3x()
        l3a()
        l3f()

        @on("sp")
        def _(sp):
            sp.wait_ge(V.sem, V.at("l3f.x"))
            nc.sync.dma_start(out, xs[:, 1 - x_at["l3f"], :]).then_inc(stored, 16)
            sp.wait_ge(stored, 16)

        block = ctx.enter_context(nc.Block())

        @block.tensor
        def _(pe):
            for part in parts["pe"]:
                part(pe)

        @block.vector
        def _(dve):
            for part in parts["dve"]:
                part(dve)

        @block.scalar
        def _(act):
            for part in parts["act"]:
                part(act)

        @block.gpsimd
        def _(pool):
            for part in parts["pool"]:
                part(pool)

        @block.sync
        def _(sp):
            for part in parts["sp"]:
                part(sp)


def constants():
    i = np.arange(P)
    f = np.float32
    c = {"ident": np.eye(P, dtype=f), "causal": np.where(i[None, :] <= i[:, None], 0.0, HIDDEN).astype(f)}
    freq = (f(1.0) / np.power(f(10000.0), np.arange(0, 8, 2, dtype=f))).astype(f)
    angle = (i.astype(f)[:, None] * freq[None, :]).astype(f)
    c["cos"] = np.tile(np.repeat(np.cos(angle), 2, axis=1), (1, H))
    sin = np.stack([-np.sin(angle), np.sin(angle)], axis=2).reshape(P, 8)
    c["sin"] = np.tile(sin, (1, H))
    c["tri"] = (i[:, None] <= i[None, :])
    c["iota1"] = np.tile(i[None, :] + 1.0, (P, 1))
    c["hm8"] = (i[:, None] // 8 == np.arange(H)[None, :])
    c["hm4"] = (i[:, None] // 4 == np.arange(H)[None, :])
    c["bm8"] = (i[:, None] // 8 == i[None, :] // 8)
    c["bm4"] = (i[:, None] // 4 == i[None, :] // 4)
    e = np.arange(E)
    c["before"] = np.tile((e[None, :] < e[:, None]).reshape(1, E * E), (P, 1))
    c["gather"] = np.arange(15 * 16)[None, :] - 112 == 8 * (i[:, None] // 64) + i[:, None] % 8
    c["hm32"] = ((i[:, None] % 32) // 8 == np.arange(4)[None, :])
    c["hm32m"] = np.where(i[:, None] < 96, c["hm32"], i[:, None] == 96)
    c["strip"] = ((np.arange(2 * P - 8)[None, :] == 120 + i[:, None] % 32) & (i[:, None] % 32 < 8))
    c["flip"] = (i[:, None] + i[None, :] == P - 1)
    r = np.arange(64)
    ramp = np.linspace(0.0, 1.0, 64).astype(f)
    lag = r[None, :] - r[:, None]
    c["ramp"] = np.concatenate([np.where(lag >= 0, ramp[np.clip(lag, 0, 63)], 0.0), np.zeros((64, 64))])
    far = (np.abs(np.arange(255) - 127).astype(f) / f(P - 1)).astype(f)
    step = np.clip(np.round(far * f(63)), 0, 63)
    c["dist"] = (i[:, None] == step[None, :])
    far = np.arange(224) - 96
    c["place"] = (far[None, :] == 8 * (i[:, None] // 32) + i[:, None] % 32) & (i[:, None] % 32 < 8)
    c["places"] = (far[None, :] // 8 == i[:, None] // 32) & (i[:, None] % 32 == 8)
    c["leaf"] = np.tile(np.arange(LEAVES)[None, :], (P, 1))
    return {name: np.concatenate([c[n].astype(f).reshape(P, w) for n, w in pack], axis=1)
            for name, pack in (("first", FIRST), ("const", CONST))}


def packed(inputs):
    a = {k: np.asarray(v) for k, v in inputs.items()}

    def tall(m):
        n = m.shape[0] // P
        return m.reshape(n, P, -1).transpose(1, 0, 2).reshape(P, -1)

    def col(v, n=P):
        return np.concatenate([v.reshape(-1, 1), np.zeros((P - v.size, 1), v.dtype)]) if v.size < P else v.reshape(-1, P).T

    def pad(m):
        return np.concatenate([m, np.zeros((P - m.shape[0], m.shape[1]), m.dtype)])

    def side(parts, pack):
        got = [np.ascontiguousarray(p).reshape(P, -1) for p in parts]
        assert [g.shape[1] for g in got] == [w for _, w in pack], [(g.shape[1], n, w) for g, (n, w) in zip(got, pack)]
        return np.ascontiguousarray(np.concatenate(got, axis=1))

    def fourfold(m):
        return np.tile(m.reshape(-1, 4, 1, 32), (1, 1, 4, 1)).reshape(m.shape[0], 4 * P)

    def wider(m):
        m = m.reshape(-1, H, 4)
        return np.concatenate([m, np.zeros_like(m)], axis=2).reshape(-1, P)

    ws = a["L0_xattn_w_sim"]
    d = constants()
    d["x"] = a["x"].reshape(P, P)
    ctx = a["ctx_1024"].reshape(CTX, P)
    d["ctxT"] = np.ascontiguousarray(ctx.T)
    d["ctx"] = np.ascontiguousarray(ctx.reshape(KT_N, P, P).transpose(1, 0, 2))
    d["mask"] = a["mask_Bx1x1xS2_if1"].reshape(1, CTX)
    bq = a["L2_ffn_b_qkv"]
    d["cols"] = side([col(ws[P:2 * P]), col(ws[2 * P:]), col(a["L0_ffn_q_b"].reshape(H, 8)[:, :4].reshape(-1)),
                      col(a["L0_ffn_k_b"]), a["L0_ffn_b1"].reshape(16, P).T, fourfold(a["L1_xattn_bq"].reshape(1, P)).reshape(4, P).T, col(a["L1_xattn_bk"]), col(a["L1_xattn_bv"]),
                      col(bq[0:P]), col(bq[P:2 * P]), a["L2_ffn_b_fc"].reshape(32, P).T,
                      col(a["L3_attn_bm1"]), col(a["L3_attn_bm2"])], COLS)
    rows = [a["L0_xattn_b_sim"], ws[0:P], a["L0_xattn_b_qv"], a["L0_attn_bq"], a["L0_attn_bk"], a["L0_attn_bv"],
            a["L0_attn_bo"], wider(a["L0_ffn_v_b"]), a["L0_ffn_o_b"], a["L0_ffn_router_b"], a["L1_xattn_bo"],
            a["L1_attn_proj_bias"], a["L2_xattn_b_o"], a["L2_ffn_ln1_scale"], a["L2_ffn_ln1_bias"], bq[2 * P:],
            a["L2_ffn_b_attnproj"], a["L2_ffn_ln2_scale"], a["L2_ffn_ln2_bias"], a["L2_ffn_b_gate"],
            a["L3_xattn_gamma"], a["L3_ffn_conf_b"], a["L3_ffn_wealth"]]
    assert [r.size for r in rows] == [w for _, w in ROWS]
    d["rows"] = np.concatenate([r.reshape(-1) for r in rows])
    d["w_a"] = side([tall(a["L0_xattn_W_qv"]), a["L0_attn_Wq"], a["L0_attn_Wk"], a["L0_attn_Wv"], a["L0_attn_Wo"],
                     a["L0_ffn_q_w"].reshape(P, H, 8)[:, :, :4], a["L0_ffn_k_w"], wider(a["L0_ffn_v_w"]), wider(a["L0_ffn_o_w"][:64].T).T, a["L0_ffn_router_w"],
                     fourfold(a["L1_xattn_Wq"].T), a["L1_xattn_Wk"].T, a["L1_xattn_Wv"].T, a["L1_xattn_Wo"].T,
                     a["L1_attn_qkv_weight"].T, a["L1_attn_proj_weight"].T, pad(a["L2_attn_coeffs"][:, :64].T),
                     pad(a["L2_attn_Wpos"].T)], W_A)
    d["w_l0f"] = side([a["L0_ffn_w1"].transpose(1, 0, 2).reshape(P, -1), tall(a["L0_ffn_w2"].reshape(-1, P))], W_L0F)
    d["l0f_b2"] = a["L0_ffn_b2"].reshape(-1)
    for t in "qkvf":
        d["tree1_" + t] = np.concatenate([a[f"L1_ffn_{t}_w1"].transpose(0, 2, 1).reshape(LEAVES, -1),
                                          a[f"L1_ffn_{t}_b1"]], axis=1)
        d["tree2_" + t] = np.concatenate([a[f"L1_ffn_{t}_w2"].reshape(LEAVES, -1), a[f"L1_ffn_{t}_b2"]], axis=1)
    d["node"] = np.concatenate([a[f"L1_ffn_{t}_nw"].T for t in "qkvf"], axis=1)
    d["nbias"] = np.concatenate([a[f"L1_ffn_{t}_nb"] for t in "qkvf"])
    wkv = a["L3_xattn_w_kv"]
    d["w_b"] = side([fourfold(a["L2_xattn_W_q"]), a["L2_xattn_W_k"], a["L2_xattn_W_v"], a["L2_xattn_W_o"], a["L2_attn_Wqkv"].T,
                     a["L2_attn_Wout"].T, a["L2_ffn_w_qkv"], a["L2_ffn_w_attnproj"], a["L2_ffn_w_gate"],
                     a["L3_xattn_w_q"], tall(np.ascontiguousarray(wkv[:, :8 * P].T)), tall(np.ascontiguousarray(wkv[:, 8 * P:].T)),
                     tall(a["L3_xattn_w_out1"]), a["L3_xattn_w_out2"]], W_B)
    d["w_c"] = side([a["L3_attn_Wq"].T, a["L3_attn_Wk"].T, a["L3_attn_Wv"].T, a["L3_attn_Wm1"].T,
                     pad(a["L3_attn_Wm2"].T), a["L3_attn_Wproj"].T, a["L3_attn_Wfc"].T,
                     tall(np.ascontiguousarray(a["L3_attn_Wcp"].T)), a["L3_ffn_conf_w"].T], W_C)
    d["w_l2f"] = side([a["L2_ffn_w_fc"].transpose(1, 0, 2).reshape(P, -1), tall(a["L2_ffn_w_fcproj"].reshape(-1, P))],
                      W_L2F)
    d["l2f_b2"] = a["L2_ffn_b_fcproj"].reshape(-1)
    d["w_l3f"] = side([a["L3_ffn_gate_w"].transpose(2, 0, 1).reshape(P, -1),
                       a["L3_ffn_up_w"].transpose(2, 0, 1).reshape(P, -1)], W_L3F)
    d["w_l3d"] = side([tall(np.ascontiguousarray(a["L3_ffn_down_w"].transpose(0, 2, 1)).reshape(-1, P))], W_L3D)
    return {k: np.ascontiguousarray(v) for k, v in d.items()}


def kernel(**inputs):
    from concourse import bacc
    from concourse.bass_utils import run_bass_kernel_spmd

    arrays = packed(inputs)
    nc = bacc.Bacc("TRN2", target_bir_lowering=False, num_devices=1)
    dram = {}
    for n, v in arrays.items():
        dram[n] = nc.dram_tensor("in_" + n, v.shape, mybir.dt.from_np(v.dtype), kind="ExternalInput").ap()
    out = nc.dram_tensor("out_0", (P, P), F32, kind="ExternalOutput").ap()
    scratch = nc.dram_tensor("distance_rows", (H, 255), F32).ap()
    build(nc, dram, out, scratch)
    r = run_bass_kernel_spmd(nc, [{"in_" + n: v for n, v in arrays.items()}], core_ids=[0])
    return r.results[0]["out_0"].reshape(1, P, P)
```
